# Optimizing a Trainium2 kernel written in Bass

```python
import numpy as np
import jax
import jax.numpy as jnp

def _softmax(x, axis=-1):
    return jax.nn.softmax(x, axis=axis)

def _gelu(x):
    return jax.nn.gelu(x, approximate=True)

def _silu(x):
    return jax.nn.silu(x)

def _sigmoid(x):
    return jax.nn.sigmoid(x)

def _layernorm(x, axis=-1, eps=1e-05):
    m = jnp.mean(x, axis=axis, keepdims=True)
    v = jnp.var(x, axis=axis, keepdims=True)
    return (x - m) / jnp.sqrt(v + eps)

def _scatter_add(tgt, idx, src, axis=0):
    return tgt.at[idx].add(src)

def _segment_sum(src, seg, n):
    return jax.ops.segment_sum(src, seg, n)
kernel_name = 'mk_decoder_postln_d2_seqx_r4_4caf9d'

def setup_inputs(seed: int=0):
    np.random.seed(seed)
    _w = jnp.asarray

    def _rec_inputs():
        import jax
        import jax.numpy as jnp
        _rk = jax.random.key(seed)
        x = -0.0002928 + 1 * jax.random.normal(jax.random.fold_in(_rk, 1), (4, 1024, 256), jnp.float32)
        _lenS = 1024 - jax.random.randint(jax.random.fold_in(_rk, 7), (4,), 0, max(1, 1024 // 4) + 1, jnp.int32)
        _lenS2 = 64 - jax.random.randint(jax.random.fold_in(_rk, 8), (4,), 0, max(1, 64 // 4) + 1, jnp.int32)
        _ctx_1024P = jax.random.normal(jax.random.fold_in(_rk, 11), (4, 16, 256), jnp.float32)
        _ctx_1024c = jax.random.dirichlet(jax.random.fold_in(_rk, 511), 0.3 * jnp.ones((16,), jnp.float32), (4, 64))
        _ctx_1024t = jnp.einsum('bsk,bkd->bsd', _ctx_1024c, _ctx_1024P)
        _ctx_1024t = _ctx_1024t * jax.lax.rsqrt(jnp.mean(jnp.square(_ctx_1024t)) + 1e-12) * 0.953939
        ctx_1024 = -1.39393e-06 + 0.999914 * (_ctx_1024t + 0.3 * jax.random.normal(jax.random.fold_in(_rk, 611), (4, 64, 256), jnp.float32))
        return (x, ctx_1024)
    x, ctx_1024 = _rec_inputs()

    def _L0_attn_setup():
        import jax, jax.numpy as jnp
        import numpy as np
        from jax.scipy.linalg import solve_triangular
        B, L, D, H = (1, 512, 256, 4)
        DK = DV = D // H
        CONV = 4
        FIR_S, FIR_M, FIR_L = (3, 15, 63)
        CHUNK = 32

        def _l2norm(x):
            return x * jax.lax.rsqrt(jnp.sum(x * x, -1, keepdims=True) + 1e-06)

        def _short_conv(x, w):
            K = w.shape[-1]
            l = x.shape[1]
            xp = jnp.pad(x, ((0, 0), (K - 1, 0), (0, 0)))
            y = sum((xp[:, j:j + l, :] * w[:, j] for j in range(K)))
            return jax.nn.silu(y)

        def _fir(x, filt):
            b, l, h, d = x.shape
            K = filt.shape[-1]
            xf = jnp.transpose(x.reshape(b, l, h * d), (0, 2, 1))
            y = jax.lax.conv_general_dilated(xf, filt.reshape(h * d, 1, K), (1,), [(K - 1, 0)], feature_group_count=h * d)
            return jnp.transpose(y, (0, 2, 1)).reshape(b, l, h, d)

        def _delta_rule_chunkwise(q, k, v, beta):
            b, h, Lq, dk = q.shape
            c = CHUNK
            n = Lq // c
            q = _l2norm(q)
            k = _l2norm(k)
            v = v * beta[..., None]
            kb = k * beta[..., None]
            rs = lambda t: t.reshape(b, h, n, c, t.shape[-1])
            qc, kc, vc, kbc = (rs(q), rs(k), rs(v), rs(kb))
            tri_strict = jnp.tril(jnp.ones((c, c), bool), -1)
            A = jnp.where(tri_strict, -(kbc @ jnp.swapaxes(kc, -1, -2)), 0.0)
            eye = jnp.eye(c, dtype=q.dtype)
            M = eye - A
            T = solve_triangular(M, jnp.broadcast_to(eye, M.shape), lower=True)
            u = T @ vc
            w = T @ kbc
            causal = jnp.tril(jnp.ones((c, c), bool))

            def step(S, inp):
                q_i, k_i, u_i, w_i = inp
                attn = jnp.where(causal, q_i @ jnp.swapaxes(k_i, -1, -2), 0.0)
                u_adj = u_i - w_i @ S
                o_i = q_i @ S + attn @ u_adj
                return (S + jnp.swapaxes(k_i, -1, -2) @ u_adj, o_i)
            S0 = jnp.zeros((b, h, dk, v.shape[-1]), q.dtype)
            mv = lambda t: jnp.moveaxis(t, 2, 0)
            _, o = jax.lax.scan(step, S0, (mv(qc), mv(kc), mv(u), mv(w)))
            return jnp.moveaxis(o, 0, 2).reshape(b, h, Lq, -1)

        def _rmsnorm(x, w, eps=1e-05):
            return x * jax.lax.rsqrt(jnp.mean(x * x, -1, keepdims=True) + eps) * w
        key = jax.random.key(seed)
        ks = jax.random.split(key, 16)
        wn = lambda k, shape, s: jax.random.normal(k, shape, jnp.float32) * s

        def fir_init(k, K):
            f = jnp.zeros((H, DV, K), jnp.float32).at[..., -1].set(1.0)
            return f + wn(k, (H, DV, K), 0.01)
        return {'hidden_states': jax.random.normal(ks[0], (B, L, D), jnp.float32), 'Wq': wn(ks[1], (D, D), 0.02), 'Wk': wn(ks[2], (D, D), 0.02), 'Wv': wn(ks[3], (D, D), 0.02), 'Wb': wn(ks[4], (H, D), 0.02), 'conv_q': wn(ks[5], (D, CONV), 0.1), 'conv_k': wn(ks[6], (D, CONV), 0.1), 'conv_v': wn(ks[7], (D, CONV), 0.1), 'fir_s': fir_init(ks[8], FIR_S), 'fir_m': fir_init(ks[9], FIR_M), 'fir_l': fir_init(ks[10], FIR_L), 'gate_w': wn(ks[11], (H, 5, D), 1.0 / np.sqrt(D)), 'gate_b': jnp.zeros((H, 5), jnp.float32), 'log_temp': jnp.zeros((H, 1), jnp.float32), 'eps_param': jnp.full((H, 1), 0.02, jnp.float32), 'norm_w': jnp.ones((DV,), jnp.float32), 'Wo': wn(ks[12], (D, D), 0.02)}
    _L0_attn_all = _L0_attn_setup()
    _L0_attn_in = {k: v for k, v in _L0_attn_all.items() if k in ('Wq', 'Wk', 'Wv', 'Wb', 'conv_q', 'conv_k', 'conv_v', 'fir_s', 'fir_m', 'fir_l', 'gate_w', 'gate_b', 'log_temp', 'eps_param', 'norm_w', 'Wo')}
    del _L0_attn_all

    def _L0_xattn_setup():
        import jax, jax.numpy as jnp
        import numpy as np
        DMODEL = 256
        NHEAD = 16
        DHEAD = DMODEL // NHEAD

        def _layernorm(x, g, b, eps=1e-05):
            mu = jnp.mean(x, axis=-1, keepdims=True)
            var = jnp.var(x, axis=-1, keepdims=True)
            return (x - mu) * jax.lax.rsqrt(var + eps) * g + b
        key = jax.random.key(seed)
        ks = jax.random.split(key, 12)
        b, lq, lv, d = (2, 512, 512, DMODEL)
        s = 1.0 / np.sqrt(d)
        return {'q': jax.random.normal(ks[0], (b, lq, d), jnp.float32), 'k': jax.random.normal(ks[1], (b, lv, d), jnp.float32), 'v': jax.random.normal(ks[2], (b, lv, d), jnp.float32), 'qln_g': jnp.ones((d,), jnp.float32), 'qln_b': jnp.zeros((d,), jnp.float32), 'kvln_g': jnp.ones((d,), jnp.float32), 'kvln_b': jnp.zeros((d,), jnp.float32), 'Wq': jax.random.normal(ks[3], (d, d), jnp.float32) * s, 'Wk': jax.random.normal(ks[4], (d, d), jnp.float32) * s, 'Wv': jax.random.normal(ks[5], (d, d), jnp.float32) * s, 'Wg': jax.random.normal(ks[6], (d, d), jnp.float32) * s, 'bg': jnp.zeros((d,), jnp.float32), 'Wo': jax.random.normal(ks[7], (d, d), jnp.float32) * s}
    _L0_xattn_all = _L0_xattn_setup()
    _L0_xattn_in = {k: v for k, v in _L0_xattn_all.items() if k in ('qln_g', 'qln_b', 'kvln_g', 'kvln_b', 'Wq', 'Wk', 'Wv', 'Wg', 'bg', 'Wo')}
    del _L0_xattn_all

    def _L0_ffn_setup():
        import jax, jax.numpy as jnp
        import numpy as np
        E, D, F = (8, 256, 1024)
        B, S = (4, 512)

        def _layernorm(x, g, b, eps=1e-05):
            mu = jnp.mean(x, axis=-1, keepdims=True)
            var = jnp.var(x, axis=-1, keepdims=True)
            return (x - mu) * jax.lax.rsqrt(var + eps) * g + b
        key = jax.random.key(seed)
        ks = jax.random.split(key, 5)
        return {'input_features': jax.random.normal(ks[0], (B, S, D), jnp.float32), 'centroids': jax.random.normal(ks[1], (E, D), jnp.float32) * 0.1, 'ln_g': jnp.ones((E, D), jnp.float32), 'ln_b': jnp.zeros((E, D), jnp.float32), 'w1': jax.random.normal(ks[2], (E, F, D), jnp.float32) * (1.0 / np.sqrt(D).astype(np.float32)), 'b1': jnp.zeros((E, F), jnp.float32), 'w2': jax.random.normal(ks[3], (E, D, F), jnp.float32) * (1.0 / np.sqrt(F).astype(np.float32)), 'b2': jnp.zeros((E, D), jnp.float32)}
    _L0_ffn_all = _L0_ffn_setup()
    _L0_ffn_in = {k: v for k, v in _L0_ffn_all.items() if k in ('centroids', 'ln_g', 'ln_b', 'w1', 'b1', 'w2', 'b2')}
    del _L0_ffn_all

    def _L1_attn_setup():
        import jax, jax.numpy as jnp
        import numpy as np
        B, T, D, H = (4, 512, 256, 16)
        HD = D // H

        def l2_norm(x, eps=1e-12):
            return x / jnp.maximum(jnp.linalg.norm(x, axis=-1, keepdims=True), eps)
        key = jax.random.key(seed)
        ks = jax.random.split(key, 11)
        std = 0.02
        w = lambda k, shape: jax.random.normal(k, shape, jnp.float32) * std
        return dict(x=jax.random.normal(ks[0], (B, T, D), jnp.float32), Wq=w(ks[1], (D, D)), Wk=w(ks[2], (D, D)), Wv=w(ks[3], (D, D)), Wgamma=w(ks[4], (D, H)), Wf1=w(ks[5], (D, HD)), Wf2=w(ks[6], (HD, D)), Wog1=w(ks[7], (D, HD)), Wog2=w(ks[8], (HD, D)), norm_w=jnp.ones((D,), jnp.float32), Wo=w(ks[9], (D, D)))
    _L1_attn_all = _L1_attn_setup()
    _L1_attn_in = {k: v for k, v in _L1_attn_all.items() if k in ('Wq', 'Wk', 'Wv', 'Wgamma', 'Wf1', 'Wf2', 'Wog1', 'Wog2', 'norm_w', 'Wo')}
    del _L1_attn_all

    def _L1_xattn_setup():
        import jax, jax.numpy as jnp
        import numpy as np
        DIM = 256
        NUM_HEADS = 16
        HEAD_DIM = DIM // NUM_HEADS
        key = jax.random.key(seed)
        ks = jax.random.split(key, 11)
        B, N, C = (2, 512, DIM)
        s = 1.0 / np.sqrt(C)
        inp = {'q': jax.random.normal(ks[0], (B, N, C), jnp.float32), 'k': jax.random.normal(ks[1], (B, N, C), jnp.float32), 'v': jax.random.normal(ks[2], (B, N, C), jnp.float32), 'Wq': jax.random.normal(ks[3], (C, C), jnp.float32) * s, 'bq': jnp.zeros((C,), jnp.float32), 'Wk': jax.random.normal(ks[4], (C, C), jnp.float32) * s, 'bk': jnp.zeros((C,), jnp.float32), 'Wv': jax.random.normal(ks[5], (C, C), jnp.float32) * s, 'bv': jnp.zeros((C,), jnp.float32), 'Wo': jax.random.normal(ks[6], (C, C), jnp.float32) * s, 'bo': jnp.zeros((C,), jnp.float32)}
        return inp
    _L1_xattn_all = _L1_xattn_setup()
    _L1_xattn_in = {k: v for k, v in _L1_xattn_all.items() if k in ('Wq', 'bq', 'Wk', 'bk', 'Wv', 'bv', 'Wo', 'bo')}
    del _L1_xattn_all

    def _L1_ffn_setup():
        import jax, jax.numpy as jnp
        import numpy as np
        BITS = 8
        LORA_RANK = 16
        LORA_ALPHA = 32
        SCALING = LORA_ALPHA / LORA_RANK

        def fake_quant_weight(w, bits=BITS):
            qmax = 2.0 ** (bits - 1) - 1
            scale = jnp.max(jnp.abs(w)) / qmax
            wq = jnp.clip(jnp.round(w / scale), -qmax - 1, qmax) * scale
            return w + jax.lax.stop_gradient(wq - w)

        def qat_lora_linear(x, W, b, A, B):
            Wq = fake_quant_weight(W)
            base = jnp.einsum('bsi,oi->bso', x, Wq) + b
            lora = jnp.einsum('bsr,or->bso', jnp.einsum('bsi,ri->bsr', x, A), B)
            return base + SCALING * lora
        key = jax.random.key(seed)
        ks = jax.random.split(key, 9)
        d, f = (256, 1024)
        s_in = 1.0 / np.sqrt(d)
        s_ff = 1.0 / np.sqrt(f)
        return {'hidden_states': jax.random.normal(ks[0], (4, 512, d), jnp.float32), 'W_fc': jax.random.normal(ks[1], (f, d), jnp.float32) * s_in, 'b_fc': jnp.zeros((f,), jnp.float32), 'A_fc': jax.random.normal(ks[2], (LORA_RANK, d), jnp.float32) * s_in, 'B_fc': jnp.zeros((f, LORA_RANK), jnp.float32), 'W_proj': jax.random.normal(ks[3], (d, f), jnp.float32) * s_ff, 'b_proj': jnp.zeros((d,), jnp.float32), 'A_proj': jax.random.normal(ks[4], (LORA_RANK, f), jnp.float32) * s_ff, 'B_proj': jnp.zeros((d, LORA_RANK), jnp.float32)}
    _L1_ffn_all = _L1_ffn_setup()
    _L1_ffn_in = {k: v for k, v in _L1_ffn_all.items() if k in ('W_fc', 'b_fc', 'A_fc', 'B_fc', 'W_proj', 'b_proj', 'A_proj', 'B_proj')}
    del _L1_ffn_all
    return {'x': x, 'ctx_1024': ctx_1024, 'L0_attn_Wq': _L0_attn_in['Wq'], 'L0_attn_Wk': _L0_attn_in['Wk'], 'L0_attn_Wv': _L0_attn_in['Wv'], 'L0_attn_Wb': _L0_attn_in['Wb'], 'L0_attn_conv_q': _L0_attn_in['conv_q'], 'L0_attn_conv_k': _L0_attn_in['conv_k'], 'L0_attn_conv_v': _L0_attn_in['conv_v'], 'L0_attn_fir_s': _L0_attn_in['fir_s'], 'L0_attn_fir_m': _L0_attn_in['fir_m'], 'L0_attn_fir_l': _L0_attn_in['fir_l'], 'L0_attn_gate_w': _L0_attn_in['gate_w'], 'L0_attn_gate_b': _L0_attn_in['gate_b'], 'L0_attn_log_temp': _L0_attn_in['log_temp'], 'L0_attn_eps_param': _L0_attn_in['eps_param'], 'L0_attn_norm_w': _L0_attn_in['norm_w'], 'L0_attn_Wo': _L0_attn_in['Wo'], 'L0_xattn_qln_g': _L0_xattn_in['qln_g'], 'L0_xattn_qln_b': _L0_xattn_in['qln_b'], 'L0_xattn_kvln_g': _L0_xattn_in['kvln_g'], 'L0_xattn_kvln_b': _L0_xattn_in['kvln_b'], 'L0_xattn_Wq': _L0_xattn_in['Wq'], 'L0_xattn_Wk': _L0_xattn_in['Wk'], 'L0_xattn_Wv': _L0_xattn_in['Wv'], 'L0_xattn_Wg': _L0_xattn_in['Wg'], 'L0_xattn_bg': _L0_xattn_in['bg'], 'L0_xattn_Wo': _L0_xattn_in['Wo'], 'L0_ffn_centroids': _L0_ffn_in['centroids'], 'L0_ffn_ln_g': _L0_ffn_in['ln_g'], 'L0_ffn_ln_b': _L0_ffn_in['ln_b'], 'L0_ffn_w1': _L0_ffn_in['w1'], 'L0_ffn_b1': _L0_ffn_in['b1'], 'L0_ffn_w2': _L0_ffn_in['w2'], 'L0_ffn_b2': _L0_ffn_in['b2'], 'L1_attn_Wq': _L1_attn_in['Wq'], 'L1_attn_Wk': _L1_attn_in['Wk'], 'L1_attn_Wv': _L1_attn_in['Wv'], 'L1_attn_Wgamma': _L1_attn_in['Wgamma'], 'L1_attn_Wf1': _L1_attn_in['Wf1'], 'L1_attn_Wf2': _L1_attn_in['Wf2'], 'L1_attn_Wog1': _L1_attn_in['Wog1'], 'L1_attn_Wog2': _L1_attn_in['Wog2'], 'L1_attn_norm_w': _L1_attn_in['norm_w'], 'L1_attn_Wo': _L1_attn_in['Wo'], 'L1_xattn_Wq': _L1_xattn_in['Wq'], 'L1_xattn_bq': _L1_xattn_in['bq'], 'L1_xattn_Wk': _L1_xattn_in['Wk'], 'L1_xattn_bk': _L1_xattn_in['bk'], 'L1_xattn_Wv': _L1_xattn_in['Wv'], 'L1_xattn_bv': _L1_xattn_in['bv'], 'L1_xattn_Wo': _L1_xattn_in['Wo'], 'L1_xattn_bo': _L1_xattn_in['bo'], 'L1_ffn_W_fc': _L1_ffn_in['W_fc'], 'L1_ffn_b_fc': _L1_ffn_in['b_fc'], 'L1_ffn_A_fc': _L1_ffn_in['A_fc'], 'L1_ffn_B_fc': _L1_ffn_in['B_fc'], 'L1_ffn_W_proj': _L1_ffn_in['W_proj'], 'L1_ffn_b_proj': _L1_ffn_in['b_proj'], 'L1_ffn_A_proj': _L1_ffn_in['A_proj'], 'L1_ffn_B_proj': _L1_ffn_in['B_proj']}

def reference(x, ctx_1024, L0_attn_Wq, L0_attn_Wk, L0_attn_Wv, L0_attn_Wb, L0_attn_conv_q, L0_attn_conv_k, L0_attn_conv_v, L0_attn_fir_s, L0_attn_fir_m, L0_attn_fir_l, L0_attn_gate_w, L0_attn_gate_b, L0_attn_log_temp, L0_attn_eps_param, L0_attn_norm_w, L0_attn_Wo, L0_xattn_qln_g, L0_xattn_qln_b, L0_xattn_kvln_g, L0_xattn_kvln_b, L0_xattn_Wq, L0_xattn_Wk, L0_xattn_Wv, L0_xattn_Wg, L0_xattn_bg, L0_xattn_Wo, L0_ffn_centroids, L0_ffn_ln_g, L0_ffn_ln_b, L0_ffn_w1, L0_ffn_b1, L0_ffn_w2, L0_ffn_b2, L1_attn_Wq, L1_attn_Wk, L1_attn_Wv, L1_attn_Wgamma, L1_attn_Wf1, L1_attn_Wf2, L1_attn_Wog1, L1_attn_Wog2, L1_attn_norm_w, L1_attn_Wo, L1_xattn_Wq, L1_xattn_bq, L1_xattn_Wk, L1_xattn_bk, L1_xattn_Wv, L1_xattn_bv, L1_xattn_Wo, L1_xattn_bo, L1_ffn_W_fc, L1_ffn_b_fc, L1_ffn_A_fc, L1_ffn_B_fc, L1_ffn_W_proj, L1_ffn_b_proj, L1_ffn_A_proj, L1_ffn_B_proj):
    import jax
    import jax.numpy as jnp

    def _L0_attn_ref(hidden_states, Wq, Wk, Wv, Wb, conv_q, conv_k, conv_v, fir_s, fir_m, fir_l, gate_w, gate_b, log_temp, eps_param, norm_w, Wo):
        import jax, jax.numpy as jnp
        import numpy as np
        from jax.scipy.linalg import solve_triangular
        B, L, D, H = (1, 512, 256, 4)
        DK = DV = D // H
        CONV = 4
        FIR_S, FIR_M, FIR_L = (3, 15, 63)
        CHUNK = 32

        def _l2norm(x):
            return x * jax.lax.rsqrt(jnp.sum(x * x, -1, keepdims=True) + 1e-06)

        def _short_conv(x, w):
            K = w.shape[-1]
            l = x.shape[1]
            xp = jnp.pad(x, ((0, 0), (K - 1, 0), (0, 0)))
            y = sum((xp[:, j:j + l, :] * w[:, j] for j in range(K)))
            return jax.nn.silu(y)

        def _fir(x, filt):
            b, l, h, d = x.shape
            K = filt.shape[-1]
            xf = jnp.transpose(x.reshape(b, l, h * d), (0, 2, 1))
            y = jax.lax.conv_general_dilated(xf, filt.reshape(h * d, 1, K), (1,), [(K - 1, 0)], feature_group_count=h * d)
            return jnp.transpose(y, (0, 2, 1)).reshape(b, l, h, d)

        def _delta_rule_chunkwise(q, k, v, beta):
            b, h, Lq, dk = q.shape
            c = CHUNK
            n = Lq // c
            q = _l2norm(q)
            k = _l2norm(k)
            v = v * beta[..., None]
            kb = k * beta[..., None]
            rs = lambda t: t.reshape(b, h, n, c, t.shape[-1])
            qc, kc, vc, kbc = (rs(q), rs(k), rs(v), rs(kb))
            tri_strict = jnp.tril(jnp.ones((c, c), bool), -1)
            A = jnp.where(tri_strict, -(kbc @ jnp.swapaxes(kc, -1, -2)), 0.0)
            eye = jnp.eye(c, dtype=q.dtype)
            M = eye - A
            T = solve_triangular(M, jnp.broadcast_to(eye, M.shape), lower=True)
            u = T @ vc
            w = T @ kbc
            causal = jnp.tril(jnp.ones((c, c), bool))

            def step(S, inp):
                q_i, k_i, u_i, w_i = inp
                attn = jnp.where(causal, q_i @ jnp.swapaxes(k_i, -1, -2), 0.0)
                u_adj = u_i - w_i @ S
                o_i = q_i @ S + attn @ u_adj
                return (S + jnp.swapaxes(k_i, -1, -2) @ u_adj, o_i)
            S0 = jnp.zeros((b, h, dk, v.shape[-1]), q.dtype)
            mv = lambda t: jnp.moveaxis(t, 2, 0)
            _, o = jax.lax.scan(step, S0, (mv(qc), mv(kc), mv(u), mv(w)))
            return jnp.moveaxis(o, 0, 2).reshape(b, h, Lq, -1)

        def _rmsnorm(x, w, eps=1e-05):
            return x * jax.lax.rsqrt(jnp.mean(x * x, -1, keepdims=True) + eps) * w
        b, l, d = hidden_states.shape
        q = _short_conv(hidden_states @ Wq.T, conv_q).reshape(b, l, H, DK)
        k = _short_conv(hidden_states @ Wk.T, conv_k).reshape(b, l, H, DK)
        v_direct = _short_conv(hidden_states @ Wv.T, conv_v).reshape(b, l, H, DV)
        beta = jax.nn.sigmoid(hidden_states @ Wb.T)
        tp = lambda t: jnp.transpose(t, (0, 2, 1, 3))
        delta_out = tp(_delta_rule_chunkwise(tp(q), tp(k), tp(v_direct), jnp.transpose(beta, (0, 2, 1))))
        local_s = _fir(v_direct, fir_s)
        local_m = _fir(v_direct, fir_m)
        local_l = _fir(v_direct, fir_l)
        logits = jnp.einsum('bld,hpd->blhp', hidden_states, gate_w) + gate_b
        temp = jnp.exp(log_temp).reshape(1, 1, H, 1)
        probs = jax.nn.softmax(logits / temp, -1)
        eps = jnp.clip(eps_param, 0.0, 0.2).reshape(1, 1, H, 1)
        probs = probs * (1.0 - 5.0 * eps) + eps
        o = probs[..., 0:1] * local_s + probs[..., 1:2] * local_m + probs[..., 2:3] * local_l + probs[..., 3:4] * delta_out + probs[..., 4:5] * v_direct
        o = _rmsnorm(o, norm_w)
        return o.reshape(b, l, H * DV) @ Wo.T

    def _L0_xattn_ref(q, k, v, qln_g, qln_b, kvln_g, kvln_b, Wq, Wk, Wv, Wg, bg, Wo):
        import jax, jax.numpy as jnp
        import numpy as np
        DMODEL = 256
        NHEAD = 16
        DHEAD = DMODEL // NHEAD

        def _layernorm(x, g, b, eps=1e-05):
            mu = jnp.mean(x, axis=-1, keepdims=True)
            var = jnp.var(x, axis=-1, keepdims=True)
            return (x - mu) * jax.lax.rsqrt(var + eps) * g + b
        b, lq, d = q.shape
        lv = v.shape[1]
        qn = _layernorm(q, qln_g, qln_b)
        q_ = qn @ Wq.T
        kk = _layernorm(k, kvln_g, kvln_b) @ Wk.T
        vv = _layernorm(v, kvln_g, kvln_b) @ Wv.T
        qh = q_.reshape(b, lq, NHEAD, DHEAD)
        kh = kk.reshape(b, lv, NHEAD, DHEAD)
        vh = vv.reshape(b, lv, NHEAD, DHEAD)
        scores = jnp.einsum('bqhd,bkhd->bhqk', qh, kh) / np.sqrt(DHEAD)
        attn = jax.nn.softmax(scores, axis=-1)
        y = jnp.einsum('bhqk,bkhd->bqhd', attn, vh).reshape(b, lq, d)
        g = jax.nn.sigmoid(qn @ Wg.T + bg)
        return y * g @ Wo.T

    def _L0_ffn_ref(input_features, centroids, ln_g, ln_b, w1, b1, w2, b2):
        import jax, jax.numpy as jnp
        import numpy as np
        E, D, F = (8, 256, 1024)
        B, S = (4, 512)

        def _layernorm(x, g, b, eps=1e-05):
            mu = jnp.mean(x, axis=-1, keepdims=True)
            var = jnp.var(x, axis=-1, keepdims=True)
            return (x - mu) * jax.lax.rsqrt(var + eps) * g + b
        Bf, Sf, Df = input_features.shape
        x = input_features.reshape(-1, Df)
        aff = x @ centroids.T
        assign = jnp.argmax(aff, axis=1)
        order = jnp.argsort(assign)
        xs = x[order]
        es = assign[order]
        alpha = jax.nn.sigmoid(jnp.take_along_axis(aff[order], es[:, None], axis=1))
        nE = centroids.shape[0]
        y = jnp.zeros_like(xs)
        for e in range(nE):
            h = _layernorm(xs, ln_g[e], ln_b[e])
            h = jax.nn.relu(h @ w1[e].T + b1[e])
            ye = xs + h @ w2[e].T + b2[e]
            y = y + jnp.where((es == e)[:, None], ye, 0.0)
        out_sorted = alpha * y + (1.0 - alpha) * xs
        inv = jnp.argsort(order)
        return out_sorted[inv].reshape(Bf, Sf, Df)

    def _L1_attn_ref(x, Wq, Wk, Wv, Wgamma, Wf1, Wf2, Wog1, Wog2, norm_w, Wo):
        import jax, jax.numpy as jnp
        import numpy as np
        B, T, D, H = (4, 512, 256, 16)
        HD = D // H

        def l2_norm(x, eps=1e-12):
            return x / jnp.maximum(jnp.linalg.norm(x, axis=-1, keepdims=True), eps)
        b, n, d = x.shape
        q = jax.nn.silu(x @ Wq)
        k = jax.nn.silu(x @ Wk)
        v = x @ Wv
        log_f = jax.nn.log_sigmoid(x @ Wf1 @ Wf2)
        gamma = -jax.nn.sigmoid(x @ Wgamma)
        q = q.reshape(b, n, H, HD)
        k = l2_norm(k.reshape(b, n, H, HD))
        v = v.reshape(b, n, H, HD)
        gk = log_f.reshape(b, n, H, HD)
        a = k * gamma[..., None] * jnp.exp(gk)

        def step(S, inp):
            qt, kt, vt, at, gkt = inp
            S = S * jnp.exp(gkt)[..., None]
            sab = jnp.einsum('bhk,bhkv->bhv', at, S)
            S = S + kt[..., None] * (sab[..., None, :] + vt[..., None, :])
            ot = jnp.einsum('bhk,bhkv->bhv', qt, S)
            return (S, ot)
        seq = tuple((jnp.moveaxis(t, 1, 0) for t in (q, k, v, a, gk)))
        S0 = jnp.zeros((b, H, HD, HD), x.dtype)
        _, o = jax.lax.scan(step, S0, seq)
        o = jnp.moveaxis(o, 0, 1).reshape(b, n, d)
        o = o * jax.nn.sigmoid(x @ Wog1 @ Wog2)
        mu = o.mean(-1, keepdims=True)
        var = ((o - mu) ** 2).mean(-1, keepdims=True)
        o = (o - mu) * jax.lax.rsqrt(var + 1e-05) * norm_w
        return o @ Wo

    def _L1_xattn_ref(q, k, v, Wq, bq, Wk, bk, Wv, bv, Wo, bo):
        import jax, jax.numpy as jnp
        import numpy as np
        DIM = 256
        NUM_HEADS = 16
        HEAD_DIM = DIM // NUM_HEADS
        B, Nq, C = q.shape
        Nkv = k.shape[1]
        H, D = (NUM_HEADS, HEAD_DIM)
        qh = (q @ Wq.T + bq).reshape(B, Nq, H, D).transpose(0, 2, 1, 3)
        kh = (k @ Wk.T + bk).reshape(B, Nkv, H, D).transpose(0, 2, 1, 3)
        vh = (v @ Wv.T + bv).reshape(B, Nkv, H, D).transpose(0, 2, 1, 3)
        scale = D ** (-0.5)
        attn = jax.nn.softmax(jnp.einsum('bhqd,bhkd->bhqk', qh, kh) * scale, axis=-1)
        out = jnp.einsum('bhqk,bhkd->bhqd', attn, vh)
        out = out.transpose(0, 2, 1, 3).reshape(B, Nq, C)
        return out @ Wo.T + bo

    def _L1_ffn_ref(hidden_states, W_fc, b_fc, A_fc, B_fc, W_proj, b_proj, A_proj, B_proj):
        import jax, jax.numpy as jnp
        import numpy as np
        BITS = 8
        LORA_RANK = 16
        LORA_ALPHA = 32
        SCALING = LORA_ALPHA / LORA_RANK

        def fake_quant_weight(w, bits=BITS):
            qmax = 2.0 ** (bits - 1) - 1
            scale = jnp.max(jnp.abs(w)) / qmax
            wq = jnp.clip(jnp.round(w / scale), -qmax - 1, qmax) * scale
            return w + jax.lax.stop_gradient(wq - w)

        def qat_lora_linear(x, W, b, A, B):
            Wq = fake_quant_weight(W)
            base = jnp.einsum('bsi,oi->bso', x, Wq) + b
            lora = jnp.einsum('bsr,or->bso', jnp.einsum('bsi,ri->bsr', x, A), B)
            return base + SCALING * lora
        h = qat_lora_linear(hidden_states, W_fc, b_fc, A_fc, B_fc)
        h = jax.nn.gelu(h, approximate=False)
        h = qat_lora_linear(h, W_proj, b_proj, A_proj, B_proj)
        return h
    x = _layernorm(x + _L0_attn_ref(x, L0_attn_Wq, L0_attn_Wk, L0_attn_Wv, L0_attn_Wb, L0_attn_conv_q, L0_attn_conv_k, L0_attn_conv_v, L0_attn_fir_s, L0_attn_fir_m, L0_attn_fir_l, L0_attn_gate_w, L0_attn_gate_b, L0_attn_log_temp, L0_attn_eps_param, L0_attn_norm_w, L0_attn_Wo), axis=-1)
    x = _layernorm(x + _L0_xattn_ref(x, ctx_1024, ctx_1024, L0_xattn_qln_g, L0_xattn_qln_b, L0_xattn_kvln_g, L0_xattn_kvln_b, L0_xattn_Wq, L0_xattn_Wk, L0_xattn_Wv, L0_xattn_Wg, L0_xattn_bg, L0_xattn_Wo), axis=-1)
    x = _layernorm(x + _L0_ffn_ref(x, L0_ffn_centroids, L0_ffn_ln_g, L0_ffn_ln_b, L0_ffn_w1, L0_ffn_b1, L0_ffn_w2, L0_ffn_b2), axis=-1)
    x = _layernorm(x + _L1_attn_ref(x, L1_attn_Wq, L1_attn_Wk, L1_attn_Wv, L1_attn_Wgamma, L1_attn_Wf1, L1_attn_Wf2, L1_attn_Wog1, L1_attn_Wog2, L1_attn_norm_w, L1_attn_Wo), axis=-1)
    x = _layernorm(x + _L1_xattn_ref(x, ctx_1024, ctx_1024, L1_xattn_Wq, L1_xattn_bq, L1_xattn_Wk, L1_xattn_bk, L1_xattn_Wv, L1_xattn_bv, L1_xattn_Wo, L1_xattn_bo), axis=-1)
    x = _layernorm(x + _L1_ffn_ref(x, L1_ffn_W_fc, L1_ffn_b_fc, L1_ffn_A_fc, L1_ffn_B_fc, L1_ffn_W_proj, L1_ffn_b_proj, L1_ffn_A_proj, L1_ffn_B_proj), axis=-1)
    return x

_drawn_inputs = setup_inputs


def setup_inputs(seed=0):
    import zlib

    import numpy as np

    out = dict(_drawn_inputs(seed))
    spreads = {'L0_attn_gate_b': (0.0, 0.279),
     'L0_attn_log_temp': (0.0, 0.397),
     'L0_attn_eps_param': (0.019999999552965164, 0.6),
     'L0_attn_norm_w': (1.0, 0.2),
     'L0_xattn_qln_g': (1.0, 0.2),
     'L0_xattn_qln_b': (0.0, 0.1),
     'L0_xattn_kvln_g': (1.0, 0.2),
     'L0_xattn_kvln_b': (0.0, 0.1),
     'L0_xattn_bg': (0.0, 0.1),
     'L0_ffn_ln_g': (1.0, 0.2),
     'L0_ffn_ln_b': (0.0, 0.28),
     'L0_ffn_b1': (0.0, 0.269),
     'L0_ffn_b2': (0.0, 0.1),
     'L1_attn_norm_w': (1.0, 0.2),
     'L1_xattn_bq': (0.0, 0.387),
     'L1_xattn_bk': (0.0, 0.8),
     'L1_xattn_bv': (0.0, 0.1),
     'L1_xattn_bo': (0.0, 0.1),
     'L1_ffn_b_fc': (0.0, 0.1),
     'L1_ffn_B_fc': (0.0, 0.1),
     'L1_ffn_b_proj': (0.0, 0.1),
     'L1_ffn_B_proj': (0.0, 0.1)}
    factors = {'L1_attn_Wgamma': 8.0,
     'L1_attn_Wf1': 8.0,
     'L1_attn_Wf2': 8.0,
     'L1_attn_Wog1': 8.0,
     'L1_attn_Wog2': 8.0}
    for name, (base, spread) in spreads.items():
        noise = np.random.default_rng([zlib.crc32(name.encode()), seed]).standard_normal(out[name].shape)
        drawn = base * np.exp(spread * noise) if base else spread * noise
        out[name] = jnp.asarray(drawn.astype(out[name].dtype))
    for name, factor in factors.items():
        out[name] = (out[name] * factor).astype(out[name].dtype)
    return out
```

```python
from contextlib import ExitStack

import concourse.bass as bass
from concourse import mybir

STAGES = (0, 1, 2, 3, 4, 5)

P = 128
D = 256
C2 = D // P
BATCH = 4
SEQ = 1024
TOK = BATCH * SEQ
NT = 512
TILES = TOK // NT
EPS = 1e-5

F32 = mybir.dt.float32
I32 = mybir.dt.int32
U32 = mybir.dt.uint32
ALU = mybir.AluOpType
ACT = mybir.ActivationFunctionType
AX = mybir.AxisListType
ds = bass.ds


class Phase:

    def __init__(self, nc, name):
        self.nc, self.name, self.ctx, self.sems = nc, name, ExitStack(), []

    def __enter__(self):
        self.ctx.__enter__()
        return self

    def __exit__(self, *a):
        self.ctx.__exit__(*a)
        if self.sems:
            self.nc.clear_and_free_semaphores(self.sems)
            self.nc.all_engine_barrier()

    def sb(self, name, shape, dt=F32):
        return self.ctx.enter_context(self.nc.sbuf_tensor(f"{self.name}_{name}", shape, dt))

    def ps(self, name, shape, dt=F32):
        return self.ctx.enter_context(self.nc.psum_tensor(f"{self.name}_{name}", shape, dt))

    def sem(self, name):
        self.sems.append(self.nc.alloc_semaphore(f"{self.name}_{name}"))
        return self.sems[-1]

    def block(self):
        return self.ctx.enter_context(self.nc.Block())


def recurrence_stage(nc, X, ones_mean, w):
    HEADS, HD = 16, D // 16
    with Phase(nc, "rec") as ph:
        G = ph.sb("out_gate", [P, C2, TOK])
        Wo = ph.sb("Wo", [P, C2, D])
        norm_w = ph.sb("norm_w", [P, C2])
        epsb = ph.sb("epsb", [P, 1])
        scratch = {n: nc.dram_tensor(f"rec_{n}", (D, TOK), F32).ap() for n in ("q", "k", "f", "a", "v", "o")}

        with Phase(nc, "recA") as pa:
            W = {n: pa.sb(n, [P, C2, D]) for n in ("Wq", "Wk", "Wv", "Wf", "Wog", "Wga")}
            small = {n: pa.sb(n, [HD, D]) for n in ("Wf1", "Wf2", "Wog1", "Wog2")}
            wgamma = pa.sb("wgamma", [P, C2, HEADS])
            group_ones = pa.sb("group_ones", [P, P])
            bufs = {n: [pa.sb(f"{n}{b}", [P, C2, NT]) for b in range(2)]
                    for n in ("sigq", "sigk", "q", "k", "f", "sg", "v", "norm", "ff", "a")}
            slot = [pa.ps(f"slot{s}", [P, C2, NT]) for s in range(4)]
            full = [pa.sem(f"slot_full{s}") for s in range(4)]
            free = [pa.sem(f"slot_free{s}") for s in range(4)]
            USE = {"q": (0, 0), "k": (1, 0), "f": (2, 0), "ga": (3, 0), "og": (0, 1), "v": (1, 1), "ss": (2, 1)}
            PER = [2, 2, 2, 1]
            loaded = pa.sem("loaded")
            consts = pa.sem("consts")
            fold_psum = pa.sem("fold_psum")
            folded = pa.sem("folded")
            weights_ready = pa.sem("weights_ready")
            sig_done = {n: pa.sem(f"{n}_done") for n in ("sigq", "sigk", "f", "sg", "og", "v", "sq", "norm")}
            did = {n: pa.sem(f"did_{n}") for n in ("q", "k", "clamp", "rn", "kn", "a", "ff", "fff")}
            stored = [pa.sem(f"stored{b}") for b in range(2)]
            block = pa.block()

            def slot_free(pe, n, key):
                s, u = USE[key]
                pe.wait_ge(free[s], n * PER[s] + (u + 1))
                return slot[s], full[s]

            def slot_full(eng, n, key):
                s, u = USE[key]
                eng.wait_ge(full[s], n * PER[s] + (u + 1))
                return slot[s], free[s]

            def buffers_free(eng, i, b):
                eng.wait_ge(stored[b], (i + 1) * 80)

            @block.sync
            def _(sp):
                for n in ("Wq", "Wk", "Wv"):
                    sp.dma_start(W[n][:], w[f"L1_attn_{n}"].rearrange("(c p) o -> p c o", p=P)).then_inc(loaded, 16)
                sp.dma_start(Wo[:], w["L1_attn_Wo"].rearrange("(c p) o -> p c o", p=P)).then_inc(loaded, 16)
                for n in small:
                    sp.dma_start(small[n][:], w[f"L1_attn_{n}"]).then_inc(loaded, 16)
                sp.dma_start(wgamma[:], w["L1_attn_Wgamma"].rearrange("(c p) o -> p c o", p=P)).then_inc(loaded, 16)
                sp.dma_start(norm_w[:], w["L1_attn_norm_w"]).then_inc(loaded, 16)
                sp.sem_inc(stored[0], 80)
                sp.sem_inc(stored[1], 80)
                with sp.Fori(0, TILES // 2) as i:
                    for b in range(2):
                        n = i * 2 + b
                        for name, sem, buf in (("v", sig_done["v"], "v"), ("f", sig_done["f"], "f"), ("q", did["q"], "q"),
                                               ("k", did["kn"], "k"), ("a", did["a"], "a")):
                            sp.wait_ge(sem, n + 1)
                            sp.dma_start(scratch[name].rearrange("(c p) t -> p c t", p=P)[:, :, ds(n * NT, NT)],
                                         bufs[buf][b][:]).then_inc(stored[b], 16)
                for b in range(2):
                    sp.wait_ge(stored[b], 80 * (TILES // 2 + 1))

            @block.gpsimd
            def _(pool):
                nc.gpsimd.memset(group_ones[:], 1.0).then_inc(consts, 1)
                pool.wait_ge(consts, 1)
                g3 = group_ones[:].rearrange("p (h c) -> p h c", c=HD)
                nc.gpsimd.affine_select(out=g3, in_=g3, compare_op=ALU.is_ge, fill=0.0, base=0,
                                        pattern=[[-HD, P // HD], [0, HD]], channel_multiplier=1).then_inc(consts, 1)
                pool.wait_ge(consts, 2)
                nc.gpsimd.affine_select(out=g3, in_=g3, compare_op=ALU.is_ge, fill=0.0, base=HD - 1,
                                        pattern=[[HD, P // HD], [0, HD]], channel_multiplier=-1).then_inc(consts, 1)
                with pool.Fori(0, TILES // 2) as i:
                    for b in range(2):
                        n = i * 2 + b
                        buffers_free(pool, i, b)
                        pool.wait_ge(sig_done["f"], n + 1)
                        pool.wait_ge(sig_done["sg"], n + 1)
                        nc.gpsimd.tensor_tensor(bufs["ff"][b][:], bufs["f"][b][:], bufs["f"][b][:], ALU.mult).then_inc(did["ff"], 1)
                        pool.wait_ge(did["ff"], n + 1)
                        nc.gpsimd.tensor_tensor(bufs["ff"][b][:], bufs["ff"][b][:], bufs["sg"][b][:], ALU.mult).then_inc(did["fff"], 1)

            @block.tensor
            def _(pe):
                pe.wait_ge(loaded, 16 * 10)
                pe.wait_ge(consts, 3)
                for s, (a, bb) in enumerate((("Wf1", "Wf2"), ("Wog1", "Wog2"))):
                    for c in range(C2):
                        mm = nc.tensor.matmul(slot[s][:, c, 0:D], small[a][:, P * c:P * c + P], small[bb][:], start=True, stop=True)
                mm.then_inc(fold_psum, 1)
                pe.wait_ge(weights_ready, 1)

                def project(n, key, name):
                    dst, sem = slot_free(pe, n, key)
                    for c in range(C2):
                        for kk in range(C2):
                            mm = nc.tensor.matmul(dst[:, c, :], W[name][:, kk, P * c:P * c + P], X[:, kk, ds(n * NT, NT)],
                                                  start=(kk == 0), stop=(kk == C2 - 1))
                    mm.then_inc(sem, 1)

                with pe.Fori(0, TILES // 2) as i:
                    for b in range(2):
                        n = i * 2 + b
                        for key, name in (("k", "Wk"), ("q", "Wq"), ("f", "Wf"), ("ga", "Wga"), ("og", "Wog"), ("v", "Wv")):
                            project(n, key, name)
                        pe.wait_ge(sig_done["sq"], n + 1)
                        dst, sem = slot_free(pe, n, "ss")
                        for c in range(C2):
                            mm = nc.tensor.matmul(dst[:, c, :], group_ones[:], bufs["norm"][b][:, c, :], start=True, stop=True)
                        mm.then_inc(sem, 1)

            @block.scalar
            def _(act):
                with act.Fori(0, TILES // 2) as i:
                    for b in range(2):
                        n = i * 2 + b
                        buffers_free(act, i, b)

                        def read(key, out, func, done, frees):
                            src, sem = slot_full(act, n, key)
                            nc.scalar.activation(out, src[:], func).then_inc(sig_done[done], 1)
                            if frees:
                                act.wait_ge(sig_done[done], n + 1)
                                act.sem_inc(sem, 1)
                        read("k", bufs["sigk"][b][:], ACT.Sigmoid, "sigk", False)
                        read("q", bufs["sigq"][b][:], ACT.Sigmoid, "sigq", False)
                        read("f", bufs["f"][b][:], ACT.Sigmoid, "f", True)
                        read("ga", bufs["sg"][b][:], ACT.Sigmoid, "sg", True)
                        read("og", G[:, :, ds(n * NT, NT)], ACT.Sigmoid, "og", True)
                        act.wait_ge(did["k"], n + 1)
                        nc.scalar.activation(bufs["norm"][b][:], bufs["k"][b][:], ACT.Square).then_inc(sig_done["sq"], 1)
                        read("v", bufs["v"][b][:], ACT.Copy, "v", True)
                        read("ss", bufs["norm"][b][:], ACT.Sqrt, "norm", True)

            @block.vector
            def _(dve):
                nc.vector.memset(epsb[:], EPS)
                dve.wait_ge(loaded, 16 * 10)
                nc.vector.tensor_copy(W["Wga"][:].rearrange("p c (h k) -> p c h k", k=HD),
                                      wgamma[:].unsqueeze(3).to_broadcast([P, C2, HEADS, HD])).then_inc(folded, 1)
                for c in range(C2):
                    nc.vector.tensor_scalar(Wo[:, c, :], Wo[:, c, :], norm_w[:, c:c + 1], None, ALU.mult).then_inc(folded, 1)
                dve.wait_ge(fold_psum, 1)
                nc.vector.tensor_copy(W["Wf"][:], slot[0][:, :, 0:D]).then_inc(folded, 1)
                nc.vector.tensor_copy(W["Wog"][:], slot[1][:, :, 0:D]).then_inc(folded, 1)
                dve.wait_ge(folded, 5)
                for s in range(4):
                    dve.sem_inc(free[s], 1)
                dve.sem_inc(weights_ready, 1)
                with dve.Fori(0, TILES // 2) as i:
                    for b in range(2):
                        n = i * 2 + b
                        buffers_free(dve, i, b)
                        for key in ("k", "q"):
                            dve.wait_ge(sig_done["sig" + key], n + 1)
                            src, sem = slot_full(dve, n, key)
                            nc.vector.tensor_tensor(bufs[key][b][:], src[:], bufs["sig" + key][b][:], ALU.mult).then_inc(did[key], 1)
                            dve.wait_ge(did[key], n + 1)
                            dve.sem_inc(sem, 1)
                        dve.wait_ge(sig_done["norm"], n + 1)
                        nrm = bufs["norm"][b][:]
                        nc.vector.tensor_scalar(nrm, nrm, 1e-12, None, ALU.max).then_inc(did["clamp"], 1)
                        dve.wait_ge(did["clamp"], n + 1)
                        nc.vector.reciprocal(nrm, nrm).then_inc(did["rn"], 1)
                        dve.wait_ge(did["rn"], n + 1)
                        nc.vector.tensor_tensor(bufs["k"][b][:], bufs["k"][b][:], nrm, ALU.mult).then_inc(did["kn"], 1)
                        dve.wait_ge(did["kn"], n + 1)
                        dve.wait_ge(did["fff"], n + 1)
                        nc.vector.scalar_tensor_tensor(out=bufs["a"][b][:], in0=bufs["k"][b][:], scalar=-1.0,
                                                       in1=bufs["ff"][b][:], op0=ALU.mult, op1=ALU.mult).then_inc(did["a"], 1)

        with Phase(nc, "recB") as pb:
            SEG = 128
            GR = 8
            GPS = SEG // GR
            VH = HD // 2
            FA = [pb.sb(f"fa{b}", [P, 2, HD, SEG]) for b in range(2)]
            K = [pb.sb(f"k{b}", [P, HD, SEG]) for b in range(2)]
            Q = [pb.sb(f"q{b}", [P, HD, SEG]) for b in range(2)]
            V = [pb.sb(f"v{b}", [P, VH, SEG]) for b in range(2)]
            O = [pb.sb(f"o{b}", [P, VH, SEG]) for b in range(2)]
            hist = [pb.sb(f"hist{b}", [P, GR, VH, HD]) for b in range(2)]
            U = pb.sb("U", [P, 2, VH, HD])
            T = pb.sb("T", [P, VH, HD])
            sab = pb.sb("sab", [P, VH])
            wv = pb.sb("wv", [P, VH])
            prod = [pb.sb(f"prod{b}", [P, GR, VH, HD]) for b in range(2)]
            seg_loaded = [pb.sem(f"seg_loaded{b}") for b in range(2)]
            seg_read = pb.sem("seg_read")
            step = pb.sem("step")
            group_done = pb.sem("group_done")
            prod_done = pb.sem("prod_done")
            halved = pb.sem("halved")
            out_done = pb.sem("out_done")
            out_stored = [pb.sem(f"out_stored{b}") for b in range(2)]
            block = pb.block()
            NSEG = SEQ // SEG

            def loads(sp, s, b):
                t0 = s * SEG
                for bt in range(BATCH):
                    for vh in range(2):
                        p0 = bt * 32 + vh * 16
                        for name, dst in (("f", FA[b][p0:p0 + 16, 0, :, :]), ("a", FA[b][p0:p0 + 16, 1, :, :]),
                                          ("k", K[b][p0:p0 + 16, :, :]), ("q", Q[b][p0:p0 + 16, :, :])):
                            src = scratch[name].rearrange("(h c) t -> h c t", c=HD)[:, :, ds(bt * SEQ + t0, SEG)]
                            sp.dma_start(dst, src).then_inc(seg_loaded[b], 16)
                        src = scratch["v"].rearrange("(h x c) t -> h x c t", c=VH, x=2)[:, vh, :, ds(bt * SEQ + t0, SEG)]
                        sp.dma_start(V[b][p0:p0 + 16, :, :], src).then_inc(seg_loaded[b], 16)

            def stores(sp, s, b):
                for bt in range(BATCH):
                    for vh in range(2):
                        p0 = bt * 32 + vh * 16
                        dst = scratch["o"].rearrange("(h x c) t -> h x c t", c=VH, x=2)[:, vh, :, ds(bt * SEQ + s * SEG, SEG)]
                        sp.dma_start(dst, O[b][p0:p0 + 16, :, :]).then_inc(out_stored[b], 16)

            @block.sync
            def _(sp):
                loads(sp, 0, 0)
                loads(sp, 1, 1)
                sp.sem_inc(out_stored[0], 128)
                sp.sem_inc(out_stored[1], 128)
                with sp.Fori(0, NSEG // 2 - 1) as i:
                    for b in range(2):
                        s = i * 2 + b
                        sp.wait_ge(out_done, (s + 1) * GPS)
                        stores(sp, s, b)
                        loads(sp, s + 2, b)
                for b in range(2):
                    s = NSEG - 2 + b
                    sp.wait_ge(out_done, (s + 1) * GPS)
                    stores(sp, s, b)
                for b in range(2):
                    sp.wait_ge(out_stored[b], 128 * (NSEG // 2 + 1))

            @block.vector
            def _(dve):
                nc.vector.memset(hist[1][:, GR - 1, :, :], 0.0).then_inc(step, 1)
                dve.sem_inc(prod_done, 2)
                dve.wait_ge(step, 1)
                dve.sem_clear(step)
                with dve.Fori(0, NSEG // 2) as i:
                    for b in range(2):
                        with dve.Fori(0, GPS // 2) as g:
                            for par in range(2):
                                dve.wait_ge(seg_loaded[b], (i + 1) * 640)
                                dve.wait_ge(prod_done, i * (2 * GPS) + g * 2 + (b * GPS + par + 1))
                                n = 0
                                for j in range(GR):
                                    prev = hist[par][:, j - 1, :, :] if j else hist[1 - par][:, GR - 1, :, :]
                                    t = ds(g * (2 * GR) + (par * GR + j), 1)
                                    fa = FA[b][:, :, :, t].rearrange("p x k t -> p x (k t)")
                                    kt = K[b][:, :, t].rearrange("p k t -> p (k t)")
                                    vt = V[b][:, :, t].rearrange("p v t -> p (v t)")
                                    nc.vector.tensor_tensor(U[:], prev.unsqueeze(1).to_broadcast([P, 2, VH, HD]),
                                                            fa.unsqueeze(2).to_broadcast([P, 2, VH, HD]), ALU.mult).then_inc(step, 1)
                                    dve.wait_ge(step, n + 1)
                                    nc.vector.tensor_reduce(sab[:], U[:, 1, :, :], AX.X, ALU.add).then_inc(step, 1)
                                    dve.wait_ge(step, n + 2)
                                    nc.vector.tensor_tensor(wv[:], sab[:], vt, ALU.add).then_inc(step, 1)
                                    dve.wait_ge(step, n + 3)
                                    nc.vector.tensor_tensor(T[:], wv[:].unsqueeze(2).to_broadcast([P, VH, HD]),
                                                            kt.unsqueeze(1).to_broadcast([P, VH, HD]), ALU.mult).then_inc(step, 1)
                                    dve.wait_ge(step, n + 4)
                                    nc.vector.tensor_tensor(hist[par][:, j, :, :], U[:, 0, :, :], T[:], ALU.add).then_inc(step, 1)
                                    dve.wait_ge(step, n + 5)
                                    n += 5
                                dve.sem_clear(step)
                                dve.sem_inc(group_done, 1)

            @block.gpsimd
            def _(pool):
                with pool.Fori(0, NSEG // 2) as i:
                    for b in range(2):
                        with pool.Fori(0, GPS // 2) as g:
                            for par in range(2):
                                n = i * (2 * GPS) + g * 2 + (b * GPS + par)
                                pool.wait_ge(out_stored[b], (i + 1) * 128)
                                pool.wait_ge(seg_loaded[b], (i + 1) * 640)
                                pool.wait_ge(group_done, n + 1)
                                t = ds(g * (2 * GR) + par * GR, GR)
                                nc.gpsimd.tensor_tensor(prod[par][:], hist[par][:],
                                                        Q[b][:, :, t].rearrange("p k t -> p t k").unsqueeze(2).to_broadcast([P, GR, VH, HD]),
                                                        ALU.mult).then_inc(prod_done, 1)
                                pool.wait_ge(prod_done, n + 3)
                                pr = prod[par]
                                for h, width in enumerate((8, 4, 2)):
                                    nc.gpsimd.tensor_tensor(pr[:, :, :, 0:width], pr[:, :, :, 0:width],
                                                            pr[:, :, :, width:2 * width], ALU.add).then_inc(halved, 1)
                                    pool.wait_ge(halved, n * 3 + (h + 1))
                                nc.gpsimd.tensor_tensor(O[b][:, :, t].rearrange("p v t -> p t v"), pr[:, :, :, 0],
                                                        pr[:, :, :, 1], ALU.add).then_inc(out_done, 1)

        with Phase(nc, "recC") as pc:
            O = [pc.sb(f"o{b}", [P, C2, NT]) for b in range(2)]
            OG = pc.sb("og", [P, C2, NT])
            XC = pc.sb("XC", [P, C2, NT])
            SQ = pc.sb("SQ", [P, C2, NT])
            R = pc.sb("R", [P, C2, NT])
            std = pc.sb("std", [P, NT])
            rstd = pc.sb("rstd", [P, NT])
            ps_m = pc.ps("ps_m", [P, NT])
            ps_v = pc.ps("ps_v", [P, NT])
            ps_o = pc.ps("ps_o", [P, C2, NT])
            o_loaded = [pc.sem(f"o_loaded{b}") for b in range(2)]
            og_done = pc.sem("og_done")
            mean_psum = pc.sem("mean_psum")
            centred = pc.sem("centred")
            squared = pc.sem("squared")
            var_psum = pc.sem("var_psum")
            std_done = pc.sem("std_done")
            rstd_done = pc.sem("rstd_done")
            on_done = pc.sem("on_done")
            o_psum = pc.sem("o_psum")
            resid = pc.sem("resid")
            x_done = pc.sem("x_done")
            block = pc.block()

            @block.sync
            def _(sp):
                src = scratch["o"].rearrange("(c p) t -> p c t", p=P)
                for b in range(2):
                    sp.dma_start(O[b][:], src[:, :, NT * b:NT * b + NT]).then_inc(o_loaded[b], 16)
                with sp.Fori(0, TILES // 2 - 1) as i:
                    for b in range(2):
                        sp.wait_ge(og_done, i * 2 + (b + 1))
                        sp.dma_start(O[b][:], src[:, :, ds((i * 2 + (b + 2)) * NT, NT)]).then_inc(o_loaded[b], 16)

            @block.tensor
            def _(pe):
                def stat(n, which):
                    src = (OG, R)[which]
                    if which == 0:
                        pe.wait_ge(og_done, n + 1)
                    else:
                        pe.wait_ge(resid, n + 1)
                    for c in range(C2):
                        mm = nc.tensor.matmul(ps_m[:], ones_mean[:], src[:, c, :], start=(c == 0), stop=(c == C2 - 1))
                    mm.then_inc(mean_psum, 1)
                    pe.wait_ge(squared, n * 2 + (which + 1))
                    for c in range(C2):
                        mm = nc.tensor.matmul(ps_v[:], ones_mean[:], SQ[:, c, :], start=(c == 0), stop=(c == C2 - 1))
                    mm.then_inc(var_psum, 1)

                with pe.Fori(0, TILES // 2) as i:
                    for b in range(2):
                        n = i * 2 + b
                        stat(n, 0)
                        pe.wait_ge(on_done, n + 1)
                        for c in range(C2):
                            for kk in range(C2):
                                mm = nc.tensor.matmul(ps_o[:, c, :], Wo[:, kk, P * c:P * c + P], XC[:, kk, :],
                                                      start=(kk == 0), stop=(kk == C2 - 1))
                        mm.then_inc(o_psum, 1)
                        stat(n, 1)

            @block.scalar
            def _(act):
                with act.Fori(0, TILES // 2) as i:
                    for b in range(2):
                        n = i * 2 + b
                        for which in range(2):
                            act.wait_ge(centred, n * 2 + (which + 1))
                            nc.scalar.activation(SQ[:], XC[:], ACT.Square).then_inc(squared, 1)
                            act.wait_ge(var_psum, n * 2 + (which + 1))
                            nc.scalar.activation(std[:], ps_v[:], ACT.Sqrt, bias=epsb[:, 0:1]).then_inc(std_done, 1)

            @block.vector
            def _(dve):
                bc = lambda ap: ap.unsqueeze(1).to_broadcast([P, C2, NT])

                def centre(n, which, src):
                    dve.wait_ge(mean_psum, n * 2 + (which + 1))
                    nc.vector.tensor_tensor(XC[:], src, bc(ps_m[:]), ALU.subtract).then_inc(centred, 1)
                    dve.wait_ge(centred, n * 2 + (which + 1))
                    dve.wait_ge(std_done, n * 2 + (which + 1))
                    nc.vector.reciprocal(rstd[:], std[:]).then_inc(rstd_done, 1)
                    dve.wait_ge(rstd_done, n * 2 + (which + 1))

                with dve.Fori(0, TILES // 2) as i:
                    for b in range(2):
                        n = i * 2 + b
                        tile = X[:, :, ds(n * NT, NT)]
                        dve.wait_ge(o_loaded[b], (i + 1) * 16)
                        nc.vector.tensor_tensor(OG[:], O[b][:], G[:, :, ds(n * NT, NT)], ALU.mult).then_inc(og_done, 1)
                        dve.wait_ge(og_done, n + 1)
                        centre(n, 0, OG[:])
                        nc.vector.tensor_tensor(XC[:], XC[:], bc(rstd[:]), ALU.mult).then_inc(on_done, 1)
                        dve.wait_ge(o_psum, n + 1)
                        nc.vector.tensor_tensor(R[:], ps_o[:], tile, ALU.add).then_inc(resid, 1)
                        dve.wait_ge(resid, n + 1)
                        centre(n, 1, R[:])
                        nc.vector.tensor_tensor(tile, XC[:], bc(rstd[:]), ALU.mult).then_inc(x_done, 1)


def cross_attention_stage(nc, X, ones_mean, ident, w, gated):
    HEADS, DH, KEYS = 16, D // 16, 64
    HC = HEADS // C2
    PAIRS = HEADS // 2
    PC = PAIRS // C2
    CT = BATCH * KEYS
    CHUNKS = NT // P
    pre = "L0_xattn" if gated else "L1_xattn"
    with Phase(nc, "xg" if gated else "xp") as ph:
        names = ["Wq", "Wk", "Wv", "Wo"] + (["Wg"] if gated else [])
        W = {n: ph.sb(n, [P, C2, D]) for n in names}
        vecs = (["qln_g", "qln_b", "kvln_g", "kvln_b", "bg"] if gated else ["bq", "bk", "bv", "bo"])
        V = {n: ph.sb(n, [P, C2]) for n in vecs}
        bias = {n: ph.sb(f"bias_{n}", [P, C2]) for n in (["q", "k", "v", "g"] if gated else [])}
        if not gated:
            bias = {"q": V["bq"], "k": V["bk"], "v": V["bv"]}
        CTX = ph.sb("ctx", [P, C2, CT])
        CXC = ph.sb("ctx_centred", [P, C2, CT])
        CSQ = ph.sb("ctx_squared", [P, C2, CT])
        cstd = ph.sb("ctx_std", [P, CT])
        crstd = ph.sb("ctx_rstd", [P, CT])
        ctx2 = ph.sb("ctx2", [P, C2, 2, KEYS])
        KT = ph.sb("KT", [P, C2, KEYS])
        head_mask = ph.sb("head_mask", [P, HC])
        pair_mask = ph.sb("pair_mask", [P, PC, P])
        VT = ph.sb("VT", [P, D])
        kblk = ph.sb("kblk", [P, C2, HC, KEYS])
        vblk = ph.sb("vblk", [P, PAIRS, P])
        epsb = ph.sb("epsb", [P, 1])
        N = ph.sb("normed", [P, C2, NT]) if gated else None
        G = ph.sb("gate", [P, C2, NT]) if gated else None
        QT = ph.sb("QT", [P, C2, NT])
        MX = ph.sb("MX", [P, 2, HEADS])
        SUM = ph.sb("SUM", [P, 2, HEADS])
        RIN = ph.sb("RIN", [P, 2, HEADS])
        S = ph.sb("S", [P, 2, HEADS * KEYS])
        E = ph.sb("E", [P, 2, HEADS * KEYS])
        PN = ph.sb("PN", [P, 2, HEADS * KEYS])
        PT = ph.sb("PT", [P, PAIRS, NT])
        Y = ph.sb("Y", [P, C2, NT])
        R = ph.sb("R", [P, C2, NT])
        XC = ph.sb("XC", [P, C2, NT])
        SQ = ph.sb("SQ", [P, C2, NT])
        std = ph.sb("std", [P, NT])
        rstd = ph.sb("rstd", [P, NT])
        ps_s = [ph.ps(f"ps_s{b}", [P, HEADS * KEYS]) for b in range(2)]
        ps_t = ph.ps("ps_t", [P, PAIRS, P])
        bank = [ph.ps(f"bank{b}", [P, NT]) for b in range(2)]
        loaded = ph.sem("loaded")
        masks_done = ph.sem("masks_done")
        prep = ph.sem("prep")
        full = [ph.sem(f"bank_full{b}") for b in range(2)]
        free = [ph.sem(f"bank_free{b}") for b in range(2)]
        ctx_squared = ph.sem("ctx_squared_done")
        ctx_std = ph.sem("ctx_std_done")
        ctx_ready = ph.sem("ctx_ready")
        ctx2_ready = ph.sem("ctx2_ready")
        kv_copied = ph.sem("kv_copied")
        blocks_ready = ph.sem("blocks_ready")
        centred = ph.sem("centred")
        squared = ph.sem("squared")
        std_done = ph.sem("std_done")
        rstd_done = ph.sem("rstd_done")
        normed = ph.sem("normed_done")
        q_ready = ph.sem("q_ready")
        g_ready = ph.sem("g_ready")
        scores = ph.sem("scores")
        max_done = ph.sem("max_done")
        shifted = ph.sem("shifted")
        exp_done = ph.sem("exp_done")
        sum_done = ph.sem("sum_done")
        rinv_done = ph.sem("rinv_done")
        norm_done = ph.sem("norm_done")
        turned = ph.sem("turned")
        pt_ready = ph.sem("pt_ready")
        y_ready = ph.sem("y_ready")
        resid = ph.sem("resid")
        x_done = ph.sem("x_done")
        block = ph.block()

        PRE = [0, 0]
        pre_uses = {}
        if gated:
            for n, key in enumerate(["cmean", "cvar"] + [("bias", v, c) for v in "qkvg" for c in range(C2)]):
                pre_uses[key] = (n % 2, PRE[n % 2])
                PRE[n % 2] += 1
        order = [("k", 0), ("k", 1), "v"]
        for t in range(2):
            if gated:
                order += [("m1", t), ("s1", t)]
            order += [("q", 0, t), ("q", 1, t)]
            if gated:
                order += [("g", 0, t), ("g", 1, t)]
            order += [("y", 0, t), ("y", 1, t), ("o", 0, t), ("o", 1, t), ("m2", t), ("s2", t)]
        use, per = {}, [0, 0]
        for n, key in enumerate(order):
            use[key] = (n % 2, per[n % 2])
            per[n % 2] += 1

        def at(b, key):
            k, n = use[key]
            return k, b * per[k] + (PRE[k] + n + 1)

        def wait_free(pe, b, key):
            k, n = at(b, key) if key in use else (pre_uses[key][0], pre_uses[key][1] + 1)
            pe.wait_ge(free[k], n)
            return bank[k], full[k]

        def wait_full(eng, b, key):
            k, n = at(b, key) if key in use else (pre_uses[key][0], pre_uses[key][1] + 1)
            eng.wait_ge(full[k], n)
            return bank[k], free[k]

        @block.sync
        def _(sp):
            for n in names:
                sp.dma_start(W[n][:], w[f"{pre}_{n}"].rearrange("(c p) o -> p c o", p=P)).then_inc(loaded, 16)
            for n in vecs:
                sp.dma_start(V[n][:], w[f"{pre}_{n}"]).then_inc(loaded, 16)
            sp.dma_start(CTX[:], w["ctx_1024"].rearrange("(c p) t -> p c t", p=P)).then_inc(loaded, 16)
        LOADED = 16 * (len(names) + len(vecs) + 1)
        kv_src = CXC if gated else CTX

        @block.gpsimd
        def _(pool):
            nc.gpsimd.memset(head_mask[:], 1.0).then_inc(masks_done, 1)
            pool.wait_ge(masks_done, 1)
            nc.gpsimd.affine_select(out=head_mask[:], in_=head_mask[:], compare_op=ALU.is_ge, fill=0.0, base=0,
                                    pattern=[[-DH, HC]], channel_multiplier=1).then_inc(masks_done, 1)
            pool.wait_ge(masks_done, 2)
            nc.gpsimd.affine_select(out=head_mask[:], in_=head_mask[:], compare_op=ALU.is_ge, fill=0.0, base=DH - 1,
                                    pattern=[[DH, HC]], channel_multiplier=-1).then_inc(masks_done, 1)
            nc.gpsimd.memset(pair_mask[:], 0.0).then_inc(masks_done, 1)
            pool.wait_ge(masks_done, 4)
            for hh in range(2):
                for j in range(PC):
                    f0 = DH * (2 * j + hh)
                    nc.gpsimd.memset(pair_mask[KEYS * hh:KEYS * hh + KEYS, j, f0:f0 + DH], 1.0).then_inc(masks_done, 1)
            with pool.Fori(0, BATCH) as b:
                for t in range(2):
                    for k in range(CHUNKS):
                        n = CHUNKS * t + k
                        pool.wait_ge(rinv_done, b * (2 * CHUNKS) + n + 1)
                        pool.wait_ge(turned, b * (2 * CHUNKS) + n + 1 - 2 + 2)
                        nc.gpsimd.tensor_tensor(PN[:, k % 2, :].rearrange("p (h k) -> p h k", h=HEADS),
                                                E[:, k % 2, :].rearrange("p (h k) -> p h k", h=HEADS),
                                                RIN[:, k % 2, :].unsqueeze(2).to_broadcast([P, HEADS, KEYS]),
                                                ALU.mult).then_inc(norm_done, 1)

        @block.tensor
        def _(pe):
            pe.wait_ge(loaded, LOADED)
            pe.sem_inc(turned, 2)

            def accumulate(dst, pairs):
                for n, (lhs, rhs) in enumerate(pairs):
                    mm = nc.tensor.matmul(dst, lhs, rhs, start=(n == 0), stop=(n == len(pairs) - 1))
                return mm

            if gated:
                dst, sem = wait_free(pe, 0, "cmean")
                accumulate(dst[:, 0:CT], [(ones_mean[:], CTX[:, c, :]) for c in range(C2)]).then_inc(sem, 1)
                dst, sem = wait_free(pe, 0, "cvar")
                pe.wait_ge(ctx_squared, 1)
                accumulate(dst[:, 0:CT], [(ones_mean[:], CSQ[:, c, :]) for c in range(C2)]).then_inc(sem, 1)
                for v in "qkvg":
                    for c in range(C2):
                        dst, sem = wait_free(pe, 0, ("bias", v, c))
                        lnb = V["kvln_b"] if v in "kv" else V["qln_b"]
                        accumulate(dst[:, 0:1], [(W["W" + v][:, kk, P * c:P * c + P], lnb[:, kk:kk + 1])
                                                 for kk in range(C2)]).then_inc(sem, 1)
            pe.wait_ge(ctx_ready, 1)

            def mean_var(b, t, which):
                src = X[:, :, ds((b * 2 + t) * NT, NT)] if which == "1" else R[:]
                if which == "2":
                    pe.wait_ge(resid, b * 4 + (2 * t + 2))
                dst, sem = wait_free(pe, b, ("m" + which, t))
                accumulate(dst[:], [(ones_mean[:], src[:, c, :]) for c in range(C2)]).then_inc(sem, 1)
                dst, sem = wait_free(pe, b, ("s" + which, t))
                lns = 2 if gated else 1
                pe.wait_ge(squared, b * (2 * lns) + (lns * t + (lns if which == "2" else 1)))
                accumulate(dst[:], [(ones_mean[:], SQ[:, c, :]) for c in range(C2)]).then_inc(sem, 1)

            with pe.Fori(0, BATCH) as b:
                for c in range(C2):
                    dst, sem = wait_free(pe, b, ("k", c))
                    accumulate(dst[:, 0:KEYS], [(W["Wk"][:, kk, P * c:P * c + P], kv_src[:, kk, ds(b * KEYS, KEYS)])
                                                for kk in range(C2)]).then_inc(sem, 1)
                dst, sem = wait_free(pe, b, "v")
                pe.wait_ge(ctx2_ready, b + 1)
                accumulate(dst[:, 0:D], [(ctx2[:, kk, :, :], W["Wv"][:, kk, :]) for kk in range(C2)]).then_inc(sem, 1)
                for t in range(2):
                    pe.wait_ge(x_done, b * 2 + (t + 1))
                    if gated:
                        mean_var(b, t, "1")
                        pe.wait_ge(normed, b * 2 + (t + 1))
                    rhs = N[:] if gated else X[:, :, ds((b * 2 + t) * NT, NT)]
                    for v in (("q", "g") if gated else ("q",)):
                        for c in range(C2):
                            dst, sem = wait_free(pe, b, (v, c, t))
                            accumulate(dst[:], [(W["W" + v][:, kk, P * c:P * c + P], rhs[:, kk, :])
                                                for kk in range(C2)]).then_inc(sem, 1)
                    pe.wait_ge(q_ready, b * 4 + (2 * t + 2))
                    pe.wait_ge(blocks_ready, b + 1)

                    def score(k):
                        n = CHUNKS * t + k
                        pe.wait_ge(shifted, b * (2 * CHUNKS) + n + 1)
                        for c in range(C2):
                            mm = nc.tensor.matmul(ps_s[k % 2][:, 512 * c:512 * c + 512], QT[:, c, P * k:P * k + P],
                                                  kblk[:, c, :, :].rearrange("p h k -> p (h k)"), start=True, stop=True)
                        mm.then_inc(scores, 1)

                    def turn(k):
                        n = CHUNKS * t + k
                        pe.wait_ge(norm_done, b * (2 * CHUNKS) + n + 1)
                        pe.wait_ge(pt_ready, b * (2 * CHUNKS) + n + 1)
                        for j in range(PAIRS):
                            mm = nc.tensor.transpose(ps_t[:, j, :], PN[:, k % 2, P * j:P * j + P], ident[:])
                        mm.then_inc(turned, 1)

                    score(0)
                    for k in range(1, CHUNKS):
                        score(k)
                        turn(k - 1)
                    turn(CHUNKS - 1)
                    pe.wait_ge(pt_ready, b * (2 * CHUNKS) + (CHUNKS * (t + 1) + 1))
                    for c in range(C2):
                        dst, sem = wait_free(pe, b, ("y", c, t))
                        accumulate(dst[:], [(vblk[:, PC * c + j, :], PT[:, PC * c + j, :]) for j in range(PC)]).then_inc(sem, 1)
                    pe.wait_ge(y_ready, b * 4 + (2 * t + 2))
                    for c in range(C2):
                        dst, sem = wait_free(pe, b, ("o", c, t))
                        accumulate(dst[:], [(W["Wo"][:, kk, P * c:P * c + P], Y[:, kk, :]) for kk in range(C2)]).then_inc(sem, 1)
                    mean_var(b, t, "2")

        @block.scalar
        def _(act):
            act.wait_ge(loaded, LOADED)
            act.sem_inc(pt_ready, 1)
            act.sem_inc(free[0], 1)
            act.sem_inc(free[1], 1)
            if gated:
                act.wait_ge(prep, 2)
                nc.scalar.activation(CSQ[:], CXC[:], ACT.Square).then_inc(ctx_squared, 1)
                src, sem = wait_full(act, 0, "cvar")
                nc.scalar.activation(cstd[:], src[:, 0:CT], ACT.Sqrt, bias=epsb[:, 0:1]).then_inc(ctx_std, 1)
                act.wait_ge(ctx_std, 1)
                act.sem_inc(sem, 1)

            def square_root(b, t, which):
                lns = 2 if gated else 1
                n = lns * t + (lns if which == "2" else 1)
                act.wait_ge(centred, b * (2 * lns) + n)
                nc.scalar.activation(SQ[:], XC[:], ACT.Square).then_inc(squared, 1)
                src, sem = wait_full(act, b, ("s" + which, t))
                nc.scalar.activation(std[:], src[:], ACT.Sqrt, bias=epsb[:, 0:1]).then_inc(std_done, 1)
                act.wait_ge(std_done, b * (2 * lns) + n)
                act.sem_inc(sem, 1)

            act.wait_ge(ctx_ready, 1)
            with act.Fori(0, BATCH) as b:
                for c in range(C2):
                    src, sem = wait_full(act, b, ("k", c))
                    act.wait_ge(x_done, b * 2 + 1)
                    nc.scalar.activation(KT[:, c, :], src[:, 0:KEYS], ACT.Identity,
                                         bias=bias["k"][:, c:c + 1]).then_inc(kv_copied, 1)
                    act.wait_ge(kv_copied, b * 3 + (c + 1))
                    act.sem_inc(sem, 1)
                src, sem = wait_full(act, b, "v")
                nc.scalar.activation(VT[:], src[:, 0:D], ACT.Copy).then_inc(kv_copied, 1)
                act.wait_ge(kv_copied, b * 3 + 3)
                act.sem_inc(sem, 1)
                for t in range(2):
                    act.wait_ge(x_done, b * 2 + (t + 1))
                    if gated:
                        square_root(b, t, "1")
                    for c in range(C2):
                        src, sem = wait_full(act, b, ("q", c, t))
                        nc.scalar.activation(QT[:, c, :], src[:], ACT.Identity, bias=bias["q"][:, c:c + 1]).then_inc(q_ready, 1)
                        act.wait_ge(q_ready, b * 4 + (2 * t + c + 1))
                        act.sem_inc(sem, 1)
                    if gated:
                        for c in range(C2):
                            src, sem = wait_full(act, b, ("g", c, t))
                            nc.scalar.activation(G[:, c, :], src[:], ACT.Sigmoid, bias=bias["g"][:, c:c + 1]).then_inc(g_ready, 1)
                            act.wait_ge(g_ready, b * 4 + (2 * t + c + 1))
                            act.sem_inc(sem, 1)

                    def exps(k):
                        n = CHUNKS * t + k
                        act.wait_ge(shifted, b * (2 * CHUNKS) + n + 3)
                        act.wait_ge(norm_done, b * (2 * CHUNKS) + n + 1 - 2) if n >= 2 else None
                        if n < 2:
                            act.wait_ge(x_done, b * 2 + 1)
                        nc.scalar.activation(E[:, k % 2, :], S[:, k % 2, :], ACT.Exp, scale=float(DH) ** -0.5).then_inc(exp_done, 1)

                    def copies(k):
                        n = CHUNKS * t + k
                        act.wait_ge(turned, b * (2 * CHUNKS) + n + 3)
                        nc.scalar.activation(PT[:, :, P * k:P * k + P], ps_t[:], ACT.Copy).then_inc(pt_ready, 1)

                    exps(0)
                    for k in range(1, CHUNKS):
                        exps(k)
                        copies(k - 1)
                    copies(CHUNKS - 1)
                    square_root(b, t, "2")

        @block.vector
        def _(dve):
            nc.vector.memset(epsb[:], EPS).then_inc(prep, 1)
            dve.wait_ge(prep, 1)
            dve.wait_ge(loaded, LOADED)
            dve.sem_inc(shifted, 2)
            dve.sem_inc(x_done, 1)
            if gated:
                src, sem = wait_full(dve, 0, "cmean")
                nc.vector.tensor_tensor(CXC[:], CTX[:], src[:, 0:CT].unsqueeze(1).to_broadcast([P, C2, CT]),
                                        ALU.subtract).then_inc(prep, 1)
                dve.wait_ge(prep, 2)
                dve.sem_inc(sem, 1)
                dve.wait_ge(ctx_std, 1)
                nc.vector.reciprocal(crstd[:], cstd[:]).then_inc(prep, 1)
                dve.wait_ge(prep, 3)
                nc.vector.tensor_tensor(CXC[:], CXC[:], crstd[:].unsqueeze(1).to_broadcast([P, C2, CT]), ALU.mult).then_inc(prep, 1)
                n = 4
                for v in "qkvg":
                    for c in range(C2):
                        src, sem = wait_full(dve, 0, ("bias", v, c))
                        if v == "g":
                            ins = nc.vector.tensor_tensor(bias[v][:, c:c + 1], src[:, 0:1], V["bg"][:, c:c + 1], ALU.add)
                        else:
                            ins = nc.vector.tensor_copy(bias[v][:, c:c + 1], src[:, 0:1])
                        ins.then_inc(prep, 1)
                        n += 1
                        dve.wait_ge(prep, n)
                        dve.sem_inc(sem, 1)
                for v in "qkvg":
                    lng = V["kvln_g"] if v in "kv" else V["qln_g"]
                    for c in range(C2):
                        nc.vector.tensor_scalar(W["W" + v][:, c, :], W["W" + v][:, c, :], lng[:, c:c + 1], None,
                                                ALU.mult).then_inc(prep, 1)
                        n += 1
                dve.wait_ge(prep, n)
            dve.sem_inc(ctx_ready, 1)
            dve.wait_ge(masks_done, 4 + 2 * PC)

            def centre(b, t, which):
                src, sem = wait_full(dve, b, ("m" + which, t))
                lns = 2 if gated else 1
                n = lns * t + (lns if which == "2" else 1)
                data = X[:, :, ds((b * 2 + t) * NT, NT)] if which == "1" else R[:]
                nc.vector.tensor_tensor(XC[:], data, src[:].unsqueeze(1).to_broadcast([P, C2, NT]), ALU.subtract).then_inc(centred, 1)
                dve.wait_ge(centred, b * (2 * lns) + n)
                dve.sem_inc(sem, 1)
                dve.wait_ge(std_done, b * (2 * lns) + n)
                nc.vector.reciprocal(rstd[:], std[:]).then_inc(rstd_done, 1)
                dve.wait_ge(rstd_done, b * (2 * lns) + n)

            with dve.Fori(0, BATCH) as b:
                dve.wait_ge(x_done, b * 2 + 1)
                nc.vector.tensor_copy(ctx2[:], kv_src[:, :, ds(b * KEYS, KEYS)].unsqueeze(2).to_broadcast([P, C2, 2, KEYS])).then_inc(ctx2_ready, 1)
                dve.wait_ge(kv_copied, b * 3 + 3)
                for c in range(C2):
                    nc.vector.tensor_tensor(kblk[:, c, :, :], KT[:, c, :].unsqueeze(1).to_broadcast([P, HC, KEYS]),
                                            head_mask[:].unsqueeze(2).to_broadcast([P, HC, KEYS]), ALU.mult)
                for c in range(C2):
                    last = nc.vector.tensor_tensor(vblk[:, PC * c:PC * c + PC, :],
                                                   VT[:, P * c:P * c + P].unsqueeze(1).to_broadcast([P, PC, P]),
                                                   pair_mask[:], ALU.mult)
                last.then_inc(blocks_ready, 1)
                for t in range(2):
                    tile = X[:, :, ds((b * 2 + t) * NT, NT)]
                    dve.wait_ge(x_done, b * 2 + (t + 1))
                    if gated:
                        centre(b, t, "1")
                        nc.vector.tensor_tensor(N[:], XC[:], rstd[:].unsqueeze(1).to_broadcast([P, C2, NT]), ALU.mult).then_inc(normed, 1)

                    def shift(k):
                        n = CHUNKS * t + k
                        base = b * (2 * CHUNKS)
                        ps3 = ps_s[k % 2][:].rearrange("p (h k) -> p h k", h=HEADS)
                        dve.wait_ge(scores, base + n + 1)
                        nc.vector.tensor_reduce(MX[:, k % 2, :], ps3, AX.X, ALU.max).then_inc(max_done, 1)
                        dve.wait_ge(max_done, base + n + 1)
                        if n >= 2:
                            dve.wait_ge(exp_done, base + n - 1)
                        nc.vector.tensor_tensor(S[:, k % 2, :].rearrange("p (h k) -> p h k", h=HEADS), ps3,
                                                MX[:, k % 2, :].unsqueeze(2).to_broadcast([P, HEADS, KEYS]),
                                                ALU.subtract).then_inc(shifted, 1)

                    def invert(k):
                        n = CHUNKS * t + k
                        base = b * (2 * CHUNKS)
                        dve.wait_ge(exp_done, base + n + 1)
                        nc.vector.tensor_reduce(SUM[:, k % 2, :], E[:, k % 2, :].rearrange("p (h k) -> p h k", h=HEADS),
                                                AX.X, ALU.add).then_inc(sum_done, 1)
                        dve.wait_ge(sum_done, base + n + 1)
                        if n >= 2:
                            dve.wait_ge(norm_done, base + n - 1)
                        nc.vector.reciprocal(RIN[:, k % 2, :], SUM[:, k % 2, :]).then_inc(rinv_done, 1)

                    shift(0)
                    for k in range(1, CHUNKS):
                        shift(k)
                        invert(k - 1)
                    invert(CHUNKS - 1)
                    if gated:
                        dve.wait_ge(g_ready, b * 4 + (2 * t + 2))
                    for c in range(C2):
                        src, sem = wait_full(dve, b, ("y", c, t))
                        if gated:
                            ins = nc.vector.scalar_tensor_tensor(out=Y[:, c, :], in0=src[:], scalar=bias["v"][:, c:c + 1],
                                                                 in1=G[:, c, :], op0=ALU.add, op1=ALU.mult)
                        else:
                            ins = nc.vector.tensor_scalar(Y[:, c, :], src[:], bias["v"][:, c:c + 1], None, ALU.add)
                        ins.then_inc(y_ready, 1)
                        dve.wait_ge(y_ready, b * 4 + (2 * t + c + 1))
                        dve.sem_inc(sem, 1)
                    for c in range(C2):
                        src, sem = wait_full(dve, b, ("o", c, t))
                        if gated:
                            ins = nc.vector.tensor_tensor(R[:, c, :], src[:], tile[:, c, :], ALU.add)
                        else:
                            ins = nc.vector.scalar_tensor_tensor(out=R[:, c, :], in0=src[:], scalar=V["bo"][:, c:c + 1],
                                                                 in1=tile[:, c, :], op0=ALU.add, op1=ALU.add)
                        ins.then_inc(resid, 1)
                        dve.wait_ge(resid, b * 4 + (2 * t + c + 1))
                        dve.sem_inc(sem, 1)
                    centre(b, t, "2")
                    nc.vector.tensor_tensor(tile, XC[:], rstd[:].unsqueeze(1).to_broadcast([P, C2, NT]), ALU.mult).then_inc(x_done, 1)


def expert_stage(nc, X, ones_mean, ident, w, sorted_in, sorted_out, zeros_written):
    EX, FF = 8, 1024
    KF = FF // P
    CH = TOK // P
    TC = NT // P
    BLOCKS = (TOK + EX * (P - 1)) // P
    BLOCKS += BLOCKS % 2
    with Phase(nc, "moe") as ph:
        W1 = ph.sb("W1", [P, EX, C2, FF])
        W2 = ph.sb("W2", [P, EX, KF, D])
        XTM = ph.sb("x_tokens", [P, CH, D])
        stage_buf = ph.sb("stage_buf", [P, 2 * NT])
        XS = stage_buf[:].rearrange("p (c t) -> p c t", c=C2)
        NTM = stage_buf[:].rearrange("p (r d) -> p r d", r=4)
        cent = ph.sb("cent", [P, C2, EX])
        stats = ph.sb("stats", [P, CH, 6])
        MV = ph.sb("mean_var", [P, CH, 2])
        std = ph.sb("std", [P, CH])
        rstd = ph.sb("rstd", [P, CH])
        alpha = ph.sb("alpha", [P, CH])
        pos = ph.sb("pos", [P, CH], I32)
        block_expert = ph.sb("block_expert", [P, BLOCKS], I32)
        ln_g = ph.sb("ln_g", [P, EX, C2])
        ln_b = ph.sb("ln_b", [P, EX, C2])
        b1 = ph.sb("b1", [P, EX, KF])
        epsb = ph.sb("epsb", [P, 1])
        ps_aff = ph.ps("ps_aff", [P, CH, EX])
        xf = X[:].rearrange("p c t -> p (c t)")
        weights_loaded = ph.sem("weights_loaded")
        small_loaded = ph.sem("small_loaded")
        b2_loaded = ph.sem("b2_loaded")

        with Phase(nc, "moeA") as pa:
            ps_x = [pa.ps(f"ps_x{b}", [P, TC, D]) for b in range(2)]
            ps_b1 = pa.ps("ps_b1", [P, EX, KF])
            staged = pa.sem("staged")
            turned = pa.sem("turned")
            copied = pa.sem("copied")
            stats_done = pa.sem("stats_done")
            b1_psum = pa.sem("b1_psum")
            block = pa.block()

            @block.sync
            def _(sp):
                sp.dma_start(cent[:], w["L0_ffn_centroids"].rearrange("(c p) e -> p c e", p=P)).then_inc(small_loaded, 16)
                sp.dma_start(ln_g[:], w["L0_ffn_ln_g"]).then_inc(small_loaded, 16)
                sp.dma_start(ln_b[:], w["L0_ffn_ln_b"]).then_inc(small_loaded, 16)
                sp.dma_start(b1[:], w["L0_ffn_b1"]).then_inc(small_loaded, 16)
                for e in range(EX):
                    sp.dma_start(W1[:, e, :, :], w["L0_ffn_w1"][e].rearrange("(c p) f -> p c f", p=P)).then_inc(weights_loaded, 16)
                for e in range(EX):
                    sp.dma_start(W2[:, e, :, :], w["L0_ffn_w2"][e].rearrange("(c p) f -> p c f", p=P)).then_inc(weights_loaded, 16)

            @block.scalar
            def _(act):
                act.sem_inc(turned, 1)
                act.sem_inc(copied, 2)
                with act.Fori(0, TILES // 2) as i:
                    for h in range(2):
                        n = i * 2 + h
                        act.wait_ge(turned, n + 1)
                        nc.scalar.activation(XS, X[:, :, ds(n * NT, NT)], ACT.Copy).then_inc(staged, 1)
                        act.wait_ge(turned, n + 2)
                        nc.scalar.activation(XTM[:, ds(n * TC, TC), :], ps_x[h][:], ACT.Copy).then_inc(copied, 1)

            @block.tensor
            def _(pe):
                pe.wait_ge(small_loaded, 16 * 4)
                with pe.Fori(0, TILES // 2) as i:
                    for h in range(2):
                        n = i * 2 + h
                        pe.wait_ge(staged, n + 1)
                        pe.wait_ge(copied, n + 1)
                        for k in range(TC):
                            for c in range(C2):
                                nc.tensor.transpose(ps_x[h][:, k, P * c:P * c + P], XS[:, c, P * k:P * k + P], ident[:])
                        for k in range(TC):
                            for c in range(C2):
                                mm = nc.tensor.matmul(ps_aff[:, ds(n * TC + k, 1), :].rearrange("p k e -> p (k e)"),
                                                      XS[:, c, P * k:P * k + P], cent[:, c, :],
                                                      start=(c == 0), stop=(c == C2 - 1))
                        mm.then_inc(turned, 1)
                pe.wait_ge(weights_loaded, 16 * 2 * EX)
                for e in range(EX):
                    for m in range(KF):
                        for c in range(C2):
                            mm = nc.tensor.matmul(ps_b1[:, e, m:m + 1], W1[:, e, c, P * m:P * m + P], ln_b[:, e, c:c + 1],
                                                  start=(c == 0), stop=(c == C2 - 1))
                mm.then_inc(b1_psum, 1)

            @block.vector
            def _(dve):
                nc.vector.memset(epsb[:], EPS)
                with dve.Fori(0, TILES // 2) as i:
                    for h in range(2):
                        n = i * 2 + h
                        dve.wait_ge(copied, n + 3)
                        for k in range(TC):
                            ins = nc.vector.bn_stats(stats[:, ds(n * TC + k, 1), :].rearrange("p k s -> p (k s)"),
                                                     XTM[:, ds(n * TC + k, 1), :].rearrange("p k d -> p (k d)"))
                        ins.then_inc(stats_done, 1)
                dve.wait_ge(stats_done, TILES)
                for j in range(CH):
                    nc.vector.bn_aggr(MV[:, j, :], stats[:, j, :])
                dve.wait_ge(b1_psum, 1)
                nc.vector.tensor_tensor(b1[:], b1[:], ps_b1[:], ALU.add)
                for e in range(EX):
                    for c in range(C2):
                        nc.vector.tensor_scalar(W1[:, e, c, :], W1[:, e, c, :], ln_g[:, e, c:c + 1], None, ALU.mult)

        with Phase(nc, "moeB") as pb:
            AFF, EQ, OH, SC0, SC1, ENDB = (xf[:, CH * EX * n:CH * EX * (n + 1)].rearrange("p (j e) -> p j e", e=EX)
                                           for n in range(6))
            rest = xf[:, CH * EX * 6:]
            MAXV, BEST, POSF = (rest[:, CH * n:CH * (n + 1)] for n in range(3))
            rest = rest[:, CH * 3:]
            CNT, NB, S1, S2, S3 = (rest[:, EX * n:EX * (n + 1)] for n in range(5))
            rest = rest[:, EX * 5:]
            BE = rest[:, 0:BLOCKS]
            rest = rest[:, BLOCKS:]
            GTS = rest[:, 0:EX * CH].rearrange("p (e m) -> p e m", e=EX)
            rest = rest[:, EX * CH:]
            LES = rest[:, 0:BLOCKS * EX].rearrange("p (m e) -> p m e", e=EX)
            rest = rest[:, BLOCKS * EX:]
            prefer = rest[:, 0:EX]
            chunk_edge = rest[:, EX:EX + CH]
            block_no = rest[:, EX + CH:EX + CH + BLOCKS]
            before = rest[:, EX + CH + BLOCKS:EX + CH + BLOCKS + P]
            ones = rest[:, EX + CH + BLOCKS + P:EX + CH + BLOCKS + 2 * P]
            ps_pre = pb.ps("ps_pre", [P, CH, EX])
            ps_tot = pb.ps("ps_tot", [P, CH, EX])
            consts = pb.sem("consts")
            aff_psum = pb.sem("aff_psum")
            step = pb.sem("step")
            onehot_done = pb.sem("onehot_done")
            counted = pb.sem("counted")
            std_done = pb.sem("std_done")
            alpha_done = pb.sem("alpha_done")
            normed = pb.sem("normed")
            pos_done = pb.sem("pos_done")
            scattered = [pb.sem(f"scattered{b}") for b in range(4)]
            block = pb.block()

            @block.sync
            def _(sp):
                sp.dma_start(xf[:, 6144:8192], w["L0_ffn_b2"].rearrange("e d -> (e d)").unsqueeze(0).to_broadcast([P, EX * D])).then_inc(b2_loaded, 16)

            @block.gpsimd
            def _(pool):
                nc.gpsimd.iota(prefer, pattern=[[-1, EX]], base=EX, channel_multiplier=0,
                               allow_small_or_imprecise_dtypes=True).then_inc(consts, 1)
                nc.gpsimd.iota(chunk_edge, pattern=[[P, CH]], base=0, channel_multiplier=0,
                               allow_small_or_imprecise_dtypes=True).then_inc(consts, 1)
                nc.gpsimd.iota(block_no, pattern=[[1, BLOCKS]], base=0, channel_multiplier=0,
                               allow_small_or_imprecise_dtypes=True).then_inc(consts, 1)
                nc.gpsimd.memset(ones, 1.0).then_inc(consts, 1)
                pool.wait_ge(consts, 4)
                nc.gpsimd.affine_select(out=before, in_=ones, compare_op=ALU.is_gt, fill=0.0, base=0,
                                        pattern=[[1, P]], channel_multiplier=-1).then_inc(consts, 1)
                pool.wait_ge(zeros_written, 16)
                pool.wait_ge(pos_done, 1)
                for j in range(CH):
                    pool.wait_ge(normed, j + 1)
                    nc.gpsimd.indirect_dma_start(sorted_in, bass.IndirectOffsetOnAxis(pos[:, j:j + 1], 0),
                                                 NTM[:, j % 4, :], None).then_inc(scattered[j % 4], 16)
                for b in range(4):
                    pool.wait_ge(scattered[b], 16 * CH // 4)

            @block.scalar
            def _(act):
                act.wait_ge(step, 1)
                nc.scalar.activation(std[:], MV[:, :, 1], ACT.Sqrt, bias=epsb[:, 0:1]).then_inc(std_done, 1)
                act.wait_ge(step, 2)
                nc.scalar.activation(alpha[:], MAXV, ACT.Sigmoid).then_inc(alpha_done, 1)

            @block.tensor
            def _(pe):
                pe.wait_ge(onehot_done, 1)
                oh = OH.rearrange("p j e -> p (j e)")
                nc.tensor.matmul(ps_pre[:].rearrange("p j e -> p (j e)"), before, oh, start=True, stop=True)
                nc.tensor.matmul(ps_tot[:].rearrange("p j e -> p (j e)"), ones, oh, start=True, stop=True).then_inc(counted, 1)

            @block.vector
            def _(dve):
                n = [0]

                def then(ins):
                    n[0] += 1
                    ins.then_inc(step, 1)
                    dve.wait_ge(step, n[0])

                dve.wait_ge(consts, 5)
                then(nc.vector.tensor_copy(AFF, ps_aff[:]))
                then(nc.vector.tensor_reduce(MAXV, AFF, AX.X, ALU.max))
                then(nc.vector.tensor_tensor(EQ, AFF, MAXV.unsqueeze(2).to_broadcast([P, CH, EX]), ALU.is_equal))
                then(nc.vector.tensor_tensor(EQ, EQ, prefer.unsqueeze(1).to_broadcast([P, CH, EX]), ALU.mult))
                then(nc.vector.tensor_reduce(BEST, EQ, AX.X, ALU.max))
                nc.vector.tensor_tensor(OH, EQ, BEST.unsqueeze(2).to_broadcast([P, CH, EX]), ALU.is_equal).then_inc(onehot_done, 1)
                dve.wait_ge(counted, 1)
                then(nc.vector.tensor_copy(SC0, ps_tot[:]))
                a, b, s = SC0, SC1, 1
                while s < CH:
                    nc.vector.tensor_copy(b[:, 0:s, :], a[:, 0:s, :])
                    then(nc.vector.tensor_tensor(b[:, s:, :], a[:, s:, :], a[:, 0:CH - s, :], ALU.add))
                    a, b, s = b, a, s * 2
                incl, tmp = a, b
                then(nc.vector.tensor_copy(CNT, incl[:, CH - 1, :]))
                then(nc.vector.tensor_tensor(GTS, CNT.unsqueeze(2).to_broadcast([P, EX, CH]),
                                             chunk_edge.unsqueeze(1).to_broadcast([P, EX, CH]), ALU.is_gt))
                then(nc.vector.tensor_reduce(NB, GTS, AX.X, ALU.add))
                a, b, s, other = NB, S1, 1, S2
                while s < EX:
                    nc.vector.tensor_copy(b[:, 0:s], a[:, 0:s])
                    then(nc.vector.tensor_tensor(b[:, s:], a[:, s:], a[:, 0:EX - s], ALU.add))
                    a, b, other, s = b, other, (a if a is not NB else S3), s * 2
                ends = a
                then(nc.vector.tensor_tensor(LES, ends.unsqueeze(1).to_broadcast([P, BLOCKS, EX]),
                                             block_no.unsqueeze(2).to_broadcast([P, BLOCKS, EX]), ALU.is_le))
                then(nc.vector.tensor_reduce(BE, LES, AX.X, ALU.add))
                then(nc.vector.tensor_scalar(block_expert[:], BE, float(EX - 1), None, ALU.min))
                then(nc.vector.tensor_tensor(CNT, ends, NB, ALU.subtract))
                then(nc.vector.tensor_scalar(CNT, CNT, float(P), None, ALU.mult))
                then(nc.vector.tensor_tensor(tmp, incl, ps_tot[:], ALU.subtract))
                then(nc.vector.tensor_tensor(tmp, tmp, ps_pre[:], ALU.add))
                then(nc.vector.tensor_tensor(tmp, tmp, CNT.unsqueeze(1).to_broadcast([P, CH, EX]), ALU.add))
                then(nc.vector.tensor_tensor(tmp, tmp, OH, ALU.mult))
                then(nc.vector.tensor_reduce(POSF, tmp, AX.X, ALU.add))
                nc.vector.tensor_copy(pos[:], POSF).then_inc(pos_done, 1)
                dve.wait_ge(std_done, 1)
                then(nc.vector.reciprocal(rstd[:], std[:]))
                for j in range(CH):
                    if j >= 4:
                        dve.wait_ge(scattered[j % 4], 16 * (j // 4))
                    nc.vector.tensor_scalar(NTM[:, j % 4, :], XTM[:, j, :], MV[:, j, 0:1], rstd[:, j:j + 1],
                                            ALU.subtract, ALU.mult).then_inc(normed, 1)

        with Phase(nc, "moeC") as pc:
            b2 = xf[:, 6144:8192].rearrange("p (e d) -> p e d", e=EX)
            rows = xf[:, 0:512].rearrange("p (b d) -> p b d", b=2)
            rowsT = xf[:, 512:1024].rearrange("p (b c t) -> p b c t", b=2, c=C2)
            hid = xf[:, 1024:3072].rearrange("p (b f) -> p b f", b=2)
            hidT = xf[:, 3072:5120].rearrange("p (b m t) -> p b m t", b=2, m=KF)
            yrow = xf[:, 5120:5632].rearrange("p (b d) -> p b d", b=2)
            ps_r = ps_aff[:].rearrange("p j e -> p (j e)").rearrange("p (c t) -> p c t", c=C2)
            ps_h = [pc.ps(f"ps_h{b}", [P, FF]) for b in range(2)]
            ps_t = pc.ps("ps_t", [P, KF, P])
            ps_y = pc.ps("ps_y", [P, D])
            row_loaded = [pc.sem(f"row_loaded{b}") for b in range(2)]
            row_turned = pc.sem("row_turned")
            rowT_ready = pc.sem("rowT_ready")
            h_psum = pc.sem("h_psum")
            h_copied = pc.sem("h_copied")
            h_turned = pc.sem("h_turned")
            bias_added = pc.sem("bias_added")
            relu_done = pc.sem("relu_done")
            y_psum = pc.sem("y_psum")
            y_done = pc.sem("y_done")
            y_stored = [pc.sem(f"y_stored{b}") for b in range(2)]
            block = pc.block()
            in_blk = sorted_in.rearrange("(m p) d -> m p d", p=P)
            out_blk = sorted_out.rearrange("(m p) d -> m p d", p=P)

            @block.sync
            def _(sp):
                for q in range(2):
                    sp.dma_start(rows[:, q, :], in_blk[q, :, :]).then_inc(row_loaded[q], 16)
                sp.sem_inc(y_stored[0], 16)
                sp.sem_inc(y_stored[1], 16)
                with sp.Fori(0, BLOCKS // 2 - 1) as i:
                    for q in range(2):
                        sp.wait_ge(row_turned, i * 2 + (q + 1))
                        sp.dma_start(rows[:, q, :], in_blk[ds(i * 2 + (q + 2), 1), :, :].rearrange("m p d -> (m p) d")).then_inc(row_loaded[q], 16)
                        sp.wait_ge(y_done, i * 2 + (q + 2))
                        sp.dma_start(out_blk[ds(i * 2 + q, 1), :, :].rearrange("m p d -> (m p) d"), yrow[:, q, :]).then_inc(y_stored[q], 16)
                for q in range(2):
                    sp.wait_ge(y_done, BLOCKS + q)
                    sp.dma_start(out_blk[BLOCKS - 2 + q, :, :], yrow[:, q, :]).then_inc(y_stored[q], 16)
                for q in range(2):
                    sp.wait_ge(y_stored[q], 16 * (BLOCKS // 2 + 1))

            @block.tensor
            def _(pe):
                pe.sem_inc(h_turned, 2)

                def expert(m):
                    return pe.value_load(block_expert[0:1, ds(m, 1)], min_val=0, max_val=EX - 1)

                def turn_rows(i, q):
                    m = i * 2 + q
                    pe.wait_ge(row_loaded[q], (i + 1) * 16)
                    pe.wait_ge(rowT_ready, m + 1)
                    for c in range(C2):
                        mm = nc.tensor.transpose(ps_r[:, c, :], rows[:, q, P * c:P * c + P], ident[:])
                    mm.then_inc(row_turned, 1)

                def up(i, q):
                    m = i * 2 + q
                    e = expert(m)
                    pe.wait_ge(rowT_ready, m + 2)
                    pe.wait_ge(h_copied, m + 1)
                    for n in range(FF // 512):
                        for c in range(C2):
                            mm = nc.tensor.matmul(ps_h[q][:, 512 * n:512 * n + 512], rowsT[:, q, c, :],
                                                  W1[:, ds(e, 1), c, 512 * n:512 * n + 512].rearrange("p e f -> p (e f)"),
                                                  start=(c == 0), stop=(c == C2 - 1))
                    mm.then_inc(h_psum, 1)

                def turn_hidden(i, q):
                    m = i * 2 + q
                    pe.wait_ge(h_copied, m + 3)
                    pe.wait_ge(bias_added, m + 1)
                    for k in range(KF):
                        mm = nc.tensor.transpose(ps_t[:, k, :], hid[:, q, P * k:P * k + P], ident[:])
                    mm.then_inc(h_turned, 1)

                def down(i, q):
                    m = i * 2 + q
                    e = expert(m)
                    pe.wait_ge(relu_done, m + 1)
                    pe.wait_ge(y_done, m + 1)
                    for k in range(KF):
                        mm = nc.tensor.matmul(ps_y[:], hidT[:, q, k, :],
                                              W2[:, ds(e, 1), k, :].rearrange("p e d -> p (e d)"),
                                              start=(k == 0), stop=(k == KF - 1))
                    mm.then_inc(y_psum, 1)

                turn_rows(0, 0)
                up(0, 0)
                turn_hidden(0, 0)
                with pe.Fori(0, BLOCKS // 2 - 1) as i:
                    turn_rows(i, 1)
                    up(i, 1)
                    down(i, 0)
                    turn_hidden(i, 1)
                    turn_rows(i + 1, 0)
                    up(i + 1, 0)
                    down(i, 1)
                    turn_hidden(i + 1, 0)
                turn_rows(BLOCKS // 2 - 1, 1)
                up(BLOCKS // 2 - 1, 1)
                down(BLOCKS // 2 - 1, 0)
                turn_hidden(BLOCKS // 2 - 1, 1)
                down(BLOCKS // 2 - 1, 1)

            @block.scalar
            def _(act):
                act.sem_inc(rowT_ready, 1)
                act.sem_inc(h_copied, 2)

                def rows_out(i, q):
                    act.wait_ge(row_turned, i * 2 + (q + 1))
                    nc.scalar.activation(rowsT[:, q, :, :], ps_r, ACT.Copy).then_inc(rowT_ready, 1)

                def hidden_out(i, q):
                    m = i * 2 + q
                    act.wait_ge(h_psum, m + 1)
                    act.wait_ge(h_turned, m + 1)
                    nc.scalar.activation(hid[:, q, :], ps_h[q][:], ACT.Copy).then_inc(h_copied, 1)

                def relu(i, q):
                    act.wait_ge(bias_added, i * 2 + (q + 2))
                    nc.scalar.activation(hidT[:, q, :, :], hidT[:, q, :, :], ACT.Relu).then_inc(relu_done, 1)

                rows_out(0, 0)
                hidden_out(0, 0)
                with act.Fori(0, BLOCKS // 2 - 1) as i:
                    rows_out(i, 1)
                    relu(i, 0)
                    hidden_out(i, 1)
                    rows_out(i + 1, 0)
                    relu(i, 1)
                    hidden_out(i + 1, 0)
                rows_out(BLOCKS // 2 - 1, 1)
                relu(BLOCKS // 2 - 1, 0)
                hidden_out(BLOCKS // 2 - 1, 1)
                relu(BLOCKS // 2 - 1, 1)

            @block.vector
            def _(dve):
                dve.sem_inc(bias_added, 1)
                dve.sem_inc(y_done, 1)
                dve.wait_ge(b2_loaded, 16)

                def add_b1(i, q):
                    m = i * 2 + q
                    e = dve.value_load(block_expert[0:1, ds(m, 1)], min_val=0, max_val=EX - 1)
                    dve.wait_ge(h_turned, m + 3)
                    nc.vector.tensor_tensor(hidT[:, q, :, :], ps_t[:],
                                            b1[:, ds(e, 1), :].rearrange("p e m -> p (e m)").unsqueeze(2).to_broadcast([P, KF, P]),
                                            ALU.add).then_inc(bias_added, 1)

                def add_b2(i, q):
                    m = i * 2 + q
                    e = dve.value_load(block_expert[0:1, ds(m, 1)], min_val=0, max_val=EX - 1)
                    dve.wait_ge(y_psum, m + 1)
                    dve.wait_ge(y_stored[q], (i + 1) * 16)
                    nc.vector.tensor_tensor(yrow[:, q, :], ps_y[:], b2[:, ds(e, 1), :].rearrange("p e d -> p (e d)"),
                                            ALU.add).then_inc(y_done, 1)

                add_b1(0, 0)
                with dve.Fori(0, BLOCKS // 2 - 1) as i:
                    add_b2(i, 0)
                    add_b1(i, 1)
                    add_b2(i, 1)
                    add_b1(i + 1, 0)
                add_b2(BLOCKS // 2 - 1, 0)
                add_b1(BLOCKS // 2 - 1, 1)
                add_b2(BLOCKS // 2 - 1, 1)

        with Phase(nc, "moeD") as pd:
            GY = W1[:].rearrange("p e c f -> p (e c f)")[:, 0:CH * D].rearrange("p (j d) -> p j d", d=D)
            ps_f = [pd.ps(f"ps_f{b}", [P, C2, NT]) for b in range(2)]
            gathered = pd.sem("gathered")
            summed = pd.sem("summed")
            doubled = pd.sem("doubled")
            stats_done = pd.sem("stats_done")
            aggr_done = pd.sem("aggr_done")
            std_done = pd.sem("std_done")
            rstd_done = pd.sem("rstd_done")
            normed = pd.sem("normed")
            turned = pd.sem("turned")
            copied = pd.sem("copied")
            block = pd.block()

            @block.gpsimd
            def _(pool):
                for j in range(CH):
                    nc.gpsimd.indirect_dma_start(GY[:, j, :], None, sorted_out,
                                                 bass.IndirectOffsetOnAxis(pos[:, j:j + 1], 0)).then_inc(gathered, 16)

            @block.vector
            def _(dve):
                dve.wait_ge(gathered, 16 * CH)
                with dve.Fori(0, CH // 4) as i:
                    for k in range(4):
                        j = i * 4 + k
                        g = GY[:, ds(j, 1), :].rearrange("p j d -> p (j d)")
                        nc.vector.tensor_scalar(g, g, alpha[:, ds(j, 1)], None, ALU.mult).then_inc(summed, 1)
                    dve.wait_ge(summed, i * 4 + 4)
                    nc.vector.scalar_tensor_tensor(out=XTM[:, ds(i * 4, 4), :], in0=XTM[:, ds(i * 4, 4), :], scalar=2.0,
                                                   in1=GY[:, ds(i * 4, 4), :], op0=ALU.mult, op1=ALU.add).then_inc(doubled, 1)
                    dve.wait_ge(doubled, i + 1)
                    for k in range(4):
                        j = i * 4 + k
                        ins = nc.vector.bn_stats(stats[:, ds(j, 1), :].rearrange("p k s -> p (k s)"),
                                                 XTM[:, ds(j, 1), :].rearrange("p j d -> p (j d)"))
                    ins.then_inc(stats_done, 1)
                dve.wait_ge(stats_done, CH // 4)
                for j in range(CH):
                    ins = nc.vector.bn_aggr(MV[:, j, :], stats[:, j, :])
                ins.then_inc(aggr_done, 1)
                dve.wait_ge(std_done, 1)
                nc.vector.reciprocal(rstd[:], std[:]).then_inc(rstd_done, 1)
                dve.wait_ge(rstd_done, 1)
                for j in range(CH):
                    nc.vector.tensor_scalar(GY[:, j, :], XTM[:, j, :], MV[:, j, 0:1], rstd[:, j:j + 1],
                                            ALU.subtract, ALU.mult).then_inc(normed, 1)

            @block.scalar
            def _(act):
                act.wait_ge(aggr_done, 1)
                nc.scalar.activation(std[:], MV[:, :, 1], ACT.Sqrt, bias=epsb[:, 0:1]).then_inc(std_done, 1)
                for n in range(TILES):
                    act.wait_ge(turned, n + 1)
                    nc.scalar.activation(X[:, :, NT * n:NT * n + NT], ps_f[n % 2][:], ACT.Copy).then_inc(copied, 1)

            @block.tensor
            def _(pe):
                for n in range(TILES):
                    pe.wait_ge(normed, TC * (n + 1))
                    if n >= 2:
                        pe.wait_ge(copied, n - 1)
                    for k in range(TC):
                        for c in range(C2):
                            mm = nc.tensor.transpose(ps_f[n % 2][:, c, P * k:P * k + P], GY[:, TC * n + k, P * c:P * c + P], ident[:])
                    mm.then_inc(turned, 1)


def delta_stage(nc, X, ones_mean, ident, w):
    HEADS, HD = 4, D // 4
    TAPS = 4
    HALO = TAPS - 1
    FIRS = (3, 15, 63)
    PAD = FIRS[-1] - 1
    PATHS = 5
    HP = HEADS * PATHS
    CH = TOK // P
    TC = NT // P
    ON_PE = 36
    with Phase(nc, "del") as ph:
        VD = ph.sb("values", [P, C2, BATCH, PAD + SEQ])
        LG = ph.sb("path_logits", [P, CH, HP])
        epsb = ph.sb("epsb", [P, 1])
        epsk = ph.sb("epsk", [P, 1])
        scratch = {n: nc.dram_tensor(f"del_{n}", (D, TOK), F32).ap() for n in ("q", "k", "kb", "vb", "o")}

        with Phase(nc, "delA") as pa:
            W = {n: pa.sb(n, [P, C2, D]) for n in ("q", "k", "v", "b")}
            wb = pa.sb("wb", [P, C2, HEADS])
            conv = {n: pa.sb(f"conv_{n}", [P, C2, TAPS]) for n in "qkv"}
            gate_w = pa.sb("gate_w", [P, C2, HP])
            head_ones = pa.sb("head_ones", [P, P])
            XS = pa.sb("XS", [P, C2, NT])
            pre = {n: [pa.sb(f"pre_{n}{b}", [P, C2, HALO + NT]) for b in range(2)] for n in "qkv"}
            y = {n: [pa.sb(f"y_{n}{b}", [P, C2, NT]) for b in range(2)] for n in "qkv"}
            sig = {n: pa.sb(f"sig_{n}", [P, C2, NT]) for n in "qkv"}
            nrm = {n: pa.sb(f"nrm_{n}", [P, C2, NT]) for n in "qk"}
            beta = pa.sb("beta", [P, C2, NT])
            kb = [pa.sb(f"kb{b}", [P, C2, NT]) for b in range(2)]
            vb = [pa.sb(f"vb{b}", [P, C2, NT]) for b in range(2)]
            slot = [pa.ps(f"slot{s}", [P, C2, NT]) for s in range(4)]
            full = [pa.sem(f"slot_full{s}") for s in range(4)]
            free = [pa.sem(f"slot_free{s}") for s in range(4)]
            USE = {"k": (0, 0), "q": (1, 0), "v": (2, 0), "b": (3, 0), "lg": (0, 1), "ssk": (1, 1), "ssq": (2, 1)}
            PER = [2, 2, 2, 1]
            loaded = pa.sem("loaded")
            consts = pa.sem("consts")
            wb_spread = pa.sem("wb_spread")
            halo_done = pa.sem("halo_done")
            weights_ready = pa.sem("weights_ready")
            x_staged = pa.sem("x_staged")
            projected = {n: pa.sem(f"projected_{n}") for n in "qkv"}
            beta_done = pa.sem("beta_done")
            conv_step = {n: pa.sem(f"conv_step_{n}") for n in "qkv"}
            sig_done = {n: pa.sem(f"sig_done_{n}") for n in "qkv"}
            silu_done = {n: pa.sem(f"silu_done_{n}") for n in "qkv"}
            sq_done = {n: pa.sem(f"sq_done_{n}") for n in "qk"}
            ln_done = {n: pa.sem(f"ln_done_{n}") for n in "qk"}
            rn_done = {n: pa.sem(f"rn_done_{n}") for n in "qk"}
            unit = {n: pa.sem(f"unit_{n}") for n in "qk"}
            kb_done = pa.sem("kb_done")
            vb_done = pa.sem("vb_done")
            lg_done = pa.sem("lg_done")
            stored = [pa.sem(f"stored{b}") for b in range(2)]
            block = pa.block()

            def slot_free(pe, n, key):
                s, u = USE[key]
                pe.wait_ge(free[s], n * PER[s] + (u + 1))
                return slot[s], full[s]

            def slot_full(eng, n, key):
                s, u = USE[key]
                eng.wait_ge(full[s], n * PER[s] + (u + 1))
                return slot[s], free[s]

            def buffers_free(eng, i, b):
                eng.wait_ge(stored[b], (i + 1) * 64)

            @block.sync
            def _(sp):
                for n in "qkv":
                    sp.dma_start(W[n][:], w[f"L0_attn_W{n}"].rearrange("(c p) o -> p c o", p=P)).then_inc(loaded, 16)
                    sp.dma_start(conv[n][:], w[f"L0_attn_conv_{n}"].rearrange("(c p) o -> p c o", p=P)).then_inc(loaded, 16)
                sp.dma_start(wb[:], w["L0_attn_Wb"].rearrange("(c p) o -> p c o", p=P)).then_inc(loaded, 16)
                sp.dma_start(gate_w[:], w["L0_attn_gate_w"].rearrange("(c p) o -> p c o", p=P)).then_inc(loaded, 16)
                sp.sem_inc(stored[0], 64)
                sp.sem_inc(stored[1], 64)
                with sp.Fori(0, BATCH) as i:
                    for b in range(2):
                        n = i * 2 + b
                        for name, sem, credit, buf in (("q", unit["q"], 0, y["q"][b]), ("k", unit["k"], 0, y["k"][b]),
                                                       ("kb", kb_done, 1, kb[b]), ("vb", vb_done, 1, vb[b])):
                            sp.wait_ge(sem, n + (1 + credit))
                            sp.dma_start(scratch[name].rearrange("(c p) t -> p c t", p=P)[:, :, ds(n * NT, NT)],
                                         buf[:]).then_inc(stored[b], 16)
                for b in range(2):
                    sp.wait_ge(stored[b], 64 * (BATCH + 1))

            @block.gpsimd
            def _(pool):
                nc.gpsimd.memset(head_ones[:], 1.0).then_inc(consts, 1)
                nc.gpsimd.memset(VD[:, :, :, 0:PAD], 0.0)
                pool.sem_inc(kb_done, 1)
                pool.wait_ge(consts, 1)
                g3 = head_ones[:].rearrange("p (h c) -> p h c", c=HD)
                nc.gpsimd.affine_select(out=g3, in_=g3, compare_op=ALU.is_ge, fill=0.0, base=0,
                                        pattern=[[-HD, P // HD], [0, HD]], channel_multiplier=1).then_inc(consts, 1)
                pool.wait_ge(consts, 2)
                nc.gpsimd.affine_select(out=g3, in_=g3, compare_op=ALU.is_ge, fill=0.0, base=HD - 1,
                                        pattern=[[HD, P // HD], [0, HD]], channel_multiplier=-1).then_inc(consts, 1)
                with pool.Fori(0, BATCH) as i:
                    for b in range(2):
                        n = i * 2 + b
                        pool.wait_ge(lg_done, n + 1)
                        nc.gpsimd.tensor_copy(XS[:], X[:, :, ds(n * NT, NT)]).then_inc(x_staged, 1)
                        for key in "kq":
                            pool.wait_ge(sig_done[key], n + 1)
                            nc.gpsimd.tensor_tensor(y[key][b][:], y[key][b][:], sig[key][:], ALU.mult).then_inc(silu_done[key], 1)
                        for key in "kq":
                            pool.wait_ge(rn_done[key], n + 1)
                            nc.gpsimd.tensor_tensor(y[key][b][:], y[key][b][:], nrm[key][:], ALU.mult).then_inc(unit[key], 1)
                        pool.wait_ge(unit["k"], n + 1)
                        pool.wait_ge(beta_done, n + 1)
                        nc.gpsimd.tensor_tensor(kb[b][:], y["k"][b][:], beta[:], ALU.mult).then_inc(kb_done, 1)

            @block.tensor
            def _(pe):
                pe.wait_ge(loaded, 16 * 8)
                pe.wait_ge(consts, 3)
                pe.wait_ge(weights_ready, 1)

                def project(n, key):
                    dst, sem = slot_free(pe, n, key)
                    for c in range(C2):
                        for kk in range(C2):
                            mm = nc.tensor.matmul(dst[:, c, :], W[key][:, kk, P * c:P * c + P], X[:, kk, ds(n * NT, NT)],
                                                  start=(kk == 0), stop=(kk == C2 - 1))
                    mm.then_inc(sem, 1)

                with pe.Fori(0, BATCH) as i:
                    for b in range(2):
                        n = i * 2 + b
                        for key in "kqvb":
                            project(n, key)
                        pe.wait_ge(x_staged, n + 1)
                        dst, sem = slot_free(pe, n, "lg")
                        for k in range(TC):
                            for kk in range(C2):
                                mm = nc.tensor.matmul(dst[:, 0, HP * k:HP * k + HP], XS[:, kk, P * k:P * k + P], gate_w[:, kk, :],
                                                      start=(kk == 0), stop=(kk == C2 - 1))
                        mm.then_inc(sem, 1)
                        for key in "kq":
                            pe.wait_ge(sq_done[key], n + 1)
                            dst, sem = slot_free(pe, n, "ss" + key)
                            for c in range(C2):
                                mm = nc.tensor.matmul(dst[:, c, :], head_ones[:], nrm[key][:, c, :], start=True, stop=True)
                            mm.then_inc(sem, 1)

            @block.scalar
            def _(act):
                act.wait_ge(weights_ready, 1)
                with act.Fori(0, BATCH) as i:
                    for b in range(2):
                        n = i * 2 + b
                        buffers_free(act, i, b)
                        for key in "kqv":
                            src, sem = slot_full(act, n, key)
                            nc.scalar.activation(pre[key][b][:, :, HALO:], src[:], ACT.Copy).then_inc(projected[key], 1)
                            act.wait_ge(projected[key], n + 1)
                            act.sem_inc(sem, 1)
                        src, sem = slot_full(act, n, "b")
                        act.wait_ge(kb_done, n + 1)
                        act.wait_ge(vb_done, n + 1)
                        nc.scalar.activation(beta[:], src[:], ACT.Sigmoid).then_inc(beta_done, 1)
                        act.wait_ge(beta_done, n + 1)
                        act.sem_inc(sem, 1)
                        for key in "kqv":
                            act.wait_ge(conv_step[key], n * TAPS + TAPS)
                            nc.scalar.activation(sig[key][:], y[key][b][:], ACT.Sigmoid).then_inc(sig_done[key], 1)
                        for key in "kq":
                            act.wait_ge(silu_done[key], n + 1)
                            nc.scalar.activation(nrm[key][:], y[key][b][:], ACT.Square).then_inc(sq_done[key], 1)
                        for key in "kq":
                            src, sem = slot_full(act, n, "ss" + key)
                            nc.scalar.activation(nrm[key][:], src[:], ACT.Ln, bias=epsk[:, 0:1]).then_inc(ln_done[key], 1)
                            act.wait_ge(ln_done[key], n + 1)
                            act.sem_inc(sem, 1)
                            nc.scalar.activation(nrm[key][:], nrm[key][:], ACT.Exp, scale=-0.5).then_inc(rn_done[key], 1)

            @block.vector
            def _(dve):
                nc.vector.memset(epsb[:], EPS)
                nc.vector.memset(epsk[:], 1e-6)
                for key in "qkv":
                    nc.vector.memset(pre[key][0][:, :, 0:HALO], 0.0)
                dve.wait_ge(loaded, 16 * 8)
                nc.vector.tensor_copy(W["b"][:].rearrange("p c (h k) -> p c h k", k=HD),
                                      wb[:].unsqueeze(3).to_broadcast([P, C2, HEADS, HD])).then_inc(wb_spread, 1)
                dve.wait_ge(wb_spread, 1)
                for s in range(4):
                    dve.sem_inc(free[s], 1)
                dve.sem_inc(lg_done, 1)
                dve.sem_inc(vb_done, 1)
                dve.sem_inc(weights_ready, 1)
                with dve.Fori(0, BATCH) as i:
                    for b in range(2):
                        n = i * 2 + b
                        buffers_free(dve, i, b)
                        for key in "kqv":
                            dve.wait_ge(projected[key], n + 1)
                            if b == 1:
                                nc.vector.tensor_copy(pre[key][1][:, :, 0:HALO], pre[key][0][:, :, NT:NT + HALO]).then_inc(halo_done, 1)
                        if b == 1:
                            dve.wait_ge(halo_done, i * 3 + 3)
                        for j in range(TAPS):
                            for key in "kqv":
                                if j:
                                    dve.wait_ge(conv_step[key], n * TAPS + j)
                                for c in range(C2):
                                    src = pre[key][b][:, c, j:j + NT]
                                    tap = conv[key][:, c, j:j + 1]
                                    dst = y[key][b][:, c, :]
                                    if j == 0:
                                        ins = nc.vector.tensor_scalar(dst, src, tap, None, ALU.mult)
                                    else:
                                        ins = nc.vector.scalar_tensor_tensor(out=dst, in0=src, scalar=tap, in1=dst,
                                                                             op0=ALU.mult, op1=ALU.add)
                                ins.then_inc(conv_step[key], 1)
                        dve.wait_ge(sig_done["v"], n + 1)
                        vals = VD[:, :, ds(i, 1), PAD + NT * b:PAD + NT * b + NT].rearrange("p c i t -> p c (i t)")
                        nc.vector.tensor_tensor(vals, y["v"][b][:], sig["v"][:], ALU.mult).then_inc(silu_done["v"], 1)
                        dve.wait_ge(silu_done["v"], n + 1)
                        dve.wait_ge(beta_done, n + 1)
                        nc.vector.tensor_tensor(vb[b][:], vals, beta[:], ALU.mult).then_inc(vb_done, 1)
                        src, sem = slot_full(dve, n, "lg")
                        nc.vector.tensor_copy(LG[:, ds(n * TC, TC), :], src[:, 0, 0:HP * TC].rearrange("p (k g) -> p k g", k=TC)).then_inc(lg_done, 1)
                        dve.wait_ge(lg_done, n + 2)
                        dve.sem_inc(sem, 1)


        with Phase(nc, "delB") as pb:
            LEVELS = 7
            CPB = SEQ // P
            flip = pb.sb("level_masks", [P, LEVELS, P])
            low1 = pb.sb("low1", [P, P])
            causal = pb.sb("causal", [P, P])
            ink, invb = ([pb.sb(f"in_{n}{b}", [P, C2, P]) for b in range(2)] for n in ("k", "vb"))
            inq, inkb = ([pb.sb(f"in_{n}{b}", [P, HEADS, P]) for b in range(2)] for n in ("q", "kb"))
            Lsb = pb.sb("L", [P, HEADS, P])
            T = pb.sb("T", [P, HEADS, P])
            TT = pb.sb("TT", [P, HEADS, P])
            Wsb = pb.sb("W", [P, HEADS, P])
            attn = pb.sb("attn", [P, HEADS, P])
            KV = pb.sb("KV", [P, 2, D])
            S = pb.sb("S", [P, C2, HD])
            Rsb = pb.sb("R", [P, HEADS, HD])
            U = pb.sb("U", [P, HEADS, HD])
            Osb = [pb.sb(f"O{b}", [P, C2, P]) for b in range(2)]
            pL, pLT, pQK, pW, pD, pDT = (pb.ps(n, [P, HEADS, P]) for n in ("pL", "pLT", "pQK", "pW", "pD", "pDT"))
            pKV = pb.ps("pKV", [P, 2, D])
            pRU = pb.ps("pRU", [P, 2, HEADS, HD])
            pS = pL[:].rearrange("p h j -> p (h j)")[:, 0:C2 * HD].rearrange("p (c v) -> p c v", c=C2)
            pO = pLT[:].rearrange("p h j -> p (h j)")[:, 0:C2 * P].rearrange("p (c t) -> p c t", c=C2)
            masks = pb.sem("masks")
            pads_zero = pb.sem("pads_zero")
            in_loaded = [pb.sem(f"in_loaded{b}") for b in range(2)]
            grams = pb.sem("grams")
            l_copied = pb.sem("l_copied")
            kv_copied = pb.sem("kv_copied")
            first_half = pb.sem("first_half")
            start_done = pb.sem("start_done")
            w_psum = pb.sem("w_psum")
            w_masked = pb.sem("w_masked")
            d_psum = pb.sem("d_psum")
            level_done = pb.sem("level_done")
            r_psum = pb.sem("r_psum")
            r_done = pb.sem("r_done")
            u_psum = pb.sem("u_psum")
            u_copied = pb.sem("u_copied")
            so_psum = pb.sem("so_psum")
            s_done = pb.sem("s_done")
            s_zero = pb.sem("s_zero")
            o_copied = pb.sem("o_copied")
            o_stored = [pb.sem(f"o_stored{b}") for b in range(2)]
            block = pb.block()

            def load_chunk(sp, n, q):
                for name, buf in (("k", ink), ("vb", invb)):
                    sp.dma_start(buf[q][:], chunk_in_dram(name, n)).then_inc(in_loaded[q], 16)
                for name, buf in (("q", inq), ("kb", inkb)):
                    for r in range(2):
                        rows = slice(HD * r, HD * r + HD)
                        sp.dma_start(buf[q][rows, r::2, :], chunk_in_dram(name, n)[rows, :, :]).then_inc(in_loaded[q], 16)

            def chunk_in_dram(name, n):
                return scratch[name].rearrange("(c p) t -> p c t", p=P)[:, :, ds(n * P, P)]

            @block.sync
            def _(sp):
                sp.wait_ge(pads_zero, 4)
                for q in range(2):
                    load_chunk(sp, q, q)
                sp.sem_inc(o_stored[0], 16)
                sp.sem_inc(o_stored[1], 16)
                with sp.Fori(0, CH // 2 - 1) as i:
                    for q in range(2):
                        n = i * 2 + q
                        sp.wait_ge(so_psum, n + 1)
                        load_chunk(sp, n + 2, q)
                        sp.wait_ge(o_copied, n + 2)
                        sp.dma_start(chunk_in_dram("o", n), Osb[q][:]).then_inc(o_stored[q], 16)
                for q in range(2):
                    sp.wait_ge(o_copied, CH + q)
                    sp.dma_start(chunk_in_dram("o", CH - 2 + q), Osb[q][:]).then_inc(o_stored[q], 16)
                for q in range(2):
                    sp.wait_ge(o_stored[q], 16 * (CH // 2 + 1))

            @block.gpsimd
            def _(pool):
                nc.gpsimd.memset(flip[:], 0.0).then_inc(masks, 1)
                nc.gpsimd.memset(low1[:], 0.0).then_inc(masks, 1)
                nc.gpsimd.memset(causal[:], 1.0).then_inc(masks, 1)
                pool.wait_ge(masks, 3)
                m = 3
                for l in range(LEVELS):
                    s = 2 ** l
                    odd = flip[:, l, :].rearrange("p (m x s) -> p m x s", x=2, s=s)[:, :, 1, :]
                    pairs = P // (2 * s)
                    nc.gpsimd.memset(odd, -1.0).then_inc(masks, 1)
                    m += 1
                    pool.wait_ge(masks, m)
                    for base, sign in ((0, 1), (s - 1, -1)):
                        nc.gpsimd.affine_select(out=odd, in_=odd, compare_op=ALU.is_ge, fill=0.0, base=base,
                                                pattern=[[-2 * s * sign, pairs], [0, s]], channel_multiplier=sign).then_inc(masks, 1)
                        m += 1
                        pool.wait_ge(masks, m)
                even = low1[:].rearrange("p (m x) -> p m x", x=2)[:, :, 0]
                nc.gpsimd.memset(even, -1.0).then_inc(masks, 1)
                pool.wait_ge(masks, m + 1)
                nc.gpsimd.affine_select(out=even, in_=even, compare_op=ALU.is_equal, fill=0.0, base=-1,
                                        pattern=[[-2, P // 2]], channel_multiplier=1).then_inc(masks, 1)
                nc.gpsimd.affine_select(out=causal[:], in_=causal[:], compare_op=ALU.is_ge, fill=0.0, base=0,
                                        pattern=[[1, P]], channel_multiplier=-1).then_inc(masks, 1)
            MASKS = 3 + 3 * LEVELS + 3

            def hp(h):
                return slice(HD * (h % 2), HD * (h % 2) + HD), h // 2

            @block.tensor
            def _(pe):
                with pe.Fori(0, BATCH) as bt:
                    with pe.Fori(0, CPB // 2) as i:
                        for q in range(2):
                            n = bt * CPB + i * 2 + q
                            pe.wait_ge(in_loaded[q], bt * (96 * CPB // 2) + i * 96 + 96)
                            pe.wait_ge(s_done, n + 1)
                            pe.wait_ge(o_copied, n + 1)
                            pe.wait_ge(s_zero, bt + 1)
                            for h in range(HEADS):
                                r, c = hp(h)
                                nc.tensor.matmul(pL[:, h, :], inkb[q][:, h, :], ink[q][:, c, :], start=True, stop=True)
                            for h in range(HEADS):
                                r, c = hp(h)
                                nc.tensor.matmul(pLT[:, h, :], ink[q][:, c, :], inkb[q][:, h, :], start=True, stop=True)
                                nc.tensor.matmul(pQK[:, h, :], ink[q][:, c, :], inq[q][:, h, :], start=True, stop=True)
                            for x, src in enumerate((ink, invb)):
                                for c in range(C2):
                                    mm = nc.tensor.transpose(pKV[:, x, P * c:P * c + P], src[q][:, c, :], ident[:])
                            mm.then_inc(grams, 1)
                            pe.wait_ge(start_done, n + 1)
                            for l in range(1, LEVELS):
                                base = n * (LEVELS - 1)
                                if l > 1:
                                    pe.wait_ge(level_done, base + (l - 1))
                                for h in range(HEADS):
                                    mm = nc.tensor.matmul(pW[:, h, :], Lsb[:, h, :], TT[:, h, :], start=True, stop=True)
                                mm.then_inc(w_psum, 1)
                                pe.wait_ge(w_masked, base + l)
                                for h in range(HEADS):
                                    mm = nc.tensor.matmul(pD[:, h, :], T[:, h, :], Wsb[:, h, :], start=True, stop=True)
                                if l < LEVELS - 1:
                                    for h in range(HEADS):
                                        mm = nc.tensor.matmul(pDT[:, h, :], Wsb[:, h, :], T[:, h, :], start=True, stop=True)
                                mm.then_inc(d_psum, 1)
                            for h in range(HEADS):
                                r, c = hp(h)
                                mm = nc.tensor.matmul(pRU[:, 0, h, :], inkb[q][:, h, :], S[:, c, :], start=True, stop=True)
                            mm.then_inc(r_psum, 1)
                            pe.wait_ge(r_done, n + 1)
                            pe.wait_ge(level_done, n * (LEVELS - 1) + (LEVELS - 1))
                            for h in range(HEADS):
                                mm = nc.tensor.matmul(pRU[:, 1, h, :], TT[:, h, :], Rsb[:, h, :], start=True, stop=True)
                            mm.then_inc(u_psum, 1)
                            pe.wait_ge(u_copied, n + 1)
                            for h in range(HEADS):
                                r, c = hp(h)
                                nc.tensor.matmul(pS[r, c, :], KV[:, 0, HD * h:HD * h + HD], U[:, h, :], start=True, stop=True)
                            for h in range(HEADS):
                                r, c = hp(h)
                                nc.tensor.matmul(pO[r, c, :], S[:, c, :], inq[q][:, h, :], start=True, stop=False)
                                mm = nc.tensor.matmul(pO[r, c, :], U[:, h, :], attn[:, h, :], start=False, stop=True)
                            mm.then_inc(so_psum, 1)

            @block.scalar
            def _(act):
                act.sem_inc(o_copied, 1)
                with act.Fori(0, CH // 2) as i:
                    for q in range(2):
                        n = i * 2 + q
                        act.wait_ge(grams, n + 1)
                        nc.scalar.activation(Lsb[:], pL[:], ACT.Copy).then_inc(l_copied, 1)
                        nc.scalar.activation(KV[:], pKV[:], ACT.Copy).then_inc(kv_copied, 1)
                        act.wait_ge(u_psum, n + 1)
                        nc.scalar.activation(U[:], pRU[:, 1, :, :], ACT.Copy).then_inc(u_copied, 1)
                        act.wait_ge(so_psum, n + 1)
                        act.wait_ge(o_stored[q], (i + 1) * 16)
                        nc.scalar.activation(Osb[q][:], pO, ACT.Copy).then_inc(o_copied, 1)

            @block.vector
            def _(dve):
                bc = lambda ap: ap.unsqueeze(1).to_broadcast([P, HEADS, P])
                for buf in inq + inkb:
                    nc.vector.memset(buf[:], 0.0).then_inc(pads_zero, 1)
                dve.wait_ge(masks, MASKS)
                dve.sem_inc(s_done, 1)
                with dve.Fori(0, BATCH) as bt:
                    dve.wait_ge(s_done, bt * CPB + 1)
                    nc.vector.memset(S[:], 0.0).then_inc(s_zero, 1)
                    with dve.Fori(0, CPB // 2) as i:
                        for q in range(2):
                            n = bt * CPB + i * 2 + q
                            dve.wait_ge(grams, n + 1)
                            nc.vector.tensor_tensor(TT[:], pLT[:], bc(flip[:, 0, :]), ALU.mult).then_inc(first_half, 1)
                            nc.vector.tensor_tensor(attn[:], pQK[:], bc(causal[:]), ALU.mult)
                            dve.wait_ge(l_copied, n + 1)
                            nc.vector.tensor_tensor(T[:], Lsb[:], bc(low1[:]), ALU.mult).then_inc(first_half, 1)
                            dve.wait_ge(first_half, n * 2 + 2)
                            nc.vector.tensor_tensor(TT[:], TT[:], bc(ident[:]), ALU.add)
                            nc.vector.tensor_tensor(T[:], T[:], bc(ident[:]), ALU.add).then_inc(start_done, 1)
                            for l in range(1, LEVELS):
                                base = n * (LEVELS - 1)
                                dve.wait_ge(w_psum, base + l)
                                nc.vector.tensor_tensor(Wsb[:], pW[:], bc(flip[:, l, :]), ALU.mult).then_inc(w_masked, 1)
                                dve.wait_ge(d_psum, base + l)
                                ins = nc.vector.tensor_tensor(TT[:], TT[:], pD[:], ALU.add)
                                if l < LEVELS - 1:
                                    ins = nc.vector.tensor_tensor(T[:], T[:], pDT[:], ALU.add)
                                ins.then_inc(level_done, 1)
                            dve.wait_ge(kv_copied, n + 1)
                            dve.wait_ge(r_psum, n + 1)
                            nc.vector.tensor_tensor(Rsb[:], KV[:, 1, :].rearrange("p (h v) -> p h v", h=HEADS), pRU[:, 0, :, :],
                                                    ALU.subtract).then_inc(r_done, 1)
                            dve.wait_ge(so_psum, n + 1)
                            nc.vector.tensor_tensor(S[:], S[:], pS, ALU.add).then_inc(s_done, 1)

        with Phase(nc, "delC") as pc:
            ON_DVE = FIRS[-1] - ON_PE
            Wo = pc.sb("Wo", [P, C2, D])
            fir = [pc.sb(f"fir{k}", [P, C2, k]) for k in FIRS]
            norm_w = pc.sb("norm_w", [P, 1])
            gate_b = pc.sb("gate_b", [P, HP])
            ltemp = pc.sb("log_temp", [P, HEADS])
            epar = pc.sb("eps_param", [P, HEADS])
            keep = pc.sb("keep", [P, HEADS])
            smax = pc.sb("smax", [P, CH, HEADS])
            diag = pc.sb("diag", [P, ON_PE, C2, P])
            mean_ones = pc.sb("head_mean", [P, P])
            PRt = pc.sb("PRt", [P, TC, HP])
            PRT = pc.sb("PRT", [HP, NT])
            sel = pc.sb("sel", [HP, PATHS, C2, P])
            PB = pc.sb("PB", [P, PATHS, C2, NT])
            Od = pc.sb("Od", [P, C2, NT])
            acc = [pc.sb(f"acc{k}", [P, C2, NT]) for k in FIRS]
            mix = pc.sb("mix", [P, C2, NT])
            SQ = pc.sb("SQ", [P, C2, NT])
            rr = pc.sb("rr", [P, C2, NT])
            ps_f = pc.ps("ps_f", [P, C2, NT])
            ps_p = [pc.ps(f"ps_p{b}", [P, C2, NT]) for b in range(2)]
            ps_a = pc.ps("ps_a", [P, C2, NT])
            loaded = pc.sem("loaded")
            consts = pc.sem("consts")
            prep = pc.sem("prep")
            act_prep = pc.sem("act_prep")
            ready = pc.sem("ready")
            od_loaded = pc.sem("od_loaded")
            pr_staged = pc.sem("pr_staged")
            pr_turned = pc.sem("pr_turned")
            prt_ready = pc.sem("prt_ready")
            spread = pc.sem("spread")
            pb_copied = pc.sem("pb_copied")
            fir_psum = pc.sem("fir_psum")
            tap = pc.sem("tap")
            pool_mix = pc.sem("pool_mix")
            mix_step = pc.sem("mix_step")
            mix_done = pc.sem("mix_done")
            squared = pc.sem("squared")
            stat_psum = pc.sem("stat_psum")
            ln_done = pc.sem("ln_done")
            rr_done = pc.sem("rr_done")
            on_done = pc.sem("on_done")
            o_psum = pc.sem("o_psum")
            resid = pc.sem("resid")
            mean_psum = pc.sem("mean_psum")
            centred = pc.sem("centred")
            x_done = pc.sem("x_done")
            block = pc.block()

            @block.sync
            def _(sp):
                sp.dma_start(Wo[:], w["L0_attn_Wo"].rearrange("(c p) o -> p c o", p=P)).then_inc(loaded, 16)
                for k, n in enumerate(("s", "m", "l")):
                    sp.dma_start(fir[k][:], w[f"L0_attn_fir_{n}"].rearrange("(c p) o -> p c o", p=P)).then_inc(loaded, 16)
                for r in range(2):
                    sp.dma_start(norm_w[HD * r:HD * r + HD, :], w["L0_attn_norm_w"]).then_inc(loaded, 16)
                for t, n in ((gate_b, "gate_b"), (ltemp, "log_temp"), (epar, "eps_param")):
                    sp.dma_start(t[:], w[f"L0_attn_{n}"].to_broadcast(t.shape)).then_inc(loaded, 16)
                with sp.Fori(0, TILES) as n:
                    sp.wait_ge(x_done, n + 1)
                    sp.dma_start(Od[:], scratch["o"].rearrange("(c p) t -> p c t", p=P)[:, :, ds(n * NT, NT)]).then_inc(od_loaded, 16)

            @block.gpsimd
            def _(pool):
                nc.gpsimd.memset(mean_ones[:], 1.0 / HD).then_inc(consts, 1)
                pool.wait_ge(consts, 1)
                g3 = mean_ones[:].rearrange("p (h c) -> p h c", c=HD)
                nc.gpsimd.affine_select(out=g3, in_=g3, compare_op=ALU.is_ge, fill=0.0, base=0,
                                        pattern=[[-HD, P // HD], [0, HD]], channel_multiplier=1).then_inc(consts, 1)
                pool.wait_ge(consts, 2)
                nc.gpsimd.affine_select(out=g3, in_=g3, compare_op=ALU.is_ge, fill=0.0, base=HD - 1,
                                        pattern=[[HD, P // HD], [0, HD]], channel_multiplier=-1).then_inc(consts, 1)
                nc.gpsimd.memset(sel[:], 1.0).then_inc(consts, 1)
                pool.wait_ge(consts, 4)
                sel5 = sel[:].rearrange("r p c (h f) -> r p c h f", h=2)
                for p in range(PATHS):
                    nc.gpsimd.affine_select(out=sel5[:, p], in_=sel5[:, p], compare_op=ALU.is_equal, fill=0.0, base=-p,
                                            pattern=[[-2 * PATHS, C2], [-PATHS, 2], [0, HD]], channel_multiplier=1).then_inc(consts, 1)
                pool.wait_ge(ready, 1)
                with pool.Fori(0, BATCH) as i:
                    for b in range(2):
                        n = i * 2 + b
                        pool.wait_ge(spread, n * PATHS + 1)
                        nc.gpsimd.tensor_copy(PRt[:], LG[:, ds(n * TC, TC), :]).then_inc(pr_staged, 1)
                        pool.wait_ge(od_loaded, n * 16 + 16)
                        pool.wait_ge(pb_copied, n * PATHS + PATHS)
                        nc.gpsimd.tensor_tensor(Od[:], Od[:], PB[:, 3, :, :], ALU.mult).then_inc(pool_mix, 1)
                        vals = VD[:, :, ds(i, 1), PAD + NT * b:PAD + NT * b + NT].rearrange("p c i t -> p c (i t)")
                        nc.gpsimd.tensor_tensor(PB[:, 4, :, :], vals, PB[:, 4, :, :], ALU.mult).then_inc(pool_mix, 1)
                        pool.wait_ge(pool_mix, n * 3 + 2)
                        nc.gpsimd.tensor_tensor(Od[:], Od[:], PB[:, 4, :, :], ALU.add).then_inc(pool_mix, 1)

            @block.tensor
            def _(pe):
                pe.wait_ge(ready, 1)
                pe.sem_inc(spread, 1)
                with pe.Fori(0, BATCH) as i:
                    for b in range(2):
                        n = i * 2 + b
                        pe.wait_ge(pr_staged, n + 1)
                        pe.wait_ge(x_done, n + 1)
                        for k in range(TC):
                            mm = nc.tensor.transpose(ps_p[1][0:HP, 0, P * k:P * k + P], PRt[:, k, :], ident[:])
                        mm.then_inc(pr_turned, 1)
                        pe.wait_ge(prt_ready, n + 1)
                        for p in range(PATHS):
                            if p >= 2:
                                pe.wait_ge(pb_copied, n * PATHS + (p - 1))
                            for c in range(C2):
                                mm = nc.tensor.matmul(ps_p[p % 2][:, c, :], sel[:, p, c, :], PRT[:], start=True, stop=True)
                            mm.then_inc(spread, 1)
                        pe.wait_ge(x_done, n + 1)
                        for c in range(C2):
                            for j in range(ON_PE):
                                win = VD[:, c:c + 1, ds(i, 1), NT * b + j:NT * b + j + NT].rearrange("p c i t -> p (c i t)")
                                mm = nc.tensor.matmul(ps_f[:, c, :], diag[:, j, c, :], win, start=(j == 0), stop=(j == ON_PE - 1))
                        mm.then_inc(fir_psum, 1)
                        pe.wait_ge(squared, n * 2 + 1)
                        for c in range(C2):
                            mm = nc.tensor.matmul(ps_a[:, c, :], mean_ones[:], SQ[:, c, :], start=True, stop=True)
                        mm.then_inc(stat_psum, 1)
                        pe.wait_ge(on_done, n + 1)
                        for c in range(C2):
                            for kk in range(C2):
                                mm = nc.tensor.matmul(ps_a[:, c, :], Wo[:, kk, P * c:P * c + P], mix[:, kk, :],
                                                      start=(kk == 0), stop=(kk == C2 - 1))
                        mm.then_inc(o_psum, 1)
                        pe.wait_ge(resid, n + 1)
                        for kk in range(C2):
                            mm = nc.tensor.matmul(ps_a[:, 0, :], ones_mean[:], mix[:, kk, :], start=(kk == 0), stop=(kk == C2 - 1))
                        mm.then_inc(mean_psum, 1)
                        pe.wait_ge(squared, n * 2 + 2)
                        for kk in range(C2):
                            mm = nc.tensor.matmul(ps_a[:, 1, :], ones_mean[:], SQ[:, kk, :], start=(kk == 0), stop=(kk == C2 - 1))
                        mm.then_inc(stat_psum, 1)

            @block.scalar
            def _(act):
                act.wait_ge(prep, 3)
                act.wait_ge(loaded, 16 * 9)
                nc.scalar.activation(ltemp[:], ltemp[:], ACT.Exp, scale=-1.0).then_inc(act_prep, 1)
                act.wait_ge(prep, 6)
                nc.scalar.activation(LG[:], LG[:], ACT.Exp).then_inc(act_prep, 1)
                with act.Fori(0, BATCH) as i:
                    for b in range(2):
                        n = i * 2 + b
                        act.wait_ge(x_done, n + 1)
                        act.wait_ge(pr_turned, n + 1)
                        nc.scalar.activation(PRT[:], ps_p[1][0:HP, 0, :], ACT.Copy).then_inc(prt_ready, 1)
                        for p in range(PATHS):
                            act.wait_ge(spread, n * PATHS + (p + 2))
                            nc.scalar.activation(PB[:, p, :, :], ps_p[p % 2][:], ACT.Copy).then_inc(pb_copied, 1)
                        act.wait_ge(mix_done, n + 1)
                        nc.scalar.activation(SQ[:], mix[:], ACT.Square).then_inc(squared, 1)
                        act.wait_ge(stat_psum, n * 2 + 1)
                        nc.scalar.activation(rr[:], ps_a[:], ACT.Ln, bias=epsb[:, 0:1]).then_inc(ln_done, 1)
                        act.wait_ge(ln_done, n * 2 + 1)
                        nc.scalar.activation(rr[:], rr[:], ACT.Exp, scale=-0.5).then_inc(rr_done, 1)
                        act.wait_ge(centred, n + 1)
                        nc.scalar.activation(SQ[:], mix[:], ACT.Square).then_inc(squared, 1)
                        act.wait_ge(stat_psum, n * 2 + 2)
                        nc.scalar.activation(rr[:, 0, :], ps_a[:, 1, :], ACT.Ln, bias=epsb[:, 0:1]).then_inc(ln_done, 1)
                        act.wait_ge(ln_done, n * 2 + 2)
                        nc.scalar.activation(rr[:, 0, :], rr[:, 0, :], ACT.Exp, scale=-0.5).then_inc(rr_done, 1)

            @block.vector
            def _(dve):
                lg = LG[:].rearrange("p j (h x) -> p j h x", h=HEADS)
                per_head = lambda ap: ap.unsqueeze(1).to_broadcast([P, CH, HEADS]).unsqueeze(3).to_broadcast([P, CH, HEADS, PATHS])
                n_prep = [0]

                def then(ins):
                    n_prep[0] += 1
                    ins.then_inc(prep, 1)
                    dve.wait_ge(prep, n_prep[0])

                dve.wait_ge(loaded, 16 * 9)
                then(nc.vector.tensor_scalar(epar[:], epar[:], 0.0, 0.2, ALU.max, ALU.min))
                then(nc.vector.tensor_scalar(keep[:], epar[:], -float(PATHS), 1.0, ALU.mult, ALU.add))
                then(nc.vector.tensor_tensor(LG[:], LG[:], gate_b[:].unsqueeze(1).to_broadcast([P, CH, HP]), ALU.add))
                dve.wait_ge(act_prep, 1)
                for h in range(HEADS):
                    ins = nc.vector.tensor_scalar(lg[:, :, h, :], lg[:, :, h, :], ltemp[:, h:h + 1], None, ALU.mult)
                then(ins)
                then(nc.vector.tensor_reduce(smax[:], lg, AX.X, ALU.max))
                then(nc.vector.tensor_tensor(lg, lg, smax[:].unsqueeze(3).to_broadcast([P, CH, HEADS, PATHS]), ALU.subtract))
                dve.wait_ge(act_prep, 2)
                then(nc.vector.tensor_reduce(smax[:], lg, AX.X, ALU.add))
                then(nc.vector.reciprocal(smax[:], smax[:]))
                then(nc.vector.tensor_tensor(lg, lg, smax[:].unsqueeze(3).to_broadcast([P, CH, HEADS, PATHS]), ALU.mult))
                for h in range(HEADS):
                    ins = nc.vector.tensor_scalar(lg[:, :, h, :], lg[:, :, h, :], keep[:, h:h + 1], epar[:, h:h + 1], ALU.mult, ALU.add)
                then(ins)
                for c in range(C2):
                    nc.vector.tensor_scalar(Wo[:, c, :], Wo[:, c, :], norm_w[:, 0:1], None, ALU.mult)
                    for j in range(ON_PE):
                        ins = nc.vector.tensor_scalar(diag[:, j, c, :], ident[:], fir[2][:, c, j:j + 1], None, ALU.mult)
                then(ins)
                dve.wait_ge(consts, 4 + PATHS)
                dve.sem_inc(ready, 1)
                dve.sem_inc(x_done, 1)
                counts = [FIRS[0], FIRS[1], ON_DVE]
                ROUNDS = max(counts)
                with dve.Fori(0, BATCH) as i:
                    for b in range(2):
                        n = i * 2 + b
                        tile = X[:, :, ds(n * NT, NT)]
                        dve.wait_ge(x_done, n + 1)
                        for j in range(ROUNDS):
                            if j:
                                dve.wait_ge(tap, n * ROUNDS + j)
                            for f, k in enumerate(FIRS):
                                if j >= counts[f]:
                                    continue
                                first = ON_PE if f == 2 else 0
                                for c in range(C2):
                                    o = PAD - (k - 1) + first + j + NT * b
                                    src = VD[:, c:c + 1, ds(i, 1), o:o + NT].rearrange("p c i t -> p (c i t)")
                                    dst = acc[f][:, c, :]
                                    wt = fir[f][:, c, first + j:first + j + 1]
                                    if j == 0:
                                        ins = nc.vector.tensor_scalar(dst, src, wt, None, ALU.mult)
                                    else:
                                        ins = nc.vector.scalar_tensor_tensor(out=dst, in0=src, scalar=wt, in1=dst,
                                                                             op0=ALU.mult, op1=ALU.add)
                            ins.then_inc(tap, 1)
                        dve.wait_ge(tap, n * ROUNDS + ROUNDS)
                        dve.wait_ge(fir_psum, n + 1)
                        dve.wait_ge(pb_copied, n * PATHS + PATHS)
                        steps = 0

                        def mixed(ins):
                            nonlocal steps
                            steps += 1
                            ins.then_inc(mix_step, 1)
                            dve.wait_ge(mix_step, n * 4 + steps)
                        nc.vector.tensor_tensor(acc[0][:], acc[0][:], PB[:, 0, :, :], ALU.mult)
                        nc.vector.tensor_tensor(acc[1][:], acc[1][:], PB[:, 1, :, :], ALU.mult)
                        mixed(nc.vector.tensor_tensor(acc[2][:], acc[2][:], ps_f[:], ALU.add))
                        mixed(nc.vector.tensor_tensor(acc[2][:], acc[2][:], PB[:, 2, :, :], ALU.mult))
                        mixed(nc.vector.tensor_tensor(acc[0][:], acc[0][:], acc[1][:], ALU.add))
                        mixed(nc.vector.tensor_tensor(acc[0][:], acc[0][:], acc[2][:], ALU.add))
                        dve.wait_ge(pool_mix, n * 3 + 3)
                        nc.vector.tensor_tensor(mix[:], acc[0][:], Od[:], ALU.add).then_inc(mix_done, 1)
                        dve.wait_ge(mix_done, n + 1)
                        dve.wait_ge(rr_done, n * 2 + 1)
                        nc.vector.tensor_tensor(mix[:], mix[:], rr[:], ALU.mult).then_inc(on_done, 1)
                        dve.wait_ge(o_psum, n + 1)
                        nc.vector.tensor_tensor(mix[:], ps_a[:], tile, ALU.add).then_inc(resid, 1)
                        dve.wait_ge(resid, n + 1)
                        dve.wait_ge(mean_psum, n + 1)
                        nc.vector.tensor_tensor(mix[:], mix[:], ps_a[:, 0, :].unsqueeze(1).to_broadcast([P, C2, NT]),
                                                ALU.subtract).then_inc(centred, 1)
                        dve.wait_ge(centred, n + 1)
                        dve.wait_ge(rr_done, n * 2 + 2)
                        nc.vector.tensor_tensor(tile, mix[:], rr[:, 0, :].unsqueeze(1).to_broadcast([P, C2, NT]),
                                                ALU.mult).then_inc(x_done, 1)


def lora_ffn_stage(nc, X, ones_mean, w):
    FF = 1024
    KF = FF // P
    HALFM = KF // 2
    RANK = 16
    MAGIC = 1.5 * 2.0 ** 23
    with Phase(nc, "ffn") as ph:
        w_fc = ph.sb("w_fc", [P, C2, FF])
        w_pr = ph.sb("w_pr", [P, KF, D])
        a_fc = ph.sb("a_fc", [RANK, D])
        bt_fc = ph.sb("bt_fc", [RANK, FF])
        a_pr = ph.sb("a_pr", [RANK, FF])
        bt_pr = ph.sb("bt_pr", [RANK, D])
        b_fc = ph.sb("b_fc", [P, KF])
        b_pr = ph.sb("b_pr", [P, C2])
        amax = ph.sb("amax", [P, 2])
        amax_all = ph.sb("amax_all", [P, 2])
        qstep = ph.sb("qstep", [P, 2])
        qinv = ph.sb("qinv", [P, 2])
        H = ph.sb("H", [P, KF, NT])
        R = ph.sb("R", [P, C2, NT])
        XC = ph.sb("XC", [P, C2, NT])
        SQ = ph.sb("SQ", [P, C2, NT])
        std = ph.sb("std", [P, NT])
        rstd = ph.sb("rstd", [P, NT])
        epsb = ph.sb("epsb", [P, 1])
        ps_h = [ph.ps(f"ps_h{b}", [P, NT]) for b in range(4)]
        ps_y = [ph.ps(f"ps_y{c}", [P, NT]) for c in range(C2)]
        ps_mean = ph.ps("ps_mean", [P, NT])
        ps_var = ph.ps("ps_var", [P, NT])
        loaded = ph.sem("loaded")
        dve_prep = ph.sem("dve_prep")
        amax_ready = ph.sem("amax_ready")
        fold_ready = ph.sem("fold_ready")
        fold_used = ph.sem("fold_used")
        weights_ready = ph.sem("weights_ready")
        h_psum = ph.sem("h_psum")
        h_done = ph.sem("h_done")
        y_psum = ph.sem("y_psum")
        resid = ph.sem("resid")
        mean_psum = ph.sem("mean_psum")
        centred = ph.sem("centred")
        squared = ph.sem("squared")
        var_psum = ph.sem("var_psum")
        std_done = ph.sem("std_done")
        rstd_done = ph.sem("rstd_done")
        x_done = ph.sem("x_done")
        block = ph.block()
        folds = [(w_fc[:, c, 512 * n:512 * n + 512], a_fc[:, P * c:P * c + P], bt_fc[:, 512 * n:512 * n + 512])
                 for c in range(C2) for n in range(FF // 512)]
        folds += [(w_pr[:, m, :], a_pr[:, P * m:P * m + P], bt_pr[:, :]) for m in range(KF)]

        @block.sync
        def _(sp):
            sp.dma_start(w_fc[:], w["L1_ffn_W_fc"].rearrange("(c p) f -> p c f", p=P)).then_inc(loaded, 16)
            sp.dma_start(w_pr[:], w["L1_ffn_W_proj"].rearrange("(c p) f -> p c f", p=P)).then_inc(loaded, 16)
            sp.dma_start(a_fc[:], w["L1_ffn_A_fc"]).then_inc(loaded, 16)
            sp.dma_start(bt_fc[:], w["L1_ffn_B_fc"]).then_inc(loaded, 16)
            sp.dma_start(a_pr[:], w["L1_ffn_A_proj"]).then_inc(loaded, 16)
            sp.dma_start(bt_pr[:], w["L1_ffn_B_proj"]).then_inc(loaded, 16)
            sp.dma_start(b_fc[:], w["L1_ffn_b_fc"]).then_inc(loaded, 16)
            sp.dma_start(b_pr[:], w["L1_ffn_b_proj"]).then_inc(loaded, 16)

        @block.gpsimd
        def _(pool):
            pool.wait_ge(dve_prep, 3)
            nc.gpsimd.partition_all_reduce(amax_all[:], amax[:], P, bass.bass_isa.ReduceOp.max).then_inc(amax_ready, 1)

        @block.tensor
        def _(pe):
            pe.wait_ge(loaded, 16 * 8)
            for n, (dst, a, bt) in enumerate(folds):
                if n >= 4:
                    pe.wait_ge(fold_used, n - 3)
                size = dst.shape[-1]
                nc.tensor.matmul(ps_h[n % 4][:, 0:size], a, bt, start=True, stop=True).then_inc(fold_ready, 1)
            pe.wait_ge(weights_ready, 1)

            def up(i, m0, m1):
                for m in range(m0, m1):
                    pe.wait_ge(h_done, i * KF + m + 1)
                    for c in range(C2):
                        mm = nc.tensor.matmul(ps_h[m % 4][:], w_fc[:, c, P * m:P * m + P], X[:, c, ds(i * NT, NT)],
                                              start=(c == 0), stop=(c == C2 - 1))
                    mm.then_inc(h_psum, 1)

            def down(i):
                pe.wait_ge(resid, C2 * i + 1)
                for c in range(C2):
                    for m in range(KF):
                        if c == 0:
                            pe.wait_ge(h_done, i * KF + m + 5)
                        mm = nc.tensor.matmul(ps_y[c][:], w_pr[:, m, P * c:P * c + P], H[:, m, :],
                                              start=(m == 0), stop=(m == KF - 1))
                    mm.then_inc(y_psum, 1)

            def mean(i):
                pe.wait_ge(resid, C2 * (i + 1) + 1)
                for c in range(C2):
                    mm = nc.tensor.matmul(ps_mean[:], ones_mean[:], R[:, c, :], start=(c == 0), stop=(c == C2 - 1))
                mm.then_inc(mean_psum, 1)

            def var(i):
                pe.wait_ge(squared, i + 1)
                for c in range(C2):
                    mm = nc.tensor.matmul(ps_var[:], ones_mean[:], SQ[:, c, :], start=(c == 0), stop=(c == C2 - 1))
                mm.then_inc(var_psum, 1)

            up(0, 0, KF)
            with pe.Fori(0, TILES - 1) as i:
                down(i)
                up(i + 1, 0, HALFM)
                mean(i)
                up(i + 1, HALFM, KF)
                var(i)
            down(TILES - 1)
            mean(TILES - 1)
            var(TILES - 1)

        @block.scalar
        def _(act):
            act.sem_inc(h_done, 4)

            def gelu(i, m0, m1):
                for m in range(m0, m1):
                    act.wait_ge(h_psum, i * KF + m + 1)
                    if m == 0:
                        act.wait_ge(y_psum, C2 * i + 2)
                    nc.scalar.activation(H[:, m, :], ps_h[m % 4][:], ACT.Gelu, bias=b_fc[:, m:m + 1]).then_inc(h_done, 1)

            def squares(i):
                act.wait_ge(centred, i + 1)
                act.wait_ge(var_psum, i + 1)
                nc.scalar.activation(SQ[:], XC[:], ACT.Square).then_inc(squared, 1)

            def roots(i):
                act.wait_ge(var_psum, i + 2)
                nc.scalar.activation(std[:], ps_var[:], ACT.Sqrt, bias=epsb[:, 0:1]).then_inc(std_done, 1)

            act.sem_inc(y_psum, C2)
            act.sem_inc(var_psum, 1)
            act.wait_ge(weights_ready, 1)
            gelu(0, 0, KF)
            with act.Fori(0, TILES - 1) as i:
                gelu(i + 1, 0, HALFM)
                squares(i)
                gelu(i + 1, HALFM, KF)
                roots(i)
            squares(TILES - 1)
            roots(TILES - 1)

        @block.vector
        def _(dve):
            nc.vector.memset(epsb[:], EPS).then_inc(dve_prep, 1)
            dve.wait_ge(loaded, 16 * 8)
            nc.vector.tensor_reduce(amax[:, 0:1], w_fc[:], AX.XY, ALU.max, apply_absolute_value=True).then_inc(dve_prep, 1)
            nc.vector.tensor_reduce(amax[:, 1:2], w_pr[:], AX.XY, ALU.max, apply_absolute_value=True).then_inc(dve_prep, 1)
            dve.wait_ge(amax_ready, 1)
            nc.vector.tensor_scalar(qstep[:], amax_all[:], 1.0 / 127.0, None, ALU.mult).then_inc(dve_prep, 1)
            dve.wait_ge(dve_prep, 4)
            nc.vector.reciprocal(qinv[:], qstep[:]).then_inc(dve_prep, 1)
            dve.wait_ge(dve_prep, 5)
            for n, W in enumerate((w_fc, w_pr)):
                nc.vector.tensor_scalar(W[:], W[:], qinv[:, n:n + 1], MAGIC, ALU.mult, ALU.add).then_inc(dve_prep, 1)
                dve.wait_ge(dve_prep, 6 + 3 * n)
                nc.vector.tensor_scalar(W[:], W[:], -MAGIC, 127.0, ALU.add, ALU.min).then_inc(dve_prep, 1)
                dve.wait_ge(dve_prep, 7 + 3 * n)
                nc.vector.tensor_scalar(W[:], W[:], -128.0, qstep[:, n:n + 1], ALU.max, ALU.mult).then_inc(dve_prep, 1)
                dve.wait_ge(dve_prep, 8 + 3 * n)
            for n, (dst, a, bt) in enumerate(folds):
                dve.wait_ge(fold_ready, n + 1)
                size = dst.shape[-1]
                nc.vector.scalar_tensor_tensor(out=dst, in0=ps_h[n % 4][:, 0:size], scalar=2.0, in1=dst,
                                               op0=ALU.mult, op1=ALU.add).then_inc(fold_used, 1)
            dve.wait_ge(fold_used, len(folds))
            dve.sem_inc(weights_ready, 1)
            dve.sem_inc(resid, 1)

            def tail(i):
                for c in range(C2):
                    dve.wait_ge(y_psum, C2 * i + C2 + c + 1)
                    dve.wait_ge(mean_psum, i)
                    nc.vector.scalar_tensor_tensor(out=R[:, c, :], in0=ps_y[c][:], scalar=b_pr[:, c:c + 1],
                                                   in1=X[:, c, ds(i * NT, NT)], op0=ALU.add, op1=ALU.add).then_inc(resid, 1)
                dve.wait_ge(mean_psum, i + 1)
                dve.wait_ge(resid, C2 * (i + 1) + 1)
                nc.vector.tensor_tensor(XC[:], R[:], ps_mean[:].unsqueeze(1).to_broadcast([P, C2, NT]),
                                        ALU.subtract).then_inc(centred, 1)
                dve.wait_ge(std_done, i + 1)
                nc.vector.reciprocal(rstd[:], std[:]).then_inc(rstd_done, 1)
                dve.wait_ge(rstd_done, i + 1)
                nc.vector.tensor_tensor(X[:, :, ds(i * NT, NT)], XC[:], rstd[:].unsqueeze(1).to_broadcast([P, C2, NT]),
                                        ALU.mult).then_inc(x_done, 1)
            with dve.Fori(0, TILES) as i:
                tail(i)


def program(nc, w, out):
    with Phase(nc, "top") as top:
        X = top.sb("x_stream", [P, C2, TOK])
        ones_mean = top.sb("ones_mean", [P, P])
        ident = top.sb("ident", [P, P])
        zeros_written = top.sem("zeros_written")
        BLOCK_ROWS = 40 * P
        sorted_in = nc.dram_tensor("sorted_in", (BLOCK_ROWS, D), F32).ap()
        sorted_out = nc.dram_tensor("sorted_out", (BLOCK_ROWS, D), F32).ap()
        with Phase(nc, "load") as ph:
            zeros = ph.sb("zeros", [P, D])
            x_loaded = ph.sem("x_loaded")
            zeroed = ph.sem("zeroed")
            zeros_set = ph.sem("zeros_set")
            block = ph.block()

            @block.sync
            def _(sp):
                sp.dma_start(X[:], w["x"].rearrange("(c p) t -> p c t", p=P)).then_inc(x_loaded, 16)
                sp.wait_ge(x_loaded, 16)

                sp.wait_ge(zeros_set, 1)
                sp.dma_start(sorted_in.rearrange("(m p) d -> p m d", p=P),
                             zeros[:].unsqueeze(1).to_broadcast([P, BLOCK_ROWS // P, D])).then_inc(zeros_written, 16)
                sp.wait_ge(zeros_written, 16)

            @block.vector
            def _(dve):
                nc.vector.memset(zeros[:], 0.0).then_inc(zeros_set, 1)
                nc.vector.memset(ones_mean[:], 1.0 / D)

            @block.gpsimd
            def _(pool):
                nc.gpsimd.memset(ident[:], 0.0).then_inc(zeroed, 1)
                pool.wait_ge(zeroed, 1)
                nc.gpsimd.affine_select(out=ident[:], in_=ident[:], compare_op=ALU.not_equal, fill=1.0, base=0,
                                        pattern=[[-1, P]], channel_multiplier=1)

        if 0 in STAGES:
            delta_stage(nc, X, ones_mean, ident, w)
        if 1 in STAGES:
            cross_attention_stage(nc, X, ones_mean, ident, w, gated=True)
        if 2 in STAGES:
            expert_stage(nc, X, ones_mean, ident, w, sorted_in, sorted_out, zeros_written)
        if 3 in STAGES:
            recurrence_stage(nc, X, ones_mean, w)
        if 4 in STAGES:
            cross_attention_stage(nc, X, ones_mean, ident, w, gated=False)

        if 5 in STAGES:
            lora_ffn_stage(nc, X, ones_mean, w)

        with Phase(nc, "store") as ph:
            stored = ph.sem("stored")
            block = ph.block()

            @block.sync
            def _(sp):
                sp.dma_start(out.rearrange("(c p) t -> p c t", p=P), X[:]).then_inc(stored, 16)
                sp.wait_ge(stored, 16)


def _layout(name, a):
    import numpy as _np
    if name == "x":
        return a.reshape(TOK, D).T
    if name == "ctx_1024":
        return a.reshape(-1, D).T
    if name in TRANSPOSED:
        return a.T
    if name in ("L0_ffn_w1", "L0_ffn_w2"):
        return a.transpose(0, 2, 1)
    if name in ("L0_ffn_ln_g", "L0_ffn_ln_b", "L0_ffn_b1"):
        return a.reshape(a.shape[0], -1, P).transpose(2, 0, 1)
    if name == "L0_attn_gate_w":
        return a.reshape(-1, D).T
    if name.startswith("L0_attn_fir"):
        return a.reshape(D, -1)
    if name == "L0_attn_norm_w":
        return a.reshape(-1, 1)
    if name in ("L0_attn_gate_b", "L0_attn_log_temp", "L0_attn_eps_param"):
        return a.reshape(1, -1)
    if name in PARTITIONED:
        return a.reshape(-1, P).T
    return a


TRANSPOSED = ("L0_attn_Wq", "L0_attn_Wk", "L0_attn_Wv", "L0_attn_Wb", "L0_attn_Wo", "L0_xattn_Wq", "L0_xattn_Wk",
              "L0_xattn_Wv", "L0_xattn_Wg", "L0_xattn_Wo", "L0_ffn_centroids", "L1_attn_Wf1", "L1_attn_Wog1",
              "L1_xattn_Wq", "L1_xattn_Wk", "L1_xattn_Wv", "L1_xattn_Wo",
              "L1_ffn_W_fc", "L1_ffn_B_fc", "L1_ffn_W_proj", "L1_ffn_B_proj")
PARTITIONED = ("L1_ffn_b_fc", "L1_ffn_b_proj", "L1_xattn_bq", "L1_xattn_bk", "L1_xattn_bv", "L1_xattn_bo",
               "L0_xattn_qln_g", "L0_xattn_qln_b", "L0_xattn_kvln_g", "L0_xattn_kvln_b", "L0_xattn_bg",
               "L1_attn_norm_w")


def kernel(**inputs):
    import numpy as _np
    import concourse.bacc as _bacc
    from concourse import mybir as _mybir
    from concourse.bass_utils import run_bass_kernel_spmd as _run

    nc = _bacc.Bacc("TRN2", target_bir_lowering=False, num_devices=1)
    arrays, w = {}, {}
    for name, a in inputs.items():
        a = _np.ascontiguousarray(_layout(name, _np.asarray(a)))
        arrays[f"in_{name}"] = a
        w[name] = nc.dram_tensor(f"in_{name}", a.shape, _mybir.dt.from_np(a.dtype), kind="ExternalInput").ap()
    out = nc.dram_tensor("out_x", (D, TOK), F32, kind="ExternalOutput").ap()
    program(nc, w, out)
    r = _run(nc, [arrays], core_ids=[0])
    return _np.ascontiguousarray(_np.asarray(r.results[0]["out_x"]).reshape(D, BATCH, SEQ).transpose(1, 2, 0))
```

```python
from contextlib import ExitStack

import numpy as np

import concourse.bass as bass
from concourse import mybir

STAGES = (0, 1, 2, 3, 4, 5)

P = 128
D = 256
C2 = D // P
BATCH = 4
SEQ = 1024
TOK = BATCH * SEQ
NT = 512
TILES = TOK // NT
EPS = 1e-5

F32 = mybir.dt.float32
I32 = mybir.dt.int32
U32 = mybir.dt.uint32
ALU = mybir.AluOpType
ACT = mybir.ActivationFunctionType
AX = mybir.AxisListType
ds = bass.ds


class Phase:

    def __init__(self, nc, name):
        self.nc, self.name, self.ctx, self.sems = nc, name, ExitStack(), []

    def __enter__(self):
        self.ctx.__enter__()
        return self

    def __exit__(self, *a):
        self.ctx.__exit__(*a)
        if self.sems:
            self.nc.clear_and_free_semaphores(self.sems)
            self.nc.all_engine_barrier()

    def sb(self, name, shape, dt=F32):
        return self.ctx.enter_context(self.nc.sbuf_tensor(f"{self.name}_{name}", shape, dt))

    def ps(self, name, shape, dt=F32):
        return self.ctx.enter_context(self.nc.psum_tensor(f"{self.name}_{name}", shape, dt))

    def sem(self, name):
        self.sems.append(self.nc.alloc_semaphore(f"{self.name}_{name}"))
        return self.sems[-1]

    def block(self):
        return self.ctx.enter_context(self.nc.Block())


def recurrence_stage(nc, X, ones_mean, w):
    HEADS, HD = 16, D // 16
    BL = 2
    HB = NT // BL
    ROWS = 7
    ROW_F, ROW_A, ROW_K, ROW_Q = 0, 1, 3, 5
    LOG_SCALE = 40.0
    with Phase(nc, "rec") as ph:
        G = ph.sb("out_gate", [P, C2, TOK])
        Wo = ph.sb("Wo", [P, C2, D])
        norm_w = ph.sb("norm_w", [P, C2])
        epsb = ph.sb("epsb", [P, 1])
        rows_dram = nc.dram_tensor("rec_rows", (D, ROWS, TOK // BL), F32).ap()
        v_dram, w_dram, o_dram = (nc.dram_tensor(f"rec_{n}", (D, BL, TOK // BL), F32).ap() for n in ("v", "w", "o"))

        with Phase(nc, "recA") as pa:
            W = {n: pa.sb(n, [P, C2, D]) for n in ("Wq", "Wk", "Wv", "Wf", "Wog", "Wga")}
            small = {n: pa.sb(n, [HD, D]) for n in ("Wf1", "Wf2", "Wog1", "Wog2")}
            wgamma = pa.sb("wgamma", [P, C2, HEADS])
            group_ones = pa.sb("group_ones", [P, P])
            norm_bias = pa.sb("norm_bias", [P, 1])
            bufs = {n: [pa.sb(f"{n}{b}", [P, C2, BL, HB]) for b in range(2)]
                    for n in ("sigq", "sigk", "q", "k", "f", "sg", "v", "norm", "ff", "a", "w")}
            tmp = pa.sb("tmp", [P, C2, BL, HB])
            slot = [pa.ps(f"slot{s}", [P, C2, NT]) for s in range(4)]
            full = [pa.sem(f"slot_full{s}") for s in range(4)]
            free = [pa.sem(f"slot_free{s}") for s in range(4)]
            USE = {"q": (0, 0), "k": (1, 0), "f": (2, 0), "ga": (3, 0), "og": (0, 1), "v": (1, 1), "ss": (2, 1),
                   "nn": (3, 3), "mn": (0, 5)}
            PER = [3, 2, 2, 2]
            loaded = pa.sem("loaded")
            consts = pa.sem("consts")
            fold_psum = pa.sem("fold_psum")
            folded = pa.sem("folded")
            weights_ready = pa.sem("weights_ready")
            sig_done = {n: pa.sem(f"{n}_done") for n in ("sigq", "sigk", "f", "sg", "og", "v", "sq", "ln", "norm")}
            did = {n: pa.sem(f"did_{n}") for n in ("q", "k", "clamp", "kn", "a", "ff", "fff", "pool_products", "qk",
                                                   "row_a", "row_v", "rows_q", "rows_w", "step_m", "step_n")}
            stored = [pa.sem(f"stored{b}") for b in range(2)]
            STORES = 16 * 11
            block = pa.block()

            SKIPPED = {"nn": 1, "mn": 2}

            def slot_free(pe, n, key, last=False):
                s, u = USE[key]
                pe.wait_ge(free[s], n * PER[s] + (u + 1 - (SKIPPED[key] if last else 0)))
                return slot[s], full[s]

            def slot_full(eng, n, key, last=False):
                s, u = USE[key]
                eng.wait_ge(full[s], n * PER[s] + (u + 1 - (SKIPPED[key] if last else 0)))
                return slot[s], free[s]

            def buffers_free(eng, i, b):
                eng.wait_ge(stored[b], (i + 1) * STORES)

            def rounds(eng, part1, part2, first=lambda: None):
                part1(0, 0, 0)
                first()
                with eng.Fori(0, TILES // 2 - 1) as i:
                    part1(i * 2 + 1, i, 1)
                    part2(i * 2, i, 0)
                    part1(i * 2 + 2, i + 1, 0)
                    part2(i * 2 + 1, i, 1)
                part1(TILES - 1, TILES // 2 - 1, 1)
                part2(TILES - 2, TILES // 2 - 1, 0)
                part2(TILES - 1, TILES // 2 - 1, 1, last=True)

            planes = lambda ap: ap.rearrange("p c (t x) -> p c x t", x=BL)

            @block.sync
            def _(sp):
                for n in ("Wq", "Wk", "Wv"):
                    sp.dma_start(W[n][:], w[f"L1_attn_{n}"].rearrange("(c p) o -> p c o", p=P)).then_inc(loaded, 16)
                sp.dma_start(Wo[:], w["L1_attn_Wo"].rearrange("(c p) o -> p c o", p=P)).then_inc(loaded, 16)
                for n in small:
                    sp.dma_start(small[n][:], w[f"L1_attn_{n}"]).then_inc(loaded, 16)
                sp.dma_start(wgamma[:], w["L1_attn_Wgamma"].rearrange("(c p) o -> p c o", p=P)).then_inc(loaded, 16)
                sp.dma_start(norm_w[:], w["L1_attn_norm_w"]).then_inc(loaded, 16)
                sp.sem_inc(stored[0], STORES)
                sp.sem_inc(stored[1], STORES)
                with sp.Fori(0, TILES // 2) as i:
                    for b in range(2):
                        n = i * 2 + b

                        def store(dram, x, buf, plane):
                            sp.dma_start(dram.rearrange("(c p) x t -> p c x t", p=P)[:, :, x, ds(n * HB, HB)],
                                         bufs[buf][b][:, :, plane, :]).then_inc(stored[b], 16)
                        sp.wait_ge(sig_done["v"], n + 1)
                        store(v_dram, 0, "v", 0)
                        sp.wait_ge(did["kn"], n + 1)
                        store(rows_dram, ROW_K + 1, "k", 1)
                        sp.wait_ge(did["a"], n + 1)
                        store(rows_dram, ROW_A, "a", 0)
                        sp.wait_ge(did["pool_products"], (n + 1) * 6)
                        store(rows_dram, ROW_K, "ff", 0)
                        store(rows_dram, ROW_F, "ff", 1)
                        sp.wait_ge(did["row_a"], n + 1)
                        store(rows_dram, ROW_A + 1, "sg", 0)
                        sp.wait_ge(did["row_v"], n + 1)
                        store(v_dram, 1, "sg", 1)
                        sp.wait_ge(did["rows_q"], n + 1)
                        for x in range(BL):
                            store(rows_dram, ROW_Q + x, "sigk", x)
                        sp.wait_ge(did["rows_w"], n + 1)
                        for x in range(BL):
                            store(w_dram, x, "w", x)
                for b in range(2):
                    sp.wait_ge(stored[b], STORES * (TILES // 2 + 1))

            @block.gpsimd
            def _(pool):
                nc.gpsimd.memset(group_ones[:], 1.0).then_inc(consts, 1)
                pool.wait_ge(consts, 1)
                g3 = group_ones[:].rearrange("p (h c) -> p h c", c=HD)
                nc.gpsimd.affine_select(out=g3, in_=g3, compare_op=ALU.is_ge, fill=0.0, base=0,
                                        pattern=[[-HD, P // HD], [0, HD]], channel_multiplier=1).then_inc(consts, 1)
                pool.wait_ge(consts, 2)
                nc.gpsimd.affine_select(out=g3, in_=g3, compare_op=ALU.is_ge, fill=0.0, base=HD - 1,
                                        pattern=[[HD, P // HD], [0, HD]], channel_multiplier=-1).then_inc(consts, 1)

                def gates(n, i, b):
                    buffers_free(pool, i, b)
                    pool.wait_ge(sig_done["f"], n + 1)
                    pool.wait_ge(sig_done["sg"], n + 1)
                    nc.gpsimd.tensor_tensor(bufs["ff"][b][:], bufs["f"][b][:], bufs["f"][b][:], ALU.mult).then_inc(did["ff"], 1)
                    pool.wait_ge(did["ff"], n + 1)
                    nc.gpsimd.tensor_tensor(bufs["ff"][b][:], bufs["ff"][b][:], bufs["sg"][b][:], ALU.mult).then_inc(did["fff"], 1)

                def products(n, i, b, last=False):
                    k, q, f, a = (bufs[x][b] for x in ("k", "q", "f", "a"))
                    K0, F = bufs["ff"][b][:, :, 0, :], bufs["ff"][b][:, :, 1, :]
                    mul = lambda o, x, y: nc.gpsimd.tensor_tensor(o, x, y, ALU.mult)
                    done = did["pool_products"]
                    pool.wait_ge(did["kn"], n + 1)
                    pool.wait_ge(did["q"], n + 1)
                    mul(bufs["sigq"][b][:], q[:], k[:]).then_inc(did["qk"], 1)
                    pool.wait_ge(did["a"], n + 1)
                    mul(K0, f[:, :, 1, :], k[:, :, 0, :]).then_inc(done, 1)
                    mul(F, f[:, :, 1, :], f[:, :, 0, :]).then_inc(done, 1)
                    mul(bufs["norm"][b][:, :, 0, :], a[:, :, 1, :], k[:, :, 0, :]).then_inc(done, 1)
                    mul(bufs["sigk"][b][:, :, 0, :], q[:, :, 0, :], f[:, :, 0, :]).then_inc(done, 1)
                    pool.wait_ge(done, n * 6 + 2)
                    mul(bufs["norm"][b][:, :, 1, :], q[:, :, 1, :], K0).then_inc(done, 1)
                    mul(bufs["sigk"][b][:, :, 1, :], q[:, :, 1, :], F).then_inc(done, 1)
                rounds(pool, gates, products)

            @block.tensor
            def _(pe):
                pe.wait_ge(loaded, 16 * 10)
                pe.wait_ge(consts, 3)
                for s, (a, bb) in enumerate((("Wf1", "Wf2"), ("Wog1", "Wog2"))):
                    for c in range(C2):
                        mm = nc.tensor.matmul(slot[s][:, c, 0:D], small[a][:, P * c:P * c + P], small[bb][:], start=True, stop=True)
                mm.then_inc(fold_psum, 1)
                pe.wait_ge(weights_ready, 1)

                def pass_over():
                    for s in (0, 3):
                        pe.wait_ge(free[s], PER[s])
                        pe.sem_inc(full[s], 1)
                        pe.sem_inc(free[s], 1)

                def project(n, i, b):
                    for key, name in (("k", "Wk"), ("q", "Wq"), ("f", "Wf"), ("ga", "Wga"), ("og", "Wog"), ("v", "Wv")):
                        dst, sem = slot_free(pe, n, key)
                        for c in range(C2):
                            for kk in range(C2):
                                mm = nc.tensor.matmul(dst[:, c, :], W[name][:, kk, P * c:P * c + P], X[:, kk, ds(n * NT, NT)],
                                                      start=(kk == 0), stop=(kk == C2 - 1))
                        mm.then_inc(sem, 1)
                    head_sums(n, "ss", sig_done["sq"], n + 1, bufs["norm"][b], False)

                def head_sums(n, key, sem_in, count, src, last):
                    pe.wait_ge(sem_in, count)
                    dst, sem = slot_free(pe, n, key, last)
                    for c in range(C2):
                        mm = nc.tensor.matmul(dst[:, c, :], group_ones[:], src[:, c, :, :].rearrange("p x t -> p (x t)"),
                                              start=True, stop=True)
                    mm.then_inc(sem, 1)

                def sums(n, i, b, last=False):
                    head_sums(n, "nn", did["qk"], n + 1, bufs["sigq"][b], last)
                    head_sums(n, "mn", did["pool_products"], (n + 1) * 6, bufs["norm"][b], last)
                rounds(pe, project, sums, pass_over)

            @block.scalar
            def _(act):
                def tile(n, i, b):
                    buffers_free(act, i, b)

                    def read(key, out, func, done, frees):
                        src, sem = slot_full(act, n, key)
                        nc.scalar.activation(out, src[:] if key == "og" else planes(src[:]), func).then_inc(sig_done[done], 1)
                        if frees:
                            act.wait_ge(sig_done[done], n + 1)
                            act.sem_inc(sem, 1)
                    read("k", bufs["sigk"][b][:], ACT.Sigmoid, "sigk", False)
                    read("q", bufs["sigq"][b][:], ACT.Sigmoid, "sigq", False)
                    read("f", bufs["f"][b][:], ACT.Sigmoid, "f", True)
                    read("ga", bufs["sg"][b][:], ACT.Sigmoid, "sg", True)
                    read("og", G[:, :, ds(n * NT, NT)], ACT.Sigmoid, "og", True)
                    act.wait_ge(did["k"], n + 1)
                    nc.scalar.activation(bufs["norm"][b][:], bufs["k"][b][:], ACT.Square).then_inc(sig_done["sq"], 1)
                    read("v", bufs["v"][b][:], ACT.Copy, "v", True)
                    act.wait_ge(did["clamp"], n + 1)
                    norm = bufs["norm"][b][:]
                    nc.scalar.activation(norm, norm, ACT.Ln, scale=2.0 ** LOG_SCALE).then_inc(sig_done["ln"], 1)
                    act.wait_ge(sig_done["ln"], n + 1)
                    nc.scalar.activation(norm, norm, ACT.Exp, scale=-0.5, bias=norm_bias[:, 0:1]).then_inc(sig_done["norm"], 1)

                with act.Fori(0, TILES // 2) as i:
                    for b in range(2):
                        tile(i * 2 + b, i, b)

            @block.vector
            def _(dve):
                nc.vector.memset(epsb[:], EPS)
                nc.vector.memset(norm_bias[:], 0.5 * LOG_SCALE * float(np.log(2.0)))
                dve.wait_ge(loaded, 16 * 10)
                nc.vector.tensor_copy(W["Wga"][:].rearrange("p c (h k) -> p c h k", k=HD),
                                      wgamma[:].unsqueeze(3).to_broadcast([P, C2, HEADS, HD])).then_inc(folded, 1)
                for c in range(C2):
                    nc.vector.tensor_scalar(Wo[:, c, :], Wo[:, c, :], norm_w[:, c:c + 1], None, ALU.mult).then_inc(folded, 1)
                dve.wait_ge(fold_psum, 1)
                nc.vector.tensor_copy(W["Wf"][:], slot[0][:, :, 0:D]).then_inc(folded, 1)
                nc.vector.tensor_copy(W["Wog"][:], slot[1][:, :, 0:D]).then_inc(folded, 1)
                dve.wait_ge(folded, 5)
                for s in range(4):
                    dve.sem_inc(free[s], 1)
                dve.sem_inc(weights_ready, 1)

                def keys(n, i, b):
                    buffers_free(dve, i, b)
                    for key in ("k", "q"):
                        dve.wait_ge(sig_done["sig" + key], n + 1)
                        src, sem = slot_full(dve, n, key)
                        nc.vector.tensor_tensor(bufs[key][b][:], planes(src[:]), bufs["sig" + key][b][:], ALU.mult).then_inc(did[key], 1)
                        dve.wait_ge(did[key], n + 1)
                        dve.sem_inc(sem, 1)
                    nrm = bufs["norm"][b][:]
                    src, sem = slot_full(dve, n, "ss")
                    nc.vector.tensor_scalar(nrm, src[:].rearrange("p c (x t) -> p c x t", x=BL), 1e-24, None,
                                            ALU.max).then_inc(did["clamp"], 1)
                    dve.wait_ge(did["clamp"], n + 1)
                    dve.sem_inc(sem, 1)
                    dve.wait_ge(sig_done["norm"], n + 1)
                    nc.vector.tensor_tensor(bufs["k"][b][:], bufs["k"][b][:], nrm, ALU.mult).then_inc(did["kn"], 1)
                    dve.wait_ge(did["kn"], n + 1)
                    dve.wait_ge(did["fff"], n + 1)
                    nc.vector.scalar_tensor_tensor(out=bufs["a"][b][:], in0=bufs["k"][b][:], scalar=-1.0,
                                                   in1=bufs["ff"][b][:], op0=ALU.mult, op1=ALU.mult).then_inc(did["a"], 1)

                def rows(n, i, b, last=False):
                    tt = nc.vector.tensor_tensor
                    a, v, f, Q, Wr = (bufs[x][b] for x in ("a", "v", "f", "sigk", "w"))
                    A0, V0, A1, V1 = a[:, :, 0, :], v[:, :, 0, :], bufs["sg"][b][:, :, 0, :], bufs["sg"][b][:, :, 1, :]
                    t0, t1 = tmp[:, :, 0, :], tmp[:, :, 1, :]
                    nn, nn_free = slot_full(dve, n, "nn", last)
                    mn, mn_free = slot_full(dve, n, "mn", last)
                    m, n10 = mn[:, :, 0:HB], mn[:, :, HB:NT]
                    n00, n11 = nn[:, :, 0:HB], nn[:, :, HB:NT]
                    sm, sn = did["step_m"], did["step_n"]
                    dve.wait_ge(sig_done["v"], n + 1)
                    tt(A1, a[:, :, 1, :], f[:, :, 0, :], ALU.mult).then_inc(sm, 1)
                    tt(t0, m, A0, ALU.mult).then_inc(sm, 1)
                    tt(t1, m, V0, ALU.mult).then_inc(sm, 1)
                    dve.wait_ge(sm, n * 3 + 3)
                    tt(A1, A1, t0, ALU.add).then_inc(did["row_a"], 1)
                    tt(V1, v[:, :, 1, :], t1, ALU.add).then_inc(did["row_v"], 1)
                    dve.wait_ge(did["row_a"], n + 1)
                    dve.wait_ge(did["row_v"], n + 1)
                    tt(t0, n00, A0, ALU.mult).then_inc(sn, 1)
                    tt(t1, n11, A1, ALU.mult).then_inc(sn, 1)
                    tt(Wr[:, :, 0, :], n00, V0, ALU.mult).then_inc(sn, 1)
                    tt(Wr[:, :, 1, :], n11, V1, ALU.mult).then_inc(sn, 1)
                    dve.wait_ge(sn, n * 7 + 2)
                    tt(Q[:], Q[:], tmp[:], ALU.add).then_inc(sn, 1)
                    dve.wait_ge(sn, n * 7 + 5)
                    tt(t0, n10, A0, ALU.mult).then_inc(sn, 1)
                    tt(t1, n10, V0, ALU.mult).then_inc(sn, 1)
                    dve.wait_ge(sn, n * 7 + 7)
                    dve.sem_inc(nn_free, 1)
                    dve.sem_inc(mn_free, 1)
                    tt(Q[:, :, 1, :], Q[:, :, 1, :], t0, ALU.add).then_inc(did["rows_q"], 1)
                    tt(Wr[:, :, 1, :], Wr[:, :, 1, :], t1, ALU.add).then_inc(did["rows_w"], 1)
                    dve.wait_ge(did["rows_w"], n + 1)
                rounds(dve, keys, rows)

        with Phase(nc, "recB") as pb:
            SEG = 64
            GR = 8
            GPS = SEG // GR
            NSEG = SEQ // BL // SEG
            VH = HD // 2
            VQ = VH // 2
            CHAINS = 2
            R = [pb.sb(f"rows{b}", [P, HD, ROWS, SEG]) for b in range(2)]
            V = [pb.sb(f"v{b}", [P, VH, BL, SEG]) for b in range(2)]
            O = [pb.sb(f"o{b}", [P, VH, BL, SEG]) for b in range(2)]
            hist = [pb.sb(f"hist{b}", [P, GR, VH, HD]) for b in range(2)]
            U = [pb.sb(f"U{b}", [P, GR, 1 + BL, VH, HD + 1]) for b in range(2)]
            u = pb.sb("u", [P, BL, VH])
            prod = [pb.sb(f"prod{b}", [P, GR, BL, VH, HD]) for b in range(2)]
            seg_loaded = [pb.sem(f"seg_loaded{b}") for b in range(2)]
            step = pb.sem("step")
            v_placed = pb.sem("v_placed")
            u_free = pb.sem("u_free")
            group_done = pb.sem("group_done")
            prod_done = pb.sem("prod_done")
            halved = pb.sem("halved")
            out_done = pb.sem("out_done")
            out_stored = [pb.sem(f"out_stored{b}") for b in range(2)]
            block = pb.block()
            PARTS = 2 * BATCH
            LOADS = 16 * 2 * PARTS
            STORED = 16 * PARTS

            def loads(sp, s, b):
                for bt in range(BATCH):
                    for vh in range(2):
                        p0 = bt * 32 + vh * 16
                        t = ds(s * SEG + bt * (SEQ // BL), SEG)
                        sp.dma_start(R[b][p0:p0 + 16].rearrange("h c x t -> h (c x) t"),
                                     rows_dram.rearrange("(h c) x t -> h (c x) t", c=HD)[:, :, t]).then_inc(seg_loaded[b], 16)
                        src = v_dram.rearrange("(h y c) x t -> h y (c x) t", c=VH, y=2)[:, vh, :, t]
                        sp.dma_start(V[b][p0:p0 + 16].rearrange("h c x t -> h (c x) t"), src).then_inc(seg_loaded[b], 16)

            def stores(sp, s, b):
                for bt in range(BATCH):
                    for vh in range(2):
                        p0 = bt * 32 + vh * 16
                        t = ds(s * SEG + bt * (SEQ // BL), SEG)
                        dst = o_dram.rearrange("(h y c) x t -> h y (c x) t", c=VH, y=2)[:, vh, :, t]
                        sp.dma_start(dst, O[b][p0:p0 + 16].rearrange("h c x t -> h (c x) t")).then_inc(out_stored[b], 16)

            @block.sync
            def _(sp):
                loads(sp, 0, 0)
                loads(sp, 1, 1)
                sp.sem_inc(out_stored[0], STORED)
                sp.sem_inc(out_stored[1], STORED)
                with sp.Fori(0, NSEG // 2 - 1) as i:
                    for b in range(2):
                        s = i * 2 + b
                        sp.wait_ge(out_done, (s + 1) * GPS)
                        stores(sp, s, b)
                        loads(sp, s + 2, b)
                for b in range(2):
                    s = NSEG - 2 + b
                    sp.wait_ge(out_done, (s + 1) * GPS)
                    stores(sp, s, b)
                for b in range(2):
                    sp.wait_ge(out_stored[b], STORED * (NSEG // 2 + 1))

            @block.scalar
            def _(act):
                with act.Fori(0, NSEG // 2) as i:
                    for b in range(2):
                        with act.Fori(0, GPS // 2) as g:
                            for par in range(2):
                                n = i * (2 * GPS) + g * 2 + (b * GPS + par)
                                act.wait_ge(seg_loaded[b], (i + 1) * LOADS)
                                act.wait_ge(u_free, n + 1)
                                t = ds(g * (2 * GR) + par * GR, GR)
                                nc.scalar.activation(U[par][:, :, 1:1 + BL, :, HD], V[b][:, :, :, t].rearrange("p v x t -> p t x v"),
                                                     ACT.Copy).then_inc(v_placed, 1)

            @block.vector
            def _(dve):
                nc.vector.memset(hist[0][:, 0, :, :], 0.0).then_inc(step, 1)
                dve.sem_inc(prod_done, 2)
                dve.sem_inc(u_free, 2)
                dve.wait_ge(step, 1)
                dve.sem_clear(step)
                OPS = 4 * CHAINS
                with dve.Fori(0, NSEG // 2) as i:
                    for b in range(2):
                        with dve.Fori(0, GPS // 2) as g:
                            for par in range(2):
                                n = i * (2 * GPS) + g * 2 + (b * GPS + par)
                                dve.wait_ge(seg_loaded[b], (i + 1) * LOADS)
                                dve.wait_ge(v_placed, n + 1)
                                dve.wait_ge(prod_done, n + 1)
                                for j in range(GR):
                                    t = ds(g * (2 * GR) + (par * GR + j), 1)
                                    row = lambda x, num: R[b][:, :, x:x + num, t].rearrange("p k x t -> p x (k t)")
                                    last = j == GR - 1
                                    after = hist[1 - par][:, 0] if last else hist[par][:, j + 1]
                                    half = [slice(c * VQ, c * VQ + VQ) for c in range(CHAINS)]

                                    for c in range(CHAINS):
                                        if j:
                                            dve.wait_ge(step, j * OPS + (c - 1))
                                        nc.vector.tensor_tensor(U[par][:, j, :, half[c], 0:HD],
                                                                hist[par][:, j, half[c], :].unsqueeze(1).to_broadcast([P, 1 + BL, VQ, HD]),
                                                                row(ROW_F, 1 + BL).unsqueeze(2).to_broadcast([P, 1 + BL, VQ, HD]),
                                                                ALU.mult).then_inc(step, 1)
                                    for c in range(CHAINS):
                                        dve.wait_ge(step, j * OPS + CHAINS + (c - 1))
                                        nc.vector.tensor_reduce(u[:, :, half[c]], U[par][:, j, 1:1 + BL, half[c], :], AX.X,
                                                                ALU.add).then_inc(step, 1)
                                    if last:
                                        dve.wait_ge(prod_done, n + 2)
                                    for c in range(CHAINS):
                                        dve.wait_ge(step, j * OPS + 2 * CHAINS + (c - 1))
                                        nc.vector.tensor_tensor(U[par][:, j, 1:1 + BL, half[c], 0:HD],
                                                                u[:, :, half[c]].unsqueeze(3).to_broadcast([P, BL, VQ, HD]),
                                                                row(ROW_K, BL).unsqueeze(2).to_broadcast([P, BL, VQ, HD]),
                                                                ALU.mult).then_inc(step, 1)
                                    for c in range(CHAINS):
                                        dve.wait_ge(step, j * OPS + 3 * CHAINS + (c - 1))
                                        nc.vector.tensor_reduce(after[:, half[c], :], U[par][:, j, :, half[c], 0:HD].rearrange("p x v k -> p v k x"),
                                                                AX.X, ALU.add).then_inc(step, 1)
                                dve.wait_ge(step, GR * OPS)
                                dve.sem_clear(step)
                                dve.sem_inc(group_done, 1)
                                dve.sem_inc(u_free, 1)

            @block.gpsimd
            def _(pool):
                with pool.Fori(0, NSEG // 2) as i:
                    for b in range(2):
                        with pool.Fori(0, GPS // 2) as g:
                            for par in range(2):
                                n = i * (2 * GPS) + g * 2 + (b * GPS + par)
                                pool.wait_ge(out_stored[b], (i + 1) * STORED)
                                pool.wait_ge(seg_loaded[b], (i + 1) * LOADS)
                                pool.wait_ge(group_done, n + 1)
                                t = ds(g * (2 * GR) + par * GR, GR)
                                for x in range(BL):
                                    q = R[b][:, :, ROW_Q + x, t].rearrange("p k t -> p t k")
                                    mul = nc.gpsimd.tensor_tensor(prod[par][:, :, x], hist[par][:],
                                                                  q.unsqueeze(2).to_broadcast([P, GR, VH, HD]), ALU.mult)
                                    mul.then_inc(prod_done if x else halved, 1)
                                pool.wait_ge(prod_done, n + 3)
                                pr = prod[par][:].rearrange("p g x v k -> p (g x v) k")
                                for h, width in enumerate((8, 4, 2)):
                                    pool.wait_ge(halved, n * 4 + (h + 1))
                                    nc.gpsimd.tensor_tensor(pr[:, :, 0:width], pr[:, :, 0:width],
                                                            pr[:, :, width:2 * width], ALU.add).then_inc(halved, 1)
                                pool.wait_ge(halved, n * 4 + 4)
                                nc.gpsimd.tensor_tensor(O[b][:, :, :, t].rearrange("p v x t -> p t x v"), prod[par][:, :, :, :, 0],
                                                        prod[par][:, :, :, :, 1], ALU.add).then_inc(out_done, 1)

        with Phase(nc, "recC") as pc:
            pair = lambda name, shape: [pc.sb(f"{name}{b}", shape) for b in range(2)]
            O, WR = pair("o", [P, C2, BL, HB]), pair("w", [P, C2, BL, HB])
            OG, XC, SQ, R = (pair(n, [P, C2, NT]) for n in ("og", "xc", "sq", "r"))
            lnv, rstd = pair("lnv", [P, NT]), pair("rstd", [P, NT])
            ps_m, ps_v = ([pc.ps(f"{n}{b}", [P, NT]) for b in range(2)] for n in ("ps_m", "ps_v"))
            ps_o = [pc.ps(f"ps_o{b}", [P, C2, NT]) for b in range(2)]
            o_loaded = [pc.sem(f"o_loaded{b}") for b in range(2)]
            summed, og_done, mean_psum, centred, squared, var_psum = (
                pc.sem(n) for n in ("summed", "og_done", "mean_psum", "centred", "squared", "var_psum"))
            ln_done, rstd_done, on_done, o_psum, resid, x_done = (
                pc.sem(n) for n in ("ln_done", "rstd_done", "on_done", "o_psum", "resid", "x_done"))
            block = pc.block()

            norm_no = lambda i, which, b: i * 4 + (which * 2 + b + 1)
            tile_no = lambda i, b: i * 2 + (b + 1)

            @block.sync
            def _(sp):
                def load(n, b):
                    for dst, dram in ((O[b], o_dram), (WR[b], w_dram)):
                        for x in range(BL):
                            sp.dma_start(dst[:, :, x, :], dram.rearrange("(c p) x t -> p c x t", p=P)[:, :, x, ds(n * HB, HB)]).then_inc(o_loaded[b], 16)
                for b in range(2):
                    load(b, b)
                with sp.Fori(0, TILES // 2 - 1) as i:
                    for b in range(2):
                        sp.wait_ge(og_done, tile_no(i, b))
                        load(i * 2 + (b + 2), b)

            @block.gpsimd
            def _(pool):
                with pool.Fori(0, TILES // 2) as i:
                    for b in range(2):
                        pool.wait_ge(o_loaded[b], (i + 1) * 64)
                        nc.gpsimd.tensor_tensor(O[b][:], O[b][:], WR[b][:], ALU.add).then_inc(summed, 1)

            @block.tensor
            def _(pe):
                def means(i, which):
                    for b in range(2):
                        pe.wait_ge(resid if which else og_done, tile_no(i, b))
                        for c in range(C2):
                            mm = nc.tensor.matmul(ps_m[b][:], ones_mean[:], (R if which else OG)[b][:, c, :], start=(c == 0), stop=(c == C2 - 1))
                        mm.then_inc(mean_psum, 1)
                    for b in range(2):
                        pe.wait_ge(squared, norm_no(i, which, b))
                        for c in range(C2):
                            mm = nc.tensor.matmul(ps_v[b][:], ones_mean[:], SQ[b][:, c, :], start=(c == 0), stop=(c == C2 - 1))
                        mm.then_inc(var_psum, 1)

                with pe.Fori(0, TILES // 2) as i:
                    means(i, 0)
                    for b in range(2):
                        pe.wait_ge(on_done, tile_no(i, b))
                        for c in range(C2):
                            for kk in range(C2):
                                mm = nc.tensor.matmul(ps_o[b][:, c, :], Wo[:, kk, P * c:P * c + P], XC[b][:, kk, :],
                                                      start=(kk == 0), stop=(kk == C2 - 1))
                        mm.then_inc(o_psum, 1)
                    means(i, 1)

            @block.scalar
            def _(act):
                with act.Fori(0, TILES // 2) as i:
                    for which in range(2):
                        for b in range(2):
                            act.wait_ge(centred, norm_no(i, which, b))
                            nc.scalar.activation(SQ[b][:], XC[b][:], ACT.Square).then_inc(squared, 1)
                        for b in range(2):
                            act.wait_ge(var_psum, norm_no(i, which, b))
                            nc.scalar.activation(lnv[b][:], ps_v[b][:], ACT.Ln, bias=epsb[:, 0:1]).then_inc(ln_done, 1)
                            act.wait_ge(ln_done, norm_no(i, which, b))
                            nc.scalar.activation(rstd[b][:], lnv[b][:], ACT.Exp, scale=-0.5).then_inc(rstd_done, 1)

            @block.vector
            def _(dve):
                bc = lambda ap: ap.unsqueeze(1).to_broadcast([P, C2, NT])

                def centre(i, which, b, src):
                    dve.wait_ge(mean_psum, norm_no(i, which, b))
                    nc.vector.tensor_tensor(XC[b][:], src, bc(ps_m[b][:]), ALU.subtract).then_inc(centred, 1)

                def scale(i, which, b, dst, done):
                    dve.wait_ge(centred, norm_no(i, which, b))
                    dve.wait_ge(rstd_done, norm_no(i, which, b))
                    nc.vector.tensor_tensor(dst, XC[b][:], bc(rstd[b][:]), ALU.mult).then_inc(done, 1)

                with dve.Fori(0, TILES // 2) as i:
                    tile = [X[:, :, ds((i * 2 + b) * NT, NT)] for b in range(2)]
                    for b in range(2):
                        dve.wait_ge(summed, tile_no(i, b))
                        g = G[:, :, ds((i * 2 + b) * NT, NT)].rearrange("p c (t x) -> p c x t", x=BL)
                        nc.vector.tensor_tensor(OG[b][:].rearrange("p c (t x) -> p c x t", x=BL), O[b][:], g, ALU.mult).then_inc(og_done, 1)
                    for b in range(2):
                        dve.wait_ge(og_done, tile_no(i, b))
                        centre(i, 0, b, OG[b][:])
                    for b in range(2):
                        scale(i, 0, b, XC[b][:], on_done)
                    for b in range(2):
                        dve.wait_ge(o_psum, tile_no(i, b))
                        nc.vector.tensor_tensor(R[b][:], ps_o[b][:], tile[b], ALU.add).then_inc(resid, 1)
                    for b in range(2):
                        dve.wait_ge(resid, tile_no(i, b))
                        centre(i, 1, b, R[b][:])
                    for b in range(2):
                        scale(i, 1, b, tile[b], x_done)


def cross_attention_stage(nc, X, ones_mean, ident, w, gated):
    HEADS, DH, KEYS = 16, D // 16, 64
    HC = HEADS // C2
    PAIRS = HEADS // 2
    PC = PAIRS // C2
    CT = BATCH * KEYS
    CHUNKS = NT // P
    pre = "L0_xattn" if gated else "L1_xattn"
    with Phase(nc, "xg" if gated else "xp") as ph:
        names = ["Wq", "Wk", "Wv", "Wo"] + (["Wg"] if gated else [])
        W = {n: ph.sb(n, [P, C2, D]) for n in names}
        vecs = (["qln_g", "qln_b", "kvln_g", "kvln_b", "bg"] if gated else ["bq", "bk", "bv", "bo"])
        V = {n: ph.sb(n, [P, C2]) for n in vecs}
        bias = {n: ph.sb(f"bias_{n}", [P, C2]) for n in (["q", "k", "v", "g"] if gated else [])}
        if not gated:
            bias = {"q": V["bq"], "k": V["bk"], "v": V["bv"]}
        CTX = ph.sb("ctx", [P, C2, CT])
        CXC = ph.sb("ctx_centred", [P, C2, CT])
        CSQ = ph.sb("ctx_squared", [P, C2, CT])
        cstd = ph.sb("ctx_std", [P, CT])
        crstd = ph.sb("ctx_rstd", [P, CT])
        ctx2 = ph.sb("ctx2", [P, C2, 2, KEYS])
        KT = ph.sb("KT", [P, C2, KEYS])
        head_mask = ph.sb("head_mask", [P, HC])
        pair_mask = ph.sb("pair_mask", [P, PC, P])
        VT = ph.sb("VT", [P, D])
        kblk = ph.sb("kblk", [P, C2, HC, KEYS])
        vblk = ph.sb("vblk", [P, PAIRS, P])
        epsb = ph.sb("epsb", [P, 1])
        N = ph.sb("normed", [P, C2, NT]) if gated else None
        G = ph.sb("gate", [P, C2, NT]) if gated else None
        QT = ph.sb("QT", [P, C2, NT])
        MX = ph.sb("MX", [P, 2, HEADS])
        SUM = ph.sb("SUM", [P, 2, HEADS])
        RIN = ph.sb("RIN", [P, 2, HEADS])
        S = ph.sb("S", [P, 2, HEADS * KEYS])
        E = ph.sb("E", [P, 2, HEADS * KEYS])
        PN = ph.sb("PN", [P, 2, HEADS * KEYS])
        PT = ph.sb("PT", [P, PAIRS, NT])
        Y = ph.sb("Y", [P, C2, NT])
        R = ph.sb("R", [P, C2, NT])
        XC = ph.sb("XC", [P, C2, NT])
        SQ = ph.sb("SQ", [P, C2, NT])
        std = ph.sb("std", [P, NT])
        rstd = ph.sb("rstd", [P, NT])
        ps_s = [ph.ps(f"ps_s{b}", [P, HEADS * KEYS]) for b in range(2)]
        ps_t = ph.ps("ps_t", [P, PAIRS, P])
        bank = [ph.ps(f"bank{b}", [P, NT]) for b in range(2)]
        loaded = ph.sem("loaded")
        masks_done = ph.sem("masks_done")
        prep = ph.sem("prep")
        full = [ph.sem(f"bank_full{b}") for b in range(2)]
        free = [ph.sem(f"bank_free{b}") for b in range(2)]
        ctx_squared = ph.sem("ctx_squared_done")
        ctx_std = ph.sem("ctx_std_done")
        ctx_ready = ph.sem("ctx_ready")
        ctx2_ready = ph.sem("ctx2_ready")
        kv_copied = ph.sem("kv_copied")
        blocks_ready = ph.sem("blocks_ready")
        centred = ph.sem("centred")
        squared = ph.sem("squared")
        std_done = ph.sem("std_done")
        rstd_done = ph.sem("rstd_done")
        normed = ph.sem("normed_done")
        q_ready = ph.sem("q_ready")
        g_ready = ph.sem("g_ready")
        scores = ph.sem("scores")
        max_done = ph.sem("max_done")
        shifted = ph.sem("shifted")
        exp_done = ph.sem("exp_done")
        sum_done = ph.sem("sum_done")
        rinv_done = ph.sem("rinv_done")
        norm_done = ph.sem("norm_done")
        turned = ph.sem("turned")
        pt_ready = ph.sem("pt_ready")
        y_ready = ph.sem("y_ready")
        resid = ph.sem("resid")
        x_done = ph.sem("x_done")
        block = ph.block()

        PRE = [0, 0]
        pre_uses = {}
        if gated:
            for n, key in enumerate(["cmean", "cvar"] + [("bias", v, c) for v in "qkvg" for c in range(C2)]):
                pre_uses[key] = (n % 2, PRE[n % 2])
                PRE[n % 2] += 1
        order = [("k", 0), ("k", 1), "v"]
        for t in range(2):
            if gated:
                order += [("m1", t), ("s1", t)]
            order += [("q", 0, t), ("q", 1, t)]
            if gated:
                order += [("g", 0, t), ("g", 1, t)]
            order += [("y", 0, t), ("y", 1, t), ("o", 0, t), ("o", 1, t), ("m2", t), ("s2", t)]
        use, per = {}, [0, 0]
        for n, key in enumerate(order):
            use[key] = (n % 2, per[n % 2])
            per[n % 2] += 1

        def at(b, key):
            k, n = use[key]
            return k, b * per[k] + (PRE[k] + n + 1)

        def wait_free(pe, b, key):
            k, n = at(b, key) if key in use else (pre_uses[key][0], pre_uses[key][1] + 1)
            pe.wait_ge(free[k], n)
            return bank[k], full[k]

        def wait_full(eng, b, key):
            k, n = at(b, key) if key in use else (pre_uses[key][0], pre_uses[key][1] + 1)
            eng.wait_ge(full[k], n)
            return bank[k], free[k]

        @block.sync
        def _(sp):
            for n in names:
                sp.dma_start(W[n][:], w[f"{pre}_{n}"].rearrange("(c p) o -> p c o", p=P)).then_inc(loaded, 16)
            for n in vecs:
                sp.dma_start(V[n][:], w[f"{pre}_{n}"]).then_inc(loaded, 16)
            sp.dma_start(CTX[:], w["ctx_1024"].rearrange("(c p) t -> p c t", p=P)).then_inc(loaded, 16)
        LOADED = 16 * (len(names) + len(vecs) + 1)
        kv_src = CXC if gated else CTX

        @block.gpsimd
        def _(pool):
            nc.gpsimd.memset(head_mask[:], 1.0).then_inc(masks_done, 1)
            pool.wait_ge(masks_done, 1)
            nc.gpsimd.affine_select(out=head_mask[:], in_=head_mask[:], compare_op=ALU.is_ge, fill=0.0, base=0,
                                    pattern=[[-DH, HC]], channel_multiplier=1).then_inc(masks_done, 1)
            pool.wait_ge(masks_done, 2)
            nc.gpsimd.affine_select(out=head_mask[:], in_=head_mask[:], compare_op=ALU.is_ge, fill=0.0, base=DH - 1,
                                    pattern=[[DH, HC]], channel_multiplier=-1).then_inc(masks_done, 1)
            nc.gpsimd.memset(pair_mask[:], 0.0).then_inc(masks_done, 1)
            pool.wait_ge(masks_done, 4)
            for hh in range(2):
                for j in range(PC):
                    f0 = DH * (2 * j + hh)
                    nc.gpsimd.memset(pair_mask[KEYS * hh:KEYS * hh + KEYS, j, f0:f0 + DH], 1.0).then_inc(masks_done, 1)
            with pool.Fori(0, BATCH) as b:
                for t in range(2):
                    for k in range(CHUNKS):
                        n = CHUNKS * t + k
                        pool.wait_ge(rinv_done, b * (2 * CHUNKS) + n + 1)
                        pool.wait_ge(turned, b * (2 * CHUNKS) + n + 1 - 2 + 2)
                        nc.gpsimd.tensor_tensor(PN[:, k % 2, :].rearrange("p (h k) -> p h k", h=HEADS),
                                                E[:, k % 2, :].rearrange("p (h k) -> p h k", h=HEADS),
                                                RIN[:, k % 2, :].unsqueeze(2).to_broadcast([P, HEADS, KEYS]),
                                                ALU.mult).then_inc(norm_done, 1)

        @block.tensor
        def _(pe):
            pe.wait_ge(loaded, LOADED)
            pe.sem_inc(turned, 2)

            def accumulate(dst, pairs):
                for n, (lhs, rhs) in enumerate(pairs):
                    mm = nc.tensor.matmul(dst, lhs, rhs, start=(n == 0), stop=(n == len(pairs) - 1))
                return mm

            if gated:
                dst, sem = wait_free(pe, 0, "cmean")
                accumulate(dst[:, 0:CT], [(ones_mean[:], CTX[:, c, :]) for c in range(C2)]).then_inc(sem, 1)
                dst, sem = wait_free(pe, 0, "cvar")
                pe.wait_ge(ctx_squared, 1)
                accumulate(dst[:, 0:CT], [(ones_mean[:], CSQ[:, c, :]) for c in range(C2)]).then_inc(sem, 1)
                for v in "qkvg":
                    for c in range(C2):
                        dst, sem = wait_free(pe, 0, ("bias", v, c))
                        lnb = V["kvln_b"] if v in "kv" else V["qln_b"]
                        accumulate(dst[:, 0:1], [(W["W" + v][:, kk, P * c:P * c + P], lnb[:, kk:kk + 1])
                                                 for kk in range(C2)]).then_inc(sem, 1)
            pe.wait_ge(ctx_ready, 1)

            def mean_var(b, t, which):
                src = X[:, :, ds((b * 2 + t) * NT, NT)] if which == "1" else R[:]
                if which == "2":
                    pe.wait_ge(resid, b * 4 + (2 * t + 2))
                dst, sem = wait_free(pe, b, ("m" + which, t))
                accumulate(dst[:], [(ones_mean[:], src[:, c, :]) for c in range(C2)]).then_inc(sem, 1)
                dst, sem = wait_free(pe, b, ("s" + which, t))
                lns = 2 if gated else 1
                pe.wait_ge(squared, b * (2 * lns) + (lns * t + (lns if which == "2" else 1)))
                accumulate(dst[:], [(ones_mean[:], SQ[:, c, :]) for c in range(C2)]).then_inc(sem, 1)

            with pe.Fori(0, BATCH) as b:
                for c in range(C2):
                    dst, sem = wait_free(pe, b, ("k", c))
                    accumulate(dst[:, 0:KEYS], [(W["Wk"][:, kk, P * c:P * c + P], kv_src[:, kk, ds(b * KEYS, KEYS)])
                                                for kk in range(C2)]).then_inc(sem, 1)
                dst, sem = wait_free(pe, b, "v")
                pe.wait_ge(ctx2_ready, b + 1)
                accumulate(dst[:, 0:D], [(ctx2[:, kk, :, :], W["Wv"][:, kk, :]) for kk in range(C2)]).then_inc(sem, 1)
                for t in range(2):
                    pe.wait_ge(x_done, b * 2 + (t + 1))
                    if gated:
                        mean_var(b, t, "1")
                        pe.wait_ge(normed, b * 2 + (t + 1))
                    rhs = N[:] if gated else X[:, :, ds((b * 2 + t) * NT, NT)]
                    for v in (("q", "g") if gated else ("q",)):
                        for c in range(C2):
                            dst, sem = wait_free(pe, b, (v, c, t))
                            accumulate(dst[:], [(W["W" + v][:, kk, P * c:P * c + P], rhs[:, kk, :])
                                                for kk in range(C2)]).then_inc(sem, 1)
                    pe.wait_ge(q_ready, b * 4 + (2 * t + 2))
                    pe.wait_ge(blocks_ready, b + 1)

                    def score(k):
                        n = CHUNKS * t + k
                        pe.wait_ge(shifted, b * (2 * CHUNKS) + n + 1)
                        for c in range(C2):
                            mm = nc.tensor.matmul(ps_s[k % 2][:, 512 * c:512 * c + 512], QT[:, c, P * k:P * k + P],
                                                  kblk[:, c, :, :].rearrange("p h k -> p (h k)"), start=True, stop=True)
                        mm.then_inc(scores, 1)

                    def turn(k):
                        n = CHUNKS * t + k
                        pe.wait_ge(norm_done, b * (2 * CHUNKS) + n + 1)
                        pe.wait_ge(pt_ready, b * (2 * CHUNKS) + n + 1)
                        for j in range(PAIRS):
                            mm = nc.tensor.transpose(ps_t[:, j, :], PN[:, k % 2, P * j:P * j + P], ident[:])
                        mm.then_inc(turned, 1)

                    score(0)
                    for k in range(1, CHUNKS):
                        score(k)
                        turn(k - 1)
                    turn(CHUNKS - 1)
                    pe.wait_ge(pt_ready, b * (2 * CHUNKS) + (CHUNKS * (t + 1) + 1))
                    for c in range(C2):
                        dst, sem = wait_free(pe, b, ("y", c, t))
                        accumulate(dst[:], [(vblk[:, PC * c + j, :], PT[:, PC * c + j, :]) for j in range(PC)]).then_inc(sem, 1)
                    pe.wait_ge(y_ready, b * 4 + (2 * t + 2))
                    for c in range(C2):
                        dst, sem = wait_free(pe, b, ("o", c, t))
                        accumulate(dst[:], [(W["Wo"][:, kk, P * c:P * c + P], Y[:, kk, :]) for kk in range(C2)]).then_inc(sem, 1)
                    mean_var(b, t, "2")

        @block.scalar
        def _(act):
            act.wait_ge(loaded, LOADED)
            act.sem_inc(pt_ready, 1)
            act.sem_inc(free[0], 1)
            act.sem_inc(free[1], 1)
            if gated:
                act.wait_ge(prep, 2)
                nc.scalar.activation(CSQ[:], CXC[:], ACT.Square).then_inc(ctx_squared, 1)
                src, sem = wait_full(act, 0, "cvar")
                nc.scalar.activation(cstd[:], src[:, 0:CT], ACT.Sqrt, bias=epsb[:, 0:1]).then_inc(ctx_std, 1)
                act.wait_ge(ctx_std, 1)
                act.sem_inc(sem, 1)

            def square_root(b, t, which):
                lns = 2 if gated else 1
                n = lns * t + (lns if which == "2" else 1)
                act.wait_ge(centred, b * (2 * lns) + n)
                nc.scalar.activation(SQ[:], XC[:], ACT.Square).then_inc(squared, 1)
                src, sem = wait_full(act, b, ("s" + which, t))
                nc.scalar.activation(std[:], src[:], ACT.Sqrt, bias=epsb[:, 0:1]).then_inc(std_done, 1)
                act.wait_ge(std_done, b * (2 * lns) + n)
                act.sem_inc(sem, 1)

            act.wait_ge(ctx_ready, 1)
            with act.Fori(0, BATCH) as b:
                for c in range(C2):
                    src, sem = wait_full(act, b, ("k", c))
                    act.wait_ge(x_done, b * 2 + 1)
                    nc.scalar.activation(KT[:, c, :], src[:, 0:KEYS], ACT.Identity,
                                         bias=bias["k"][:, c:c + 1]).then_inc(kv_copied, 1)
                    act.wait_ge(kv_copied, b * 3 + (c + 1))
                    act.sem_inc(sem, 1)
                src, sem = wait_full(act, b, "v")
                nc.scalar.activation(VT[:], src[:, 0:D], ACT.Copy).then_inc(kv_copied, 1)
                act.wait_ge(kv_copied, b * 3 + 3)
                act.sem_inc(sem, 1)
                for t in range(2):
                    act.wait_ge(x_done, b * 2 + (t + 1))
                    if gated:
                        square_root(b, t, "1")
                    for c in range(C2):
                        src, sem = wait_full(act, b, ("q", c, t))
                        nc.scalar.activation(QT[:, c, :], src[:], ACT.Identity, bias=bias["q"][:, c:c + 1]).then_inc(q_ready, 1)
                        act.wait_ge(q_ready, b * 4 + (2 * t + c + 1))
                        act.sem_inc(sem, 1)
                    if gated:
                        for c in range(C2):
                            src, sem = wait_full(act, b, ("g", c, t))
                            nc.scalar.activation(G[:, c, :], src[:], ACT.Sigmoid, bias=bias["g"][:, c:c + 1]).then_inc(g_ready, 1)
                            act.wait_ge(g_ready, b * 4 + (2 * t + c + 1))
                            act.sem_inc(sem, 1)

                    def exps(k):
                        n = CHUNKS * t + k
                        act.wait_ge(shifted, b * (2 * CHUNKS) + n + 3)
                        act.wait_ge(norm_done, b * (2 * CHUNKS) + n + 1 - 2) if n >= 2 else None
                        if n < 2:
                            act.wait_ge(x_done, b * 2 + 1)
                        nc.scalar.activation(E[:, k % 2, :], S[:, k % 2, :], ACT.Exp, scale=float(DH) ** -0.5).then_inc(exp_done, 1)

                    def copies(k):
                        n = CHUNKS * t + k
                        act.wait_ge(turned, b * (2 * CHUNKS) + n + 3)
                        nc.scalar.activation(PT[:, :, P * k:P * k + P], ps_t[:], ACT.Copy).then_inc(pt_ready, 1)

                    exps(0)
                    for k in range(1, CHUNKS):
                        exps(k)
                        copies(k - 1)
                    copies(CHUNKS - 1)
                    square_root(b, t, "2")

        @block.vector
        def _(dve):
            nc.vector.memset(epsb[:], EPS).then_inc(prep, 1)
            dve.wait_ge(prep, 1)
            dve.wait_ge(loaded, LOADED)
            dve.sem_inc(shifted, 2)
            dve.sem_inc(x_done, 1)
            if gated:
                src, sem = wait_full(dve, 0, "cmean")
                nc.vector.tensor_tensor(CXC[:], CTX[:], src[:, 0:CT].unsqueeze(1).to_broadcast([P, C2, CT]),
                                        ALU.subtract).then_inc(prep, 1)
                dve.wait_ge(prep, 2)
                dve.sem_inc(sem, 1)
                dve.wait_ge(ctx_std, 1)
                nc.vector.reciprocal(crstd[:], cstd[:]).then_inc(prep, 1)
                dve.wait_ge(prep, 3)
                nc.vector.tensor_tensor(CXC[:], CXC[:], crstd[:].unsqueeze(1).to_broadcast([P, C2, CT]), ALU.mult).then_inc(prep, 1)
                n = 4
                for v in "qkvg":
                    for c in range(C2):
                        src, sem = wait_full(dve, 0, ("bias", v, c))
                        if v == "g":
                            ins = nc.vector.tensor_tensor(bias[v][:, c:c + 1], src[:, 0:1], V["bg"][:, c:c + 1], ALU.add)
                        else:
                            ins = nc.vector.tensor_copy(bias[v][:, c:c + 1], src[:, 0:1])
                        ins.then_inc(prep, 1)
                        n += 1
                        dve.wait_ge(prep, n)
                        dve.sem_inc(sem, 1)
                for v in "qkvg":
                    lng = V["kvln_g"] if v in "kv" else V["qln_g"]
                    for c in range(C2):
                        nc.vector.tensor_scalar(W["W" + v][:, c, :], W["W" + v][:, c, :], lng[:, c:c + 1], None,
                                                ALU.mult).then_inc(prep, 1)
                        n += 1
                dve.wait_ge(prep, n)
            dve.sem_inc(ctx_ready, 1)
            dve.wait_ge(masks_done, 4 + 2 * PC)

            def centre(b, t, which):
                src, sem = wait_full(dve, b, ("m" + which, t))
                lns = 2 if gated else 1
                n = lns * t + (lns if which == "2" else 1)
                data = X[:, :, ds((b * 2 + t) * NT, NT)] if which == "1" else R[:]
                nc.vector.tensor_tensor(XC[:], data, src[:].unsqueeze(1).to_broadcast([P, C2, NT]), ALU.subtract).then_inc(centred, 1)
                dve.wait_ge(centred, b * (2 * lns) + n)
                dve.sem_inc(sem, 1)
                dve.wait_ge(std_done, b * (2 * lns) + n)
                nc.vector.reciprocal(rstd[:], std[:]).then_inc(rstd_done, 1)
                dve.wait_ge(rstd_done, b * (2 * lns) + n)

            with dve.Fori(0, BATCH) as b:
                dve.wait_ge(x_done, b * 2 + 1)
                nc.vector.tensor_copy(ctx2[:], kv_src[:, :, ds(b * KEYS, KEYS)].unsqueeze(2).to_broadcast([P, C2, 2, KEYS])).then_inc(ctx2_ready, 1)
                dve.wait_ge(kv_copied, b * 3 + 3)
                for c in range(C2):
                    nc.vector.tensor_tensor(kblk[:, c, :, :], KT[:, c, :].unsqueeze(1).to_broadcast([P, HC, KEYS]),
                                            head_mask[:].unsqueeze(2).to_broadcast([P, HC, KEYS]), ALU.mult)
                for c in range(C2):
                    last = nc.vector.tensor_tensor(vblk[:, PC * c:PC * c + PC, :],
                                                   VT[:, P * c:P * c + P].unsqueeze(1).to_broadcast([P, PC, P]),
                                                   pair_mask[:], ALU.mult)
                last.then_inc(blocks_ready, 1)
                for t in range(2):
                    tile = X[:, :, ds((b * 2 + t) * NT, NT)]
                    dve.wait_ge(x_done, b * 2 + (t + 1))
                    if gated:
                        centre(b, t, "1")
                        nc.vector.tensor_tensor(N[:], XC[:], rstd[:].unsqueeze(1).to_broadcast([P, C2, NT]), ALU.mult).then_inc(normed, 1)

                    def shift(k):
                        n = CHUNKS * t + k
                        base = b * (2 * CHUNKS)
                        ps3 = ps_s[k % 2][:].rearrange("p (h k) -> p h k", h=HEADS)
                        dve.wait_ge(scores, base + n + 1)
                        nc.vector.tensor_reduce(MX[:, k % 2, :], ps3, AX.X, ALU.max).then_inc(max_done, 1)
                        dve.wait_ge(max_done, base + n + 1)
                        if n >= 2:
                            dve.wait_ge(exp_done, base + n - 1)
                        nc.vector.tensor_tensor(S[:, k % 2, :].rearrange("p (h k) -> p h k", h=HEADS), ps3,
                                                MX[:, k % 2, :].unsqueeze(2).to_broadcast([P, HEADS, KEYS]),
                                                ALU.subtract).then_inc(shifted, 1)

                    def invert(k):
                        n = CHUNKS * t + k
                        base = b * (2 * CHUNKS)
                        dve.wait_ge(exp_done, base + n + 1)
                        nc.vector.tensor_reduce(SUM[:, k % 2, :], E[:, k % 2, :].rearrange("p (h k) -> p h k", h=HEADS),
                                                AX.X, ALU.add).then_inc(sum_done, 1)
                        dve.wait_ge(sum_done, base + n + 1)
                        if n >= 2:
                            dve.wait_ge(norm_done, base + n - 1)
                        nc.vector.reciprocal(RIN[:, k % 2, :], SUM[:, k % 2, :]).then_inc(rinv_done, 1)

                    shift(0)
                    for k in range(1, CHUNKS):
                        shift(k)
                        invert(k - 1)
                    invert(CHUNKS - 1)
                    if gated:
                        dve.wait_ge(g_ready, b * 4 + (2 * t + 2))
                    for c in range(C2):
                        src, sem = wait_full(dve, b, ("y", c, t))
                        if gated:
                            ins = nc.vector.scalar_tensor_tensor(out=Y[:, c, :], in0=src[:], scalar=bias["v"][:, c:c + 1],
                                                                 in1=G[:, c, :], op0=ALU.add, op1=ALU.mult)
                        else:
                            ins = nc.vector.tensor_scalar(Y[:, c, :], src[:], bias["v"][:, c:c + 1], None, ALU.add)
                        ins.then_inc(y_ready, 1)
                        dve.wait_ge(y_ready, b * 4 + (2 * t + c + 1))
                        dve.sem_inc(sem, 1)
                    for c in range(C2):
                        src, sem = wait_full(dve, b, ("o", c, t))
                        if gated:
                            ins = nc.vector.tensor_tensor(R[:, c, :], src[:], tile[:, c, :], ALU.add)
                        else:
                            ins = nc.vector.scalar_tensor_tensor(out=R[:, c, :], in0=src[:], scalar=V["bo"][:, c:c + 1],
                                                                 in1=tile[:, c, :], op0=ALU.add, op1=ALU.add)
                        ins.then_inc(resid, 1)
                        dve.wait_ge(resid, b * 4 + (2 * t + c + 1))
                        dve.sem_inc(sem, 1)
                    centre(b, t, "2")
                    nc.vector.tensor_tensor(tile, XC[:], rstd[:].unsqueeze(1).to_broadcast([P, C2, NT]), ALU.mult).then_inc(x_done, 1)


def expert_stage(nc, X, ones_mean, ident, w, sorted_in, sorted_out, zeros_written):
    EX, FF = 8, 1024
    KF = FF // P
    CH = TOK // P
    TC = NT // P
    BLOCKS = (TOK + EX * (P - 1)) // P
    BLOCKS += BLOCKS % 2
    with Phase(nc, "moe") as ph:
        W1 = ph.sb("W1", [P, EX, C2, FF])
        W2 = ph.sb("W2", [P, EX, KF, D])
        XTM = ph.sb("x_tokens", [P, CH, D])
        stage_buf = ph.sb("stage_buf", [P, 2 * NT])
        XS = stage_buf[:].rearrange("p (c t) -> p c t", c=C2)
        NTM = stage_buf[:].rearrange("p (r d) -> p r d", r=4)
        cent = ph.sb("cent", [P, C2, EX])
        stats = ph.sb("stats", [P, CH, 6])
        MV = ph.sb("mean_var", [P, CH, 2])
        std = ph.sb("std", [P, CH])
        rstd = ph.sb("rstd", [P, CH])
        alpha = ph.sb("alpha", [P, CH])
        pos = ph.sb("pos", [P, CH], I32)
        block_expert = ph.sb("block_expert", [P, BLOCKS], I32)
        ln_g = ph.sb("ln_g", [P, EX, C2])
        ln_b = ph.sb("ln_b", [P, EX, C2])
        b1 = ph.sb("b1", [P, EX, KF])
        epsb = ph.sb("epsb", [P, 1])
        ps_aff = ph.ps("ps_aff", [P, CH, EX])
        xf = X[:].rearrange("p c t -> p (c t)")
        weights_loaded = ph.sem("weights_loaded")
        small_loaded = ph.sem("small_loaded")
        b2_loaded = ph.sem("b2_loaded")

        with Phase(nc, "moeA") as pa:
            ps_x = [pa.ps(f"ps_x{b}", [P, TC, D]) for b in range(2)]
            ps_b1 = pa.ps("ps_b1", [P, EX, KF])
            staged = pa.sem("staged")
            turned = pa.sem("turned")
            copied = pa.sem("copied")
            stats_done = pa.sem("stats_done")
            b1_psum = pa.sem("b1_psum")
            block = pa.block()

            @block.sync
            def _(sp):
                sp.dma_start(cent[:], w["L0_ffn_centroids"].rearrange("(c p) e -> p c e", p=P)).then_inc(small_loaded, 16)
                sp.dma_start(ln_g[:], w["L0_ffn_ln_g"]).then_inc(small_loaded, 16)
                sp.dma_start(ln_b[:], w["L0_ffn_ln_b"]).then_inc(small_loaded, 16)
                sp.dma_start(b1[:], w["L0_ffn_b1"]).then_inc(small_loaded, 16)
                for e in range(EX):
                    sp.dma_start(W1[:, e, :, :], w["L0_ffn_w1"][e].rearrange("(c p) f -> p c f", p=P)).then_inc(weights_loaded, 16)
                for e in range(EX):
                    sp.dma_start(W2[:, e, :, :], w["L0_ffn_w2"][e].rearrange("(c p) f -> p c f", p=P)).then_inc(weights_loaded, 16)

            @block.scalar
            def _(act):
                act.sem_inc(turned, 1)
                act.sem_inc(copied, 2)
                with act.Fori(0, TILES // 2) as i:
                    for h in range(2):
                        n = i * 2 + h
                        act.wait_ge(turned, n + 1)
                        nc.scalar.activation(XS, X[:, :, ds(n * NT, NT)], ACT.Copy).then_inc(staged, 1)
                        act.wait_ge(turned, n + 2)
                        nc.scalar.activation(XTM[:, ds(n * TC, TC), :], ps_x[h][:], ACT.Copy).then_inc(copied, 1)

            @block.tensor
            def _(pe):
                pe.wait_ge(small_loaded, 16 * 4)
                with pe.Fori(0, TILES // 2) as i:
                    for h in range(2):
                        n = i * 2 + h
                        pe.wait_ge(staged, n + 1)
                        pe.wait_ge(copied, n + 1)
                        for k in range(TC):
                            for c in range(C2):
                                nc.tensor.transpose(ps_x[h][:, k, P * c:P * c + P], XS[:, c, P * k:P * k + P], ident[:])
                        for k in range(TC):
                            for c in range(C2):
                                mm = nc.tensor.matmul(ps_aff[:, ds(n * TC + k, 1), :].rearrange("p k e -> p (k e)"),
                                                      XS[:, c, P * k:P * k + P], cent[:, c, :],
                                                      start=(c == 0), stop=(c == C2 - 1))
                        mm.then_inc(turned, 1)
                pe.wait_ge(weights_loaded, 16 * 2 * EX)
                for e in range(EX):
                    for m in range(KF):
                        for c in range(C2):
                            mm = nc.tensor.matmul(ps_b1[:, e, m:m + 1], W1[:, e, c, P * m:P * m + P], ln_b[:, e, c:c + 1],
                                                  start=(c == 0), stop=(c == C2 - 1))
                mm.then_inc(b1_psum, 1)

            @block.vector
            def _(dve):
                nc.vector.memset(epsb[:], EPS)
                with dve.Fori(0, TILES // 2) as i:
                    for h in range(2):
                        n = i * 2 + h
                        dve.wait_ge(copied, n + 3)
                        for k in range(TC):
                            ins = nc.vector.bn_stats(stats[:, ds(n * TC + k, 1), :].rearrange("p k s -> p (k s)"),
                                                     XTM[:, ds(n * TC + k, 1), :].rearrange("p k d -> p (k d)"))
                        ins.then_inc(stats_done, 1)
                dve.wait_ge(stats_done, TILES)
                for j in range(CH):
                    nc.vector.bn_aggr(MV[:, j, :], stats[:, j, :])
                dve.wait_ge(b1_psum, 1)
                nc.vector.tensor_tensor(b1[:], b1[:], ps_b1[:], ALU.add)
                for e in range(EX):
                    for c in range(C2):
                        nc.vector.tensor_scalar(W1[:, e, c, :], W1[:, e, c, :], ln_g[:, e, c:c + 1], None, ALU.mult)

        with Phase(nc, "moeB") as pb:
            AFF, EQ, OH, SC0, SC1, ENDB = (xf[:, CH * EX * n:CH * EX * (n + 1)].rearrange("p (j e) -> p j e", e=EX)
                                           for n in range(6))
            rest = xf[:, CH * EX * 6:]
            MAXV, BEST, POSF = (rest[:, CH * n:CH * (n + 1)] for n in range(3))
            rest = rest[:, CH * 3:]
            CNT, NB, S1, S2, S3 = (rest[:, EX * n:EX * (n + 1)] for n in range(5))
            rest = rest[:, EX * 5:]
            BE = rest[:, 0:BLOCKS]
            rest = rest[:, BLOCKS:]
            GTS = rest[:, 0:EX * CH].rearrange("p (e m) -> p e m", e=EX)
            rest = rest[:, EX * CH:]
            LES = rest[:, 0:BLOCKS * EX].rearrange("p (m e) -> p m e", e=EX)
            rest = rest[:, BLOCKS * EX:]
            prefer = rest[:, 0:EX]
            chunk_edge = rest[:, EX:EX + CH]
            block_no = rest[:, EX + CH:EX + CH + BLOCKS]
            before = rest[:, EX + CH + BLOCKS:EX + CH + BLOCKS + P]
            ones = rest[:, EX + CH + BLOCKS + P:EX + CH + BLOCKS + 2 * P]
            ps_pre = pb.ps("ps_pre", [P, CH, EX])
            ps_tot = pb.ps("ps_tot", [P, CH, EX])
            consts = pb.sem("consts")
            aff_psum = pb.sem("aff_psum")
            step = pb.sem("step")
            onehot_done = pb.sem("onehot_done")
            counted = pb.sem("counted")
            std_done = pb.sem("std_done")
            alpha_done = pb.sem("alpha_done")
            normed = pb.sem("normed")
            pos_done = pb.sem("pos_done")
            scattered = [pb.sem(f"scattered{b}") for b in range(4)]
            block = pb.block()

            @block.sync
            def _(sp):
                sp.dma_start(xf[:, 6144:8192], w["L0_ffn_b2"].rearrange("e d -> (e d)").unsqueeze(0).to_broadcast([P, EX * D])).then_inc(b2_loaded, 16)

            @block.gpsimd
            def _(pool):
                nc.gpsimd.iota(prefer, pattern=[[-1, EX]], base=EX, channel_multiplier=0,
                               allow_small_or_imprecise_dtypes=True).then_inc(consts, 1)
                nc.gpsimd.iota(chunk_edge, pattern=[[P, CH]], base=0, channel_multiplier=0,
                               allow_small_or_imprecise_dtypes=True).then_inc(consts, 1)
                nc.gpsimd.iota(block_no, pattern=[[1, BLOCKS]], base=0, channel_multiplier=0,
                               allow_small_or_imprecise_dtypes=True).then_inc(consts, 1)
                nc.gpsimd.memset(ones, 1.0).then_inc(consts, 1)
                pool.wait_ge(consts, 4)
                nc.gpsimd.affine_select(out=before, in_=ones, compare_op=ALU.is_gt, fill=0.0, base=0,
                                        pattern=[[1, P]], channel_multiplier=-1).then_inc(consts, 1)
                pool.wait_ge(zeros_written, 16)
                pool.wait_ge(pos_done, 1)
                for j in range(CH):
                    pool.wait_ge(normed, j + 1)
                    nc.gpsimd.indirect_dma_start(sorted_in, bass.IndirectOffsetOnAxis(pos[:, j:j + 1], 0),
                                                 NTM[:, j % 4, :], None).then_inc(scattered[j % 4], 16)
                for b in range(4):
                    pool.wait_ge(scattered[b], 16 * CH // 4)

            @block.scalar
            def _(act):
                act.wait_ge(step, 1)
                nc.scalar.activation(std[:], MV[:, :, 1], ACT.Sqrt, bias=epsb[:, 0:1]).then_inc(std_done, 1)
                act.wait_ge(step, 2)
                nc.scalar.activation(alpha[:], MAXV, ACT.Sigmoid).then_inc(alpha_done, 1)

            @block.tensor
            def _(pe):
                pe.wait_ge(onehot_done, 1)
                oh = OH.rearrange("p j e -> p (j e)")
                nc.tensor.matmul(ps_pre[:].rearrange("p j e -> p (j e)"), before, oh, start=True, stop=True)
                nc.tensor.matmul(ps_tot[:].rearrange("p j e -> p (j e)"), ones, oh, start=True, stop=True).then_inc(counted, 1)

            @block.vector
            def _(dve):
                n = [0]

                def then(ins):
                    n[0] += 1
                    ins.then_inc(step, 1)
                    dve.wait_ge(step, n[0])

                dve.wait_ge(consts, 5)
                then(nc.vector.tensor_copy(AFF, ps_aff[:]))
                then(nc.vector.tensor_reduce(MAXV, AFF, AX.X, ALU.max))
                then(nc.vector.tensor_tensor(EQ, AFF, MAXV.unsqueeze(2).to_broadcast([P, CH, EX]), ALU.is_equal))
                then(nc.vector.tensor_tensor(EQ, EQ, prefer.unsqueeze(1).to_broadcast([P, CH, EX]), ALU.mult))
                then(nc.vector.tensor_reduce(BEST, EQ, AX.X, ALU.max))
                nc.vector.tensor_tensor(OH, EQ, BEST.unsqueeze(2).to_broadcast([P, CH, EX]), ALU.is_equal).then_inc(onehot_done, 1)
                dve.wait_ge(counted, 1)
                then(nc.vector.tensor_copy(SC0, ps_tot[:]))
                a, b, s = SC0, SC1, 1
                while s < CH:
                    nc.vector.tensor_copy(b[:, 0:s, :], a[:, 0:s, :])
                    then(nc.vector.tensor_tensor(b[:, s:, :], a[:, s:, :], a[:, 0:CH - s, :], ALU.add))
                    a, b, s = b, a, s * 2
                incl, tmp = a, b
                then(nc.vector.tensor_copy(CNT, incl[:, CH - 1, :]))
                then(nc.vector.tensor_tensor(GTS, CNT.unsqueeze(2).to_broadcast([P, EX, CH]),
                                             chunk_edge.unsqueeze(1).to_broadcast([P, EX, CH]), ALU.is_gt))
                then(nc.vector.tensor_reduce(NB, GTS, AX.X, ALU.add))
                a, b, s, other = NB, S1, 1, S2
                while s < EX:
                    nc.vector.tensor_copy(b[:, 0:s], a[:, 0:s])
                    then(nc.vector.tensor_tensor(b[:, s:], a[:, s:], a[:, 0:EX - s], ALU.add))
                    a, b, other, s = b, other, (a if a is not NB else S3), s * 2
                ends = a
                then(nc.vector.tensor_tensor(LES, ends.unsqueeze(1).to_broadcast([P, BLOCKS, EX]),
                                             block_no.unsqueeze(2).to_broadcast([P, BLOCKS, EX]), ALU.is_le))
                then(nc.vector.tensor_reduce(BE, LES, AX.X, ALU.add))
                then(nc.vector.tensor_scalar(block_expert[:], BE, float(EX - 1), None, ALU.min))
                then(nc.vector.tensor_tensor(CNT, ends, NB, ALU.subtract))
                then(nc.vector.tensor_scalar(CNT, CNT, float(P), None, ALU.mult))
                then(nc.vector.tensor_tensor(tmp, incl, ps_tot[:], ALU.subtract))
                then(nc.vector.tensor_tensor(tmp, tmp, ps_pre[:], ALU.add))
                then(nc.vector.tensor_tensor(tmp, tmp, CNT.unsqueeze(1).to_broadcast([P, CH, EX]), ALU.add))
                then(nc.vector.tensor_tensor(tmp, tmp, OH, ALU.mult))
                then(nc.vector.tensor_reduce(POSF, tmp, AX.X, ALU.add))
                nc.vector.tensor_copy(pos[:], POSF).then_inc(pos_done, 1)
                dve.wait_ge(std_done, 1)
                then(nc.vector.reciprocal(rstd[:], std[:]))
                for j in range(CH):
                    if j >= 4:
                        dve.wait_ge(scattered[j % 4], 16 * (j // 4))
                    nc.vector.tensor_scalar(NTM[:, j % 4, :], XTM[:, j, :], MV[:, j, 0:1], rstd[:, j:j + 1],
                                            ALU.subtract, ALU.mult).then_inc(normed, 1)

        with Phase(nc, "moeC") as pc:
            b2 = xf[:, 6144:8192].rearrange("p (e d) -> p e d", e=EX)
            rows = xf[:, 0:512].rearrange("p (b d) -> p b d", b=2)
            rowsT = xf[:, 512:1024].rearrange("p (b c t) -> p b c t", b=2, c=C2)
            hid = xf[:, 1024:3072].rearrange("p (b f) -> p b f", b=2)
            hidT = xf[:, 3072:5120].rearrange("p (b m t) -> p b m t", b=2, m=KF)
            yrow = xf[:, 5120:5632].rearrange("p (b d) -> p b d", b=2)
            ps_r = ps_aff[:].rearrange("p j e -> p (j e)").rearrange("p (c t) -> p c t", c=C2)
            ps_h = [pc.ps(f"ps_h{b}", [P, FF]) for b in range(2)]
            ps_t = pc.ps("ps_t", [P, KF, P])
            ps_y = pc.ps("ps_y", [P, D])
            row_loaded = [pc.sem(f"row_loaded{b}") for b in range(2)]
            row_turned = pc.sem("row_turned")
            rowT_ready = pc.sem("rowT_ready")
            h_psum = pc.sem("h_psum")
            h_copied = pc.sem("h_copied")
            h_turned = pc.sem("h_turned")
            bias_added = pc.sem("bias_added")
            relu_done = pc.sem("relu_done")
            y_psum = pc.sem("y_psum")
            y_done = pc.sem("y_done")
            y_stored = [pc.sem(f"y_stored{b}") for b in range(2)]
            block = pc.block()
            in_blk = sorted_in.rearrange("(m p) d -> m p d", p=P)
            out_blk = sorted_out.rearrange("(m p) d -> m p d", p=P)

            @block.sync
            def _(sp):
                for q in range(2):
                    sp.dma_start(rows[:, q, :], in_blk[q, :, :]).then_inc(row_loaded[q], 16)
                sp.sem_inc(y_stored[0], 16)
                sp.sem_inc(y_stored[1], 16)
                with sp.Fori(0, BLOCKS // 2 - 1) as i:
                    for q in range(2):
                        sp.wait_ge(row_turned, i * 2 + (q + 1))
                        sp.dma_start(rows[:, q, :], in_blk[ds(i * 2 + (q + 2), 1), :, :].rearrange("m p d -> (m p) d")).then_inc(row_loaded[q], 16)
                        sp.wait_ge(y_done, i * 2 + (q + 2))
                        sp.dma_start(out_blk[ds(i * 2 + q, 1), :, :].rearrange("m p d -> (m p) d"), yrow[:, q, :]).then_inc(y_stored[q], 16)
                for q in range(2):
                    sp.wait_ge(y_done, BLOCKS + q)
                    sp.dma_start(out_blk[BLOCKS - 2 + q, :, :], yrow[:, q, :]).then_inc(y_stored[q], 16)
                for q in range(2):
                    sp.wait_ge(y_stored[q], 16 * (BLOCKS // 2 + 1))

            @block.tensor
            def _(pe):
                pe.sem_inc(h_turned, 2)

                def expert(m):
                    return pe.value_load(block_expert[0:1, ds(m, 1)], min_val=0, max_val=EX - 1)

                def turn_rows(i, q):
                    m = i * 2 + q
                    pe.wait_ge(row_loaded[q], (i + 1) * 16)
                    pe.wait_ge(rowT_ready, m + 1)
                    for c in range(C2):
                        mm = nc.tensor.transpose(ps_r[:, c, :], rows[:, q, P * c:P * c + P], ident[:])
                    mm.then_inc(row_turned, 1)

                def up(i, q):
                    m = i * 2 + q
                    e = expert(m)
                    pe.wait_ge(rowT_ready, m + 2)
                    pe.wait_ge(h_copied, m + 1)
                    for n in range(FF // 512):
                        for c in range(C2):
                            mm = nc.tensor.matmul(ps_h[q][:, 512 * n:512 * n + 512], rowsT[:, q, c, :],
                                                  W1[:, ds(e, 1), c, 512 * n:512 * n + 512].rearrange("p e f -> p (e f)"),
                                                  start=(c == 0), stop=(c == C2 - 1))
                    mm.then_inc(h_psum, 1)

                def turn_hidden(i, q):
                    m = i * 2 + q
                    pe.wait_ge(h_copied, m + 3)
                    pe.wait_ge(bias_added, m + 1)
                    for k in range(KF):
                        mm = nc.tensor.transpose(ps_t[:, k, :], hid[:, q, P * k:P * k + P], ident[:])
                    mm.then_inc(h_turned, 1)

                def down(i, q):
                    m = i * 2 + q
                    e = expert(m)
                    pe.wait_ge(relu_done, m + 1)
                    pe.wait_ge(y_done, m + 1)
                    for k in range(KF):
                        mm = nc.tensor.matmul(ps_y[:], hidT[:, q, k, :],
                                              W2[:, ds(e, 1), k, :].rearrange("p e d -> p (e d)"),
                                              start=(k == 0), stop=(k == KF - 1))
                    mm.then_inc(y_psum, 1)

                turn_rows(0, 0)
                up(0, 0)
                turn_hidden(0, 0)
                with pe.Fori(0, BLOCKS // 2 - 1) as i:
                    turn_rows(i, 1)
                    up(i, 1)
                    down(i, 0)
                    turn_hidden(i, 1)
                    turn_rows(i + 1, 0)
                    up(i + 1, 0)
                    down(i, 1)
                    turn_hidden(i + 1, 0)
                turn_rows(BLOCKS // 2 - 1, 1)
                up(BLOCKS // 2 - 1, 1)
                down(BLOCKS // 2 - 1, 0)
                turn_hidden(BLOCKS // 2 - 1, 1)
                down(BLOCKS // 2 - 1, 1)

            @block.scalar
            def _(act):
                act.sem_inc(rowT_ready, 1)
                act.sem_inc(h_copied, 2)

                def rows_out(i, q):
                    act.wait_ge(row_turned, i * 2 + (q + 1))
                    nc.scalar.activation(rowsT[:, q, :, :], ps_r, ACT.Copy).then_inc(rowT_ready, 1)

                def hidden_out(i, q):
                    m = i * 2 + q
                    act.wait_ge(h_psum, m + 1)
                    act.wait_ge(h_turned, m + 1)
                    nc.scalar.activation(hid[:, q, :], ps_h[q][:], ACT.Copy).then_inc(h_copied, 1)

                def relu(i, q):
                    act.wait_ge(bias_added, i * 2 + (q + 2))
                    nc.scalar.activation(hidT[:, q, :, :], hidT[:, q, :, :], ACT.Relu).then_inc(relu_done, 1)

                rows_out(0, 0)
                hidden_out(0, 0)
                with act.Fori(0, BLOCKS // 2 - 1) as i:
                    rows_out(i, 1)
                    relu(i, 0)
                    hidden_out(i, 1)
                    rows_out(i + 1, 0)
                    relu(i, 1)
                    hidden_out(i + 1, 0)
                rows_out(BLOCKS // 2 - 1, 1)
                relu(BLOCKS // 2 - 1, 0)
                hidden_out(BLOCKS // 2 - 1, 1)
                relu(BLOCKS // 2 - 1, 1)

            @block.vector
            def _(dve):
                dve.sem_inc(bias_added, 1)
                dve.sem_inc(y_done, 1)
                dve.wait_ge(b2_loaded, 16)

                def add_b1(i, q):
                    m = i * 2 + q
                    e = dve.value_load(block_expert[0:1, ds(m, 1)], min_val=0, max_val=EX - 1)
                    dve.wait_ge(h_turned, m + 3)
                    nc.vector.tensor_tensor(hidT[:, q, :, :], ps_t[:],
                                            b1[:, ds(e, 1), :].rearrange("p e m -> p (e m)").unsqueeze(2).to_broadcast([P, KF, P]),
                                            ALU.add).then_inc(bias_added, 1)

                def add_b2(i, q):
                    m = i * 2 + q
                    e = dve.value_load(block_expert[0:1, ds(m, 1)], min_val=0, max_val=EX - 1)
                    dve.wait_ge(y_psum, m + 1)
                    dve.wait_ge(y_stored[q], (i + 1) * 16)
                    nc.vector.tensor_tensor(yrow[:, q, :], ps_y[:], b2[:, ds(e, 1), :].rearrange("p e d -> p (e d)"),
                                            ALU.add).then_inc(y_done, 1)

                add_b1(0, 0)
                with dve.Fori(0, BLOCKS // 2 - 1) as i:
                    add_b2(i, 0)
                    add_b1(i, 1)
                    add_b2(i, 1)
                    add_b1(i + 1, 0)
                add_b2(BLOCKS // 2 - 1, 0)
                add_b1(BLOCKS // 2 - 1, 1)
                add_b2(BLOCKS // 2 - 1, 1)

        with Phase(nc, "moeD") as pd:
            GY = W1[:].rearrange("p e c f -> p (e c f)")[:, 0:CH * D].rearrange("p (j d) -> p j d", d=D)
            ps_f = [pd.ps(f"ps_f{b}", [P, C2, NT]) for b in range(2)]
            gathered = pd.sem("gathered")
            summed = pd.sem("summed")
            doubled = pd.sem("doubled")
            stats_done = pd.sem("stats_done")
            aggr_done = pd.sem("aggr_done")
            std_done = pd.sem("std_done")
            rstd_done = pd.sem("rstd_done")
            normed = pd.sem("normed")
            turned = pd.sem("turned")
            copied = pd.sem("copied")
            block = pd.block()

            @block.gpsimd
            def _(pool):
                for j in range(CH):
                    nc.gpsimd.indirect_dma_start(GY[:, j, :], None, sorted_out,
                                                 bass.IndirectOffsetOnAxis(pos[:, j:j + 1], 0)).then_inc(gathered, 16)

            @block.vector
            def _(dve):
                dve.wait_ge(gathered, 16 * CH)
                with dve.Fori(0, CH // 4) as i:
                    for k in range(4):
                        j = i * 4 + k
                        g = GY[:, ds(j, 1), :].rearrange("p j d -> p (j d)")
                        nc.vector.tensor_scalar(g, g, alpha[:, ds(j, 1)], None, ALU.mult).then_inc(summed, 1)
                    dve.wait_ge(summed, i * 4 + 4)
                    nc.vector.scalar_tensor_tensor(out=XTM[:, ds(i * 4, 4), :], in0=XTM[:, ds(i * 4, 4), :], scalar=2.0,
                                                   in1=GY[:, ds(i * 4, 4), :], op0=ALU.mult, op1=ALU.add).then_inc(doubled, 1)
                    dve.wait_ge(doubled, i + 1)
                    for k in range(4):
                        j = i * 4 + k
                        ins = nc.vector.bn_stats(stats[:, ds(j, 1), :].rearrange("p k s -> p (k s)"),
                                                 XTM[:, ds(j, 1), :].rearrange("p j d -> p (j d)"))
                    ins.then_inc(stats_done, 1)
                dve.wait_ge(stats_done, CH // 4)
                for j in range(CH):
                    ins = nc.vector.bn_aggr(MV[:, j, :], stats[:, j, :])
                ins.then_inc(aggr_done, 1)
                dve.wait_ge(std_done, 1)
                nc.vector.reciprocal(rstd[:], std[:]).then_inc(rstd_done, 1)
                dve.wait_ge(rstd_done, 1)
                for j in range(CH):
                    nc.vector.tensor_scalar(GY[:, j, :], XTM[:, j, :], MV[:, j, 0:1], rstd[:, j:j + 1],
                                            ALU.subtract, ALU.mult).then_inc(normed, 1)

            @block.scalar
            def _(act):
                act.wait_ge(aggr_done, 1)
                nc.scalar.activation(std[:], MV[:, :, 1], ACT.Sqrt, bias=epsb[:, 0:1]).then_inc(std_done, 1)
                for n in range(TILES):
                    act.wait_ge(turned, n + 1)
                    nc.scalar.activation(X[:, :, NT * n:NT * n + NT], ps_f[n % 2][:], ACT.Copy).then_inc(copied, 1)

            @block.tensor
            def _(pe):
                for n in range(TILES):
                    pe.wait_ge(normed, TC * (n + 1))
                    if n >= 2:
                        pe.wait_ge(copied, n - 1)
                    for k in range(TC):
                        for c in range(C2):
                            mm = nc.tensor.transpose(ps_f[n % 2][:, c, P * k:P * k + P], GY[:, TC * n + k, P * c:P * c + P], ident[:])
                    mm.then_inc(turned, 1)


def delta_stage(nc, X, ones_mean, ident, w):
    HEADS, HD = 4, D // 4
    TAPS = 4
    HALO = TAPS - 1
    FIRS = (3, 15, 63)
    PAD = FIRS[-1] - 1
    PATHS = 5
    HP = HEADS * PATHS
    CH = TOK // P
    TC = NT // P
    ON_PE = 32
    with Phase(nc, "del") as ph:
        VD = ph.sb("values", [P, C2, BATCH, PAD + SEQ])
        LG = ph.sb("path_logits", [P, CH, HP])
        epsb = ph.sb("epsb", [P, 1])
        epsk = ph.sb("epsk", [P, 1])
        scratch = {n: nc.dram_tensor(f"del_{n}", (D, TOK), F32).ap() for n in ("q", "k", "kb", "vb", "o")}

        with Phase(nc, "delA") as pa:
            W = {n: pa.sb(n, [P, C2, D]) for n in ("q", "k", "v", "b")}
            wb = pa.sb("wb", [P, C2, HEADS])
            conv = {n: pa.sb(f"conv_{n}", [P, C2, TAPS]) for n in "qkv"}
            gate_w = pa.sb("gate_w", [P, C2, HP])
            head_ones = pa.sb("head_ones", [P, P])
            XS = pa.sb("XS", [P, C2, NT])
            pre = {n: [pa.sb(f"pre_{n}{b}", [P, C2, HALO + NT]) for b in range(2)] for n in "qkv"}
            y = {n: [pa.sb(f"y_{n}{b}", [P, C2, NT]) for b in range(2)] for n in "qkv"}
            sig = {n: pa.sb(f"sig_{n}", [P, C2, NT]) for n in "qkv"}
            nrm = {n: pa.sb(f"nrm_{n}", [P, C2, NT]) for n in "qk"}
            beta = pa.sb("beta", [P, C2, NT])
            kb = [pa.sb(f"kb{b}", [P, C2, NT]) for b in range(2)]
            vb = [pa.sb(f"vb{b}", [P, C2, NT]) for b in range(2)]
            slot = [pa.ps(f"slot{s}", [P, C2, NT]) for s in range(4)]
            full = [pa.sem(f"slot_full{s}") for s in range(4)]
            free = [pa.sem(f"slot_free{s}") for s in range(4)]
            USE = {"k": (0, 0), "q": (1, 0), "v": (2, 0), "b": (3, 0), "lg": (0, 1), "ssk": (1, 1), "ssq": (2, 1)}
            PER = [2, 2, 2, 1]
            loaded = pa.sem("loaded")
            consts = pa.sem("consts")
            wb_spread = pa.sem("wb_spread")
            halo_done = pa.sem("halo_done")
            weights_ready = pa.sem("weights_ready")
            x_staged = pa.sem("x_staged")
            projected = {n: pa.sem(f"projected_{n}") for n in "qkv"}
            beta_done = pa.sem("beta_done")
            conv_step = {n: pa.sem(f"conv_step_{n}") for n in "qkv"}
            sig_done = {n: pa.sem(f"sig_done_{n}") for n in "qkv"}
            silu_done = {n: pa.sem(f"silu_done_{n}") for n in "qkv"}
            sq_done = {n: pa.sem(f"sq_done_{n}") for n in "qk"}
            ln_done = {n: pa.sem(f"ln_done_{n}") for n in "qk"}
            rn_done = {n: pa.sem(f"rn_done_{n}") for n in "qk"}
            unit = {n: pa.sem(f"unit_{n}") for n in "qk"}
            kb_done = pa.sem("kb_done")
            vb_done = pa.sem("vb_done")
            lg_done = pa.sem("lg_done")
            stored = [pa.sem(f"stored{b}") for b in range(2)]
            block = pa.block()

            def slot_free(pe, n, key):
                s, u = USE[key]
                pe.wait_ge(free[s], n * PER[s] + (u + 1))
                return slot[s], full[s]

            def slot_full(eng, n, key):
                s, u = USE[key]
                eng.wait_ge(full[s], n * PER[s] + (u + 1))
                return slot[s], free[s]

            def buffers_free(eng, i, b):
                eng.wait_ge(stored[b], (i + 1) * 64)

            @block.sync
            def _(sp):
                for n in "qkv":
                    sp.dma_start(W[n][:], w[f"L0_attn_W{n}"].rearrange("(c p) o -> p c o", p=P)).then_inc(loaded, 16)
                    sp.dma_start(conv[n][:], w[f"L0_attn_conv_{n}"].rearrange("(c p) o -> p c o", p=P)).then_inc(loaded, 16)
                sp.dma_start(wb[:], w["L0_attn_Wb"].rearrange("(c p) o -> p c o", p=P)).then_inc(loaded, 16)
                sp.dma_start(gate_w[:], w["L0_attn_gate_w"].rearrange("(c p) o -> p c o", p=P)).then_inc(loaded, 16)
                sp.sem_inc(stored[0], 64)
                sp.sem_inc(stored[1], 64)
                with sp.Fori(0, BATCH) as i:
                    for b in range(2):
                        n = i * 2 + b
                        for name, sem, credit, buf in (("q", unit["q"], 0, y["q"][b]), ("k", unit["k"], 0, y["k"][b]),
                                                       ("kb", kb_done, 1, kb[b]), ("vb", vb_done, 1, vb[b])):
                            sp.wait_ge(sem, n + (1 + credit))
                            sp.dma_start(scratch[name].rearrange("(c p) t -> p c t", p=P)[:, :, ds(n * NT, NT)],
                                         buf[:]).then_inc(stored[b], 16)
                for b in range(2):
                    sp.wait_ge(stored[b], 64 * (BATCH + 1))

            @block.gpsimd
            def _(pool):
                nc.gpsimd.memset(head_ones[:], 1.0).then_inc(consts, 1)
                nc.gpsimd.memset(VD[:, :, :, 0:PAD], 0.0)
                pool.sem_inc(kb_done, 1)
                pool.wait_ge(consts, 1)
                g3 = head_ones[:].rearrange("p (h c) -> p h c", c=HD)
                nc.gpsimd.affine_select(out=g3, in_=g3, compare_op=ALU.is_ge, fill=0.0, base=0,
                                        pattern=[[-HD, P // HD], [0, HD]], channel_multiplier=1).then_inc(consts, 1)
                pool.wait_ge(consts, 2)
                nc.gpsimd.affine_select(out=g3, in_=g3, compare_op=ALU.is_ge, fill=0.0, base=HD - 1,
                                        pattern=[[HD, P // HD], [0, HD]], channel_multiplier=-1).then_inc(consts, 1)
                with pool.Fori(0, BATCH) as i:
                    for b in range(2):
                        n = i * 2 + b
                        pool.wait_ge(lg_done, n + 1)
                        nc.gpsimd.tensor_copy(XS[:], X[:, :, ds(n * NT, NT)]).then_inc(x_staged, 1)
                        for key in "kq":
                            pool.wait_ge(sig_done[key], n + 1)
                            nc.gpsimd.tensor_tensor(y[key][b][:], y[key][b][:], sig[key][:], ALU.mult).then_inc(silu_done[key], 1)
                        for key in "kq":
                            pool.wait_ge(rn_done[key], n + 1)
                            nc.gpsimd.tensor_tensor(y[key][b][:], y[key][b][:], nrm[key][:], ALU.mult).then_inc(unit[key], 1)
                        pool.wait_ge(unit["k"], n + 1)
                        pool.wait_ge(beta_done, n + 1)
                        nc.gpsimd.tensor_tensor(kb[b][:], y["k"][b][:], beta[:], ALU.mult).then_inc(kb_done, 1)

            @block.tensor
            def _(pe):
                pe.wait_ge(loaded, 16 * 8)
                pe.wait_ge(consts, 3)
                pe.wait_ge(weights_ready, 1)

                def project(n, key):
                    dst, sem = slot_free(pe, n, key)
                    for c in range(C2):
                        for kk in range(C2):
                            mm = nc.tensor.matmul(dst[:, c, :], W[key][:, kk, P * c:P * c + P], X[:, kk, ds(n * NT, NT)],
                                                  start=(kk == 0), stop=(kk == C2 - 1))
                    mm.then_inc(sem, 1)

                with pe.Fori(0, BATCH) as i:
                    for b in range(2):
                        n = i * 2 + b
                        for key in "kqvb":
                            project(n, key)
                        pe.wait_ge(x_staged, n + 1)
                        dst, sem = slot_free(pe, n, "lg")
                        for k in range(TC):
                            for kk in range(C2):
                                mm = nc.tensor.matmul(dst[:, 0, HP * k:HP * k + HP], XS[:, kk, P * k:P * k + P], gate_w[:, kk, :],
                                                      start=(kk == 0), stop=(kk == C2 - 1))
                        mm.then_inc(sem, 1)
                        for key in "kq":
                            pe.wait_ge(sq_done[key], n + 1)
                            dst, sem = slot_free(pe, n, "ss" + key)
                            for c in range(C2):
                                mm = nc.tensor.matmul(dst[:, c, :], head_ones[:], nrm[key][:, c, :], start=True, stop=True)
                            mm.then_inc(sem, 1)

            @block.scalar
            def _(act):
                act.wait_ge(weights_ready, 1)
                with act.Fori(0, BATCH) as i:
                    for b in range(2):
                        n = i * 2 + b
                        buffers_free(act, i, b)
                        for key in "kqv":
                            src, sem = slot_full(act, n, key)
                            nc.scalar.activation(pre[key][b][:, :, HALO:], src[:], ACT.Copy).then_inc(projected[key], 1)
                            act.wait_ge(projected[key], n + 1)
                            act.sem_inc(sem, 1)
                        src, sem = slot_full(act, n, "b")
                        act.wait_ge(kb_done, n + 1)
                        act.wait_ge(vb_done, n + 1)
                        nc.scalar.activation(beta[:], src[:], ACT.Sigmoid).then_inc(beta_done, 1)
                        act.wait_ge(beta_done, n + 1)
                        act.sem_inc(sem, 1)
                        for key in "kqv":
                            act.wait_ge(conv_step[key], n * TAPS + TAPS)
                            nc.scalar.activation(sig[key][:], y[key][b][:], ACT.Sigmoid).then_inc(sig_done[key], 1)
                        for key in "kq":
                            act.wait_ge(silu_done[key], n + 1)
                            nc.scalar.activation(nrm[key][:], y[key][b][:], ACT.Square).then_inc(sq_done[key], 1)
                        for key in "kq":
                            src, sem = slot_full(act, n, "ss" + key)
                            nc.scalar.activation(nrm[key][:], src[:], ACT.Ln, bias=epsk[:, 0:1]).then_inc(ln_done[key], 1)
                            act.wait_ge(ln_done[key], n + 1)
                            act.sem_inc(sem, 1)
                            nc.scalar.activation(nrm[key][:], nrm[key][:], ACT.Exp, scale=-0.5).then_inc(rn_done[key], 1)

            @block.vector
            def _(dve):
                nc.vector.memset(epsb[:], EPS)
                nc.vector.memset(epsk[:], 1e-6)
                for key in "qkv":
                    nc.vector.memset(pre[key][0][:, :, 0:HALO], 0.0)
                dve.wait_ge(loaded, 16 * 8)
                nc.vector.tensor_copy(W["b"][:].rearrange("p c (h k) -> p c h k", k=HD),
                                      wb[:].unsqueeze(3).to_broadcast([P, C2, HEADS, HD])).then_inc(wb_spread, 1)
                dve.wait_ge(wb_spread, 1)
                for s in range(4):
                    dve.sem_inc(free[s], 1)
                dve.sem_inc(lg_done, 1)
                dve.sem_inc(vb_done, 1)
                dve.sem_inc(weights_ready, 1)
                with dve.Fori(0, BATCH) as i:
                    for b in range(2):
                        n = i * 2 + b
                        buffers_free(dve, i, b)
                        for key in "kqv":
                            dve.wait_ge(projected[key], n + 1)
                            if b == 1:
                                nc.vector.tensor_copy(pre[key][1][:, :, 0:HALO], pre[key][0][:, :, NT:NT + HALO]).then_inc(halo_done, 1)
                        if b == 1:
                            dve.wait_ge(halo_done, i * 3 + 3)
                        for j in range(TAPS):
                            for key in "kqv":
                                if j:
                                    dve.wait_ge(conv_step[key], n * TAPS + j)
                                for c in range(C2):
                                    src = pre[key][b][:, c, j:j + NT]
                                    tap = conv[key][:, c, j:j + 1]
                                    dst = y[key][b][:, c, :]
                                    if j == 0:
                                        ins = nc.vector.tensor_scalar(dst, src, tap, None, ALU.mult)
                                    else:
                                        ins = nc.vector.scalar_tensor_tensor(out=dst, in0=src, scalar=tap, in1=dst,
                                                                             op0=ALU.mult, op1=ALU.add)
                                ins.then_inc(conv_step[key], 1)
                        dve.wait_ge(sig_done["v"], n + 1)
                        vals = VD[:, :, ds(i, 1), PAD + NT * b:PAD + NT * b + NT].rearrange("p c i t -> p c (i t)")
                        nc.vector.tensor_tensor(vals, y["v"][b][:], sig["v"][:], ALU.mult).then_inc(silu_done["v"], 1)
                        dve.wait_ge(silu_done["v"], n + 1)
                        dve.wait_ge(beta_done, n + 1)
                        nc.vector.tensor_tensor(vb[b][:], vals, beta[:], ALU.mult).then_inc(vb_done, 1)
                        src, sem = slot_full(dve, n, "lg")
                        nc.vector.tensor_copy(LG[:, ds(n * TC, TC), :], src[:, 0, 0:HP * TC].rearrange("p (k g) -> p k g", k=TC)).then_inc(lg_done, 1)
                        dve.wait_ge(lg_done, n + 2)
                        dve.sem_inc(sem, 1)


        with Phase(nc, "delB") as pb:
            LEVELS = 7
            CHAINS = 2
            CPB = SEQ // P
            SEQS = BATCH // CHAINS
            STEPS = SEQS * CPB
            UP = LEVELS - 1
            flip = pb.sb("level_masks", [P, LEVELS, P])
            low1 = pb.sb("low1", [P, P])
            causal = pb.sb("causal", [P, P])
            chains = lambda name, shape: [pb.sb(f"{name}{a}", shape) for a in range(CHAINS)]
            ink, invb = ([chains(f"in_{n}{q}_", [P, C2, P]) for q in range(2)] for n in ("k", "vb"))
            inq, inkb = ([chains(f"in_{n}{q}_", [P, HEADS, P]) for q in range(2)] for n in ("q", "kb"))
            Lsb, T, TT, attn = (chains(n, [P, HEADS, P]) for n in ("L", "T", "TT", "attn"))
            Wsb = [chains(f"W{l}_", [P, HEADS, P]) for l in range(LEVELS)]
            KV = chains("KV", [P, 2, D])
            S = chains("S", [P, C2, HD])
            Rsb, U = chains("R", [P, HEADS, HD]), chains("U", [P, HEADS, HD])
            Osb = [chains(f"O{q}_", [P, C2, P]) for q in range(2)]
            bankA, bankB, bankC, bankD = ([pb.ps(f"bank{n}{a}", [P, HEADS, P]) for a in range(CHAINS)] for n in "ABCD")
            flat = lambda bank: bank[:].rearrange("p h j -> p (h j)")
            pKV = [flat(x).rearrange("p (x d) -> p x d", x=2) for x in bankD]
            pRU = [flat(x).rearrange("p (x h v) -> p x h v", x=2, h=HEADS) for x in bankD]
            pO = [flat(x)[:, 0:C2 * P].rearrange("p (c t) -> p c t", c=C2) for x in bankD]
            pS = [flat(x)[:, 0:C2 * HD].rearrange("p (c v) -> p c v", c=C2) for x in bankC]

            def columns(ap, l, x):
                return ap.rearrange("p (m x s) -> p m x s", x=2, s=2 ** l)[:, :, x, :]

            def head_columns(buf, l, x):
                return buf[:].rearrange("p h (m x s) -> p (h m) x s", x=2, s=2 ** l)[:, :, x, :]

            def packed(bank, l):
                return flat(bank)[:, 0:HEADS * P // 2].rearrange("p (m s) -> p m s", s=2 ** l)

            def packed_head(bank, h, l):
                return flat(bank)[:, h * P // 2:(h + 1) * P // 2].rearrange("p (m s) -> p m s", s=2 ** l)
            masks = pb.sem("masks")
            pads_zero = pb.sem("pads_zero")
            in_loaded = [[pb.sem(f"in_loaded{q}_{a}") for a in range(CHAINS)] for q in range(2)]
            o_stored = [[pb.sem(f"o_stored{q}_{a}") for a in range(CHAINS)] for q in range(2)]
            l_psum, qk_psum, l_copied, kv_copied, tt_begun, tt_start, t_begun, t_start = (
                pb.sem(n) for n in ("l_psum", "qk_psum", "l_copied", "kv_copied", "tt_begun", "tt_start", "t_begun", "t_start"))
            w_psum, w_masked, d_psum, dt_psum, tt_done, t_done = (
                pb.sem(n) for n in ("w_psum", "w_masked", "d_psum", "dt_psum", "tt_done", "t_done"))
            r_psum, r_done, u_psum, u_copied, so_psum, s_done, s_zero, o_copied = (
                pb.sem(n) for n in ("r_psum", "r_done", "u_psum", "u_copied", "so_psum", "s_done", "s_zero", "o_copied"))
            block = pb.block()

            once = lambda m, a: m * CHAINS + (a + 1)
            level = lambda m, l, a, ups=UP: m * (ups * CHAINS) + ((l - 1) * CHAINS + a + 1)

            def steps(eng, body, new_sequence=lambda: None):
                for s in range(SEQS):
                    new_sequence()
                    tail = 1 if s == SEQS - 1 else 0
                    with eng.Fori(0, CPB // 2 - tail) as i:
                        for q in range(2):
                            body(i * 2 + (s * CPB + q), i + s * CPB // 2, q, False)
                body(STEPS - 2, STEPS // 2 - 1, 0, False)
                body(STEPS - 1, STEPS // 2 - 1, 1, True)

            def chunk_in_dram(name, m, a):
                return scratch[name].rearrange("(c p) t -> p c t", p=P)[:, :, ds((m + a * STEPS) * P, P)]

            @block.sync
            def _(sp):
                def load(m, q, a):
                    for name, buf in (("k", ink), ("vb", invb)):
                        sp.dma_start(buf[q][a][:], chunk_in_dram(name, m, a)).then_inc(in_loaded[q][a], 16)
                    for name, buf in (("q", inq), ("kb", inkb)):
                        for r in range(2):
                            rows = slice(HD * r, HD * r + HD)
                            sp.dma_start(buf[q][a][rows, r::2, :], chunk_in_dram(name, m, a)[rows, :, :]).then_inc(in_loaded[q][a], 16)

                def store(m, q, a):
                    sp.wait_ge(o_copied, once(m + 1, a))
                    sp.dma_start(chunk_in_dram("o", m, a), Osb[q][a][:]).then_inc(o_stored[q][a], 16)

                sp.wait_ge(pads_zero, 4 * CHAINS)
                for q in range(2):
                    for a in range(CHAINS):
                        load(q, q, a)
                        sp.sem_inc(o_stored[q][a], 16)
                with sp.Fori(0, STEPS // 2 - 1) as i:
                    for q in range(2):
                        for a in range(CHAINS):
                            sp.wait_ge(so_psum, once(i * 2 + q, a))
                            load(i * 2 + (q + 2), q, a)
                        for a in range(CHAINS):
                            store(i * 2 + q, q, a)
                for q in range(2):
                    for a in range(CHAINS):
                        store(STEPS - 2 + q, q, a)
                for q in range(2):
                    for a in range(CHAINS):
                        sp.wait_ge(o_stored[q][a], 16 * (STEPS // 2 + 1))

            @block.gpsimd
            def _(pool):
                nc.gpsimd.memset(flip[:], 0.0).then_inc(masks, 1)
                nc.gpsimd.memset(low1[:], 0.0).then_inc(masks, 1)
                nc.gpsimd.memset(causal[:], 1.0).then_inc(masks, 1)
                pool.wait_ge(masks, 3)
                m = 3
                for l in range(LEVELS):
                    s = 2 ** l
                    odd = flip[:, l, :].rearrange("p (m x s) -> p m x s", x=2, s=s)[:, :, 1, :]
                    pairs = P // (2 * s)
                    nc.gpsimd.memset(odd, -1.0).then_inc(masks, 1)
                    m += 1
                    pool.wait_ge(masks, m)
                    for base, sign in ((0, 1), (s - 1, -1)):
                        nc.gpsimd.affine_select(out=odd, in_=odd, compare_op=ALU.is_ge, fill=0.0, base=base,
                                                pattern=[[-2 * s * sign, pairs], [0, s]], channel_multiplier=sign).then_inc(masks, 1)
                        m += 1
                        pool.wait_ge(masks, m)
                even = low1[:].rearrange("p (m x) -> p m x", x=2)[:, :, 0]
                nc.gpsimd.memset(even, -1.0).then_inc(masks, 1)
                pool.wait_ge(masks, m + 1)
                nc.gpsimd.affine_select(out=even, in_=even, compare_op=ALU.is_equal, fill=0.0, base=-1,
                                        pattern=[[-2, P // 2]], channel_multiplier=1).then_inc(masks, 1)
                nc.gpsimd.affine_select(out=causal[:], in_=causal[:], compare_op=ALU.is_ge, fill=0.0, base=0,
                                        pattern=[[1, P]], channel_multiplier=-1).then_inc(masks, 1)
                pool.wait_ge(masks, m + 3)
                bc = lambda ap: ap.unsqueeze(1).to_broadcast([P, HEADS, P])
                with pool.Fori(0, STEPS) as m:
                    for a in range(CHAINS):
                        pool.wait_ge(l_copied, once(m, a))
                        nc.gpsimd.tensor_tensor(T[a][:], Lsb[a][:], bc(low1[:]), ALU.mult).then_inc(t_begun, 1)
                    for a in range(CHAINS):
                        pool.wait_ge(t_begun, once(m, a))
                        nc.gpsimd.tensor_tensor(T[a][:], T[a][:], bc(ident[:]), ALU.add).then_inc(t_start, 1)
            MASKS = 3 + 3 * LEVELS + 3

            @block.tensor
            def _(pe):
                def hp(h):
                    return slice(HD * (h % 2), HD * (h % 2) + HD), h // 2

                def grams_l(m, half, q):
                    for a in range(CHAINS):
                        pe.wait_ge(in_loaded[q][a], half * 96 + 96)
                        for h in range(HEADS):
                            nc.tensor.matmul(bankA[a][:, h, :], inkb[q][a][:, h, :], ink[q][a][:, h // 2, :], start=True, stop=True)
                        for c in range(C2):
                            mm = nc.tensor.matmul(bankB[a][:, 2 * c:2 * c + 2, :], ink[q][a][:, c, :], inkb[q][a][:, 2 * c:2 * c + 2, :],
                                                  start=True, stop=True)
                        mm.then_inc(l_psum, 1)

                def body(m, half, q, last):
                    for a in range(CHAINS):
                        pe.wait_ge(s_done, once(m, a))
                        pe.wait_ge(o_copied, once(m, a))
                        for c in range(C2):
                            nc.tensor.matmul(bankC[a][:, 2 * c:2 * c + 2, :], ink[q][a][:, c, :], inq[q][a][:, 2 * c:2 * c + 2, :],
                                             start=True, stop=True)
                        for x, src in enumerate((ink, invb)):
                            for c in range(C2):
                                mm = nc.tensor.transpose(pKV[a][:, x, P * c:P * c + P], src[q][a][:, c, :], ident[:])
                        mm.then_inc(qk_psum, 1)
                    for l in range(1, LEVELS):
                        for a in range(CHAINS):
                            if l == 1:
                                pe.wait_ge(l_copied, once(m, a))
                                pe.wait_ge(tt_start, once(m, a))
                            else:
                                pe.wait_ge(tt_done, level(m, l - 1, a))
                            for h in range(HEADS):
                                mm = nc.tensor.matmul(packed_head(bankA[a], h, l), Lsb[a][:, h, :], columns(TT[a][:, h, :], l, 1),
                                                      start=True, stop=True)
                            mm.then_inc(w_psum, 1)
                        if l == 1:
                            for a in range(CHAINS):
                                pe.wait_ge(kv_copied, once(m, a))
                                pe.wait_ge(s_zero, sequence[0])
                                for h in range(HEADS):
                                    mm = nc.tensor.matmul(pRU[a][:, 0, h, :], inkb[q][a][:, h, :], S[a][:, h // 2, :], start=True, stop=True)
                                mm.then_inc(r_psum, 1)
                        for a in range(CHAINS):
                            if l == 1:
                                pe.wait_ge(t_start, once(m, a))
                            else:
                                pe.wait_ge(t_done, level(m, l - 1, a, UP - 1))
                            pe.wait_ge(w_masked, level(m, l, a))
                            for h in range(HEADS):
                                mm = nc.tensor.matmul(packed_head(bankB[a], h, l), T[a][:, h, :], columns(Wsb[l][a][:, h, :], l, 1),
                                                      start=True, stop=True)
                            mm.then_inc(d_psum, 1)
                        if l < UP:
                            for a in range(CHAINS):
                                for h in range(HEADS):
                                    mm = nc.tensor.matmul(packed_head(bankC[a], h, l), Wsb[l][a][:, h, :], columns(T[a][:, h, :], l, 0),
                                                          start=True, stop=True)
                                mm.then_inc(dt_psum, 1)
                    for a in range(CHAINS):
                        pe.wait_ge(r_done, once(m, a))
                        pe.wait_ge(tt_done, level(m, UP, a))
                        for h in range(HEADS):
                            mm = nc.tensor.matmul(pRU[a][:, 1, h, :], TT[a][:, h, :], Rsb[a][:, h, :], start=True, stop=True)
                        mm.then_inc(u_psum, 1)
                    if not last:
                        grams_l(m + 1, half + q, 1 - q)
                    for a in range(CHAINS):
                        pe.wait_ge(u_copied, once(m, a))
                        for h in range(HEADS):
                            r, c = hp(h)
                            nc.tensor.matmul(pS[a][r, c, :], KV[a][:, 0, HD * h:HD * h + HD], U[a][:, h, :], start=True, stop=True)
                        for h in range(HEADS):
                            r, c = hp(h)
                            nc.tensor.matmul(pO[a][r, c, :], S[a][:, c, :], inq[q][a][:, h, :], start=True, stop=False)
                            mm = nc.tensor.matmul(pO[a][r, c, :], U[a][:, h, :], attn[a][:, h, :], start=False, stop=True)
                        mm.then_inc(so_psum, 1)

                sequence = [0]

                def new_sequence():
                    sequence[0] += 1
                grams_l(0, 0, 0)
                steps(pe, body, new_sequence)

            @block.scalar
            def _(act):
                def copy_l(m):
                    for a in range(CHAINS):
                        act.wait_ge(l_psum, once(m, a))
                        nc.scalar.activation(Lsb[a][:], bankA[a][:], ACT.Copy).then_inc(l_copied, 1)

                def body(m, half, q, last):
                    for a in range(CHAINS):
                        act.wait_ge(qk_psum, once(m, a))
                        nc.scalar.activation(KV[a][:], pKV[a], ACT.Copy).then_inc(kv_copied, 1)
                    for a in range(CHAINS):
                        act.wait_ge(u_psum, once(m, a))
                        nc.scalar.activation(U[a][:], pRU[a][:, 1, :, :], ACT.Copy).then_inc(u_copied, 1)
                    if not last:
                        copy_l(m + 1)
                    for a in range(CHAINS):
                        act.wait_ge(so_psum, once(m, a))
                        act.wait_ge(o_stored[q][a], half * 16 + 16)
                        nc.scalar.activation(Osb[q][a][:], pO[a], ACT.Copy).then_inc(o_copied, 1)
                act.sem_inc(o_copied, CHAINS)
                copy_l(0)
                steps(act, body)

            @block.vector
            def _(dve):
                bc = lambda ap: ap.unsqueeze(1).to_broadcast([P, HEADS, P])
                for q in range(2):
                    for buf in inq[q] + inkb[q]:
                        nc.vector.memset(buf[:], 0.0).then_inc(pads_zero, 1)
                for l in range(1, LEVELS):
                    for a in range(CHAINS):
                        nc.vector.memset(Wsb[l][a][:], 0.0)
                dve.wait_ge(masks, MASKS)
                dve.sem_inc(s_done, CHAINS)

                def start(m):
                    for a in range(CHAINS):
                        dve.wait_ge(l_psum, once(m, a))
                        nc.vector.tensor_tensor(TT[a][:], bankB[a][:], bc(flip[:, 0, :]), ALU.mult).then_inc(tt_begun, 1)
                    for a in range(CHAINS):
                        dve.wait_ge(tt_begun, once(m, a))
                        nc.vector.tensor_tensor(TT[a][:], TT[a][:], bc(ident[:]), ALU.add).then_inc(tt_start, 1)

                def body(m, half, q, last):
                    for a in range(CHAINS):
                        dve.wait_ge(qk_psum, once(m, a))
                        nc.vector.tensor_tensor(attn[a][:], bankC[a][:], bc(causal[:]), ALU.mult)
                    for l in range(1, LEVELS):
                        for a in range(CHAINS):
                            dve.wait_ge(w_psum, level(m, l, a))
                            flips = columns(flip[:, l, :], l, 1).unsqueeze(1).to_broadcast([P, HEADS, P >> (l + 1), 1 << l])
                            nc.vector.tensor_tensor(Wsb[l][a][:].rearrange("p h (m x s) -> p h m x s", x=2, s=2 ** l)[:, :, :, 1, :],
                                                    packed(bankA[a], l).rearrange("p (h m) s -> p h m s", h=HEADS), flips,
                                                    ALU.mult).then_inc(w_masked, 1)
                        if l == 1:
                            for a in range(CHAINS):
                                dve.wait_ge(r_psum, once(m, a))
                                nc.vector.tensor_tensor(Rsb[a][:], KV[a][:, 1, :].rearrange("p (h v) -> p h v", h=HEADS),
                                                        pRU[a][:, 0, :, :], ALU.subtract).then_inc(r_done, 1)
                        for a in range(CHAINS):
                            dve.wait_ge(d_psum, level(m, l, a))
                            part = head_columns(TT[a], l, 1)
                            nc.vector.tensor_tensor(part, part, packed(bankB[a], l), ALU.add).then_inc(tt_done, 1)
                        if l < UP:
                            for a in range(CHAINS):
                                dve.wait_ge(dt_psum, level(m, l, a, UP - 1))
                                part = head_columns(T[a], l, 0)
                                nc.vector.tensor_tensor(part, part, packed(bankC[a], l), ALU.add).then_inc(t_done, 1)
                    if not last:
                        start(m + 1)
                    for a in range(CHAINS):
                        dve.wait_ge(so_psum, once(m, a))
                        nc.vector.tensor_tensor(S[a][:], S[a][:], pS[a], ALU.add).then_inc(s_done, 1)

                sequence = [0]

                def new_sequence():
                    dve.wait_ge(s_done, once(sequence[0] * CPB, CHAINS - 1))
                    for a in range(CHAINS):
                        ins = nc.vector.memset(S[a][:], 0.0)
                    ins.then_inc(s_zero, 1)
                    sequence[0] += 1
                start(0)
                steps(dve, body, new_sequence)

        with Phase(nc, "delC") as pc:
            ON_DVE = FIRS[-1] - ON_PE
            Wo = pc.sb("Wo", [P, C2, D])
            fir = [pc.sb(f"fir{k}", [P, C2, k]) for k in FIRS]
            norm_w = pc.sb("norm_w", [P, 1])
            gate_b = pc.sb("gate_b", [P, HP])
            ltemp = pc.sb("log_temp", [P, HEADS])
            epar = pc.sb("eps_param", [P, HEADS])
            keep = pc.sb("keep", [P, HEADS])
            smax = pc.sb("smax", [P, CH, HEADS])
            diag = pc.sb("diag", [P, ON_PE, C2, P])
            mean_ones = pc.sb("head_mean", [P, P])
            PRt = pc.sb("PRt", [P, TC, HP])
            PRT = pc.sb("PRT", [HP, NT])
            sel = pc.sb("sel", [HP, PATHS, C2, P])
            PB = pc.sb("PB", [P, PATHS, C2, NT])
            Od = pc.sb("Od", [P, C2, NT])
            acc = [pc.sb(f"acc{k}", [P, C2, NT]) for k in FIRS]
            mix = pc.sb("mix", [P, C2, NT])
            SQ = pc.sb("SQ", [P, C2, NT])
            rr = pc.sb("rr", [P, C2, NT])
            ps_f = pc.ps("ps_f", [P, C2, NT])
            ps_p = [pc.ps(f"ps_p{b}", [P, C2, NT]) for b in range(2)]
            ps_a = pc.ps("ps_a", [P, C2, NT])
            loaded = pc.sem("loaded")
            consts = pc.sem("consts")
            prep = pc.sem("prep")
            act_prep = pc.sem("act_prep")
            ready = pc.sem("ready")
            od_loaded = pc.sem("od_loaded")
            pr_staged = pc.sem("pr_staged")
            pr_turned = pc.sem("pr_turned")
            prt_ready = pc.sem("prt_ready")
            spread = pc.sem("spread")
            pb_copied = pc.sem("pb_copied")
            fir_psum = pc.sem("fir_psum")
            fir_read = pc.sem("fir_read")
            tap = [pc.sem(f"tap{c}") for c in range(C2)]
            pool_mix = pc.sem("pool_mix")
            mix_step = pc.sem("mix_step")
            mix_added = pc.sem("mix_added")
            mix_done = pc.sem("mix_done")
            squared = pc.sem("squared")
            stat_psum = pc.sem("stat_psum")
            ln_done = pc.sem("ln_done")
            rr_done = pc.sem("rr_done")
            on_done = pc.sem("on_done")
            o_psum = pc.sem("o_psum")
            resid = pc.sem("resid")
            mean_psum = pc.sem("mean_psum")
            centred = pc.sem("centred")
            x_done = pc.sem("x_done")
            block = pc.block()

            def tiles(eng, prologue, body):
                prologue()
                with eng.Fori(0, BATCH - 1) as i:
                    body(i * 2, (i * 2 + 1, i, 1))
                    body(i * 2 + 1, (i * 2 + 2, i + 1, 0))
                body(TILES - 2, (TILES - 1, BATCH - 1, 1))
                body(TILES - 1, None)

            @block.sync
            def _(sp):
                sp.dma_start(Wo[:], w["L0_attn_Wo"].rearrange("(c p) o -> p c o", p=P)).then_inc(loaded, 16)
                for k, n in enumerate(("s", "m", "l")):
                    sp.dma_start(fir[k][:], w[f"L0_attn_fir_{n}"].rearrange("(c p) o -> p c o", p=P)).then_inc(loaded, 16)
                for r in range(2):
                    sp.dma_start(norm_w[HD * r:HD * r + HD, :], w["L0_attn_norm_w"]).then_inc(loaded, 16)
                for t, n in ((gate_b, "gate_b"), (ltemp, "log_temp"), (epar, "eps_param")):
                    sp.dma_start(t[:], w[f"L0_attn_{n}"].to_broadcast(t.shape)).then_inc(loaded, 16)
                with sp.Fori(0, TILES) as n:
                    sp.wait_ge(mix_done, n + 1)
                    sp.dma_start(Od[:], scratch["o"].rearrange("(c p) t -> p c t", p=P)[:, :, ds(n * NT, NT)]).then_inc(od_loaded, 16)

            @block.gpsimd
            def _(pool):
                nc.gpsimd.memset(mean_ones[:], 1.0 / HD).then_inc(consts, 1)
                pool.wait_ge(consts, 1)
                g3 = mean_ones[:].rearrange("p (h c) -> p h c", c=HD)
                nc.gpsimd.affine_select(out=g3, in_=g3, compare_op=ALU.is_ge, fill=0.0, base=0,
                                        pattern=[[-HD, P // HD], [0, HD]], channel_multiplier=1).then_inc(consts, 1)
                pool.wait_ge(consts, 2)
                nc.gpsimd.affine_select(out=g3, in_=g3, compare_op=ALU.is_ge, fill=0.0, base=HD - 1,
                                        pattern=[[HD, P // HD], [0, HD]], channel_multiplier=-1).then_inc(consts, 1)
                nc.gpsimd.memset(sel[:], 1.0).then_inc(consts, 1)
                pool.wait_ge(consts, 4)
                sel5 = sel[:].rearrange("r p c (h f) -> r p c h f", h=2)
                for p in range(PATHS):
                    nc.gpsimd.affine_select(out=sel5[:, p], in_=sel5[:, p], compare_op=ALU.is_equal, fill=0.0, base=-p,
                                            pattern=[[-2 * PATHS, C2], [-PATHS, 2], [0, HD]], channel_multiplier=1).then_inc(consts, 1)
                pool.wait_ge(ready, 1)
                with pool.Fori(0, BATCH) as i:
                    for b in range(2):
                        n = i * 2 + b
                        pool.wait_ge(pr_turned, n + 1)
                        nc.gpsimd.tensor_copy(PRt[:], LG[:, ds(n * TC, TC), :]).then_inc(pr_staged, 1)
                        pool.wait_ge(od_loaded, n * 16 + 16)
                        pool.wait_ge(pb_copied, n * PATHS + PATHS)
                        nc.gpsimd.tensor_tensor(Od[:], Od[:], PB[:, 3, :, :], ALU.mult).then_inc(pool_mix, 1)
                        vals = VD[:, :, ds(i, 1), PAD + NT * b:PAD + NT * b + NT].rearrange("p c i t -> p c (i t)")
                        nc.gpsimd.tensor_tensor(PB[:, 4, :, :], vals, PB[:, 4, :, :], ALU.mult).then_inc(pool_mix, 1)
                        pool.wait_ge(pool_mix, n * 3 + 2)
                        nc.gpsimd.tensor_tensor(Od[:], Od[:], PB[:, 4, :, :], ALU.add).then_inc(pool_mix, 1)

            @block.tensor
            def _(pe):
                pe.wait_ge(ready, 1)
                pe.sem_inc(pr_turned, 1)
                PARTS = 4
                pairs = [(c, j) for c in range(C2) for j in range(ON_PE)]
                share = len(pairs) // PARTS

                def filters(nxt, part):
                    if nxt is None:
                        return
                    n, seq, half = nxt
                    if part == 0:
                        pe.wait_ge(fir_read, n + 1)
                    for c, j in pairs[share * part:share * (part + 1)]:
                        win = VD[:, c:c + 1, ds(seq, 1), NT * half + j:NT * half + j + NT].rearrange("p c i t -> p (c i t)")
                        mm = nc.tensor.matmul(ps_f[:, c, :], diag[:, j, c, :], win, start=(j == 0), stop=(j == ON_PE - 1))
                    if part == PARTS - 1:
                        mm.then_inc(fir_psum, 1)

                def weights(nxt, first=False):
                    if nxt is None:
                        return
                    n = nxt[0]
                    pe.wait_ge(pr_staged, n + 1)
                    if not first:
                        pe.wait_ge(pb_copied, n * PATHS)
                    for k in range(TC):
                        mm = nc.tensor.transpose(ps_p[1][0:HP, 0, P * k:P * k + P], PRt[:, k, :], ident[:])
                    mm.then_inc(pr_turned, 1)
                    pe.wait_ge(prt_ready, n + 1)
                    for p in range(PATHS):
                        if p >= 2:
                            pe.wait_ge(pb_copied, n * PATHS + (p - 1))
                        for c in range(C2):
                            mm = nc.tensor.matmul(ps_p[p % 2][:, c, :], sel[:, p, c, :], PRT[:], start=True, stop=True)
                        mm.then_inc(spread, 1)

                def prologue():
                    nxt = (0, 0, 0)
                    weights(nxt, first=True)
                    for part in range(PARTS):
                        filters(nxt, part)

                def body(n, nxt):
                    filters(nxt, 0)
                    pe.wait_ge(squared, n * 2 + 1)
                    for c in range(C2):
                        mm = nc.tensor.matmul(ps_a[:, c, :], mean_ones[:], SQ[:, c, :], start=True, stop=True)
                    mm.then_inc(stat_psum, 1)
                    filters(nxt, 1)
                    pe.wait_ge(on_done, n + 1)
                    for c in range(C2):
                        for kk in range(C2):
                            mm = nc.tensor.matmul(ps_a[:, c, :], Wo[:, kk, P * c:P * c + P], mix[:, kk, :],
                                                  start=(kk == 0), stop=(kk == C2 - 1))
                    mm.then_inc(o_psum, 1)
                    filters(nxt, 2)
                    pe.wait_ge(resid, n + 1)
                    for kk in range(C2):
                        mm = nc.tensor.matmul(ps_a[:, 0, :], ones_mean[:], mix[:, kk, :], start=(kk == 0), stop=(kk == C2 - 1))
                    mm.then_inc(mean_psum, 1)
                    weights(nxt)
                    filters(nxt, 3)
                    pe.wait_ge(squared, n * 2 + 2)
                    for kk in range(C2):
                        mm = nc.tensor.matmul(ps_a[:, 1, :], ones_mean[:], SQ[:, kk, :], start=(kk == 0), stop=(kk == C2 - 1))
                    mm.then_inc(stat_psum, 1)
                tiles(pe, prologue, body)

            @block.scalar
            def _(act):
                act.wait_ge(prep, 3)
                act.wait_ge(loaded, 16 * 9)
                nc.scalar.activation(ltemp[:], ltemp[:], ACT.Exp, scale=-1.0).then_inc(act_prep, 1)
                act.wait_ge(prep, 6)
                nc.scalar.activation(LG[:], LG[:], ACT.Exp).then_inc(act_prep, 1)

                def weights(nxt):
                    if nxt is None:
                        return
                    n = nxt[0]
                    act.wait_ge(pr_turned, n + 2)
                    nc.scalar.activation(PRT[:], ps_p[1][0:HP, 0, :], ACT.Copy).then_inc(prt_ready, 1)
                    act.wait_ge(mix_done, n + 1)
                    for p in range(PATHS):
                        act.wait_ge(spread, n * PATHS + (p + 1))
                        nc.scalar.activation(PB[:, p, :, :], ps_p[p % 2][:], ACT.Copy).then_inc(pb_copied, 1)

                def body(n, nxt):
                    act.wait_ge(mix_done, n + 2)
                    nc.scalar.activation(SQ[:], mix[:], ACT.Square).then_inc(squared, 1)
                    act.wait_ge(stat_psum, n * 2 + 1)
                    nc.scalar.activation(rr[:], ps_a[:], ACT.Ln, bias=epsb[:, 0:1]).then_inc(ln_done, 1)
                    act.wait_ge(ln_done, n * 2 + 1)
                    nc.scalar.activation(rr[:], rr[:], ACT.Exp, scale=-0.5).then_inc(rr_done, 1)
                    weights(nxt)
                    act.wait_ge(centred, n + 1)
                    nc.scalar.activation(SQ[:], mix[:], ACT.Square).then_inc(squared, 1)
                    act.wait_ge(stat_psum, n * 2 + 2)
                    nc.scalar.activation(rr[:, 0, :], ps_a[:, 1, :], ACT.Ln, bias=epsb[:, 0:1]).then_inc(ln_done, 1)
                    act.wait_ge(ln_done, n * 2 + 2)
                    nc.scalar.activation(rr[:, 0, :], rr[:, 0, :], ACT.Exp, scale=-0.5).then_inc(rr_done, 1)
                tiles(act, lambda: weights((0, 0, 0)), body)

            @block.vector
            def _(dve):
                lg = LG[:].rearrange("p j (h x) -> p j h x", h=HEADS)
                per_head = lambda ap: ap.unsqueeze(1).to_broadcast([P, CH, HEADS]).unsqueeze(3).to_broadcast([P, CH, HEADS, PATHS])
                n_prep = [0]

                def then(ins):
                    n_prep[0] += 1
                    ins.then_inc(prep, 1)
                    dve.wait_ge(prep, n_prep[0])

                dve.wait_ge(loaded, 16 * 9)
                then(nc.vector.tensor_scalar(epar[:], epar[:], 0.0, 0.2, ALU.max, ALU.min))
                then(nc.vector.tensor_scalar(keep[:], epar[:], -float(PATHS), 1.0, ALU.mult, ALU.add))
                then(nc.vector.tensor_tensor(LG[:], LG[:], gate_b[:].unsqueeze(1).to_broadcast([P, CH, HP]), ALU.add))
                dve.wait_ge(act_prep, 1)
                for h in range(HEADS):
                    ins = nc.vector.tensor_scalar(lg[:, :, h, :], lg[:, :, h, :], ltemp[:, h:h + 1], None, ALU.mult)
                then(ins)
                then(nc.vector.tensor_reduce(smax[:], lg, AX.X, ALU.max))
                then(nc.vector.tensor_tensor(lg, lg, smax[:].unsqueeze(3).to_broadcast([P, CH, HEADS, PATHS]), ALU.subtract))
                dve.wait_ge(act_prep, 2)
                then(nc.vector.tensor_reduce(smax[:], lg, AX.X, ALU.add))
                then(nc.vector.reciprocal(smax[:], smax[:]))
                then(nc.vector.tensor_tensor(lg, lg, smax[:].unsqueeze(3).to_broadcast([P, CH, HEADS, PATHS]), ALU.mult))
                for h in range(HEADS):
                    ins = nc.vector.tensor_scalar(lg[:, :, h, :], lg[:, :, h, :], keep[:, h:h + 1], epar[:, h:h + 1], ALU.mult, ALU.add)
                then(ins)
                for c in range(C2):
                    nc.vector.tensor_scalar(Wo[:, c, :], Wo[:, c, :], norm_w[:, 0:1], None, ALU.mult)
                    for j in range(ON_PE):
                        ins = nc.vector.tensor_scalar(diag[:, j, c, :], ident[:], fir[2][:, c, j:j + 1], None, ALU.mult)
                then(ins)
                dve.wait_ge(consts, 4 + PATHS)
                dve.sem_inc(ready, 1)
                dve.sem_inc(mix_done, 1)
                dve.sem_inc(fir_read, 1)
                counts = [FIRS[0], FIRS[1], ON_DVE]
                ROUNDS = max(counts)
                PARTS = 4

                def filters(nxt, part):
                    if nxt is None:
                        return
                    n, seq, half = nxt
                    for j in range(ROUNDS)[CUTS[part]:CUTS[part + 1]]:
                        for c in range(C2):
                            if j:
                                dve.wait_ge(tap[c], n * ROUNDS + j)
                            for f, k in enumerate(FIRS):
                                if j >= counts[f]:
                                    continue
                                first = ON_PE if f == 2 else 0
                                o = PAD - (k - 1) + first + j + NT * half
                                src = VD[:, c:c + 1, ds(seq, 1), o:o + NT].rearrange("p c i t -> p (c i t)")
                                dst = acc[f][:, c, :]
                                wt = fir[f][:, c, first + j:first + j + 1]
                                if j == 0:
                                    ins = nc.vector.tensor_scalar(dst, src, wt, None, ALU.mult)
                                else:
                                    ins = nc.vector.scalar_tensor_tensor(out=dst, in0=src, scalar=wt, in1=dst,
                                                                         op0=ALU.mult, op1=ALU.add)
                            ins.then_inc(tap[c], 1)
                taps_by = [sum(min(j, x) for x in counts) for j in range(ROUNDS + 1)]
                CUTS = [next(j for j in range(ROUNDS + 1) if taps_by[j] * PARTS >= sum(counts) * part) for part in range(PARTS + 1)]

                def prologue():
                    for part in range(PARTS):
                        filters((0, 0, 0), part)

                def body(n, nxt):
                    tile = X[:, :, ds(n * NT, NT)]
                    for c in range(C2):
                        dve.wait_ge(tap[c], n * ROUNDS + ROUNDS)
                    dve.wait_ge(fir_psum, n + 1)
                    dve.wait_ge(pb_copied, n * PATHS + PATHS)
                    nc.vector.tensor_tensor(acc[2][:], acc[2][:], ps_f[:], ALU.add).then_inc(mix_step, 1)
                    nc.vector.tensor_tensor(acc[0][:], acc[0][:], PB[:, 0, :, :], ALU.mult)
                    nc.vector.tensor_tensor(acc[1][:], acc[1][:], PB[:, 1, :, :], ALU.mult).then_inc(mix_step, 1)
                    dve.wait_ge(mix_step, n * 4 + 1)
                    dve.sem_inc(fir_read, 1)
                    nc.vector.tensor_tensor(acc[2][:], acc[2][:], PB[:, 2, :, :], ALU.mult).then_inc(mix_step, 1)
                    dve.wait_ge(mix_step, n * 4 + 2)
                    nc.vector.tensor_tensor(acc[0][:], acc[0][:], acc[1][:], ALU.add).then_inc(mix_step, 1)
                    dve.wait_ge(pool_mix, n * 3 + 3)
                    dve.wait_ge(mix_step, n * 4 + 3)
                    nc.vector.tensor_tensor(mix[:], acc[2][:], Od[:], ALU.add).then_inc(mix_added, 1)
                    dve.wait_ge(mix_step, n * 4 + 4)
                    dve.wait_ge(mix_added, n + 1)
                    nc.vector.tensor_tensor(mix[:], mix[:], acc[0][:], ALU.add).then_inc(mix_done, 1)
                    dve.wait_ge(mix_done, n + 2)
                    filters(nxt, 0)
                    dve.wait_ge(rr_done, n * 2 + 1)
                    nc.vector.tensor_tensor(mix[:], mix[:], rr[:], ALU.mult).then_inc(on_done, 1)
                    filters(nxt, 1)
                    dve.wait_ge(o_psum, n + 1)
                    nc.vector.tensor_tensor(mix[:], ps_a[:], tile, ALU.add).then_inc(resid, 1)
                    filters(nxt, 2)
                    dve.wait_ge(resid, n + 1)
                    dve.wait_ge(mean_psum, n + 1)
                    nc.vector.tensor_tensor(mix[:], mix[:], ps_a[:, 0, :].unsqueeze(1).to_broadcast([P, C2, NT]),
                                            ALU.subtract).then_inc(centred, 1)
                    filters(nxt, 3)
                    dve.wait_ge(centred, n + 1)
                    dve.wait_ge(rr_done, n * 2 + 2)
                    nc.vector.tensor_tensor(tile, mix[:], rr[:, 0, :].unsqueeze(1).to_broadcast([P, C2, NT]),
                                            ALU.mult).then_inc(x_done, 1)
                    dve.wait_ge(x_done, n + 1)
                tiles(dve, prologue, body)


def lora_ffn_stage(nc, X, ones_mean, w):
    FF = 1024
    KF = FF // P
    HALFM = KF // 2
    RANK = 16
    MAGIC = 1.5 * 2.0 ** 23
    with Phase(nc, "ffn") as ph:
        w_fc = ph.sb("w_fc", [P, C2, FF])
        w_pr = ph.sb("w_pr", [P, KF, D])
        a_fc = ph.sb("a_fc", [RANK, D])
        bt_fc = ph.sb("bt_fc", [RANK, FF])
        a_pr = ph.sb("a_pr", [RANK, FF])
        bt_pr = ph.sb("bt_pr", [RANK, D])
        b_fc = ph.sb("b_fc", [P, KF])
        b_pr = ph.sb("b_pr", [P, C2])
        amax = ph.sb("amax", [P, 2])
        amax_all = ph.sb("amax_all", [P, 2])
        qstep = ph.sb("qstep", [P, 2])
        qinv = ph.sb("qinv", [P, 2])
        H = ph.sb("H", [P, KF, NT])
        R = ph.sb("R", [P, C2, NT])
        XC = ph.sb("XC", [P, C2, NT])
        SQ = ph.sb("SQ", [P, C2, NT])
        std = ph.sb("std", [P, NT])
        rstd = ph.sb("rstd", [P, NT])
        epsb = ph.sb("epsb", [P, 1])
        ps_h = [ph.ps(f"ps_h{b}", [P, NT]) for b in range(4)]
        ps_y = [ph.ps(f"ps_y{c}", [P, NT]) for c in range(C2)]
        ps_mean = ph.ps("ps_mean", [P, NT])
        ps_var = ph.ps("ps_var", [P, NT])
        loaded = ph.sem("loaded")
        dve_prep = ph.sem("dve_prep")
        amax_ready = ph.sem("amax_ready")
        fold_ready = ph.sem("fold_ready")
        fold_used = ph.sem("fold_used")
        weights_ready = ph.sem("weights_ready")
        h_psum = ph.sem("h_psum")
        h_done = ph.sem("h_done")
        y_psum = ph.sem("y_psum")
        resid = ph.sem("resid")
        mean_psum = ph.sem("mean_psum")
        centred = ph.sem("centred")
        squared = ph.sem("squared")
        var_psum = ph.sem("var_psum")
        std_done = ph.sem("std_done")
        rstd_done = ph.sem("rstd_done")
        x_done = ph.sem("x_done")
        block = ph.block()
        folds = [(w_fc[:, c, 512 * n:512 * n + 512], a_fc[:, P * c:P * c + P], bt_fc[:, 512 * n:512 * n + 512])
                 for c in range(C2) for n in range(FF // 512)]
        folds += [(w_pr[:, m, :], a_pr[:, P * m:P * m + P], bt_pr[:, :]) for m in range(KF)]

        @block.sync
        def _(sp):
            sp.dma_start(w_fc[:], w["L1_ffn_W_fc"].rearrange("(c p) f -> p c f", p=P)).then_inc(loaded, 16)
            sp.dma_start(w_pr[:], w["L1_ffn_W_proj"].rearrange("(c p) f -> p c f", p=P)).then_inc(loaded, 16)
            sp.dma_start(a_fc[:], w["L1_ffn_A_fc"]).then_inc(loaded, 16)
            sp.dma_start(bt_fc[:], w["L1_ffn_B_fc"]).then_inc(loaded, 16)
            sp.dma_start(a_pr[:], w["L1_ffn_A_proj"]).then_inc(loaded, 16)
            sp.dma_start(bt_pr[:], w["L1_ffn_B_proj"]).then_inc(loaded, 16)
            sp.dma_start(b_fc[:], w["L1_ffn_b_fc"]).then_inc(loaded, 16)
            sp.dma_start(b_pr[:], w["L1_ffn_b_proj"]).then_inc(loaded, 16)

        @block.gpsimd
        def _(pool):
            pool.wait_ge(dve_prep, 3)
            nc.gpsimd.partition_all_reduce(amax_all[:], amax[:], P, bass.bass_isa.ReduceOp.max).then_inc(amax_ready, 1)

        @block.tensor
        def _(pe):
            pe.wait_ge(loaded, 16 * 8)
            for n, (dst, a, bt) in enumerate(folds):
                if n >= 4:
                    pe.wait_ge(fold_used, n - 3)
                size = dst.shape[-1]
                nc.tensor.matmul(ps_h[n % 4][:, 0:size], a, bt, start=True, stop=True).then_inc(fold_ready, 1)
            pe.wait_ge(weights_ready, 1)

            def up(i, m0, m1):
                for m in range(m0, m1):
                    pe.wait_ge(h_done, i * KF + m + 1)
                    for c in range(C2):
                        mm = nc.tensor.matmul(ps_h[m % 4][:], w_fc[:, c, P * m:P * m + P], X[:, c, ds(i * NT, NT)],
                                              start=(c == 0), stop=(c == C2 - 1))
                    mm.then_inc(h_psum, 1)

            def down(i):
                pe.wait_ge(resid, C2 * i + 1)
                for c in range(C2):
                    for m in range(KF):
                        if c == 0:
                            pe.wait_ge(h_done, i * KF + m + 5)
                        mm = nc.tensor.matmul(ps_y[c][:], w_pr[:, m, P * c:P * c + P], H[:, m, :],
                                              start=(m == 0), stop=(m == KF - 1))
                    mm.then_inc(y_psum, 1)

            def mean(i):
                pe.wait_ge(resid, C2 * (i + 1) + 1)
                for c in range(C2):
                    mm = nc.tensor.matmul(ps_mean[:], ones_mean[:], R[:, c, :], start=(c == 0), stop=(c == C2 - 1))
                mm.then_inc(mean_psum, 1)

            def var(i):
                pe.wait_ge(squared, i + 1)
                for c in range(C2):
                    mm = nc.tensor.matmul(ps_var[:], ones_mean[:], SQ[:, c, :], start=(c == 0), stop=(c == C2 - 1))
                mm.then_inc(var_psum, 1)

            up(0, 0, KF)
            with pe.Fori(0, TILES - 1) as i:
                down(i)
                up(i + 1, 0, HALFM)
                mean(i)
                up(i + 1, HALFM, KF)
                var(i)
            down(TILES - 1)
            mean(TILES - 1)
            var(TILES - 1)

        @block.scalar
        def _(act):
            act.sem_inc(h_done, 4)

            def gelu(i, m0, m1):
                for m in range(m0, m1):
                    act.wait_ge(h_psum, i * KF + m + 1)
                    if m == 0:
                        act.wait_ge(y_psum, C2 * i + 2)
                    nc.scalar.activation(H[:, m, :], ps_h[m % 4][:], ACT.Gelu, bias=b_fc[:, m:m + 1]).then_inc(h_done, 1)

            def squares(i):
                act.wait_ge(centred, i + 1)
                act.wait_ge(var_psum, i + 1)
                nc.scalar.activation(SQ[:], XC[:], ACT.Square).then_inc(squared, 1)

            def roots(i):
                act.wait_ge(var_psum, i + 2)
                nc.scalar.activation(std[:], ps_var[:], ACT.Sqrt, bias=epsb[:, 0:1]).then_inc(std_done, 1)

            act.sem_inc(y_psum, C2)
            act.sem_inc(var_psum, 1)
            act.wait_ge(weights_ready, 1)
            gelu(0, 0, KF)
            with act.Fori(0, TILES - 1) as i:
                gelu(i + 1, 0, HALFM)
                squares(i)
                gelu(i + 1, HALFM, KF)
                roots(i)
            squares(TILES - 1)
            roots(TILES - 1)

        @block.vector
        def _(dve):
            nc.vector.memset(epsb[:], EPS).then_inc(dve_prep, 1)
            dve.wait_ge(loaded, 16 * 8)
            nc.vector.tensor_reduce(amax[:, 0:1], w_fc[:], AX.XY, ALU.max, apply_absolute_value=True).then_inc(dve_prep, 1)
            nc.vector.tensor_reduce(amax[:, 1:2], w_pr[:], AX.XY, ALU.max, apply_absolute_value=True).then_inc(dve_prep, 1)
            dve.wait_ge(amax_ready, 1)
            nc.vector.tensor_scalar(qstep[:], amax_all[:], 1.0 / 127.0, None, ALU.mult).then_inc(dve_prep, 1)
            dve.wait_ge(dve_prep, 4)
            nc.vector.reciprocal(qinv[:], qstep[:]).then_inc(dve_prep, 1)
            dve.wait_ge(dve_prep, 5)
            for n, W in enumerate((w_fc, w_pr)):
                nc.vector.tensor_scalar(W[:], W[:], qinv[:, n:n + 1], MAGIC, ALU.mult, ALU.add).then_inc(dve_prep, 1)
                dve.wait_ge(dve_prep, 6 + 3 * n)
                nc.vector.tensor_scalar(W[:], W[:], -MAGIC, 127.0, ALU.add, ALU.min).then_inc(dve_prep, 1)
                dve.wait_ge(dve_prep, 7 + 3 * n)
                nc.vector.tensor_scalar(W[:], W[:], -128.0, qstep[:, n:n + 1], ALU.max, ALU.mult).then_inc(dve_prep, 1)
                dve.wait_ge(dve_prep, 8 + 3 * n)
            for n, (dst, a, bt) in enumerate(folds):
                dve.wait_ge(fold_ready, n + 1)
                size = dst.shape[-1]
                nc.vector.scalar_tensor_tensor(out=dst, in0=ps_h[n % 4][:, 0:size], scalar=2.0, in1=dst,
                                               op0=ALU.mult, op1=ALU.add).then_inc(fold_used, 1)
            dve.wait_ge(fold_used, len(folds))
            dve.sem_inc(weights_ready, 1)
            dve.sem_inc(resid, 1)

            def tail(i):
                for c in range(C2):
                    dve.wait_ge(y_psum, C2 * i + C2 + c + 1)
                    dve.wait_ge(mean_psum, i)
                    nc.vector.scalar_tensor_tensor(out=R[:, c, :], in0=ps_y[c][:], scalar=b_pr[:, c:c + 1],
                                                   in1=X[:, c, ds(i * NT, NT)], op0=ALU.add, op1=ALU.add).then_inc(resid, 1)
                dve.wait_ge(mean_psum, i + 1)
                dve.wait_ge(resid, C2 * (i + 1) + 1)
                nc.vector.tensor_tensor(XC[:], R[:], ps_mean[:].unsqueeze(1).to_broadcast([P, C2, NT]),
                                        ALU.subtract).then_inc(centred, 1)
                dve.wait_ge(std_done, i + 1)
                nc.vector.reciprocal(rstd[:], std[:]).then_inc(rstd_done, 1)
                dve.wait_ge(rstd_done, i + 1)
                nc.vector.tensor_tensor(X[:, :, ds(i * NT, NT)], XC[:], rstd[:].unsqueeze(1).to_broadcast([P, C2, NT]),
                                        ALU.mult).then_inc(x_done, 1)
            with dve.Fori(0, TILES) as i:
                tail(i)


def program(nc, w, out):
    with Phase(nc, "top") as top:
        X = top.sb("x_stream", [P, C2, TOK])
        ones_mean = top.sb("ones_mean", [P, P])
        ident = top.sb("ident", [P, P])
        zeros_written = top.sem("zeros_written")
        BLOCK_ROWS = 40 * P
        sorted_in = nc.dram_tensor("sorted_in", (BLOCK_ROWS, D), F32).ap()
        sorted_out = nc.dram_tensor("sorted_out", (BLOCK_ROWS, D), F32).ap()
        with Phase(nc, "load") as ph:
            zeros = ph.sb("zeros", [P, D])
            x_loaded = ph.sem("x_loaded")
            zeroed = ph.sem("zeroed")
            zeros_set = ph.sem("zeros_set")
            block = ph.block()

            @block.sync
            def _(sp):
                sp.dma_start(X[:], w["x"].rearrange("(c p) t -> p c t", p=P)).then_inc(x_loaded, 16)
                sp.wait_ge(x_loaded, 16)

                sp.wait_ge(zeros_set, 1)
                sp.dma_start(sorted_in.rearrange("(m p) d -> p m d", p=P),
                             zeros[:].unsqueeze(1).to_broadcast([P, BLOCK_ROWS // P, D])).then_inc(zeros_written, 16)
                sp.wait_ge(zeros_written, 16)

            @block.vector
            def _(dve):
                nc.vector.memset(zeros[:], 0.0).then_inc(zeros_set, 1)
                nc.vector.memset(ones_mean[:], 1.0 / D)

            @block.gpsimd
            def _(pool):
                nc.gpsimd.memset(ident[:], 0.0).then_inc(zeroed, 1)
                pool.wait_ge(zeroed, 1)
                nc.gpsimd.affine_select(out=ident[:], in_=ident[:], compare_op=ALU.not_equal, fill=1.0, base=0,
                                        pattern=[[-1, P]], channel_multiplier=1)

        if 0 in STAGES:
            delta_stage(nc, X, ones_mean, ident, w)
        if 1 in STAGES:
            cross_attention_stage(nc, X, ones_mean, ident, w, gated=True)
        if 2 in STAGES:
            expert_stage(nc, X, ones_mean, ident, w, sorted_in, sorted_out, zeros_written)
        if 3 in STAGES:
            recurrence_stage(nc, X, ones_mean, w)
        if 4 in STAGES:
            cross_attention_stage(nc, X, ones_mean, ident, w, gated=False)

        if 5 in STAGES:
            lora_ffn_stage(nc, X, ones_mean, w)

        with Phase(nc, "store") as ph:
            stored = ph.sem("stored")
            block = ph.block()

            @block.sync
            def _(sp):
                sp.dma_start(out.rearrange("(c p) t -> p c t", p=P), X[:]).then_inc(stored, 16)
                sp.wait_ge(stored, 16)


def _layout(name, a):
    import numpy as _np
    if name == "x":
        return a.reshape(TOK, D).T
    if name == "ctx_1024":
        return a.reshape(-1, D).T
    if name in TRANSPOSED:
        return a.T
    if name in ("L0_ffn_w1", "L0_ffn_w2"):
        return a.transpose(0, 2, 1)
    if name in ("L0_ffn_ln_g", "L0_ffn_ln_b", "L0_ffn_b1"):
        return a.reshape(a.shape[0], -1, P).transpose(2, 0, 1)
    if name == "L0_attn_gate_w":
        return a.reshape(-1, D).T
    if name.startswith("L0_attn_fir"):
        return a.reshape(D, -1)
    if name == "L0_attn_norm_w":
        return a.reshape(-1, 1)
    if name in ("L0_attn_gate_b", "L0_attn_log_temp", "L0_attn_eps_param"):
        return a.reshape(1, -1)
    if name in PARTITIONED:
        return a.reshape(-1, P).T
    return a


TRANSPOSED = ("L0_attn_Wq", "L0_attn_Wk", "L0_attn_Wv", "L0_attn_Wb", "L0_attn_Wo", "L0_xattn_Wq", "L0_xattn_Wk",
              "L0_xattn_Wv", "L0_xattn_Wg", "L0_xattn_Wo", "L0_ffn_centroids", "L1_attn_Wf1", "L1_attn_Wog1",
              "L1_xattn_Wq", "L1_xattn_Wk", "L1_xattn_Wv", "L1_xattn_Wo",
              "L1_ffn_W_fc", "L1_ffn_B_fc", "L1_ffn_W_proj", "L1_ffn_B_proj")
PARTITIONED = ("L1_ffn_b_fc", "L1_ffn_b_proj", "L1_xattn_bq", "L1_xattn_bk", "L1_xattn_bv", "L1_xattn_bo",
               "L0_xattn_qln_g", "L0_xattn_qln_b", "L0_xattn_kvln_g", "L0_xattn_kvln_b", "L0_xattn_bg",
               "L1_attn_norm_w")


def kernel(**inputs):
    import numpy as _np
    import concourse.bacc as _bacc
    from concourse import mybir as _mybir
    from concourse.bass_utils import run_bass_kernel_spmd as _run

    nc = _bacc.Bacc("TRN2", target_bir_lowering=False, num_devices=1)
    arrays, w = {}, {}
    for name, a in inputs.items():
        a = _np.ascontiguousarray(_layout(name, _np.asarray(a)))
        arrays[f"in_{name}"] = a
        w[name] = nc.dram_tensor(f"in_{name}", a.shape, _mybir.dt.from_np(a.dtype), kind="ExternalInput").ap()
    out = nc.dram_tensor("out_x", (D, TOK), F32, kind="ExternalOutput").ap()
    program(nc, w, out)
    r = _run(nc, [arrays], core_ids=[0])
    return _np.ascontiguousarray(_np.asarray(r.results[0]["out_x"]).reshape(D, BATCH, SEQ).transpose(1, 2, 0))
```

```python
from contextlib import ExitStack

import numpy as np

import concourse.bass as bass
from concourse import mybir

P = 128
D = 256
C2 = D // P
BATCH = 4
SEQ = 1024
TOK = BATCH * SEQ
NT = 512
TILES = TOK // NT
EPS = 1e-5

F32 = mybir.dt.float32
I32 = mybir.dt.int32
U32 = mybir.dt.uint32
ALU = mybir.AluOpType
ACT = mybir.ActivationFunctionType
AX = mybir.AxisListType
ds = bass.ds


class Phase:

    def __init__(self, nc, name):
        self.nc, self.name, self.ctx, self.sems = nc, name, ExitStack(), []

    def __enter__(self):
        self.ctx.__enter__()
        return self

    def __exit__(self, *a):
        self.ctx.__exit__(*a)
        if self.sems:
            self.nc.clear_and_free_semaphores(self.sems)
            self.nc.all_engine_barrier()

    def sb(self, name, shape, dt=F32):
        return self.ctx.enter_context(self.nc.sbuf_tensor(f"{self.name}_{name}", shape, dt))

    def ps(self, name, shape, dt=F32):
        return self.ctx.enter_context(self.nc.psum_tensor(f"{self.name}_{name}", shape, dt))

    def sem(self, name):
        self.sems.append(self.nc.alloc_semaphore(f"{self.name}_{name}"))
        return self.sems[-1]

    def block(self):
        return self.ctx.enter_context(self.nc.Block())


def recurrence_stage(nc, X, ones_mean, ident, w):
    HEADS, HD = 16, D // 16
    BL = 2
    HB = NT // BL
    ROWS = 7
    ROW_F, ROW_A, ROW_K, ROW_Q = 0, 1, 3, 5
    LOG_SCALE = 40.0
    with Phase(nc, "rec") as ph:
        G = ph.sb("out_gate", [P, C2, TOK])
        Wo = ph.sb("Wo", [P, C2, D])
        norm_w = ph.sb("norm_w", [P, C2])
        epsb = ph.sb("epsb", [P, 1])
        rows_dram = nc.dram_tensor("rec_rows", (D, ROWS, TOK // BL), F32).ap()
        v_dram, w_dram, o_dram = (nc.dram_tensor(f"rec_{n}", (D, BL, TOK // BL), F32).ap() for n in ("v", "w", "o"))

        with Phase(nc, "recA") as pa:
            W = {n: pa.sb(n, [P, C2, D]) for n in ("Wq", "Wk", "Wv", "Wf", "Wog", "Wga")}
            small = {n: pa.sb(n, [HD, D]) for n in ("Wf1", "Wf2", "Wog1", "Wog2")}
            wgamma = pa.sb("wgamma", [P, C2, HEADS])
            group_ones = pa.sb("group_ones", [P, P])
            norm_bias = pa.sb("norm_bias", [P, 1])
            bufs = {n: [pa.sb(f"{n}{b}", [P, C2, BL, HB]) for b in range(2)]
                    for n in ("sigq", "sigk", "q", "k", "f", "sg", "v", "norm", "ff", "a", "w")}
            tmp = pa.sb("tmp", [P, C2, BL, HB])
            slot = [pa.ps(f"slot{s}", [P, C2, NT]) for s in range(4)]
            full = [pa.sem(f"slot_full{s}") for s in range(4)]
            free = [pa.sem(f"slot_free{s}") for s in range(4)]
            USE = {"q": (0, 0), "nn": (0, 3), "k": (1, 0), "ga": (1, 1), "v": (1, 2), "f": (2, 0), "og": (2, 1), "ss": (2, 2),
                   "mn": (3, 0)}
            PER = [2, 3, 3, 1]
            loaded = pa.sem("loaded")
            consts = pa.sem("consts")
            fold_psum = pa.sem("fold_psum")
            folded = pa.sem("folded")
            weights_ready = pa.sem("weights_ready")
            sig_done = {n: pa.sem(f"{n}_done") for n in ("sigq", "sigk", "f", "sg", "og", "v", "sq", "ln", "norm")}
            did = {n: pa.sem(f"did_{n}") for n in ("q", "k", "clamp", "kn", "a", "ff", "fff", "pool_products", "qk", "row_f", "q_begun",
                                                   "row_a", "row_v", "rows_q", "rows_w", "step_m", "step_n")}
            stored = [pa.sem(f"stored{b}") for b in range(2)]
            STORES = 16 * 11
            block = pa.block()

            SKIPPED = {"nn": 1, "mn": 0}

            def slot_free(pe, n, key, last=False):
                s, u = USE[key]
                pe.wait_ge(free[s], n * PER[s] + (u + 1 - (SKIPPED[key] if last else 0)))
                return slot[s], full[s]

            def slot_full(eng, n, key, last=False):
                s, u = USE[key]
                eng.wait_ge(full[s], n * PER[s] + (u + 1 - (SKIPPED[key] if last else 0)))
                return slot[s], free[s]

            def buffers_free(eng, i, b):
                eng.wait_ge(stored[b], (i + 1) * STORES)

            def rounds(eng, begin, sums, finish, first=lambda: None):
                begin(0, 0, 0)
                first()
                finish(0, 0, 0)

                def one(n, i, b, n1, i1, b1):
                    begin(n1, i1, b1)
                    sums(n, i, b)
                    finish(n1, i1, b1)
                with eng.Fori(0, TILES // 2 - 1) as i:
                    one(i * 2, i, 0, i * 2 + 1, i, 1)
                    one(i * 2 + 1, i, 1, i * 2 + 2, i + 1, 0)
                one(TILES - 2, TILES // 2 - 1, 0, TILES - 1, TILES // 2 - 1, 1)
                sums(TILES - 1, TILES // 2 - 1, 1, last=True)

            planes = lambda ap: ap.rearrange("p c (t x) -> p c x t", x=BL)

            @block.sync
            def _(sp):
                for n in ("Wq", "Wk", "Wv"):
                    sp.dma_start(W[n][:], w[f"L1_attn_{n}"].rearrange("(c p) o -> p c o", p=P)).then_inc(loaded, 16)
                sp.dma_start(Wo[:], w["L1_attn_Wo"].rearrange("(c p) o -> p c o", p=P)).then_inc(loaded, 16)
                for n in small:
                    sp.dma_start(small[n][:], w[f"L1_attn_{n}"]).then_inc(loaded, 16)
                sp.dma_start(wgamma[:], w["L1_attn_Wgamma"].rearrange("(c p) o -> p c o", p=P)).then_inc(loaded, 16)
                sp.dma_start(norm_w[:], w["L1_attn_norm_w"]).then_inc(loaded, 16)
                sp.sem_inc(stored[0], STORES)
                sp.sem_inc(stored[1], STORES)
                with sp.Fori(0, TILES // 2) as i:
                    for b in range(2):
                        n = i * 2 + b

                        def store(dram, x, buf, plane):
                            sp.dma_start(dram.rearrange("(c p) x t -> p c x t", p=P)[:, :, x, ds(n * HB, HB)],
                                         bufs[buf][b][:, :, plane, :]).then_inc(stored[b], 16)
                        sp.wait_ge(sig_done["v"], n + 1)
                        store(v_dram, 0, "v", 0)
                        sp.wait_ge(did["kn"], n + 1)
                        store(rows_dram, ROW_K + 1, "k", 1)
                        sp.wait_ge(did["a"], n + 1)
                        store(rows_dram, ROW_A, "a", 0)
                        sp.wait_ge(did["pool_products"], (n + 1) * 3)
                        store(rows_dram, ROW_K, "ff", 0)
                        sp.wait_ge(did["row_f"], n + 1)
                        store(rows_dram, ROW_F, "ff", 1)
                        sp.wait_ge(did["row_a"], n + 1)
                        store(rows_dram, ROW_A + 1, "sg", 0)
                        sp.wait_ge(did["row_v"], n + 1)
                        store(v_dram, 1, "sg", 1)
                        sp.wait_ge(did["rows_q"], n + 1)
                        for x in range(BL):
                            store(rows_dram, ROW_Q + x, "sigk", x)
                        sp.wait_ge(did["rows_w"], n + 1)
                        for x in range(BL):
                            store(w_dram, x, "w", x)
                for b in range(2):
                    sp.wait_ge(stored[b], STORES * (TILES // 2 + 1))

            @block.gpsimd
            def _(pool):
                nc.gpsimd.memset(group_ones[:], 1.0).then_inc(consts, 1)
                pool.wait_ge(consts, 1)
                g3 = group_ones[:].rearrange("p (h c) -> p h c", c=HD)
                nc.gpsimd.affine_select(out=g3, in_=g3, compare_op=ALU.is_ge, fill=0.0, base=0,
                                        pattern=[[-HD, P // HD], [0, HD]], channel_multiplier=1).then_inc(consts, 1)
                pool.wait_ge(consts, 2)
                nc.gpsimd.affine_select(out=g3, in_=g3, compare_op=ALU.is_ge, fill=0.0, base=HD - 1,
                                        pattern=[[HD, P // HD], [0, HD]], channel_multiplier=-1).then_inc(consts, 1)

                def gates(n, i, b):
                    buffers_free(pool, i, b)
                    pool.wait_ge(sig_done["f"], n + 1)
                    pool.wait_ge(sig_done["sg"], n + 1)
                    nc.gpsimd.tensor_tensor(bufs["ff"][b][:], bufs["f"][b][:], bufs["f"][b][:], ALU.mult).then_inc(did["ff"], 1)
                    pool.wait_ge(did["ff"], n + 1)
                    nc.gpsimd.tensor_tensor(bufs["ff"][b][:], bufs["ff"][b][:], bufs["sg"][b][:], ALU.mult).then_inc(did["fff"], 1)

                def products(n, i, b):
                    k, q, f, a = (bufs[x][b] for x in ("k", "q", "f", "a"))
                    K0, F = bufs["ff"][b][:, :, 0, :], bufs["ff"][b][:, :, 1, :]
                    mul = lambda o, x, y: nc.gpsimd.tensor_tensor(o, x, y, ALU.mult)
                    done = did["pool_products"]
                    pool.wait_ge(did["kn"], n + 1)
                    pool.wait_ge(did["q"], n + 1)
                    pool.wait_ge(did["a"], n + 1)
                    mul(K0, f[:, :, 1, :], k[:, :, 0, :]).then_inc(done, 1)
                    mul(bufs["norm"][b][:, :, 0, :], a[:, :, 1, :], k[:, :, 0, :]).then_inc(done, 1)
                    pool.wait_ge(done, n * 3 + 1)
                    mul(bufs["norm"][b][:, :, 1, :], q[:, :, 1, :], K0).then_inc(done, 1)
                    mul(bufs["sigq"][b][:], q[:], k[:]).then_inc(did["qk"], 1)
                    mul(F, f[:, :, 1, :], f[:, :, 0, :]).then_inc(did["row_f"], 1)
                    mul(bufs["sigk"][b][:, :, 0, :], q[:, :, 0, :], f[:, :, 0, :]).then_inc(did["q_begun"], 1)
                    pool.wait_ge(did["row_f"], n + 1)
                    mul(bufs["sigk"][b][:, :, 1, :], q[:, :, 1, :], F).then_inc(did["q_begun"], 1)
                with pool.Fori(0, TILES // 2) as i:
                    for b in range(2):
                        gates(i * 2 + b, i, b)
                        products(i * 2 + b, i, b)

            @block.tensor
            def _(pe):
                pe.wait_ge(loaded, 16 * 10)
                pe.wait_ge(consts, 3)
                for s, (a, bb) in enumerate((("Wf1", "Wf2"), ("Wog1", "Wog2"))):
                    for c in range(C2):
                        mm = nc.tensor.matmul(slot[s][:, c, 0:D], small[a][:, P * c:P * c + P], small[bb][:], start=True, stop=True)
                mm.then_inc(fold_psum, 1)
                pe.wait_ge(weights_ready, 1)

                def pass_over():
                    pe.wait_ge(free[0], PER[0])
                    pe.sem_inc(full[0], 1)
                    pe.sem_inc(free[0], 1)

                def project(n, keys):
                    for key in keys:
                        dst, sem = slot_free(pe, n, key)
                        for c in range(C2):
                            for kk in range(C2):
                                mm = nc.tensor.matmul(dst[:, c, :], W["W" + key][:, kk, P * c:P * c + P], X[:, kk, ds(n * NT, NT)],
                                                      start=(kk == 0), stop=(kk == C2 - 1))
                        mm.then_inc(sem, 1)

                def begin(n, i, b):
                    project(n, ("k", "q", "f", "ga"))

                def finish(n, i, b):
                    project(n, ("og", "v"))
                    head_sums(n, "ss", sig_done["sq"], n + 1, bufs["norm"][b], False)

                def head_sums(n, key, sem_in, count, src, last):
                    pe.wait_ge(sem_in, count)
                    dst, sem = slot_free(pe, n, key, last)
                    for c in range(C2):
                        mm = nc.tensor.matmul(dst[:, c, :], group_ones[:], src[:, c, :, :].rearrange("p x t -> p (x t)"),
                                              start=True, stop=True)
                    mm.then_inc(sem, 1)

                def sums(n, i, b, last=False):
                    head_sums(n, "mn", did["pool_products"], (n + 1) * 3, bufs["norm"][b], last)
                    head_sums(n, "nn", did["qk"], n + 1, bufs["sigq"][b], last)
                rounds(pe, begin, sums, finish, pass_over)

            @block.scalar
            def _(act):
                def tile(n, i, b):
                    buffers_free(act, i, b)

                    def read(key, out, func, done, frees):
                        src, sem = slot_full(act, n, key)
                        nc.scalar.activation(out, src[:] if key == "og" else planes(src[:]), func).then_inc(sig_done[done], 1)
                        if frees:
                            act.wait_ge(sig_done[done], n + 1)
                            act.sem_inc(sem, 1)
                    read("k", bufs["sigk"][b][:], ACT.Sigmoid, "sigk", False)
                    read("q", bufs["sigq"][b][:], ACT.Sigmoid, "sigq", False)
                    read("f", bufs["f"][b][:], ACT.Sigmoid, "f", True)
                    read("ga", bufs["sg"][b][:], ACT.Sigmoid, "sg", True)
                    read("og", G[:, :, ds(n * NT, NT)], ACT.Sigmoid, "og", True)
                    act.wait_ge(did["k"], n + 1)
                    nc.scalar.activation(bufs["norm"][b][:], bufs["k"][b][:], ACT.Square).then_inc(sig_done["sq"], 1)
                    read("v", bufs["v"][b][:], ACT.Copy, "v", True)
                    act.wait_ge(did["clamp"], n + 1)
                    norm = bufs["norm"][b][:]
                    nc.scalar.activation(norm, norm, ACT.Ln, scale=2.0 ** LOG_SCALE).then_inc(sig_done["ln"], 1)
                    act.wait_ge(sig_done["ln"], n + 1)
                    nc.scalar.activation(norm, norm, ACT.Exp, scale=-0.5, bias=norm_bias[:, 0:1]).then_inc(sig_done["norm"], 1)

                with act.Fori(0, TILES // 2) as i:
                    for b in range(2):
                        tile(i * 2 + b, i, b)

            @block.vector
            def _(dve):
                nc.vector.memset(epsb[:], EPS)
                nc.vector.memset(norm_bias[:], 0.5 * LOG_SCALE * float(np.log(2.0)))
                dve.wait_ge(loaded, 16 * 10)
                nc.vector.tensor_copy(W["Wga"][:].rearrange("p c (h k) -> p c h k", k=HD),
                                      wgamma[:].unsqueeze(3).to_broadcast([P, C2, HEADS, HD])).then_inc(folded, 1)
                for c in range(C2):
                    nc.vector.tensor_scalar(Wo[:, c, :], Wo[:, c, :], norm_w[:, c:c + 1], None, ALU.mult).then_inc(folded, 1)
                dve.wait_ge(fold_psum, 1)
                nc.vector.tensor_copy(W["Wf"][:], slot[0][:, :, 0:D]).then_inc(folded, 1)
                nc.vector.tensor_copy(W["Wog"][:], slot[1][:, :, 0:D]).then_inc(folded, 1)
                dve.wait_ge(folded, 5)
                for s in range(4):
                    dve.sem_inc(free[s], 1)
                dve.sem_inc(weights_ready, 1)

                def keys(n, i, b):
                    buffers_free(dve, i, b)
                    for key in ("k", "q"):
                        dve.wait_ge(sig_done["sig" + key], n + 1)
                        src, sem = slot_full(dve, n, key)
                        nc.vector.tensor_tensor(bufs[key][b][:], planes(src[:]), bufs["sig" + key][b][:], ALU.mult).then_inc(did[key], 1)
                        dve.wait_ge(did[key], n + 1)
                        dve.sem_inc(sem, 1)

                def norms(n, i, b):
                    nrm = bufs["norm"][b][:]
                    src, sem = slot_full(dve, n, "ss")
                    nc.vector.tensor_scalar(nrm, src[:].rearrange("p c (x t) -> p c x t", x=BL), 1e-24, None,
                                            ALU.max).then_inc(did["clamp"], 1)
                    dve.wait_ge(did["clamp"], n + 1)
                    dve.sem_inc(sem, 1)
                    dve.wait_ge(sig_done["norm"], n + 1)
                    nc.vector.tensor_tensor(bufs["k"][b][:], bufs["k"][b][:], nrm, ALU.mult).then_inc(did["kn"], 1)
                    dve.wait_ge(did["kn"], n + 1)
                    dve.wait_ge(did["fff"], n + 1)
                    nc.vector.scalar_tensor_tensor(out=bufs["a"][b][:], in0=bufs["k"][b][:], scalar=-1.0,
                                                   in1=bufs["ff"][b][:], op0=ALU.mult, op1=ALU.mult).then_inc(did["a"], 1)

                def rows(n, i, b, last=False):
                    tt = nc.vector.tensor_tensor
                    a, v, f, Q, Wr = (bufs[x][b] for x in ("a", "v", "f", "sigk", "w"))
                    A0, V0, A1, V1 = a[:, :, 0, :], v[:, :, 0, :], bufs["sg"][b][:, :, 0, :], bufs["sg"][b][:, :, 1, :]
                    t0, t1 = tmp[:, :, 0, :], tmp[:, :, 1, :]
                    mn, mn_free = slot_full(dve, n, "mn", last)
                    m, n10 = mn[:, :, 0:HB], mn[:, :, HB:NT]
                    sm, sn = did["step_m"], did["step_n"]
                    dve.wait_ge(sig_done["v"], n + 1)
                    tt(A1, a[:, :, 1, :], f[:, :, 0, :], ALU.mult).then_inc(sm, 1)
                    tt(t0, m, A0, ALU.mult).then_inc(sm, 1)
                    tt(t1, m, V0, ALU.mult).then_inc(sm, 1)
                    dve.wait_ge(sm, n * 3 + 3)
                    tt(A1, A1, t0, ALU.add).then_inc(did["row_a"], 1)
                    tt(V1, v[:, :, 1, :], t1, ALU.add).then_inc(did["row_v"], 1)
                    dve.wait_ge(did["row_a"], n + 1)
                    dve.wait_ge(did["row_v"], n + 1)
                    nn, nn_free = slot_full(dve, n, "nn", last)
                    n00, n11 = nn[:, :, 0:HB], nn[:, :, HB:NT]
                    tt(t0, n00, A0, ALU.mult).then_inc(sn, 1)
                    tt(t1, n11, A1, ALU.mult).then_inc(sn, 1)
                    tt(Wr[:, :, 0, :], n00, V0, ALU.mult).then_inc(sn, 1)
                    tt(Wr[:, :, 1, :], n11, V1, ALU.mult).then_inc(sn, 1)
                    dve.wait_ge(did["q_begun"], (n + 1) * 2)
                    dve.wait_ge(sn, n * 7 + 2)
                    tt(Q[:], Q[:], tmp[:], ALU.add).then_inc(sn, 1)
                    dve.wait_ge(sn, n * 7 + 5)
                    tt(t0, n10, A0, ALU.mult).then_inc(sn, 1)
                    tt(t1, n10, V0, ALU.mult).then_inc(sn, 1)
                    dve.wait_ge(sn, n * 7 + 7)
                    dve.sem_inc(nn_free, 1)
                    dve.sem_inc(mn_free, 1)
                    tt(Q[:, :, 1, :], Q[:, :, 1, :], t0, ALU.add).then_inc(did["rows_q"], 1)
                    tt(Wr[:, :, 1, :], Wr[:, :, 1, :], t1, ALU.add).then_inc(did["rows_w"], 1)
                    dve.wait_ge(did["rows_w"], n + 1)
                rounds(dve, keys, rows, norms)

        with Phase(nc, "recB") as pb:
            SEG = 64
            GR = 8
            GPS = SEG // GR
            NSEG = SEQ // BL // SEG
            VH = HD // 2
            VQ = VH // 2
            CHAINS = 2
            R = [pb.sb(f"rows{b}", [P, HD, ROWS, SEG]) for b in range(2)]
            V = [pb.sb(f"v{b}", [P, VH, BL, SEG]) for b in range(2)]
            O = [pb.sb(f"o{b}", [P, VH, BL, SEG]) for b in range(2)]
            hist = [pb.sb(f"hist{b}", [P, GR, VH, HD]) for b in range(2)]
            U = [pb.sb(f"U{b}", [P, GR, 1 + BL, VH, HD + 1]) for b in range(2)]
            u = pb.sb("u", [P, BL, VH])
            prod = [pb.sb(f"prod{b}", [P, GR, BL, VH, HD]) for b in range(2)]
            ps_o = [pb.ps(f"ps_o{b}", [P, GR, BL, VH]) for b in range(2)]
            seg_loaded = [pb.sem(f"seg_loaded{b}") for b in range(2)]
            step = pb.sem("step")
            v_placed = pb.sem("v_placed")
            group_done = pb.sem("group_done")
            prod_done = pb.sem("prod_done")
            prod_half = pb.sem("prod_half")
            summed = pb.sem("summed")
            prod_free = pb.sem("prod_free")
            sums_read = pb.sem("sums_read")
            out_done = pb.sem("out_done")
            out_stored = [pb.sem(f"out_stored{b}") for b in range(2)]
            block = pb.block()
            PARTS = 2 * BATCH
            LOADS = 16 * 2 * PARTS
            STORED = 16 * PARTS

            def loads(sp, s, b):
                for bt in range(BATCH):
                    for vh in range(2):
                        p0 = bt * 32 + vh * 16
                        t = ds(s * SEG + bt * (SEQ // BL), SEG)
                        sp.dma_start(R[b][p0:p0 + 16].rearrange("h c x t -> h (c x) t"),
                                     rows_dram.rearrange("(h c) x t -> h (c x) t", c=HD)[:, :, t]).then_inc(seg_loaded[b], 16)
                        src = v_dram.rearrange("(h y c) x t -> h y (c x) t", c=VH, y=2)[:, vh, :, t]
                        sp.dma_start(V[b][p0:p0 + 16].rearrange("h c x t -> h (c x) t"), src).then_inc(seg_loaded[b], 16)

            def stores(sp, s, b):
                for bt in range(BATCH):
                    for vh in range(2):
                        p0 = bt * 32 + vh * 16
                        t = ds(s * SEG + bt * (SEQ // BL), SEG)
                        dst = o_dram.rearrange("(h y c) x t -> h y (c x) t", c=VH, y=2)[:, vh, :, t]
                        sp.dma_start(dst, O[b][p0:p0 + 16].rearrange("h c x t -> h (c x) t")).then_inc(out_stored[b], 16)

            @block.sync
            def _(sp):
                loads(sp, 0, 0)
                loads(sp, 1, 1)
                sp.sem_inc(out_stored[0], STORED)
                sp.sem_inc(out_stored[1], STORED)
                with sp.Fori(0, NSEG // 2 - 1) as i:
                    for b in range(2):
                        s = i * 2 + b
                        sp.wait_ge(out_done, (s + 1) * GPS)
                        stores(sp, s, b)
                        loads(sp, s + 2, b)
                for b in range(2):
                    s = NSEG - 2 + b
                    sp.wait_ge(out_done, (s + 1) * GPS)
                    stores(sp, s, b)
                for b in range(2):
                    sp.wait_ge(out_stored[b], STORED * (NSEG // 2 + 1))

            @block.scalar
            def _(act):
                act.sem_inc(sums_read, 2)
                with act.Fori(0, NSEG // 2) as i:
                    for b in range(2):
                        with act.Fori(0, GPS // 2) as g:
                            for par in range(2):
                                n = i * (2 * GPS) + g * 2 + (b * GPS + par)
                                act.wait_ge(out_stored[b], (i + 1) * STORED)
                                act.wait_ge(summed, n + 1)
                                t = ds(g * (2 * GR) + par * GR, GR)
                                nc.scalar.activation(O[b][:, :, :, t].rearrange("p v x t -> p t x v"), ps_o[par][:],
                                                     ACT.Copy).then_inc(out_done, 1)
                                act.wait_ge(out_done, n + 1)
                                act.sem_inc(sums_read, 1)

            @block.tensor
            def _(pe):
                pe.sem_inc(prod_free, 2)
                with pe.Fori(0, NSEG * GPS // 2) as i:
                    for par in range(2):
                        n = i * 2 + par
                        pe.wait_ge(prod_done, n + 3)
                        pe.wait_ge(sums_read, n + 1)
                        for k in range(HD):
                            mm = nc.tensor.matmul(ps_o[par][:].rearrange("p g x v -> p (g x v)"), ident[:],
                                                  prod[par][:].rearrange("p g x v k -> p (g x v) k")[:, :, k],
                                                  start=(k == 0), stop=(k == HD - 1))
                        mm.then_inc(summed, 1)
                        pe.wait_ge(summed, n + 1)
                        pe.sem_inc(prod_free, 1)

            @block.vector
            def _(dve):
                nc.vector.memset(hist[0][:, 0, :, :], 0.0).then_inc(step, 1)
                dve.sem_inc(prod_done, 2)
                dve.wait_ge(step, 1)
                dve.sem_clear(step)
                OPS = 4 * CHAINS
                with dve.Fori(0, NSEG // 2) as i:
                    for b in range(2):
                        with dve.Fori(0, GPS // 2) as g:
                            for par in range(2):
                                n = i * (2 * GPS) + g * 2 + (b * GPS + par)
                                dve.wait_ge(seg_loaded[b], (i + 1) * LOADS)
                                dve.wait_ge(prod_done, n + 1)
                                nc.vector.tensor_copy(U[par][:, :, 1:1 + BL, :, HD],
                                                      V[b][:, :, :, ds(g * (2 * GR) + par * GR, GR)].rearrange("p v x t -> p t x v")
                                                      ).then_inc(v_placed, 1)
                                for j in range(GR):
                                    t = ds(g * (2 * GR) + (par * GR + j), 1)
                                    row = lambda x, num: R[b][:, :, x:x + num, t].rearrange("p k x t -> p x (k t)")
                                    last = j == GR - 1
                                    after = hist[1 - par][:, 0] if last else hist[par][:, j + 1]
                                    half = [slice(c * VQ, c * VQ + VQ) for c in range(CHAINS)]

                                    for c in range(CHAINS):
                                        if j:
                                            dve.wait_ge(step, j * OPS + (c - 1))
                                        nc.vector.tensor_tensor(U[par][:, j, :, half[c], 0:HD],
                                                                hist[par][:, j, half[c], :].unsqueeze(1).to_broadcast([P, 1 + BL, VQ, HD]),
                                                                row(ROW_F, 1 + BL).unsqueeze(2).to_broadcast([P, 1 + BL, VQ, HD]),
                                                                ALU.mult).then_inc(step, 1)
                                    if j == 0:
                                        dve.wait_ge(v_placed, n + 1)
                                    for c in range(CHAINS):
                                        dve.wait_ge(step, j * OPS + CHAINS + (c - 1))
                                        nc.vector.tensor_reduce(u[:, :, half[c]], U[par][:, j, 1:1 + BL, half[c], :], AX.X,
                                                                ALU.add).then_inc(step, 1)
                                    if last:
                                        dve.wait_ge(prod_done, n + 2)
                                    for c in range(CHAINS):
                                        dve.wait_ge(step, j * OPS + 2 * CHAINS + (c - 1))
                                        nc.vector.tensor_tensor(U[par][:, j, 1:1 + BL, half[c], 0:HD],
                                                                u[:, :, half[c]].unsqueeze(3).to_broadcast([P, BL, VQ, HD]),
                                                                row(ROW_K, BL).unsqueeze(2).to_broadcast([P, BL, VQ, HD]),
                                                                ALU.mult).then_inc(step, 1)
                                    for c in range(CHAINS):
                                        dve.wait_ge(step, j * OPS + 3 * CHAINS + (c - 1))
                                        nc.vector.tensor_reduce(after[:, half[c], :], U[par][:, j, :, half[c], 0:HD].rearrange("p x v k -> p v k x"),
                                                                AX.X, ALU.add).then_inc(step, 1)
                                dve.wait_ge(step, GR * OPS)
                                dve.sem_clear(step)
                                dve.sem_inc(group_done, 1)

            @block.gpsimd
            def _(pool):
                with pool.Fori(0, NSEG // 2) as i:
                    for b in range(2):
                        with pool.Fori(0, GPS // 2) as g:
                            for par in range(2):
                                n = i * (2 * GPS) + g * 2 + (b * GPS + par)
                                pool.wait_ge(seg_loaded[b], (i + 1) * LOADS)
                                pool.wait_ge(group_done, n + 1)
                                pool.wait_ge(prod_free, n + 1)
                                t = ds(g * (2 * GR) + par * GR, GR)
                                for x in range(BL):
                                    q = R[b][:, :, ROW_Q + x, t].rearrange("p k t -> p t k")
                                    mul = nc.gpsimd.tensor_tensor(prod[par][:, :, x], hist[par][:],
                                                                  q.unsqueeze(2).to_broadcast([P, GR, VH, HD]), ALU.mult)
                                    mul.then_inc(prod_done if x else prod_half, 1)

        with Phase(nc, "recC") as pc:
            pair = lambda name, shape: [pc.sb(f"{name}{b}", shape) for b in range(2)]
            O, WR = pair("o", [P, C2, BL, HB]), pair("w", [P, C2, BL, HB])
            OG, XC, SQ, R = (pair(n, [P, C2, NT]) for n in ("og", "xc", "sq", "r"))
            lnv, rstd = pair("lnv", [P, NT]), pair("rstd", [P, NT])
            ps_m, ps_v = ([pc.ps(f"{n}{b}", [P, NT]) for b in range(2)] for n in ("ps_m", "ps_v"))
            ps_o = [pc.ps(f"ps_o{b}", [P, C2, NT]) for b in range(2)]
            o_loaded = [pc.sem(f"o_loaded{b}") for b in range(2)]
            summed, og_done, mean_psum, centred, squared, var_psum = (
                pc.sem(n) for n in ("summed", "og_done", "mean_psum", "centred", "squared", "var_psum"))
            ln_done, rstd_done, on_done, o_psum, resid, x_done = (
                pc.sem(n) for n in ("ln_done", "rstd_done", "on_done", "o_psum", "resid", "x_done"))
            block = pc.block()

            norm_no = lambda i, which, b: i * 4 + (which * 2 + b + 1)
            tile_no = lambda i, b: i * 2 + (b + 1)

            @block.sync
            def _(sp):
                def load(n, b):
                    for dst, dram in ((O[b], o_dram), (WR[b], w_dram)):
                        for x in range(BL):
                            sp.dma_start(dst[:, :, x, :], dram.rearrange("(c p) x t -> p c x t", p=P)[:, :, x, ds(n * HB, HB)]).then_inc(o_loaded[b], 16)
                for b in range(2):
                    load(b, b)
                with sp.Fori(0, TILES // 2 - 1) as i:
                    for b in range(2):
                        sp.wait_ge(og_done, tile_no(i, b))
                        load(i * 2 + (b + 2), b)

            @block.gpsimd
            def _(pool):
                with pool.Fori(0, TILES // 2) as i:
                    for b in range(2):
                        pool.wait_ge(o_loaded[b], (i + 1) * 64)
                        nc.gpsimd.tensor_tensor(O[b][:], O[b][:], WR[b][:], ALU.add).then_inc(summed, 1)

            @block.tensor
            def _(pe):
                def means(i, which):
                    for b in range(2):
                        pe.wait_ge(resid if which else og_done, tile_no(i, b))
                        for c in range(C2):
                            mm = nc.tensor.matmul(ps_m[b][:], ones_mean[:], (R if which else OG)[b][:, c, :], start=(c == 0), stop=(c == C2 - 1))
                        mm.then_inc(mean_psum, 1)
                    for b in range(2):
                        pe.wait_ge(squared, norm_no(i, which, b))
                        for c in range(C2):
                            mm = nc.tensor.matmul(ps_v[b][:], ones_mean[:], SQ[b][:, c, :], start=(c == 0), stop=(c == C2 - 1))
                        mm.then_inc(var_psum, 1)

                with pe.Fori(0, TILES // 2) as i:
                    means(i, 0)
                    for b in range(2):
                        pe.wait_ge(on_done, tile_no(i, b))
                        for c in range(C2):
                            for kk in range(C2):
                                mm = nc.tensor.matmul(ps_o[b][:, c, :], Wo[:, kk, P * c:P * c + P], XC[b][:, kk, :],
                                                      start=(kk == 0), stop=(kk == C2 - 1))
                        mm.then_inc(o_psum, 1)
                    means(i, 1)

            @block.scalar
            def _(act):
                with act.Fori(0, TILES // 2) as i:
                    for which in range(2):
                        for b in range(2):
                            act.wait_ge(centred, norm_no(i, which, b))
                            nc.scalar.activation(SQ[b][:], XC[b][:], ACT.Square).then_inc(squared, 1)
                        for b in range(2):
                            act.wait_ge(var_psum, norm_no(i, which, b))
                            nc.scalar.activation(lnv[b][:], ps_v[b][:], ACT.Ln, bias=epsb[:, 0:1]).then_inc(ln_done, 1)
                            act.wait_ge(ln_done, norm_no(i, which, b))
                            nc.scalar.activation(rstd[b][:], lnv[b][:], ACT.Exp, scale=-0.5).then_inc(rstd_done, 1)

            @block.vector
            def _(dve):
                bc = lambda ap: ap.unsqueeze(1).to_broadcast([P, C2, NT])

                def centre(i, which, b, src):
                    dve.wait_ge(mean_psum, norm_no(i, which, b))
                    nc.vector.tensor_tensor(XC[b][:], src, bc(ps_m[b][:]), ALU.subtract).then_inc(centred, 1)

                def scale(i, which, b, dst, done):
                    dve.wait_ge(centred, norm_no(i, which, b))
                    dve.wait_ge(rstd_done, norm_no(i, which, b))
                    nc.vector.tensor_tensor(dst, XC[b][:], bc(rstd[b][:]), ALU.mult).then_inc(done, 1)

                with dve.Fori(0, TILES // 2) as i:
                    tile = [X[:, :, ds((i * 2 + b) * NT, NT)] for b in range(2)]
                    for b in range(2):
                        dve.wait_ge(summed, tile_no(i, b))
                        g = G[:, :, ds((i * 2 + b) * NT, NT)].rearrange("p c (t x) -> p c x t", x=BL)
                        nc.vector.tensor_tensor(OG[b][:].rearrange("p c (t x) -> p c x t", x=BL), O[b][:], g, ALU.mult).then_inc(og_done, 1)
                    for b in range(2):
                        dve.wait_ge(og_done, tile_no(i, b))
                        centre(i, 0, b, OG[b][:])
                    for b in range(2):
                        scale(i, 0, b, XC[b][:], on_done)
                    for b in range(2):
                        dve.wait_ge(o_psum, tile_no(i, b))
                        nc.vector.tensor_tensor(R[b][:], ps_o[b][:], tile[b], ALU.add).then_inc(resid, 1)
                    for b in range(2):
                        dve.wait_ge(resid, tile_no(i, b))
                        centre(i, 1, b, R[b][:])
                    for b in range(2):
                        scale(i, 1, b, tile[b], x_done)


def cross_attention_stage(nc, X, ones_mean, ident, w, gated):
    HEADS, DH, KEYS = 16, D // 16, 64
    HC = HEADS // C2
    PAIRS = HEADS // 2
    PC = PAIRS // C2
    CT = BATCH * KEYS
    CHUNKS = NT // P
    pre = "L0_xattn" if gated else "L1_xattn"
    with Phase(nc, "xg" if gated else "xp") as ph:
        names = ["Wq", "Wk", "Wv", "Wo"] + (["Wg"] if gated else [])
        W = {n: ph.sb(n, [P, C2, D]) for n in names}
        vecs = (["qln_g", "qln_b", "kvln_g", "kvln_b", "bg"] if gated else ["bq", "bk", "bv", "bo"])
        V = {n: ph.sb(n, [P, C2]) for n in vecs}
        bias = {n: ph.sb(f"bias_{n}", [P, C2]) for n in (["q", "k", "v", "g"] if gated else [])}
        if not gated:
            bias = {"q": V["bq"], "k": V["bk"], "v": V["bv"]}
        CTX = ph.sb("ctx", [P, C2, CT])
        CXC = ph.sb("ctx_centred", [P, C2, CT])
        CSQ = ph.sb("ctx_squared", [P, C2, CT])
        crstd = ph.sb("ctx_rstd", [P, CT])
        ctx2 = ph.sb("ctx2", [P, C2, BATCH, 2, KEYS])
        KT = ph.sb("KT", [P, C2, CT])
        head_mask = ph.sb("head_mask", [P, HC])
        pair_mask = ph.sb("pair_mask", [P, PC, P])
        VT = ph.sb("VT", [P, BATCH, D])
        kblk = ph.sb("kblk", [P, BATCH, C2, HC, KEYS])
        vblk = ph.sb("vblk", [P, PAIRS, P])
        epsb = ph.sb("epsb", [P, 1])
        N = ph.sb("normed", [P, C2, NT]) if gated else None
        G = [ph.sb(f"gate{t}", [P, C2, NT]) for t in range(2)] if gated else None
        QT = [ph.sb(f"QT{t}", [P, C2, NT]) for t in range(2)]
        MX = ph.sb("MX", [P, 2, HEADS])
        SUM = ph.sb("SUM", [P, 2, HEADS])
        RIN = ph.sb("RIN", [P, 2, HEADS])
        S = ph.sb("S", [P, 2, HEADS * KEYS])
        E = ph.sb("E", [P, 2, HEADS * KEYS])
        PN = ph.sb("PN", [P, 2, HEADS * KEYS])
        PT = ph.sb("PT", [P, PAIRS, NT])
        Y = ph.sb("Y", [P, C2, NT])
        R = ph.sb("R", [P, C2, NT])
        XC, SQ = ([ph.sb(f"{n}{x}", [P, C2, NT]) for x in range(2)] for n in ("XC", "SQ"))
        rstd = [ph.sb(f"rstd{x}", [P, NT]) for x in range(2)]
        ps_s = [ph.ps(f"ps_s{b}", [P, HEADS * KEYS]) for b in range(2)]
        ps_t = ph.ps("ps_t", [P, PAIRS, P])
        bank = [ph.ps(f"bank{b}", [P, NT]) for b in range(2)]
        loaded = ph.sem("loaded")
        masks_done = ph.sem("masks_done")
        prep = ph.sem("prep")
        full = [ph.sem(f"bank_full{b}") for b in range(2)]
        free = [ph.sem(f"bank_free{b}") for b in range(2)]
        ctx_squared = ph.sem("ctx_squared_done")
        ctx_std = ph.sem("ctx_std")
        ctx_ready, ctx2_ready, kv_copied, k_ready, v_ready = (
            ph.sem(n) for n in ("ctx_ready", "ctx2_ready", "kv_copied", "k_ready", "v_ready"))
        centred, squared, ln_done, rstd_done = ([ph.sem(f"{n}{x}") for x in range(2)]
                                                for n in ("centred", "squared", "ln_done", "rstd_done"))
        normed, q_ready, g_ready, y_ready, resid, x_done = (
            ph.sem(n) for n in ("normed", "q_ready", "g_ready", "y_ready", "resid", "x_done"))
        scores, max_done, shifted, exp_done, sum_done, rinv_done, norm_done, turned, pt_ready = (
            ph.sem(n) for n in ("scores", "max_done", "shifted", "exp_done", "sum_done", "rinv_done", "norm_done",
                                "turned", "pt_ready"))
        block = ph.block()

        begin = [("k", 0), ("k", 1)] + [("v", bt) for bt in range(BATCH)]
        if gated:
            begin = ["cmean", "cvar"] + [("bias", v, c) for v in "qkvg" for c in range(C2)] + begin
        nq = [("q", 0), ("q", 1)] + ([("g", 0), ("g", 1)] if gated else [])
        m1, s1 = (["m0"], ["s0"]) if gated else ([], [])
        y, o = [("y", 0), ("y", 1)], [("o", 0), ("o", 1)]
        ORDER = {"begin": begin + m1 + s1 + nq, "first": m1 + s1 + nq, "mid": m1 + s1 + y + o + ["m1"] + nq + ["s1"],
                 "last": y + o + ["m1", "s1"], "end": y + o + ["m1", "s1"]}
        assert len(ORDER["mid"]) % 2 == 0
        PER = len(ORDER["mid"]) // 2
        use, seen = {}, 0
        for sec in ("begin", "first", "mid", "last", "end"):
            for key in ORDER[sec]:
                use[sec, key] = (seen % 2, seen // 2 + 1)
                seen += 1
            if sec == "mid":
                seen += (TILES - 3) * len(ORDER["mid"])

        def at(sec, n, key):
            k, count = use[sec, key]
            return k, ((n - 1) * PER + count if sec == "mid" else count)

        def wait_free(pe, sec, n, key):
            k, count = at(sec, n, key)
            pe.wait_ge(free[k], count)
            return bank[k], full[k]

        def wait_full(eng, sec, n, key):
            k, count = at(sec, n, key)
            eng.wait_ge(full[k], count)
            return bank[k], free[k]

        def tiles(eng, begin, body, end):
            begin()
            body("first", 0, 0, 0)
            with eng.Fori(0, TILES // 2 - 1) as i:
                body("mid", i * 2 + 1, 1, i)
                body("mid", i * 2 + 2, 0, i + 1)
            body("last", TILES - 1, 1, BATCH - 1)
            end()

        has_post = lambda sec: sec != "first"
        has_next = lambda sec: sec != "last"
        tile_x = lambda n: X[:, :, ds(n * NT, NT)]
        spread = lambda ap: ap.unsqueeze(1).to_broadcast([P, C2, NT])
        by_head = lambda ap: ap.rearrange("p (h k) -> p h k", h=HEADS)

        @block.sync
        def _(sp):
            for n in names:
                sp.dma_start(W[n][:], w[f"{pre}_{n}"].rearrange("(c p) o -> p c o", p=P)).then_inc(loaded, 16)
            for n in vecs:
                sp.dma_start(V[n][:], w[f"{pre}_{n}"]).then_inc(loaded, 16)
            sp.dma_start(CTX[:], w["ctx_1024"].rearrange("(c p) t -> p c t", p=P)).then_inc(loaded, 16)
        LOADED = 16 * (len(names) + len(vecs) + 1)
        kv_src = CXC if gated else CTX

        @block.gpsimd
        def _(pool):
            nc.gpsimd.memset(head_mask[:], 1.0).then_inc(masks_done, 1)
            pool.wait_ge(masks_done, 1)
            nc.gpsimd.affine_select(out=head_mask[:], in_=head_mask[:], compare_op=ALU.is_ge, fill=0.0, base=0,
                                    pattern=[[-DH, HC]], channel_multiplier=1).then_inc(masks_done, 1)
            pool.wait_ge(masks_done, 2)
            nc.gpsimd.affine_select(out=head_mask[:], in_=head_mask[:], compare_op=ALU.is_ge, fill=0.0, base=DH - 1,
                                    pattern=[[DH, HC]], channel_multiplier=-1).then_inc(masks_done, 1)
            nc.gpsimd.memset(pair_mask[:], 0.0).then_inc(masks_done, 1)
            pool.wait_ge(masks_done, 4)
            for hh in range(2):
                for j in range(PC):
                    f0 = DH * (2 * j + hh)
                    nc.gpsimd.memset(pair_mask[KEYS * hh:KEYS * hh + KEYS, j, f0:f0 + DH], 1.0).then_inc(masks_done, 1)

            def body(sec, n, par, bt):
                for k in range(CHUNKS):
                    g = n * CHUNKS + k
                    pool.wait_ge(rinv_done, g + 1)
                    if sec != "first" or k >= 2:
                        pool.wait_ge(turned, g - 1)
                    nc.gpsimd.tensor_tensor(by_head(PN[:, k % 2, :]), by_head(E[:, k % 2, :]),
                                            RIN[:, k % 2, :].unsqueeze(2).to_broadcast([P, HEADS, KEYS]),
                                            ALU.mult).then_inc(norm_done, 1)
            tiles(pool, lambda: None, body, lambda: None)

        @block.tensor
        def _(pe):
            pe.wait_ge(loaded, LOADED)

            def accumulate(dst, pairs):
                for n, (lhs, rhs) in enumerate(pairs):
                    mm = nc.tensor.matmul(dst, lhs, rhs, start=(n == 0), stop=(n == len(pairs) - 1))
                return mm

            def mean(sec, n, which, src):
                dst, sem = wait_free(pe, sec, n, f"m{which}")
                accumulate(dst[:], [(ones_mean[:], src[:, c, :]) for c in range(C2)]).then_inc(sem, 1)

            def var(sec, n, which, count):
                dst, sem = wait_free(pe, sec, n, f"s{which}")
                pe.wait_ge(squared[which], count)
                accumulate(dst[:], [(ones_mean[:], SQ[which][:, c, :]) for c in range(C2)]).then_inc(sem, 1)

            def queries(sec, n, nxt):
                if gated:
                    pe.wait_ge(normed, nxt + 1)
                rhs = N[:] if gated else tile_x(nxt)
                for v, c in nq:
                    dst, sem = wait_free(pe, sec, n, (v, c))
                    accumulate(dst[:], [(W["W" + v][:, kk, P * c:P * c + P], rhs[:, kk, :]) for kk in range(C2)]).then_inc(sem, 1)

            def values(sec, n, post, bt):
                pe.wait_ge(v_ready, bt + 1)
                pe.wait_ge(pt_ready, (post + 1) * CHUNKS)
                for c in range(C2):
                    dst, sem = wait_free(pe, sec, n, ("y", c))
                    accumulate(dst[:], [(vblk[:, PC * c + j, :], PT[:, PC * c + j, :]) for j in range(PC)]).then_inc(sem, 1)

            def outputs(sec, n, post):
                pe.wait_ge(y_ready, (post + 1) * C2)
                for c in range(C2):
                    dst, sem = wait_free(pe, sec, n, ("o", c))
                    accumulate(dst[:], [(W["Wo"][:, kk, P * c:P * c + P], Y[:, kk, :]) for kk in range(C2)]).then_inc(sem, 1)

            def mean_of_sum(sec, n, post):
                pe.wait_ge(resid, (post + 1) * C2)
                mean(sec, n, 1, R)

            def begin():
                if gated:
                    dst, sem = wait_free(pe, "begin", 0, "cmean")
                    accumulate(dst[:, 0:CT], [(ones_mean[:], CTX[:, c, :]) for c in range(C2)]).then_inc(sem, 1)
                    dst, sem = wait_free(pe, "begin", 0, "cvar")
                    pe.wait_ge(ctx_squared, 1)
                    accumulate(dst[:, 0:CT], [(ones_mean[:], CSQ[:, c, :]) for c in range(C2)]).then_inc(sem, 1)
                    for v in "qkvg":
                        for c in range(C2):
                            dst, sem = wait_free(pe, "begin", 0, ("bias", v, c))
                            lnb = V["kvln_b"] if v in "kv" else V["qln_b"]
                            accumulate(dst[:, 0:1], [(W["W" + v][:, kk, P * c:P * c + P], lnb[:, kk:kk + 1])
                                                     for kk in range(C2)]).then_inc(sem, 1)
                pe.wait_ge(ctx_ready, 1)
                for c in range(C2):
                    dst, sem = wait_free(pe, "begin", 0, ("k", c))
                    accumulate(dst[:, 0:CT], [(W["Wk"][:, kk, P * c:P * c + P], kv_src[:, kk, :]) for kk in range(C2)]).then_inc(sem, 1)
                pe.wait_ge(ctx2_ready, 1)
                for bt in range(BATCH):
                    dst, sem = wait_free(pe, "begin", 0, ("v", bt))
                    accumulate(dst[:, 0:D], [(ctx2[:, kk, bt, :, :], W["Wv"][:, kk, :]) for kk in range(C2)]).then_inc(sem, 1)
                if gated:
                    mean("begin", 0, 0, tile_x(0))
                    var("begin", 0, 0, 1)
                queries("begin", 0, 0)
                pe.wait_ge(k_ready, BATCH)

            def body(sec, n, par, bt):
                post, nxt = n - 1, n + 1
                pe.wait_ge(q_ready, (n + 1) * C2)

                def score(k):
                    if sec != "first" or k >= 2:
                        pe.wait_ge(shifted, n * CHUNKS + k - 1)
                    for c in range(C2):
                        mm = nc.tensor.matmul(ps_s[k % 2][:, 512 * c:512 * c + 512], QT[par][:, c, P * k:P * k + P],
                                              kblk[:, ds(bt, 1), c, :, :].rearrange("p b h k -> p (b h k)"), start=True, stop=True)
                    mm.then_inc(scores, 1)

                def turn(k):
                    pe.wait_ge(norm_done, n * CHUNKS + k + 1)
                    if sec != "first" or k >= 1:
                        pe.wait_ge(pt_ready, n * CHUNKS + k)
                    for j in range(PAIRS):
                        mm = nc.tensor.transpose(ps_t[:, j, :], PN[:, k % 2, P * j:P * j + P], ident[:])
                    mm.then_inc(turned, 1)

                score(0)
                if has_post(sec):
                    turn(-2)
                if gated and has_next(sec):
                    mean(sec, n, 0, tile_x(nxt))
                score(1)
                if has_post(sec):
                    turn(-1)
                if gated and has_next(sec):
                    var(sec, n, 0, nxt + 1)
                score(2)
                if has_post(sec):
                    values(sec, n, post, bt if par else bt - 1)
                turn(0)
                score(3)
                if has_post(sec):
                    outputs(sec, n, post)
                turn(1)
                if has_post(sec):
                    mean_of_sum(sec, n, post)
                if has_next(sec):
                    queries(sec, n, nxt)
                if has_post(sec):
                    var(sec, n, 1, post + 1)
                if sec == "last":
                    turn(2)
                    turn(3)

            def end():
                post = TILES - 1
                values("end", 0, post, BATCH - 1)
                outputs("end", 0, post)
                mean_of_sum("end", 0, post)
                var("end", 0, 1, post + 1)
            tiles(pe, begin, body, end)

        @block.scalar
        def _(act):
            act.wait_ge(loaded, LOADED)
            act.sem_inc(free[0], 1)
            act.sem_inc(free[1], 1)

            def square(which, count):
                act.wait_ge(centred[which], count)
                nc.scalar.activation(SQ[which][:], XC[which][:], ACT.Square).then_inc(squared[which], 1)

            def root(sec, n, which, count):
                src, sem = wait_full(act, sec, n, f"s{which}")
                nc.scalar.activation(rstd[which][:], src[:], ACT.Ln, bias=epsb[:, 0:1]).then_inc(ln_done[which], 1)
                act.wait_ge(ln_done[which], count)
                act.sem_inc(sem, 1)
                nc.scalar.activation(rstd[which][:], rstd[which][:], ACT.Exp, scale=-0.5).then_inc(rstd_done[which], 1)

            def queries(sec, n, nxt, par):
                for v, c in nq:
                    src, sem = wait_full(act, sec, n, (v, c))
                    dst, func, done = ((QT, ACT.Identity, q_ready) if v == "q" else (G, ACT.Sigmoid, g_ready))
                    nc.scalar.activation(dst[par][:, c, :], src[:], func, bias=bias[v][:, c:c + 1]).then_inc(done, 1)
                    act.wait_ge(done, nxt * C2 + (c + 1))
                    act.sem_inc(sem, 1)

            def begin():
                if gated:
                    act.wait_ge(prep, 2)
                    nc.scalar.activation(CSQ[:], CXC[:], ACT.Square).then_inc(ctx_squared, 1)
                    src, sem = wait_full(act, "begin", 0, "cvar")
                    nc.scalar.activation(crstd[:], src[:, 0:CT], ACT.Ln, bias=epsb[:, 0:1]).then_inc(ctx_std, 1)
                    act.wait_ge(ctx_std, 1)
                    act.sem_inc(sem, 1)
                    nc.scalar.activation(crstd[:], crstd[:], ACT.Exp, scale=-0.5).then_inc(ctx_std, 1)
                act.wait_ge(ctx_ready, 1)
                for c in range(C2):
                    src, sem = wait_full(act, "begin", 0, ("k", c))
                    nc.scalar.activation(KT[:, c, :], src[:, 0:CT], ACT.Identity, bias=bias["k"][:, c:c + 1]).then_inc(kv_copied, 1)
                    act.wait_ge(kv_copied, c + 1)
                    act.sem_inc(sem, 1)
                for bt in range(BATCH):
                    src, sem = wait_full(act, "begin", 0, ("v", bt))
                    nc.scalar.activation(VT[:, bt, :], src[:, 0:D], ACT.Copy).then_inc(kv_copied, 1)
                    act.wait_ge(kv_copied, C2 + bt + 1)
                    act.sem_inc(sem, 1)
                if gated:
                    square(0, 1)
                    root("begin", 0, 0, 1)
                queries("begin", 0, 0, 0)

            def body(sec, n, par, bt):
                post, nxt = n - 1, n + 1

                def exps(k):
                    act.wait_ge(shifted, n * CHUNKS + k + 1)
                    if sec != "first" or k >= 2:
                        act.wait_ge(norm_done, n * CHUNKS + k - 1)
                    nc.scalar.activation(E[:, k % 2, :], S[:, k % 2, :], ACT.Exp, scale=float(DH) ** -0.5).then_inc(exp_done, 1)

                def copies(k):
                    act.wait_ge(turned, n * CHUNKS + k + 1)
                    col = P * (k % CHUNKS)
                    nc.scalar.activation(PT[:, :, col:col + P], ps_t[:], ACT.Copy).then_inc(pt_ready, 1)

                exps(0)
                if has_post(sec):
                    copies(-2)
                if gated and has_next(sec):
                    square(0, nxt + 1)
                exps(1)
                if has_post(sec):
                    copies(-1)
                if gated and has_next(sec):
                    root(sec, n, 0, nxt + 1)
                exps(2)
                copies(0)
                exps(3)
                copies(1)
                if has_post(sec):
                    square(1, post + 1)
                if has_next(sec):
                    queries(sec, n, nxt, 1 - par)
                if has_post(sec):
                    root(sec, n, 1, post + 1)
                if sec == "last":
                    copies(2)
                    copies(3)

            def end():
                square(1, TILES)
                root("end", 0, 1, TILES)
            tiles(act, begin, body, end)

        @block.vector
        def _(dve):
            def centre(sec, n, which, count, data):
                src, sem = wait_full(dve, sec, n, f"m{which}")
                nc.vector.tensor_tensor(XC[which][:], data, spread(src[:]), ALU.subtract).then_inc(centred[which], 1)
                dve.wait_ge(centred[which], count)
                dve.sem_inc(sem, 1)

            def normalise(which, count, dst, done):
                dve.wait_ge(rstd_done[which], count)
                nc.vector.tensor_tensor(dst, XC[which][:], spread(rstd[which][:]), ALU.mult).then_inc(done, 1)

            def value_blocks(bt):
                for c in range(C2):
                    ins = nc.vector.tensor_tensor(vblk[:, PC * c:PC * c + PC, :],
                                                  VT[:, ds(bt, 1), P * c:P * c + P].to_broadcast([P, PC, P]),
                                                  pair_mask[:], ALU.mult)
                ins.then_inc(v_ready, 1)

            def values(sec, n, post, par):
                if gated:
                    dve.wait_ge(g_ready, (post + 1) * C2)
                for c in range(C2):
                    src, sem = wait_full(dve, sec, n, ("y", c))
                    if gated:
                        ins = nc.vector.scalar_tensor_tensor(out=Y[:, c, :], in0=src[:], scalar=bias["v"][:, c:c + 1],
                                                             in1=G[par][:, c, :], op0=ALU.add, op1=ALU.mult)
                    else:
                        ins = nc.vector.tensor_scalar(Y[:, c, :], src[:], bias["v"][:, c:c + 1], None, ALU.add)
                    ins.then_inc(y_ready, 1)
                    dve.wait_ge(y_ready, post * C2 + (c + 1))
                    dve.sem_inc(sem, 1)

            def outputs(sec, n, post):
                tile = tile_x(post)
                for c in range(C2):
                    src, sem = wait_full(dve, sec, n, ("o", c))
                    if gated:
                        ins = nc.vector.tensor_tensor(R[:, c, :], src[:], tile[:, c, :], ALU.add)
                    else:
                        ins = nc.vector.scalar_tensor_tensor(out=R[:, c, :], in0=src[:], scalar=V["bo"][:, c:c + 1],
                                                             in1=tile[:, c, :], op0=ALU.add, op1=ALU.add)
                    ins.then_inc(resid, 1)
                    dve.wait_ge(resid, post * C2 + (c + 1))
                    dve.sem_inc(sem, 1)

            def begin():
                nc.vector.memset(epsb[:], EPS).then_inc(prep, 1)
                dve.wait_ge(prep, 1)
                dve.wait_ge(loaded, LOADED)
                if gated:
                    src, sem = wait_full(dve, "begin", 0, "cmean")
                    nc.vector.tensor_tensor(CXC[:], CTX[:], src[:, 0:CT].unsqueeze(1).to_broadcast([P, C2, CT]),
                                            ALU.subtract).then_inc(prep, 1)
                    dve.wait_ge(prep, 2)
                    dve.sem_inc(sem, 1)
                    dve.wait_ge(ctx_std, 2)
                    nc.vector.tensor_tensor(CXC[:], CXC[:], crstd[:].unsqueeze(1).to_broadcast([P, C2, CT]), ALU.mult).then_inc(prep, 1)
                    n = 3
                    for v in "qkvg":
                        for c in range(C2):
                            src, sem = wait_full(dve, "begin", 0, ("bias", v, c))
                            if v == "g":
                                ins = nc.vector.tensor_tensor(bias[v][:, c:c + 1], src[:, 0:1], V["bg"][:, c:c + 1], ALU.add)
                            else:
                                ins = nc.vector.tensor_copy(bias[v][:, c:c + 1], src[:, 0:1])
                            ins.then_inc(prep, 1)
                            n += 1
                            dve.wait_ge(prep, n)
                            dve.sem_inc(sem, 1)
                    for v in "qkvg":
                        lng = V["kvln_g"] if v in "kv" else V["qln_g"]
                        for c in range(C2):
                            nc.vector.tensor_scalar(W["W" + v][:, c, :], W["W" + v][:, c, :], lng[:, c:c + 1], None,
                                                    ALU.mult).then_inc(prep, 1)
                            n += 1
                    dve.wait_ge(prep, n)
                dve.sem_inc(ctx_ready, 1)
                for c in range(C2):
                    ins = nc.vector.tensor_copy(ctx2[:, c], kv_src[:, c, :].rearrange("p (b k) -> p b k", b=BATCH).unsqueeze(2)
                                                .to_broadcast([P, BATCH, 2, KEYS]))
                ins.then_inc(ctx2_ready, 1)
                dve.wait_ge(masks_done, 4 + 2 * PC)
                dve.wait_ge(kv_copied, C2)
                for bt in range(BATCH):
                    for c in range(C2):
                        ins = nc.vector.tensor_tensor(kblk[:, bt, c, :, :],
                                                      KT[:, c, KEYS * bt:KEYS * bt + KEYS].unsqueeze(1).to_broadcast([P, HC, KEYS]),
                                                      head_mask[:].unsqueeze(2).to_broadcast([P, HC, KEYS]), ALU.mult)
                    ins.then_inc(k_ready, 1)
                dve.wait_ge(kv_copied, C2 + BATCH)
                value_blocks(0)
                if gated:
                    centre("begin", 0, 0, 1, tile_x(0))
                    normalise(0, 1, N[:], normed)

            def body(sec, n, par, bt):
                post, nxt = n - 1, n + 1

                def shift(k):
                    g = n * CHUNKS + k
                    ps3 = by_head(ps_s[k % 2][:])
                    dve.wait_ge(scores, g + 1)
                    nc.vector.tensor_reduce(MX[:, k % 2, :], ps3, AX.X, ALU.max).then_inc(max_done, 1)
                    dve.wait_ge(max_done, g + 1)
                    if sec != "first" or k >= 2:
                        dve.wait_ge(exp_done, g - 1)
                    nc.vector.tensor_tensor(by_head(S[:, k % 2, :]), ps3, MX[:, k % 2, :].unsqueeze(2).to_broadcast([P, HEADS, KEYS]),
                                            ALU.subtract).then_inc(shifted, 1)

                def invert(k):
                    g = n * CHUNKS + k
                    dve.wait_ge(exp_done, g + 1)
                    nc.vector.tensor_reduce(SUM[:, k % 2, :], by_head(E[:, k % 2, :]), AX.X, ALU.add).then_inc(sum_done, 1)
                    dve.wait_ge(sum_done, g + 1)
                    if sec != "first" or k >= 2:
                        dve.wait_ge(norm_done, g - 1)
                    nc.vector.reciprocal(RIN[:, k % 2, :], SUM[:, k % 2, :]).then_inc(rinv_done, 1)

                shift(0)
                if has_post(sec):
                    invert(-1)
                if gated and has_next(sec):
                    centre(sec, n, 0, nxt + 1, tile_x(nxt))
                shift(1)
                invert(0)
                if gated and has_next(sec):
                    normalise(0, nxt + 1, N[:], normed)
                shift(2)
                invert(1)
                if has_post(sec):
                    values(sec, n, post, 1 - par)
                shift(3)
                invert(2)
                if has_post(sec):
                    outputs(sec, n, post)
                    centre(sec, n, 1, post + 1, R[:])
                if sec == "last":
                    invert(3)
                if has_post(sec):
                    normalise(1, post + 1, tile_x(post), x_done)
                    if par == 0:
                        value_blocks(bt)

            def end():
                post = TILES - 1
                values("end", 0, post, 1)
                outputs("end", 0, post)
                centre("end", 0, 1, post + 1, R[:])
                normalise(1, post + 1, tile_x(post), x_done)
            tiles(dve, begin, body, end)


def expert_stage(nc, X, ones_mean, ident, w, sorted_in, sorted_out, zeros_written):
    EX, FF = 8, 1024
    KF = FF // P
    CH = TOK // P
    TC = NT // P
    BLOCKS = (TOK + EX * (P - 1)) // P
    BLOCKS += BLOCKS % 2
    with Phase(nc, "moe") as ph:
        W1 = ph.sb("W1", [P, EX, C2, FF])
        W2 = ph.sb("W2", [P, EX, KF, D])
        XTM = ph.sb("x_tokens", [P, CH, D])
        stage_buf = ph.sb("stage_buf", [P, 2 * NT])
        XS = stage_buf[:].rearrange("p (c t) -> p c t", c=C2)
        NTM = stage_buf[:].rearrange("p (r d) -> p r d", r=4)
        cent = ph.sb("cent", [P, C2, EX])
        stats = ph.sb("stats", [P, CH, 6])
        MV = ph.sb("mean_var", [P, CH, 2])
        std = ph.sb("std", [P, CH])
        rstd = ph.sb("rstd", [P, CH])
        alpha = ph.sb("alpha", [P, CH])
        pos = ph.sb("pos", [P, CH], I32)
        block_expert = ph.sb("block_expert", [P, BLOCKS], I32)
        ln_g = ph.sb("ln_g", [P, EX, C2])
        ln_b = ph.sb("ln_b", [P, EX, C2])
        b1 = ph.sb("b1", [P, EX, KF])
        epsb = ph.sb("epsb", [P, 1])
        ps_aff = ph.ps("ps_aff", [P, CH, EX])
        xf = X[:].rearrange("p c t -> p (c t)")
        w1_loaded = ph.sem("w1_loaded")
        w2_loaded = ph.sem("w2_loaded")
        small_loaded = ph.sem("small_loaded")
        b2_loaded = ph.sem("b2_loaded")

        with Phase(nc, "moeA") as pa:
            ps_x = [pa.ps(f"ps_x{b}", [P, TC, D]) for b in range(2)]
            staged = pa.sem("staged")
            turned = pa.sem("turned")
            copied = pa.sem("copied")
            stats_done = pa.sem("stats_done")
            block = pa.block()

            @block.sync
            def _(sp):
                sp.dma_start(cent[:], w["L0_ffn_centroids"].rearrange("(c p) e -> p c e", p=P)).then_inc(small_loaded, 16)
                sp.dma_start(ln_g[:], w["L0_ffn_ln_g"]).then_inc(small_loaded, 16)
                sp.dma_start(ln_b[:], w["L0_ffn_ln_b"]).then_inc(small_loaded, 16)
                sp.dma_start(b1[:], w["L0_ffn_b1"]).then_inc(small_loaded, 16)
                for e in range(EX):
                    sp.dma_start(W1[:, e, :, :], w["L0_ffn_w1"][e].rearrange("(c p) f -> p c f", p=P)).then_inc(w1_loaded, 16)
                for e in range(EX):
                    sp.dma_start(W2[:, e, :, :], w["L0_ffn_w2"][e].rearrange("(c p) f -> p c f", p=P)).then_inc(w2_loaded, 16)

            @block.scalar
            def _(act):
                act.sem_inc(turned, 1)
                act.sem_inc(copied, 2)
                with act.Fori(0, TILES // 2) as i:
                    for h in range(2):
                        n = i * 2 + h
                        act.wait_ge(turned, n + 1)
                        nc.scalar.activation(XS, X[:, :, ds(n * NT, NT)], ACT.Copy).then_inc(staged, 1)
                        act.wait_ge(turned, n + 2)
                        nc.scalar.activation(XTM[:, ds(n * TC, TC), :], ps_x[h][:], ACT.Copy).then_inc(copied, 1)

            @block.tensor
            def _(pe):
                pe.wait_ge(small_loaded, 16 * 4)
                with pe.Fori(0, TILES // 2) as i:
                    for h in range(2):
                        n = i * 2 + h
                        pe.wait_ge(staged, n + 1)
                        pe.wait_ge(copied, n + 1)
                        for k in range(TC):
                            for c in range(C2):
                                nc.tensor.transpose(ps_x[h][:, k, P * c:P * c + P], XS[:, c, P * k:P * k + P], ident[:])
                        for k in range(TC):
                            for c in range(C2):
                                mm = nc.tensor.matmul(ps_aff[:, ds(n * TC + k, 1), :].rearrange("p k e -> p (k e)"),
                                                      XS[:, c, P * k:P * k + P], cent[:, c, :],
                                                      start=(c == 0), stop=(c == C2 - 1))
                        mm.then_inc(turned, 1)

            @block.vector
            def _(dve):
                nc.vector.memset(epsb[:], EPS)
                with dve.Fori(0, TILES // 2) as i:
                    for h in range(2):
                        n = i * 2 + h
                        dve.wait_ge(copied, n + 3)
                        for k in range(TC):
                            ins = nc.vector.bn_stats(stats[:, ds(n * TC + k, 1), :].rearrange("p k s -> p (k s)"),
                                                     XTM[:, ds(n * TC + k, 1), :].rearrange("p k d -> p (k d)"))
                        ins.then_inc(stats_done, 1)
                dve.wait_ge(stats_done, TILES)
                for j in range(CH):
                    nc.vector.bn_aggr(MV[:, j, :], stats[:, j, :])

        with Phase(nc, "moeB") as pb:
            AFF, EQ, OH, SC0, SC1, ENDB = (xf[:, CH * EX * n:CH * EX * (n + 1)].rearrange("p (j e) -> p j e", e=EX)
                                           for n in range(6))
            rest = xf[:, CH * EX * 6:]
            MAXV, BEST, POSF = (rest[:, CH * n:CH * (n + 1)] for n in range(3))
            rest = rest[:, CH * 3:]
            CNT, NB, S1, S2, S3 = (rest[:, EX * n:EX * (n + 1)] for n in range(5))
            rest = rest[:, EX * 5:]
            BE = rest[:, 0:BLOCKS]
            rest = rest[:, BLOCKS:]
            GTS = rest[:, 0:EX * CH].rearrange("p (e m) -> p e m", e=EX)
            rest = rest[:, EX * CH:]
            LES = rest[:, 0:BLOCKS * EX].rearrange("p (m e) -> p m e", e=EX)
            rest = rest[:, BLOCKS * EX:]
            prefer = rest[:, 0:EX]
            chunk_edge = rest[:, EX:EX + CH]
            block_no = rest[:, EX + CH:EX + CH + BLOCKS]
            before = rest[:, EX + CH + BLOCKS:EX + CH + BLOCKS + P]
            ones = rest[:, EX + CH + BLOCKS + P:EX + CH + BLOCKS + 2 * P]
            ps_pre = pb.ps("ps_pre", [P, CH, EX])
            ps_tot = pb.ps("ps_tot", [P, CH, EX])
            consts = pb.sem("consts")
            step = pb.sem("step")
            onehot_done = pb.sem("onehot_done")
            counted = pb.sem("counted")
            std_done = pb.sem("std_done")
            alpha_done = pb.sem("alpha_done")
            normed = pb.sem("normed")
            pos_done = pb.sem("pos_done")
            scattered = [pb.sem(f"scattered{b}") for b in range(4)]
            block = pb.block()

            @block.sync
            def _(sp):
                sp.dma_start(xf[:, 6144:8192], w["L0_ffn_b2"].rearrange("e d -> (e d)").unsqueeze(0).to_broadcast([P, EX * D])).then_inc(b2_loaded, 16)

            @block.gpsimd
            def _(pool):
                nc.gpsimd.iota(prefer, pattern=[[-1, EX]], base=EX, channel_multiplier=0,
                               allow_small_or_imprecise_dtypes=True).then_inc(consts, 1)
                nc.gpsimd.iota(chunk_edge, pattern=[[P, CH]], base=0, channel_multiplier=0,
                               allow_small_or_imprecise_dtypes=True).then_inc(consts, 1)
                nc.gpsimd.iota(block_no, pattern=[[1, BLOCKS]], base=0, channel_multiplier=0,
                               allow_small_or_imprecise_dtypes=True).then_inc(consts, 1)
                nc.gpsimd.memset(ones, 1.0).then_inc(consts, 1)
                pool.wait_ge(consts, 4)
                nc.gpsimd.affine_select(out=before, in_=ones, compare_op=ALU.is_gt, fill=0.0, base=0,
                                        pattern=[[1, P]], channel_multiplier=-1).then_inc(consts, 1)
                pool.wait_ge(zeros_written, 16)
                pool.wait_ge(pos_done, 1)
                for j in range(CH):
                    pool.wait_ge(normed, j + 1)
                    nc.gpsimd.indirect_dma_start(sorted_in, bass.IndirectOffsetOnAxis(pos[:, j:j + 1], 0),
                                                 NTM[:, j % 4, :], None).then_inc(scattered[j % 4], 16)
                for b in range(4):
                    pool.wait_ge(scattered[b], 16 * CH // 4)

            @block.scalar
            def _(act):
                act.wait_ge(step, 1)
                nc.scalar.activation(std[:], MV[:, :, 1], ACT.Sqrt, bias=epsb[:, 0:1]).then_inc(std_done, 1)
                act.wait_ge(step, 2)
                nc.scalar.activation(alpha[:], MAXV, ACT.Sigmoid).then_inc(alpha_done, 1)

            @block.tensor
            def _(pe):
                pe.wait_ge(onehot_done, 1)
                oh = OH.rearrange("p j e -> p (j e)")
                nc.tensor.matmul(ps_pre[:].rearrange("p j e -> p (j e)"), before, oh, start=True, stop=True)
                nc.tensor.matmul(ps_tot[:].rearrange("p j e -> p (j e)"), ones, oh, start=True, stop=True).then_inc(counted, 1)

            @block.vector
            def _(dve):
                n = [0]

                def then(ins):
                    n[0] += 1
                    ins.then_inc(step, 1)
                    dve.wait_ge(step, n[0])

                dve.wait_ge(consts, 5)
                then(nc.vector.tensor_copy(AFF, ps_aff[:]))
                then(nc.vector.tensor_reduce(MAXV, AFF, AX.X, ALU.max))
                then(nc.vector.tensor_tensor(EQ, AFF, MAXV.unsqueeze(2).to_broadcast([P, CH, EX]), ALU.is_equal))
                then(nc.vector.tensor_tensor(EQ, EQ, prefer.unsqueeze(1).to_broadcast([P, CH, EX]), ALU.mult))
                then(nc.vector.tensor_reduce(BEST, EQ, AX.X, ALU.max))
                nc.vector.tensor_tensor(OH, EQ, BEST.unsqueeze(2).to_broadcast([P, CH, EX]), ALU.is_equal).then_inc(onehot_done, 1)
                dve.wait_ge(counted, 1)
                then(nc.vector.tensor_copy(SC0, ps_tot[:]))
                a, b, s = SC0, SC1, 1
                while s < CH:
                    nc.vector.tensor_copy(b[:, 0:s, :], a[:, 0:s, :])
                    then(nc.vector.tensor_tensor(b[:, s:, :], a[:, s:, :], a[:, 0:CH - s, :], ALU.add))
                    a, b, s = b, a, s * 2
                incl, tmp = a, b
                then(nc.vector.tensor_copy(CNT, incl[:, CH - 1, :]))
                then(nc.vector.tensor_tensor(GTS, CNT.unsqueeze(2).to_broadcast([P, EX, CH]),
                                             chunk_edge.unsqueeze(1).to_broadcast([P, EX, CH]), ALU.is_gt))
                then(nc.vector.tensor_reduce(NB, GTS, AX.X, ALU.add))
                a, b, s, other = NB, S1, 1, S2
                while s < EX:
                    nc.vector.tensor_copy(b[:, 0:s], a[:, 0:s])
                    then(nc.vector.tensor_tensor(b[:, s:], a[:, s:], a[:, 0:EX - s], ALU.add))
                    a, b, other, s = b, other, (a if a is not NB else S3), s * 2
                ends = a
                then(nc.vector.tensor_tensor(LES, ends.unsqueeze(1).to_broadcast([P, BLOCKS, EX]),
                                             block_no.unsqueeze(2).to_broadcast([P, BLOCKS, EX]), ALU.is_le))
                then(nc.vector.tensor_reduce(BE, LES, AX.X, ALU.add))
                then(nc.vector.tensor_scalar(block_expert[:], BE, float(EX - 1), None, ALU.min))
                then(nc.vector.tensor_tensor(CNT, ends, NB, ALU.subtract))
                then(nc.vector.tensor_scalar(CNT, CNT, float(P), None, ALU.mult))
                then(nc.vector.tensor_tensor(tmp, incl, ps_tot[:], ALU.subtract))
                then(nc.vector.tensor_tensor(tmp, tmp, ps_pre[:], ALU.add))
                then(nc.vector.tensor_tensor(tmp, tmp, CNT.unsqueeze(1).to_broadcast([P, CH, EX]), ALU.add))
                then(nc.vector.tensor_tensor(tmp, tmp, OH, ALU.mult))
                then(nc.vector.tensor_reduce(POSF, tmp, AX.X, ALU.add))
                nc.vector.tensor_copy(pos[:], POSF).then_inc(pos_done, 1)
                dve.wait_ge(std_done, 1)
                then(nc.vector.reciprocal(rstd[:], std[:]))
                for j in range(CH):
                    if j >= 4:
                        dve.wait_ge(scattered[j % 4], 16 * (j // 4))
                    nc.vector.tensor_scalar(NTM[:, j % 4, :], XTM[:, j, :], MV[:, j, 0:1], rstd[:, j:j + 1],
                                            ALU.subtract, ALU.mult).then_inc(normed, 1)

        with Phase(nc, "moeC") as pc:
            b2 = xf[:, 6144:8192].rearrange("p (e d) -> p e d", e=EX)
            rows = xf[:, 0:512].rearrange("p (b d) -> p b d", b=2)
            rowsT = xf[:, 512:1024].rearrange("p (b c t) -> p b c t", b=2, c=C2)
            hid = xf[:, 1024:3072].rearrange("p (b f) -> p b f", b=2)
            hidT = xf[:, 3072:5120].rearrange("p (b m t) -> p b m t", b=2, m=KF)
            yrow = xf[:, 5120:5632].rearrange("p (b d) -> p b d", b=2)
            ps_r = ps_aff[:].rearrange("p j e -> p (j e)").rearrange("p (c t) -> p c t", c=C2)
            ps_h = [pc.ps(f"ps_h{b}", [P, FF]) for b in range(2)]
            ps_t = pc.ps("ps_t", [P, KF, P])
            ps_y = pc.ps("ps_y", [P, D])
            row_loaded = [pc.sem(f"row_loaded{b}") for b in range(2)]
            row_turned = pc.sem("row_turned")
            rowT_ready = pc.sem("rowT_ready")
            h_psum = pc.sem("h_psum")
            h_copied = pc.sem("h_copied")
            h_turned = pc.sem("h_turned")
            bias_added = pc.sem("bias_added")
            relu_done = pc.sem("relu_done")
            y_psum = pc.sem("y_psum")
            y_done = pc.sem("y_done")
            y_stored = [pc.sem(f"y_stored{b}") for b in range(2)]
            block = pc.block()
            in_blk = sorted_in.rearrange("(m p) d -> m p d", p=P)
            out_blk = sorted_out.rearrange("(m p) d -> m p d", p=P)

            @block.sync
            def _(sp):
                for q in range(2):
                    sp.dma_start(rows[:, q, :], in_blk[q, :, :]).then_inc(row_loaded[q], 16)
                sp.sem_inc(y_stored[0], 16)
                sp.sem_inc(y_stored[1], 16)
                with sp.Fori(0, BLOCKS // 2 - 1) as i:
                    for q in range(2):
                        sp.wait_ge(row_turned, i * 2 + (q + 1))
                        sp.dma_start(rows[:, q, :], in_blk[ds(i * 2 + (q + 2), 1), :, :].rearrange("m p d -> (m p) d")).then_inc(row_loaded[q], 16)
                        sp.wait_ge(y_done, i * 2 + (q + 2))
                        sp.dma_start(out_blk[ds(i * 2 + q, 1), :, :].rearrange("m p d -> (m p) d"), yrow[:, q, :]).then_inc(y_stored[q], 16)
                for q in range(2):
                    sp.wait_ge(y_done, BLOCKS + q)
                    sp.dma_start(out_blk[BLOCKS - 2 + q, :, :], yrow[:, q, :]).then_inc(y_stored[q], 16)
                for q in range(2):
                    sp.wait_ge(y_stored[q], 16 * (BLOCKS // 2 + 1))

            @block.tensor
            def _(pe):
                pe.sem_inc(h_turned, 2)
                pe.wait_ge(w1_loaded, 16 * EX)
                pe.wait_ge(w2_loaded, 16 * EX)

                def expert(m):
                    return pe.value_load(block_expert[0:1, ds(m, 1)], min_val=0, max_val=EX - 1)

                def turn_rows(i, q):
                    m = i * 2 + q
                    pe.wait_ge(row_loaded[q], (i + 1) * 16)
                    pe.wait_ge(rowT_ready, m + 1)
                    for c in range(C2):
                        mm = nc.tensor.transpose(ps_r[:, c, :], rows[:, q, P * c:P * c + P], ident[:])
                    mm.then_inc(row_turned, 1)

                def up(i, q):
                    m = i * 2 + q
                    e = expert(m)
                    pe.wait_ge(rowT_ready, m + 2)
                    pe.wait_ge(h_copied, m + 1)
                    for n in range(FF // 512):
                        for c in range(C2):
                            mm = nc.tensor.matmul(ps_h[q][:, 512 * n:512 * n + 512], rowsT[:, q, c, :],
                                                  W1[:, ds(e, 1), c, 512 * n:512 * n + 512].rearrange("p e f -> p (e f)"),
                                                  start=(c == 0), stop=(c == C2 - 1))
                    mm.then_inc(h_psum, 1)

                def turn_hidden(i, q):
                    m = i * 2 + q
                    pe.wait_ge(h_copied, m + 3)
                    pe.wait_ge(bias_added, m + 1)
                    for k in range(KF):
                        mm = nc.tensor.transpose(ps_t[:, k, :], hid[:, q, P * k:P * k + P], ident[:])
                    mm.then_inc(h_turned, 1)

                def down(i, q):
                    m = i * 2 + q
                    e = expert(m)
                    pe.wait_ge(relu_done, m + 1)
                    pe.wait_ge(y_done, m + 1)
                    for k in range(KF):
                        mm = nc.tensor.matmul(ps_y[:], hidT[:, q, k, :],
                                              W2[:, ds(e, 1), k, :].rearrange("p e d -> p (e d)"),
                                              start=(k == 0), stop=(k == KF - 1))
                    mm.then_inc(y_psum, 1)

                turn_rows(0, 0)
                up(0, 0)
                turn_hidden(0, 0)
                with pe.Fori(0, BLOCKS // 2 - 1) as i:
                    turn_rows(i, 1)
                    up(i, 1)
                    down(i, 0)
                    turn_hidden(i, 1)
                    turn_rows(i + 1, 0)
                    up(i + 1, 0)
                    down(i, 1)
                    turn_hidden(i + 1, 0)
                turn_rows(BLOCKS // 2 - 1, 1)
                up(BLOCKS // 2 - 1, 1)
                down(BLOCKS // 2 - 1, 0)
                turn_hidden(BLOCKS // 2 - 1, 1)
                down(BLOCKS // 2 - 1, 1)

            @block.scalar
            def _(act):
                act.sem_inc(rowT_ready, 1)
                act.sem_inc(h_copied, 2)

                def rows_out(i, q):
                    e = act.value_load(block_expert[0:1, ds(i * 2 + q, 1)], min_val=0, max_val=EX - 1)
                    act.wait_ge(row_turned, i * 2 + (q + 1))
                    for c in range(C2):
                        ins = nc.scalar.activation(rowsT[:, q, c, :], ps_r[:, c, :], ACT.Identity,
                                                   scale=ln_g[:, ds(e, 1), c:c + 1].rearrange("p e c -> p (e c)"),
                                                   bias=ln_b[:, ds(e, 1), c:c + 1].rearrange("p e c -> p (e c)"))
                    ins.then_inc(rowT_ready, 1)

                def hidden_out(i, q):
                    m = i * 2 + q
                    act.wait_ge(h_psum, m + 1)
                    act.wait_ge(h_turned, m + 1)
                    nc.scalar.activation(hid[:, q, :], ps_h[q][:], ACT.Copy).then_inc(h_copied, 1)

                def relu(i, q):
                    act.wait_ge(bias_added, i * 2 + (q + 2))
                    nc.scalar.activation(hidT[:, q, :, :], hidT[:, q, :, :], ACT.Relu).then_inc(relu_done, 1)

                rows_out(0, 0)
                hidden_out(0, 0)
                with act.Fori(0, BLOCKS // 2 - 1) as i:
                    rows_out(i, 1)
                    relu(i, 0)
                    hidden_out(i, 1)
                    rows_out(i + 1, 0)
                    relu(i, 1)
                    hidden_out(i + 1, 0)
                rows_out(BLOCKS // 2 - 1, 1)
                relu(BLOCKS // 2 - 1, 0)
                hidden_out(BLOCKS // 2 - 1, 1)
                relu(BLOCKS // 2 - 1, 1)

            @block.vector
            def _(dve):
                dve.sem_inc(bias_added, 1)
                dve.sem_inc(y_done, 1)
                dve.wait_ge(b2_loaded, 16)

                def add_b1(i, q):
                    m = i * 2 + q
                    e = dve.value_load(block_expert[0:1, ds(m, 1)], min_val=0, max_val=EX - 1)
                    dve.wait_ge(h_turned, m + 3)
                    nc.vector.tensor_tensor(hidT[:, q, :, :], ps_t[:],
                                            b1[:, ds(e, 1), :].rearrange("p e m -> p (e m)").unsqueeze(2).to_broadcast([P, KF, P]),
                                            ALU.add).then_inc(bias_added, 1)

                def add_b2(i, q):
                    m = i * 2 + q
                    e = dve.value_load(block_expert[0:1, ds(m, 1)], min_val=0, max_val=EX - 1)
                    dve.wait_ge(y_psum, m + 1)
                    dve.wait_ge(y_stored[q], (i + 1) * 16)
                    nc.vector.tensor_tensor(yrow[:, q, :], ps_y[:], b2[:, ds(e, 1), :].rearrange("p e d -> p (e d)"),
                                            ALU.add).then_inc(y_done, 1)

                add_b1(0, 0)
                with dve.Fori(0, BLOCKS // 2 - 1) as i:
                    add_b2(i, 0)
                    add_b1(i, 1)
                    add_b2(i, 1)
                    add_b1(i + 1, 0)
                add_b2(BLOCKS // 2 - 1, 0)
                add_b1(BLOCKS // 2 - 1, 1)
                add_b2(BLOCKS // 2 - 1, 1)

        with Phase(nc, "moeD") as pd:
            GY = W1[:].rearrange("p e c f -> p (e c f)")[:, 0:CH * D].rearrange("p (j d) -> p j d", d=D)
            ps_f = [pd.ps(f"ps_f{b}", [P, C2, NT]) for b in range(2)]
            gathered = [pd.sem(f"gathered{n}") for n in range(TILES)]
            summed = pd.sem("summed")
            doubled = pd.sem("doubled")
            stats_done = pd.sem("stats_done")
            aggr_done = pd.sem("aggr_done")
            std_done = pd.sem("std_done")
            rstd_done = pd.sem("rstd_done")
            normed = pd.sem("normed")
            turned = pd.sem("turned")
            copied = pd.sem("copied")
            block = pd.block()

            @block.gpsimd
            def _(pool):
                for j in range(CH):
                    nc.gpsimd.indirect_dma_start(GY[:, j, :], None, sorted_out,
                                                 bass.IndirectOffsetOnAxis(pos[:, j:j + 1], 0)).then_inc(gathered[j // TC], 16)

            @block.vector
            def _(dve):
                def add(n):
                    chunks = slice(n * TC, n * TC + TC)
                    dve.wait_ge(gathered[n], 16 * TC)
                    for j in range(n * TC, n * TC + TC):
                        ins = nc.vector.tensor_scalar(GY[:, j, :], GY[:, j, :], alpha[:, j:j + 1], None, ALU.mult)
                    ins.then_inc(summed, 1)
                    dve.wait_ge(summed, n + 1)
                    nc.vector.scalar_tensor_tensor(out=XTM[:, chunks, :], in0=XTM[:, chunks, :], scalar=2.0,
                                                   in1=GY[:, chunks, :], op0=ALU.mult, op1=ALU.add).then_inc(doubled, 1)
                    dve.wait_ge(doubled, n + 1)
                    for j in range(n * TC, n * TC + TC):
                        ins = nc.vector.bn_stats(stats[:, j, :], XTM[:, j, :])
                    ins.then_inc(stats_done, 1)
                    dve.wait_ge(stats_done, n + 1)
                    for j in range(n * TC, n * TC + TC):
                        ins = nc.vector.bn_aggr(MV[:, j, :], stats[:, j, :])
                    ins.then_inc(aggr_done, 1)

                def norm(n):
                    chunks = slice(n * TC, n * TC + TC)
                    dve.wait_ge(std_done, n + 1)
                    nc.vector.reciprocal(rstd[:, chunks], std[:, chunks]).then_inc(rstd_done, 1)
                    dve.wait_ge(rstd_done, n + 1)
                    for j in range(n * TC, n * TC + TC):
                        nc.vector.tensor_scalar(GY[:, j, :], XTM[:, j, :], MV[:, j, 0:1], rstd[:, j:j + 1],
                                                ALU.subtract, ALU.mult).then_inc(normed, 1)

                add(0)
                for n in range(1, TILES):
                    add(n)
                    norm(n - 1)
                norm(TILES - 1)

            @block.scalar
            def _(act):
                def root(n):
                    chunks = slice(n * TC, n * TC + TC)
                    act.wait_ge(aggr_done, n + 1)
                    nc.scalar.activation(std[:, chunks], MV[:, chunks, 1], ACT.Sqrt, bias=epsb[:, 0:1]).then_inc(std_done, 1)

                root(0)
                for n in range(TILES):
                    if n + 1 < TILES:
                        root(n + 1)
                    act.wait_ge(turned, n + 1)
                    nc.scalar.activation(X[:, :, NT * n:NT * n + NT], ps_f[n % 2][:], ACT.Copy).then_inc(copied, 1)

            @block.tensor
            def _(pe):
                for n in range(TILES):
                    pe.wait_ge(normed, TC * (n + 1))
                    if n >= 2:
                        pe.wait_ge(copied, n - 1)
                    for k in range(TC):
                        for c in range(C2):
                            mm = nc.tensor.transpose(ps_f[n % 2][:, c, P * k:P * k + P], GY[:, TC * n + k, P * c:P * c + P], ident[:])
                    mm.then_inc(turned, 1)


def delta_stage(nc, X, ones_mean, ident, w):
    HEADS, HD = 4, D // 4
    TAPS = 4
    HALO = TAPS - 1
    FIRS = (3, 15, 63)
    PAD = FIRS[-1] - 1
    PATHS = 5
    HP = HEADS * PATHS
    CH = TOK // P
    TC = NT // P
    ON_PE = 32
    with Phase(nc, "del") as ph:
        VD = ph.sb("values", [P, C2, BATCH, PAD + SEQ])
        LG = ph.sb("path_logits", [P, CH, HP])
        epsb = ph.sb("epsb", [P, 1])
        epsk = ph.sb("epsk", [P, 1])
        scratch = {n: nc.dram_tensor(f"del_{n}", (D, TOK), F32).ap() for n in ("q", "k", "kb", "vb", "o")}

        with Phase(nc, "delA") as pa:
            W = {n: pa.sb(n, [P, C2, D]) for n in ("q", "k", "v", "b")}
            wb = pa.sb("wb", [P, C2, HEADS])
            conv = {n: pa.sb(f"conv_{n}", [P, C2, TAPS]) for n in "qkv"}
            gate_w = pa.sb("gate_w", [P, C2, HP])
            head_ones = pa.sb("head_ones", [P, P])
            XS = pa.sb("XS", [P, C2, NT])
            pre = {n: [pa.sb(f"pre_{n}{b}", [P, C2, HALO + NT]) for b in range(2)] for n in "qkv"}
            y = {n: [pa.sb(f"y_{n}{b}", [P, C2, NT]) for b in range(2)] for n in "qkv"}
            sig = {n: pa.sb(f"sig_{n}", [P, C2, NT]) for n in "qkv"}
            nrm = {n: pa.sb(f"nrm_{n}", [P, C2, NT]) for n in "qk"}
            beta = [pa.sb(f"beta{b}", [P, C2, NT]) for b in range(2)]
            kb = [pa.sb(f"kb{b}", [P, C2, NT]) for b in range(2)]
            vb = [pa.sb(f"vb{b}", [P, C2, NT]) for b in range(2)]
            slot = [pa.ps(f"slot{s}", [P, C2, NT]) for s in range(4)]
            full = [pa.sem(f"slot_full{s}") for s in range(4)]
            free = [pa.sem(f"slot_free{s}") for s in range(4)]
            USE = {"k": (0, 0), "q": (1, 0), "v": (2, 0), "b": (3, 0), "lg": (0, 1), "ssk": (1, 3), "ssq": (2, 3)}
            PER = [2, 2, 2, 1]
            loaded = pa.sem("loaded")
            consts = pa.sem("consts")
            wb_spread = pa.sem("wb_spread")
            halo_done = pa.sem("halo_done")
            conv_read = pa.sem("conv_read")
            weights_ready = pa.sem("weights_ready")
            x_staged = pa.sem("x_staged")
            projected = {n: pa.sem(f"projected_{n}") for n in "qkv"}
            beta_done = pa.sem("beta_done")
            conv_step = {n: pa.sem(f"conv_step_{n}") for n in "qkv"}
            sig_done = {n: pa.sem(f"sig_done_{n}") for n in "qkv"}
            silu_done = {n: pa.sem(f"silu_done_{n}") for n in "qkv"}
            sq_done = {n: pa.sem(f"sq_done_{n}") for n in "qk"}
            ln_done = {n: pa.sem(f"ln_done_{n}") for n in "qk"}
            rn_done = {n: pa.sem(f"rn_done_{n}") for n in "qk"}
            unit = {n: pa.sem(f"unit_{n}") for n in "qk"}
            kb_done = pa.sem("kb_done")
            vb_done = pa.sem("vb_done")
            lg_done = pa.sem("lg_done")
            stored = [pa.sem(f"stored{b}") for b in range(2)]
            block = pa.block()

            def slot_free(pe, n, key, last=False):
                s, u = USE[key]
                pe.wait_ge(free[s], n * PER[s] + (u + (0 if last else 1)))
                return slot[s], full[s]

            def slot_full(eng, n, key, last=False):
                s, u = USE[key]
                eng.wait_ge(full[s], n * PER[s] + (u + (0 if last else 1)))
                return slot[s], free[s]

            def skewed(eng, begin, finish, first=lambda: None):
                begin(0, 0, 0)
                first()
                with eng.Fori(0, BATCH - 1) as i:
                    begin(i * 2 + 1, i, 1)
                    finish(i * 2, i, 0, False)
                    begin(i * 2 + 2, i + 1, 0)
                    finish(i * 2 + 1, i, 1, False)
                begin(TILES - 1, BATCH - 1, 1)
                finish(TILES - 2, BATCH - 1, 0, False)
                finish(TILES - 1, BATCH - 1, 1, True)

            def buffers_free(eng, i, b):
                eng.wait_ge(stored[b], (i + 1) * 64)

            @block.sync
            def _(sp):
                for n in "qkv":
                    sp.dma_start(W[n][:], w[f"L0_attn_W{n}"].rearrange("(c p) o -> p c o", p=P)).then_inc(loaded, 16)
                    sp.dma_start(conv[n][:], w[f"L0_attn_conv_{n}"].rearrange("(c p) o -> p c o", p=P)).then_inc(loaded, 16)
                sp.dma_start(wb[:], w["L0_attn_Wb"].rearrange("(c p) o -> p c o", p=P)).then_inc(loaded, 16)
                sp.dma_start(gate_w[:], w["L0_attn_gate_w"].rearrange("(c p) o -> p c o", p=P)).then_inc(loaded, 16)
                sp.sem_inc(stored[0], 64)
                sp.sem_inc(stored[1], 64)
                with sp.Fori(0, BATCH) as i:
                    for b in range(2):
                        n = i * 2 + b
                        for name, sem, buf in (("vb", vb_done, vb[b]), ("q", unit["q"], y["q"][b]), ("k", unit["k"], y["k"][b]),
                                               ("kb", kb_done, kb[b])):
                            sp.wait_ge(sem, n + 1)
                            sp.dma_start(scratch[name].rearrange("(c p) t -> p c t", p=P)[:, :, ds(n * NT, NT)],
                                         buf[:]).then_inc(stored[b], 16)
                for b in range(2):
                    sp.wait_ge(stored[b], 64 * (BATCH + 1))

            @block.gpsimd
            def _(pool):
                nc.gpsimd.memset(head_ones[:], 1.0).then_inc(consts, 1)
                nc.gpsimd.memset(VD[:, :, :, 0:PAD], 0.0)
                pool.wait_ge(consts, 1)
                g3 = head_ones[:].rearrange("p (h c) -> p h c", c=HD)
                nc.gpsimd.affine_select(out=g3, in_=g3, compare_op=ALU.is_ge, fill=0.0, base=0,
                                        pattern=[[-HD, P // HD], [0, HD]], channel_multiplier=1).then_inc(consts, 1)
                pool.wait_ge(consts, 2)
                nc.gpsimd.affine_select(out=g3, in_=g3, compare_op=ALU.is_ge, fill=0.0, base=HD - 1,
                                        pattern=[[HD, P // HD], [0, HD]], channel_multiplier=-1).then_inc(consts, 1)

                def begin(n, i, b):
                    pool.wait_ge(lg_done, n + 1)
                    nc.gpsimd.tensor_copy(XS[:], X[:, :, ds(n * NT, NT)]).then_inc(x_staged, 1)

                def finish(n, i, b, last):
                    for key in "kq":
                        pool.wait_ge(sig_done[key], n + 1)
                        nc.gpsimd.tensor_tensor(y[key][b][:], y[key][b][:], sig[key][:], ALU.mult).then_inc(silu_done[key], 1)
                    for key in "kq":
                        pool.wait_ge(rn_done[key], n + 1)
                        nc.gpsimd.tensor_tensor(y[key][b][:], y[key][b][:], nrm[key][:], ALU.mult).then_inc(unit[key], 1)
                    pool.wait_ge(unit["k"], n + 1)
                    pool.wait_ge(beta_done, n + 1)
                    nc.gpsimd.tensor_tensor(kb[b][:], y["k"][b][:], beta[b][:], ALU.mult).then_inc(kb_done, 1)
                skewed(pool, begin, finish)

            @block.tensor
            def _(pe):
                pe.wait_ge(loaded, 16 * 8)
                pe.wait_ge(consts, 3)
                pe.wait_ge(weights_ready, 1)

                def project(n, key):
                    dst, sem = slot_free(pe, n, key)
                    for c in range(C2):
                        for kk in range(C2):
                            mm = nc.tensor.matmul(dst[:, c, :], W[key][:, kk, P * c:P * c + P], X[:, kk, ds(n * NT, NT)],
                                                  start=(kk == 0), stop=(kk == C2 - 1))
                    mm.then_inc(sem, 1)

                def begin(n, i, b):
                    for key in "kqvb":
                        project(n, key)
                    pe.wait_ge(x_staged, n + 1)
                    dst, sem = slot_free(pe, n, "lg")
                    for k in range(TC):
                        for kk in range(C2):
                            mm = nc.tensor.matmul(dst[:, 0, HP * k:HP * k + HP], XS[:, kk, P * k:P * k + P], gate_w[:, kk, :],
                                                  start=(kk == 0), stop=(kk == C2 - 1))
                    mm.then_inc(sem, 1)

                def finish(n, i, b, last):
                    for key in "kq":
                        pe.wait_ge(sq_done[key], n + 1)
                        dst, sem = slot_free(pe, n, "ss" + key, last)
                        for c in range(C2):
                            mm = nc.tensor.matmul(dst[:, c, :], head_ones[:], nrm[key][:, c, :], start=True, stop=True)
                        mm.then_inc(sem, 1)

                def pass_over():
                    for s in (1, 2):
                        pe.wait_ge(free[s], PER[s])
                        pe.sem_inc(full[s], 1)
                        pe.sem_inc(free[s], 1)
                skewed(pe, begin, finish, pass_over)

            @block.scalar
            def _(act):
                act.wait_ge(weights_ready, 1)
                def begin(n, i, b):
                    act.wait_ge(conv_read, n + 1)
                    if b == 0:
                        act.wait_ge(halo_done, i * 3 + 3)
                    for key in "kqv":
                        src, sem = slot_full(act, n, key)
                        nc.scalar.activation(pre[key][b][:, :, HALO:], src[:], ACT.Copy).then_inc(projected[key], 1)
                        act.wait_ge(projected[key], n + 1)
                        act.sem_inc(sem, 1)

                def finish(n, i, b, last):
                    buffers_free(act, i, b)
                    src, sem = slot_full(act, n, "b")
                    nc.scalar.activation(beta[b][:], src[:], ACT.Sigmoid).then_inc(beta_done, 1)
                    act.wait_ge(beta_done, n + 1)
                    act.sem_inc(sem, 1)
                    for key in "kqv":
                        act.wait_ge(conv_step[key], n * TAPS + TAPS)
                        if key == "v":
                            act.wait_ge(silu_done["v"], n + 1)
                        nc.scalar.activation(sig[key][:], y[key][b][:], ACT.Sigmoid).then_inc(sig_done[key], 1)
                    for key in "kq":
                        act.wait_ge(silu_done[key], n + 1)
                        nc.scalar.activation(nrm[key][:], y[key][b][:], ACT.Square).then_inc(sq_done[key], 1)
                    for key in "kq":
                        src, sem = slot_full(act, n, "ss" + key, last)
                        nc.scalar.activation(nrm[key][:], src[:], ACT.Ln, bias=epsk[:, 0:1]).then_inc(ln_done[key], 1)
                    for key in "kq":
                        src, sem = slot_full(act, n, "ss" + key, last)
                        act.wait_ge(ln_done[key], n + 1)
                        act.sem_inc(sem, 1)
                        nc.scalar.activation(nrm[key][:], nrm[key][:], ACT.Exp, scale=-0.5).then_inc(rn_done[key], 1)
                skewed(act, begin, finish)

            @block.vector
            def _(dve):
                nc.vector.memset(epsb[:], EPS)
                nc.vector.memset(epsk[:], 1e-6)
                for key in "qkv":
                    nc.vector.memset(pre[key][0][:, :, 0:HALO], 0.0)
                dve.wait_ge(loaded, 16 * 8)
                nc.vector.tensor_copy(W["b"][:].rearrange("p c (h k) -> p c h k", k=HD),
                                      wb[:].unsqueeze(3).to_broadcast([P, C2, HEADS, HD])).then_inc(wb_spread, 1)
                dve.wait_ge(wb_spread, 1)
                for s in range(4):
                    dve.sem_inc(free[s], 1)
                dve.sem_inc(lg_done, 1)
                dve.sem_inc(halo_done, 3)
                dve.sem_inc(conv_read, 2)
                dve.sem_inc(silu_done["v"], 1)
                dve.sem_inc(weights_ready, 1)
                def begin(n, i, b):
                    buffers_free(dve, i, b)
                    for key in "kqv":
                        dve.wait_ge(projected[key], n + 1)
                        if b == 1:
                            nc.vector.tensor_copy(pre[key][1][:, :, 0:HALO], pre[key][0][:, :, NT:NT + HALO]).then_inc(halo_done, 1)
                    src, sem = slot_full(dve, n, "lg")
                    nc.vector.tensor_copy(LG[:, ds(n * TC, TC), :], src[:, 0, 0:HP * TC].rearrange("p (k g) -> p k g", k=TC)).then_inc(lg_done, 1)
                    dve.wait_ge(lg_done, n + 2)
                    dve.sem_inc(sem, 1)
                    if b == 1:
                        dve.wait_ge(halo_done, i * 3 + 6)
                    for j in range(TAPS):
                        for key in "kqv":
                            if j:
                                dve.wait_ge(conv_step[key], n * TAPS + j)
                            for c in range(C2):
                                src = pre[key][b][:, c, j:j + NT]
                                tap = conv[key][:, c, j:j + 1]
                                dst = y[key][b][:, c, :]
                                if j == 0:
                                    ins = nc.vector.tensor_scalar(dst, src, tap, None, ALU.mult)
                                else:
                                    ins = nc.vector.scalar_tensor_tensor(out=dst, in0=src, scalar=tap, in1=dst,
                                                                         op0=ALU.mult, op1=ALU.add)
                            ins.then_inc(conv_step[key], 1)
                    for key in "kqv":
                        dve.wait_ge(conv_step[key], n * TAPS + TAPS)
                    dve.sem_inc(conv_read, 1)

                def finish(n, i, b, last):
                    dve.wait_ge(sig_done["v"], n + 1)
                    vals = VD[:, :, ds(i, 1), PAD + NT * b:PAD + NT * b + NT].rearrange("p c i t -> p c (i t)")
                    nc.vector.tensor_tensor(vals, y["v"][b][:], sig["v"][:], ALU.mult).then_inc(silu_done["v"], 1)
                    dve.wait_ge(silu_done["v"], n + 2)
                    dve.wait_ge(beta_done, n + 1)
                    nc.vector.tensor_tensor(vb[b][:], vals, beta[b][:], ALU.mult).then_inc(vb_done, 1)
                skewed(dve, begin, finish)

        with Phase(nc, "delBC") as pbc:
            fir_long = pbc.sb("fir_long", [P, C2, FIRS[-1]])
            diag = pbc.sb("diag", [P, ON_PE, C2, P])

            with Phase(nc, "delB") as pb:
                LEVELS = 7
                CHAINS = 2
                CPB = SEQ // P
                SEQS = BATCH // CHAINS
                STEPS = SEQS * CPB
                UP = LEVELS - 1
                TAPS_A_STEP = ON_PE // STEPS
                assert TAPS_A_STEP * STEPS == ON_PE
                flip = pb.sb("level_masks", [P, LEVELS, P])
                low1 = pb.sb("low1", [P, P])
                causal = pb.sb("causal", [P, P])
                chains = lambda name, shape: [pb.sb(f"{name}{a}", shape) for a in range(CHAINS)]
                ink, invb = ([chains(f"in_{n}{q}_", [P, C2, P]) for q in range(2)] for n in ("k", "vb"))
                inq, inkb = ([chains(f"in_{n}{q}_", [P, HEADS, P]) for q in range(2)] for n in ("q", "kb"))
                Lsb, T, TT, attn = (chains(n, [P, HEADS, P]) for n in ("L", "T", "TT", "attn"))
                Wsb = [chains(f"W{l}_", [P, HEADS, P]) for l in range(LEVELS)]
                KV = chains("KV", [P, 2, D])
                S = chains("S", [P, C2, HD])
                Rsb, U = chains("R", [P, HEADS, HD]), chains("U", [P, HEADS, HD])
                Osb = [chains(f"O{q}_", [P, C2, P]) for q in range(2)]
                bankA, bankB, bankC, bankD = ([pb.ps(f"bank{n}{a}", [P, HEADS, P]) for a in range(CHAINS)] for n in "ABCD")
                flat = lambda bank: bank[:].rearrange("p h j -> p (h j)")
                pKV = [flat(x).rearrange("p (x d) -> p x d", x=2) for x in bankD]
                pRU = [flat(x).rearrange("p (x h v) -> p x h v", x=2, h=HEADS) for x in bankD]
                pO = [flat(x)[:, 0:C2 * P].rearrange("p (c t) -> p c t", c=C2) for x in bankD]
                pS = [flat(x)[:, 0:C2 * HD].rearrange("p (c v) -> p c v", c=C2) for x in bankC]

                def columns(ap, l, x):
                    return ap.rearrange("p (m x s) -> p m x s", x=2, s=2 ** l)[:, :, x, :]

                def head_columns(buf, l, x):
                    return buf[:].rearrange("p h (m x s) -> p (h m) x s", x=2, s=2 ** l)[:, :, x, :]

                def packed(bank, l):
                    return flat(bank)[:, 0:HEADS * P // 2].rearrange("p (m s) -> p m s", s=2 ** l)

                def packed_head(bank, h, l):
                    return flat(bank)[:, h * P // 2:(h + 1) * P // 2].rearrange("p (m s) -> p m s", s=2 ** l)
                masks = pb.sem("masks")
                pads_zero = pb.sem("pads_zero")
                in_loaded = [[pb.sem(f"in_loaded{q}_{a}") for a in range(CHAINS)] for q in range(2)]
                o_stored = [[pb.sem(f"o_stored{q}_{a}") for a in range(CHAINS)] for q in range(2)]
                l_psum, qk_psum, l_copied, kv_copied, tt_begun, tt_start, t_begun, t_start = (
                    pb.sem(n) for n in ("l_psum", "qk_psum", "l_copied", "kv_copied", "tt_begun", "tt_start", "t_begun", "t_start"))
                w_psum, w_masked, d_psum, dt_psum, tt_done, t_done = (
                    pb.sem(n) for n in ("w_psum", "w_masked", "d_psum", "dt_psum", "tt_done", "t_done"))
                r_psum, r_done, u_psum, u_copied, so_psum, s_done, s_zero, o_copied = (
                    pb.sem(n) for n in ("r_psum", "r_done", "u_psum", "u_copied", "so_psum", "s_done", "s_zero", "o_copied"))
                fir_loaded = pb.sem("fir_loaded")
                block = pb.block()

                once = lambda m, a: m * CHAINS + (a + 1)
                level = lambda m, l, a, ups=UP: m * (ups * CHAINS) + ((l - 1) * CHAINS + a + 1)

                def steps(eng, body, new_sequence=lambda: None):
                    for s in range(SEQS):
                        new_sequence()
                        tail = 1 if s == SEQS - 1 else 0
                        with eng.Fori(0, CPB // 2 - tail) as i:
                            for q in range(2):
                                body(i * 2 + (s * CPB + q), i + s * CPB // 2, q, False)
                    body(STEPS - 2, STEPS // 2 - 1, 0, False)
                    body(STEPS - 1, STEPS // 2 - 1, 1, True)

                def chunk_in_dram(name, m, a):
                    return scratch[name].rearrange("(c p) t -> p c t", p=P)[:, :, ds((m + a * STEPS) * P, P)]

                @block.sync
                def _(sp):
                    def load(m, q, a):
                        for name, buf in (("k", ink), ("vb", invb)):
                            sp.dma_start(buf[q][a][:], chunk_in_dram(name, m, a)).then_inc(in_loaded[q][a], 16)
                        for name, buf in (("q", inq), ("kb", inkb)):
                            for r in range(2):
                                rows = slice(HD * r, HD * r + HD)
                                sp.dma_start(buf[q][a][rows, r::2, :], chunk_in_dram(name, m, a)[rows, :, :]).then_inc(in_loaded[q][a], 16)

                    def store(m, q, a):
                        sp.wait_ge(o_copied, once(m + 1, a))
                        sp.dma_start(chunk_in_dram("o", m, a), Osb[q][a][:]).then_inc(o_stored[q][a], 16)

                    sp.dma_start(fir_long[:], w["L0_attn_fir_l"].rearrange("(c p) o -> p c o", p=P)).then_inc(fir_loaded, 16)
                    sp.wait_ge(pads_zero, 4 * CHAINS)
                    for q in range(2):
                        for a in range(CHAINS):
                            load(q, q, a)
                            sp.sem_inc(o_stored[q][a], 16)
                    with sp.Fori(0, STEPS // 2 - 1) as i:
                        for q in range(2):
                            for a in range(CHAINS):
                                sp.wait_ge(so_psum, once(i * 2 + q, a))
                                load(i * 2 + (q + 2), q, a)
                            for a in range(CHAINS):
                                store(i * 2 + q, q, a)
                    for q in range(2):
                        for a in range(CHAINS):
                            store(STEPS - 2 + q, q, a)
                    for q in range(2):
                        for a in range(CHAINS):
                            sp.wait_ge(o_stored[q][a], 16 * (STEPS // 2 + 1))

                @block.gpsimd
                def _(pool):
                    nc.gpsimd.memset(flip[:], 0.0).then_inc(masks, 1)
                    nc.gpsimd.memset(low1[:], 0.0).then_inc(masks, 1)
                    nc.gpsimd.memset(causal[:], 1.0).then_inc(masks, 1)
                    pool.wait_ge(masks, 3)
                    m = 3
                    for l in range(LEVELS):
                        s = 2 ** l
                        odd = flip[:, l, :].rearrange("p (m x s) -> p m x s", x=2, s=s)[:, :, 1, :]
                        pairs = P // (2 * s)
                        nc.gpsimd.memset(odd, -1.0).then_inc(masks, 1)
                        m += 1
                        pool.wait_ge(masks, m)
                        for base, sign in ((0, 1), (s - 1, -1)):
                            nc.gpsimd.affine_select(out=odd, in_=odd, compare_op=ALU.is_ge, fill=0.0, base=base,
                                                    pattern=[[-2 * s * sign, pairs], [0, s]], channel_multiplier=sign).then_inc(masks, 1)
                            m += 1
                            pool.wait_ge(masks, m)
                    even = low1[:].rearrange("p (m x) -> p m x", x=2)[:, :, 0]
                    nc.gpsimd.memset(even, -1.0).then_inc(masks, 1)
                    pool.wait_ge(masks, m + 1)
                    nc.gpsimd.affine_select(out=even, in_=even, compare_op=ALU.is_equal, fill=0.0, base=-1,
                                            pattern=[[-2, P // 2]], channel_multiplier=1).then_inc(masks, 1)
                    nc.gpsimd.affine_select(out=causal[:], in_=causal[:], compare_op=ALU.is_ge, fill=0.0, base=0,
                                            pattern=[[1, P]], channel_multiplier=-1).then_inc(masks, 1)
                    pool.wait_ge(masks, m + 3)
                    bc = lambda ap: ap.unsqueeze(1).to_broadcast([P, HEADS, P])
                    with pool.Fori(0, STEPS) as m:
                        for a in range(CHAINS):
                            pool.wait_ge(l_copied, once(m, a))
                            nc.gpsimd.tensor_tensor(T[a][:], Lsb[a][:], bc(low1[:]), ALU.mult).then_inc(t_begun, 1)
                        for a in range(CHAINS):
                            pool.wait_ge(t_begun, once(m, a))
                            nc.gpsimd.tensor_tensor(T[a][:], T[a][:], bc(ident[:]), ALU.add).then_inc(t_start, 1)
                MASKS = 3 + 3 * LEVELS + 3

                @block.tensor
                def _(pe):
                    def hp(h):
                        return slice(HD * (h % 2), HD * (h % 2) + HD), h // 2

                    def grams_l(m, half, q):
                        for a in range(CHAINS):
                            pe.wait_ge(in_loaded[q][a], half * 96 + 96)
                            for h in range(HEADS):
                                nc.tensor.matmul(bankA[a][:, h, :], inkb[q][a][:, h, :], ink[q][a][:, h // 2, :], start=True, stop=True)
                            for c in range(C2):
                                mm = nc.tensor.matmul(bankB[a][:, 2 * c:2 * c + 2, :], ink[q][a][:, c, :], inkb[q][a][:, 2 * c:2 * c + 2, :],
                                                      start=True, stop=True)
                            mm.then_inc(l_psum, 1)

                    def body(m, half, q, last):
                        for a in range(CHAINS):
                            pe.wait_ge(s_done, once(m, a))
                            pe.wait_ge(o_copied, once(m, a))
                            for c in range(C2):
                                nc.tensor.matmul(bankC[a][:, 2 * c:2 * c + 2, :], ink[q][a][:, c, :], inq[q][a][:, 2 * c:2 * c + 2, :],
                                                 start=True, stop=True)
                            for x, src in enumerate((ink, invb)):
                                for c in range(C2):
                                    mm = nc.tensor.transpose(pKV[a][:, x, P * c:P * c + P], src[q][a][:, c, :], ident[:])
                            mm.then_inc(qk_psum, 1)
                        for l in range(1, LEVELS):
                            for a in range(CHAINS):
                                if l == 1:
                                    pe.wait_ge(l_copied, once(m, a))
                                    pe.wait_ge(tt_start, once(m, a))
                                else:
                                    pe.wait_ge(tt_done, level(m, l - 1, a))
                                for h in range(HEADS):
                                    mm = nc.tensor.matmul(packed_head(bankA[a], h, l), Lsb[a][:, h, :], columns(TT[a][:, h, :], l, 1),
                                                          start=True, stop=True)
                                mm.then_inc(w_psum, 1)
                            if l == 1:
                                for a in range(CHAINS):
                                    pe.wait_ge(kv_copied, once(m, a))
                                    pe.wait_ge(s_zero, sequence[0])
                                    for h in range(HEADS):
                                        mm = nc.tensor.matmul(pRU[a][:, 0, h, :], inkb[q][a][:, h, :], S[a][:, h // 2, :], start=True, stop=True)
                                    mm.then_inc(r_psum, 1)
                            for a in range(CHAINS):
                                if l == 1:
                                    pe.wait_ge(t_start, once(m, a))
                                else:
                                    pe.wait_ge(t_done, level(m, l - 1, a, UP - 1))
                                pe.wait_ge(w_masked, level(m, l, a))
                                for h in range(HEADS):
                                    mm = nc.tensor.matmul(packed_head(bankB[a], h, l), T[a][:, h, :], columns(Wsb[l][a][:, h, :], l, 1),
                                                          start=True, stop=True)
                                mm.then_inc(d_psum, 1)
                            if l < UP:
                                for a in range(CHAINS):
                                    for h in range(HEADS):
                                        mm = nc.tensor.matmul(packed_head(bankC[a], h, l), Wsb[l][a][:, h, :], columns(T[a][:, h, :], l, 0),
                                                              start=True, stop=True)
                                    mm.then_inc(dt_psum, 1)
                        for a in range(CHAINS):
                            pe.wait_ge(r_done, once(m, a))
                            pe.wait_ge(tt_done, level(m, UP, a))
                            for h in range(HEADS):
                                mm = nc.tensor.matmul(pRU[a][:, 1, h, :], TT[a][:, h, :], Rsb[a][:, h, :], start=True, stop=True)
                            mm.then_inc(u_psum, 1)
                        if not last:
                            grams_l(m + 1, half + q, 1 - q)
                        for a in range(CHAINS):
                            pe.wait_ge(u_copied, once(m, a))
                            for h in range(HEADS):
                                r, c = hp(h)
                                nc.tensor.matmul(pS[a][r, c, :], KV[a][:, 0, HD * h:HD * h + HD], U[a][:, h, :], start=True, stop=True)
                            for h in range(HEADS):
                                r, c = hp(h)
                                nc.tensor.matmul(pO[a][r, c, :], S[a][:, c, :], inq[q][a][:, h, :], start=True, stop=False)
                                mm = nc.tensor.matmul(pO[a][r, c, :], U[a][:, h, :], attn[a][:, h, :], start=False, stop=True)
                            mm.then_inc(so_psum, 1)

                    sequence = [0]

                    def new_sequence():
                        sequence[0] += 1
                    grams_l(0, 0, 0)
                    steps(pe, body, new_sequence)

                @block.scalar
                def _(act):
                    def copy_l(m):
                        for a in range(CHAINS):
                            act.wait_ge(l_psum, once(m, a))
                            nc.scalar.activation(Lsb[a][:], bankA[a][:], ACT.Copy).then_inc(l_copied, 1)

                    def body(m, half, q, last):
                        for a in range(CHAINS):
                            act.wait_ge(qk_psum, once(m, a))
                            nc.scalar.activation(KV[a][:], pKV[a], ACT.Copy).then_inc(kv_copied, 1)
                        for x in range(TAPS_A_STEP):
                            for c in range(C2):
                                j = ds(m * TAPS_A_STEP + x, 1)
                                nc.scalar.activation(diag[:, j, c, :].rearrange("p j k -> p (j k)"), ident[:], ACT.Copy,
                                                     scale=fir_long[:, c, j])
                        for a in range(CHAINS):
                            act.wait_ge(u_psum, once(m, a))
                            nc.scalar.activation(U[a][:], pRU[a][:, 1, :, :], ACT.Copy).then_inc(u_copied, 1)
                        if not last:
                            copy_l(m + 1)
                        for a in range(CHAINS):
                            act.wait_ge(so_psum, once(m, a))
                            act.wait_ge(o_stored[q][a], half * 16 + 16)
                            nc.scalar.activation(Osb[q][a][:], pO[a], ACT.Copy).then_inc(o_copied, 1)
                    act.sem_inc(o_copied, CHAINS)
                    act.wait_ge(fir_loaded, 16)
                    copy_l(0)
                    steps(act, body)

                @block.vector
                def _(dve):
                    bc = lambda ap: ap.unsqueeze(1).to_broadcast([P, HEADS, P])
                    for q in range(2):
                        for buf in inq[q] + inkb[q]:
                            nc.vector.memset(buf[:], 0.0).then_inc(pads_zero, 1)
                    for l in range(1, LEVELS):
                        for a in range(CHAINS):
                            nc.vector.memset(Wsb[l][a][:], 0.0)
                    dve.wait_ge(masks, MASKS)
                    dve.sem_inc(s_done, CHAINS)

                    def start(m):
                        for a in range(CHAINS):
                            dve.wait_ge(l_psum, once(m, a))
                            nc.vector.tensor_tensor(TT[a][:], bankB[a][:], bc(flip[:, 0, :]), ALU.mult).then_inc(tt_begun, 1)
                        for a in range(CHAINS):
                            dve.wait_ge(tt_begun, once(m, a))
                            nc.vector.tensor_tensor(TT[a][:], TT[a][:], bc(ident[:]), ALU.add).then_inc(tt_start, 1)

                    def body(m, half, q, last):
                        for a in range(CHAINS):
                            dve.wait_ge(qk_psum, once(m, a))
                            nc.vector.tensor_tensor(attn[a][:], bankC[a][:], bc(causal[:]), ALU.mult)
                        for l in range(1, LEVELS):
                            for a in range(CHAINS):
                                dve.wait_ge(w_psum, level(m, l, a))
                                flips = columns(flip[:, l, :], l, 1).unsqueeze(1).to_broadcast([P, HEADS, P >> (l + 1), 1 << l])
                                nc.vector.tensor_tensor(Wsb[l][a][:].rearrange("p h (m x s) -> p h m x s", x=2, s=2 ** l)[:, :, :, 1, :],
                                                        packed(bankA[a], l).rearrange("p (h m) s -> p h m s", h=HEADS), flips,
                                                        ALU.mult).then_inc(w_masked, 1)
                            if l == 1:
                                for a in range(CHAINS):
                                    dve.wait_ge(r_psum, once(m, a))
                                    nc.vector.tensor_tensor(Rsb[a][:], KV[a][:, 1, :].rearrange("p (h v) -> p h v", h=HEADS),
                                                            pRU[a][:, 0, :, :], ALU.subtract).then_inc(r_done, 1)
                            for a in range(CHAINS):
                                dve.wait_ge(d_psum, level(m, l, a))
                                part = head_columns(TT[a], l, 1)
                                nc.vector.tensor_tensor(part, part, packed(bankB[a], l), ALU.add).then_inc(tt_done, 1)
                            if l < UP:
                                for a in range(CHAINS):
                                    dve.wait_ge(dt_psum, level(m, l, a, UP - 1))
                                    part = head_columns(T[a], l, 0)
                                    nc.vector.tensor_tensor(part, part, packed(bankC[a], l), ALU.add).then_inc(t_done, 1)
                        if not last:
                            start(m + 1)
                        for a in range(CHAINS):
                            dve.wait_ge(so_psum, once(m, a))
                            nc.vector.tensor_tensor(S[a][:], S[a][:], pS[a], ALU.add).then_inc(s_done, 1)

                    sequence = [0]

                    def new_sequence():
                        dve.wait_ge(s_done, once(sequence[0] * CPB, CHAINS - 1))
                        for a in range(CHAINS):
                            ins = nc.vector.memset(S[a][:], 0.0)
                        ins.then_inc(s_zero, 1)
                        sequence[0] += 1
                    start(0)
                    steps(dve, body, new_sequence)

            with Phase(nc, "delC") as pc:
                ON_DVE = FIRS[-1] - ON_PE
                Wo = pc.sb("Wo", [P, C2, D])
                fir = [pc.sb(f"fir{k}", [P, C2, k]) for k in FIRS[:2]] + [fir_long]
                norm_w = pc.sb("norm_w", [P, 1])
                gate_b = pc.sb("gate_b", [P, HP])
                ltemp = pc.sb("log_temp", [P, HEADS])
                epar = pc.sb("eps_param", [P, HEADS])
                keep = pc.sb("keep", [P, HEADS])
                smax = pc.sb("smax", [P, CH, HEADS])
                mean_ones = pc.sb("head_mean", [P, P])
                PRt = pc.sb("PRt", [P, TC, HP])
                PRT = pc.sb("PRT", [HP, NT])
                sel = pc.sb("sel", [HP, PATHS, C2, P])
                PB = pc.sb("PB", [P, PATHS, C2, NT])
                Od = pc.sb("Od", [P, C2, NT])
                acc = [pc.sb(f"acc{k}", [P, C2, NT]) for k in FIRS]
                mix = pc.sb("mix", [P, C2, NT])
                SQ = pc.sb("SQ", [P, C2, NT])
                rr = pc.sb("rr", [P, C2, NT])
                ps_f = pc.ps("ps_f", [P, C2, NT])
                ps_p = [pc.ps(f"ps_p{b}", [P, C2, NT]) for b in range(2)]
                ps_a = pc.ps("ps_a", [P, C2, NT])
                loaded = pc.sem("loaded")
                consts = pc.sem("consts")
                prep = pc.sem("prep")
                act_prep = pc.sem("act_prep")
                ready = pc.sem("ready")
                od_loaded = pc.sem("od_loaded")
                pr_staged = pc.sem("pr_staged")
                pr_turned = pc.sem("pr_turned")
                prt_ready = pc.sem("prt_ready")
                spread = pc.sem("spread")
                pb_copied = pc.sem("pb_copied")
                fir_psum = pc.sem("fir_psum")
                fir_read = pc.sem("fir_read")
                tap = [pc.sem(f"tap{c}") for c in range(C2)]
                pool_mix = pc.sem("pool_mix")
                mix_step = pc.sem("mix_step")
                mix_added = pc.sem("mix_added")
                mix_done = pc.sem("mix_done")
                squared = pc.sem("squared")
                stat_psum = pc.sem("stat_psum")
                ln_done = pc.sem("ln_done")
                rr_done = pc.sem("rr_done")
                on_done = pc.sem("on_done")
                o_psum = pc.sem("o_psum")
                resid = pc.sem("resid")
                mean_psum = pc.sem("mean_psum")
                centred = pc.sem("centred")
                x_done = pc.sem("x_done")
                block = pc.block()

                PARTS = 5

                def tiles(eng, prologue, body):
                    prologue()
                    with eng.Fori(0, BATCH - 1) as i:
                        body(i * 2, (i * 2 + 1, i, 1))
                        body(i * 2 + 1, (i * 2 + 2, i + 1, 0))
                    body(TILES - 2, (TILES - 1, BATCH - 1, 1))
                    body(TILES - 1, None)

                @block.sync
                def _(sp):
                    sp.dma_start(Wo[:], w["L0_attn_Wo"].rearrange("(c p) o -> p c o", p=P)).then_inc(loaded, 16)
                    for k, n in enumerate(("s", "m")):
                        sp.dma_start(fir[k][:], w[f"L0_attn_fir_{n}"].rearrange("(c p) o -> p c o", p=P)).then_inc(loaded, 16)
                    for r in range(2):
                        sp.dma_start(norm_w[HD * r:HD * r + HD, :], w["L0_attn_norm_w"]).then_inc(loaded, 16)
                    for t, n in ((gate_b, "gate_b"), (ltemp, "log_temp"), (epar, "eps_param")):
                        sp.dma_start(t[:], w[f"L0_attn_{n}"].to_broadcast(t.shape)).then_inc(loaded, 16)
                    with sp.Fori(0, TILES) as n:
                        sp.wait_ge(mix_done, n + 1)
                        sp.dma_start(Od[:], scratch["o"].rearrange("(c p) t -> p c t", p=P)[:, :, ds(n * NT, NT)]).then_inc(od_loaded, 16)

                @block.gpsimd
                def _(pool):
                    nc.gpsimd.memset(mean_ones[:], 1.0 / HD).then_inc(consts, 1)
                    pool.wait_ge(consts, 1)
                    g3 = mean_ones[:].rearrange("p (h c) -> p h c", c=HD)
                    nc.gpsimd.affine_select(out=g3, in_=g3, compare_op=ALU.is_ge, fill=0.0, base=0,
                                            pattern=[[-HD, P // HD], [0, HD]], channel_multiplier=1).then_inc(consts, 1)
                    pool.wait_ge(consts, 2)
                    nc.gpsimd.affine_select(out=g3, in_=g3, compare_op=ALU.is_ge, fill=0.0, base=HD - 1,
                                            pattern=[[HD, P // HD], [0, HD]], channel_multiplier=-1).then_inc(consts, 1)
                    nc.gpsimd.memset(sel[:], 1.0).then_inc(consts, 1)
                    pool.wait_ge(consts, 4)
                    sel5 = sel[:].rearrange("r p c (h f) -> r p c h f", h=2)
                    for p in range(PATHS):
                        nc.gpsimd.affine_select(out=sel5[:, p], in_=sel5[:, p], compare_op=ALU.is_equal, fill=0.0, base=-p,
                                                pattern=[[-2 * PATHS, C2], [-PATHS, 2], [0, HD]], channel_multiplier=1).then_inc(consts, 1)
                    pool.wait_ge(ready, 1)
                    with pool.Fori(0, BATCH) as i:
                        for b in range(2):
                            n = i * 2 + b
                            pool.wait_ge(pr_turned, n + 1)
                            nc.gpsimd.tensor_copy(PRt[:], LG[:, ds(n * TC, TC), :]).then_inc(pr_staged, 1)
                            pool.wait_ge(od_loaded, n * 16 + 16)
                            pool.wait_ge(pb_copied, n * PATHS + PATHS)
                            nc.gpsimd.tensor_tensor(Od[:], Od[:], PB[:, 3, :, :], ALU.mult).then_inc(pool_mix, 1)
                            vals = VD[:, :, ds(i, 1), PAD + NT * b:PAD + NT * b + NT].rearrange("p c i t -> p c (i t)")
                            nc.gpsimd.tensor_tensor(PB[:, 4, :, :], vals, PB[:, 4, :, :], ALU.mult).then_inc(pool_mix, 1)
                            pool.wait_ge(pool_mix, n * 3 + 2)
                            nc.gpsimd.tensor_tensor(Od[:], Od[:], PB[:, 4, :, :], ALU.add).then_inc(pool_mix, 1)

                @block.tensor
                def _(pe):
                    pe.wait_ge(ready, 1)
                    pe.sem_inc(pr_turned, 1)
                    pairs = [(c, j) for c in range(C2) for j in range(ON_PE)]
                    cuts = [len(pairs) * part // PARTS for part in range(PARTS + 1)]

                    def filters(nxt, part):
                        if nxt is None:
                            return
                        n, seq, half = nxt
                        if part == 0:
                            pe.wait_ge(fir_read, n + 1)
                        for c, j in pairs[cuts[part]:cuts[part + 1]]:
                            win = VD[:, c:c + 1, ds(seq, 1), NT * half + j:NT * half + j + NT].rearrange("p c i t -> p (c i t)")
                            mm = nc.tensor.matmul(ps_f[:, c, :], diag[:, j, c, :], win, start=(j == 0), stop=(j == ON_PE - 1))
                        if part == PARTS - 1:
                            mm.then_inc(fir_psum, 1)

                    def weights(nxt, first=False):
                        if nxt is None:
                            return
                        n = nxt[0]
                        pe.wait_ge(pr_staged, n + 1)
                        if not first:
                            pe.wait_ge(pb_copied, n * PATHS)
                        for k in range(TC):
                            mm = nc.tensor.transpose(ps_p[1][0:HP, 0, P * k:P * k + P], PRt[:, k, :], ident[:])
                        mm.then_inc(pr_turned, 1)
                        pe.wait_ge(prt_ready, n + 1)
                        for p in range(PATHS):
                            if p >= 2:
                                pe.wait_ge(pb_copied, n * PATHS + (p - 1))
                            for c in range(C2):
                                mm = nc.tensor.matmul(ps_p[p % 2][:, c, :], sel[:, p, c, :], PRT[:], start=True, stop=True)
                            mm.then_inc(spread, 1)

                    def prologue():
                        nxt = (0, 0, 0)
                        weights(nxt, first=True)
                        for part in range(PARTS):
                            filters(nxt, part)

                    def body(n, nxt):
                        filters(nxt, 0)
                        pe.wait_ge(squared, n * 2 + 1)
                        for c in range(C2):
                            mm = nc.tensor.matmul(ps_a[:, c, :], mean_ones[:], SQ[:, c, :], start=True, stop=True)
                        mm.then_inc(stat_psum, 1)
                        filters(nxt, 1)
                        pe.wait_ge(on_done, n + 1)
                        for c in range(C2):
                            for kk in range(C2):
                                mm = nc.tensor.matmul(ps_a[:, c, :], Wo[:, kk, P * c:P * c + P], mix[:, kk, :],
                                                      start=(kk == 0), stop=(kk == C2 - 1))
                        mm.then_inc(o_psum, 1)
                        filters(nxt, 2)
                        pe.wait_ge(resid, n + 1)
                        for kk in range(C2):
                            mm = nc.tensor.matmul(ps_a[:, 0, :], ones_mean[:], mix[:, kk, :], start=(kk == 0), stop=(kk == C2 - 1))
                        mm.then_inc(mean_psum, 1)
                        filters(nxt, 3)
                        pe.wait_ge(squared, n * 2 + 2)
                        for kk in range(C2):
                            mm = nc.tensor.matmul(ps_a[:, 1, :], ones_mean[:], SQ[:, kk, :], start=(kk == 0), stop=(kk == C2 - 1))
                        mm.then_inc(stat_psum, 1)
                        weights(nxt)
                        filters(nxt, 4)
                    tiles(pe, prologue, body)

                @block.scalar
                def _(act):
                    act.wait_ge(prep, 3)
                    act.wait_ge(loaded, 16 * 8)
                    nc.scalar.activation(ltemp[:], ltemp[:], ACT.Exp, scale=-1.0).then_inc(act_prep, 1)
                    act.wait_ge(prep, 6)
                    nc.scalar.activation(LG[:], LG[:], ACT.Exp).then_inc(act_prep, 1)

                    def weights(nxt):
                        if nxt is None:
                            return
                        n = nxt[0]
                        act.wait_ge(pr_turned, n + 2)
                        nc.scalar.activation(PRT[:], ps_p[1][0:HP, 0, :], ACT.Copy).then_inc(prt_ready, 1)
                        act.wait_ge(mix_done, n + 1)
                        for p in range(PATHS):
                            act.wait_ge(spread, n * PATHS + (p + 1))
                            nc.scalar.activation(PB[:, p, :, :], ps_p[p % 2][:], ACT.Copy).then_inc(pb_copied, 1)

                    def body(n, nxt):
                        act.wait_ge(mix_done, n + 2)
                        nc.scalar.activation(SQ[:], mix[:], ACT.Square).then_inc(squared, 1)
                        act.wait_ge(stat_psum, n * 2 + 1)
                        nc.scalar.activation(rr[:], ps_a[:], ACT.Ln, bias=epsb[:, 0:1]).then_inc(ln_done, 1)
                        act.wait_ge(ln_done, n * 2 + 1)
                        nc.scalar.activation(rr[:], rr[:], ACT.Exp, scale=-0.5).then_inc(rr_done, 1)
                        act.wait_ge(centred, n + 1)
                        nc.scalar.activation(SQ[:], mix[:], ACT.Square).then_inc(squared, 1)
                        act.wait_ge(stat_psum, n * 2 + 2)
                        nc.scalar.activation(rr[:, 0, :], ps_a[:, 1, :], ACT.Ln, bias=epsb[:, 0:1]).then_inc(ln_done, 1)
                        act.wait_ge(ln_done, n * 2 + 2)
                        nc.scalar.activation(rr[:, 0, :], rr[:, 0, :], ACT.Exp, scale=-0.5).then_inc(rr_done, 1)
                        weights(nxt)
                    tiles(act, lambda: weights((0, 0, 0)), body)

                @block.vector
                def _(dve):
                    lg = LG[:].rearrange("p j (h x) -> p j h x", h=HEADS)
                    per_head = lambda ap: ap.unsqueeze(1).to_broadcast([P, CH, HEADS]).unsqueeze(3).to_broadcast([P, CH, HEADS, PATHS])
                    n_prep = [0]

                    def then(ins):
                        n_prep[0] += 1
                        ins.then_inc(prep, 1)
                        dve.wait_ge(prep, n_prep[0])

                    dve.wait_ge(loaded, 16 * 8)
                    then(nc.vector.tensor_scalar(epar[:], epar[:], 0.0, 0.2, ALU.max, ALU.min))
                    then(nc.vector.tensor_scalar(keep[:], epar[:], -float(PATHS), 1.0, ALU.mult, ALU.add))
                    then(nc.vector.tensor_tensor(LG[:], LG[:], gate_b[:].unsqueeze(1).to_broadcast([P, CH, HP]), ALU.add))
                    dve.wait_ge(act_prep, 1)
                    for h in range(HEADS):
                        ins = nc.vector.tensor_scalar(lg[:, :, h, :], lg[:, :, h, :], ltemp[:, h:h + 1], None, ALU.mult)
                    then(ins)
                    then(nc.vector.tensor_reduce(smax[:], lg, AX.X, ALU.max))
                    then(nc.vector.tensor_tensor(lg, lg, smax[:].unsqueeze(3).to_broadcast([P, CH, HEADS, PATHS]), ALU.subtract))
                    dve.wait_ge(act_prep, 2)
                    then(nc.vector.tensor_reduce(smax[:], lg, AX.X, ALU.add))
                    then(nc.vector.reciprocal(smax[:], smax[:]))
                    then(nc.vector.tensor_tensor(lg, lg, smax[:].unsqueeze(3).to_broadcast([P, CH, HEADS, PATHS]), ALU.mult))
                    for h in range(HEADS):
                        ins = nc.vector.tensor_scalar(lg[:, :, h, :], lg[:, :, h, :], keep[:, h:h + 1], epar[:, h:h + 1], ALU.mult, ALU.add)
                    then(ins)
                    for c in range(C2):
                        ins = nc.vector.tensor_scalar(Wo[:, c, :], Wo[:, c, :], norm_w[:, 0:1], None, ALU.mult)
                    then(ins)
                    dve.wait_ge(consts, 4 + PATHS)
                    dve.sem_inc(ready, 1)
                    dve.sem_inc(mix_done, 1)
                    dve.sem_inc(fir_read, 1)
                    counts = [FIRS[0], FIRS[1], ON_DVE]
                    ROUNDS = max(counts)
                    def filters(nxt, part):
                        if nxt is None:
                            return
                        n, seq, half = nxt
                        for j in range(ROUNDS)[CUTS[part]:CUTS[part + 1]]:
                            for c in range(C2):
                                if j:
                                    dve.wait_ge(tap[c], n * ROUNDS + j)
                                for f, k in enumerate(FIRS):
                                    if j >= counts[f]:
                                        continue
                                    first = ON_PE if f == 2 else 0
                                    o = PAD - (k - 1) + first + j + NT * half
                                    src = VD[:, c:c + 1, ds(seq, 1), o:o + NT].rearrange("p c i t -> p (c i t)")
                                    dst = acc[f][:, c, :]
                                    wt = fir[f][:, c, first + j:first + j + 1]
                                    if j == 0:
                                        ins = nc.vector.tensor_scalar(dst, src, wt, None, ALU.mult)
                                    else:
                                        ins = nc.vector.scalar_tensor_tensor(out=dst, in0=src, scalar=wt, in1=dst,
                                                                             op0=ALU.mult, op1=ALU.add)
                                ins.then_inc(tap[c], 1)
                    taps_by = [sum(min(j, x) for x in counts) for j in range(ROUNDS + 1)]
                    CUTS = [next(j for j in range(ROUNDS + 1) if taps_by[j] * PARTS >= sum(counts) * part) for part in range(PARTS + 1)]

                    def prologue():
                        for part in range(PARTS):
                            filters((0, 0, 0), part)

                    def body(n, nxt):
                        tile = X[:, :, ds(n * NT, NT)]
                        for c in range(C2):
                            dve.wait_ge(tap[c], n * ROUNDS + ROUNDS)
                        dve.wait_ge(fir_psum, n + 1)
                        dve.wait_ge(pb_copied, n * PATHS + PATHS)
                        nc.vector.tensor_tensor(acc[2][:], acc[2][:], ps_f[:], ALU.add).then_inc(mix_step, 1)
                        nc.vector.tensor_tensor(acc[0][:], acc[0][:], PB[:, 0, :, :], ALU.mult)
                        nc.vector.tensor_tensor(acc[1][:], acc[1][:], PB[:, 1, :, :], ALU.mult).then_inc(mix_step, 1)
                        dve.wait_ge(mix_step, n * 4 + 1)
                        dve.sem_inc(fir_read, 1)
                        nc.vector.tensor_tensor(acc[2][:], acc[2][:], PB[:, 2, :, :], ALU.mult).then_inc(mix_step, 1)
                        dve.wait_ge(mix_step, n * 4 + 2)
                        nc.vector.tensor_tensor(acc[0][:], acc[0][:], acc[1][:], ALU.add).then_inc(mix_step, 1)
                        dve.wait_ge(pool_mix, n * 3 + 3)
                        dve.wait_ge(mix_step, n * 4 + 3)
                        nc.vector.tensor_tensor(mix[:], acc[2][:], Od[:], ALU.add).then_inc(mix_added, 1)
                        dve.wait_ge(mix_step, n * 4 + 4)
                        dve.wait_ge(mix_added, n + 1)
                        nc.vector.tensor_tensor(mix[:], mix[:], acc[0][:], ALU.add).then_inc(mix_done, 1)
                        dve.wait_ge(mix_done, n + 2)
                        filters(nxt, 0)
                        dve.wait_ge(rr_done, n * 2 + 1)
                        nc.vector.tensor_tensor(mix[:], mix[:], rr[:], ALU.mult).then_inc(on_done, 1)
                        filters(nxt, 1)
                        dve.wait_ge(o_psum, n + 1)
                        nc.vector.tensor_tensor(mix[:], ps_a[:], tile, ALU.add).then_inc(resid, 1)
                        filters(nxt, 2)
                        dve.wait_ge(resid, n + 1)
                        dve.wait_ge(mean_psum, n + 1)
                        nc.vector.tensor_tensor(mix[:], mix[:], ps_a[:, 0, :].unsqueeze(1).to_broadcast([P, C2, NT]),
                                                ALU.subtract).then_inc(centred, 1)
                        filters(nxt, 3)
                        dve.wait_ge(centred, n + 1)
                        dve.wait_ge(rr_done, n * 2 + 2)
                        nc.vector.tensor_tensor(tile, mix[:], rr[:, 0, :].unsqueeze(1).to_broadcast([P, C2, NT]),
                                                ALU.mult).then_inc(x_done, 1)
                        dve.wait_ge(x_done, n + 1)
                        filters(nxt, 4)
                    tiles(dve, prologue, body)


def lora_ffn_stage(nc, X, ones_mean, w):
    FF = 1024
    KF = FF // P
    HALFM = KF // 2
    RANK = 16
    MAGIC = 1.5 * 2.0 ** 23
    with Phase(nc, "ffn") as ph:
        w_fc = ph.sb("w_fc", [P, C2, FF])
        w_pr = ph.sb("w_pr", [P, KF, D])
        a_fc = ph.sb("a_fc", [RANK, D])
        bt_fc = ph.sb("bt_fc", [RANK, FF])
        a_pr = ph.sb("a_pr", [RANK, FF])
        bt_pr = ph.sb("bt_pr", [RANK, D])
        b_fc = ph.sb("b_fc", [P, KF])
        b_pr = ph.sb("b_pr", [P, C2])
        amax = ph.sb("amax", [P, 2])
        amax_all = ph.sb("amax_all", [P, 2])
        qstep = ph.sb("qstep", [P, 2])
        qinv = ph.sb("qinv", [P, 2])
        H = ph.sb("H", [P, KF, NT])
        R = ph.sb("R", [P, C2, NT])
        XC = ph.sb("XC", [P, C2, NT])
        SQ = ph.sb("SQ", [P, C2, NT])
        std = ph.sb("std", [P, NT])
        rstd = ph.sb("rstd", [P, NT])
        epsb = ph.sb("epsb", [P, 1])
        ps_h = [ph.ps(f"ps_h{b}", [P, NT]) for b in range(4)]
        ps_y = [ph.ps(f"ps_y{c}", [P, NT]) for c in range(C2)]
        ps_mean = ph.ps("ps_mean", [P, NT])
        ps_var = ph.ps("ps_var", [P, NT])
        loaded = ph.sem("loaded")
        dve_prep = ph.sem("dve_prep")
        amax_ready = ph.sem("amax_ready")
        fold_ready = ph.sem("fold_ready")
        fold_used = ph.sem("fold_used")
        weights_ready = ph.sem("weights_ready")
        h_psum = ph.sem("h_psum")
        h_done = ph.sem("h_done")
        y_psum = ph.sem("y_psum")
        resid = ph.sem("resid")
        mean_psum = ph.sem("mean_psum")
        centred = ph.sem("centred")
        squared = ph.sem("squared")
        var_psum = ph.sem("var_psum")
        std_done = ph.sem("std_done")
        rstd_done = ph.sem("rstd_done")
        x_done = ph.sem("x_done")
        block = ph.block()
        folds = [(w_fc[:, c, 512 * n:512 * n + 512], a_fc[:, P * c:P * c + P], bt_fc[:, 512 * n:512 * n + 512])
                 for c in range(C2) for n in range(FF // 512)]
        folds += [(w_pr[:, m, :], a_pr[:, P * m:P * m + P], bt_pr[:, :]) for m in range(KF)]

        @block.sync
        def _(sp):
            sp.dma_start(w_fc[:], w["L1_ffn_W_fc"].rearrange("(c p) f -> p c f", p=P)).then_inc(loaded, 16)
            sp.dma_start(w_pr[:], w["L1_ffn_W_proj"].rearrange("(c p) f -> p c f", p=P)).then_inc(loaded, 16)
            sp.dma_start(a_fc[:], w["L1_ffn_A_fc"]).then_inc(loaded, 16)
            sp.dma_start(bt_fc[:], w["L1_ffn_B_fc"]).then_inc(loaded, 16)
            sp.dma_start(a_pr[:], w["L1_ffn_A_proj"]).then_inc(loaded, 16)
            sp.dma_start(bt_pr[:], w["L1_ffn_B_proj"]).then_inc(loaded, 16)
            sp.dma_start(b_fc[:], w["L1_ffn_b_fc"]).then_inc(loaded, 16)
            sp.dma_start(b_pr[:], w["L1_ffn_b_proj"]).then_inc(loaded, 16)

        @block.gpsimd
        def _(pool):
            pool.wait_ge(dve_prep, 3)
            nc.gpsimd.partition_all_reduce(amax_all[:], amax[:], P, bass.bass_isa.ReduceOp.max).then_inc(amax_ready, 1)

        @block.tensor
        def _(pe):
            pe.wait_ge(loaded, 16 * 8)
            for n, (dst, a, bt) in enumerate(folds):
                if n >= 4:
                    pe.wait_ge(fold_used, n - 3)
                size = dst.shape[-1]
                nc.tensor.matmul(ps_h[n % 4][:, 0:size], a, bt, start=True, stop=True).then_inc(fold_ready, 1)
            pe.wait_ge(weights_ready, 1)

            def up(i, m0, m1):
                for m in range(m0, m1):
                    pe.wait_ge(h_done, i * KF + m + 1)
                    for c in range(C2):
                        mm = nc.tensor.matmul(ps_h[m % 4][:], w_fc[:, c, P * m:P * m + P], X[:, c, ds(i * NT, NT)],
                                              start=(c == 0), stop=(c == C2 - 1))
                    mm.then_inc(h_psum, 1)

            def down(i):
                pe.wait_ge(resid, C2 * i + 1)
                for c in range(C2):
                    for m in range(KF):
                        if c == 0:
                            pe.wait_ge(h_done, i * KF + m + 5)
                        mm = nc.tensor.matmul(ps_y[c][:], w_pr[:, m, P * c:P * c + P], H[:, m, :],
                                              start=(m == 0), stop=(m == KF - 1))
                    mm.then_inc(y_psum, 1)

            def mean(i):
                pe.wait_ge(resid, C2 * (i + 1) + 1)
                for c in range(C2):
                    mm = nc.tensor.matmul(ps_mean[:], ones_mean[:], R[:, c, :], start=(c == 0), stop=(c == C2 - 1))
                mm.then_inc(mean_psum, 1)

            def var(i):
                pe.wait_ge(squared, i + 1)
                for c in range(C2):
                    mm = nc.tensor.matmul(ps_var[:], ones_mean[:], SQ[:, c, :], start=(c == 0), stop=(c == C2 - 1))
                mm.then_inc(var_psum, 1)

            up(0, 0, KF)
            with pe.Fori(0, TILES - 1) as i:
                down(i)
                up(i + 1, 0, HALFM)
                mean(i)
                up(i + 1, HALFM, KF)
                var(i)
            down(TILES - 1)
            mean(TILES - 1)
            var(TILES - 1)

        @block.scalar
        def _(act):
            act.sem_inc(h_done, 4)

            def gelu(i, m0, m1):
                for m in range(m0, m1):
                    act.wait_ge(h_psum, i * KF + m + 1)
                    if m == 0:
                        act.wait_ge(y_psum, C2 * i + 2)
                    nc.scalar.activation(H[:, m, :], ps_h[m % 4][:], ACT.Gelu, bias=b_fc[:, m:m + 1]).then_inc(h_done, 1)

            def squares(i):
                act.wait_ge(centred, i + 1)
                act.wait_ge(var_psum, i + 1)
                nc.scalar.activation(SQ[:], XC[:], ACT.Square).then_inc(squared, 1)

            def roots(i):
                act.wait_ge(var_psum, i + 2)
                nc.scalar.activation(std[:], ps_var[:], ACT.Sqrt, bias=epsb[:, 0:1]).then_inc(std_done, 1)

            act.sem_inc(y_psum, C2)
            act.sem_inc(var_psum, 1)
            act.wait_ge(weights_ready, 1)
            gelu(0, 0, KF)
            with act.Fori(0, TILES - 1) as i:
                gelu(i + 1, 0, HALFM)
                squares(i)
                gelu(i + 1, HALFM, KF)
                roots(i)
            squares(TILES - 1)
            roots(TILES - 1)

        @block.vector
        def _(dve):
            nc.vector.memset(epsb[:], EPS).then_inc(dve_prep, 1)
            dve.wait_ge(loaded, 16 * 8)
            nc.vector.tensor_reduce(amax[:, 0:1], w_fc[:], AX.XY, ALU.max, apply_absolute_value=True).then_inc(dve_prep, 1)
            nc.vector.tensor_reduce(amax[:, 1:2], w_pr[:], AX.XY, ALU.max, apply_absolute_value=True).then_inc(dve_prep, 1)
            dve.wait_ge(amax_ready, 1)
            nc.vector.tensor_scalar(qstep[:], amax_all[:], 1.0 / 127.0, None, ALU.mult).then_inc(dve_prep, 1)
            dve.wait_ge(dve_prep, 4)
            nc.vector.reciprocal(qinv[:], qstep[:]).then_inc(dve_prep, 1)
            dve.wait_ge(dve_prep, 5)
            for n, W in enumerate((w_fc, w_pr)):
                nc.vector.tensor_scalar(W[:], W[:], qinv[:, n:n + 1], MAGIC, ALU.mult, ALU.add).then_inc(dve_prep, 1)
                dve.wait_ge(dve_prep, 6 + 3 * n)
                nc.vector.tensor_scalar(W[:], W[:], -MAGIC, 127.0, ALU.add, ALU.min).then_inc(dve_prep, 1)
                dve.wait_ge(dve_prep, 7 + 3 * n)
                nc.vector.tensor_scalar(W[:], W[:], -128.0, qstep[:, n:n + 1], ALU.max, ALU.mult).then_inc(dve_prep, 1)
                dve.wait_ge(dve_prep, 8 + 3 * n)
            for n, (dst, a, bt) in enumerate(folds):
                dve.wait_ge(fold_ready, n + 1)
                size = dst.shape[-1]
                nc.vector.scalar_tensor_tensor(out=dst, in0=ps_h[n % 4][:, 0:size], scalar=2.0, in1=dst,
                                               op0=ALU.mult, op1=ALU.add).then_inc(fold_used, 1)
            dve.wait_ge(fold_used, len(folds))
            dve.sem_inc(weights_ready, 1)
            dve.sem_inc(resid, 1)
            dve.sem_inc(mean_psum, 1)

            def tail(i):
                for c in range(C2):
                    dve.wait_ge(y_psum, C2 * i + C2 + c + 1)
                    dve.wait_ge(mean_psum, i + 1)
                    nc.vector.scalar_tensor_tensor(out=R[:, c, :], in0=ps_y[c][:], scalar=b_pr[:, c:c + 1],
                                                   in1=X[:, c, ds(i * NT, NT)], op0=ALU.add, op1=ALU.add).then_inc(resid, 1)
                dve.wait_ge(mean_psum, i + 2)
                dve.wait_ge(resid, C2 * (i + 1) + 1)
                nc.vector.tensor_tensor(XC[:], R[:], ps_mean[:].unsqueeze(1).to_broadcast([P, C2, NT]),
                                        ALU.subtract).then_inc(centred, 1)
                dve.wait_ge(std_done, i + 1)
                nc.vector.reciprocal(rstd[:], std[:]).then_inc(rstd_done, 1)
                dve.wait_ge(rstd_done, i + 1)
                nc.vector.tensor_tensor(X[:, :, ds(i * NT, NT)], XC[:], rstd[:].unsqueeze(1).to_broadcast([P, C2, NT]),
                                        ALU.mult).then_inc(x_done, 1)
            with dve.Fori(0, TILES) as i:
                tail(i)


def program(nc, w, out):
    with Phase(nc, "top") as top:
        X = top.sb("x_stream", [P, C2, TOK])
        ones_mean = top.sb("ones_mean", [P, P])
        ident = top.sb("ident", [P, P])
        zeros = top.sb("zeros", [P, D])
        zeros_written = top.sem("zeros_written")
        BLOCK_ROWS = 40 * P
        sorted_in = nc.dram_tensor("sorted_in", (BLOCK_ROWS, D), F32).ap()
        sorted_out = nc.dram_tensor("sorted_out", (BLOCK_ROWS, D), F32).ap()
        with Phase(nc, "load") as ph:
            x_loaded = ph.sem("x_loaded")
            zeroed = ph.sem("zeroed")
            zeros_set = ph.sem("zeros_set")
            block = ph.block()

            @block.sync
            def _(sp):
                sp.dma_start(X[:], w["x"].rearrange("(c p) t -> p c t", p=P)).then_inc(x_loaded, 16)
                sp.wait_ge(zeros_set, 1)
                sp.dma_start(sorted_in.rearrange("(m p) d -> p m d", p=P),
                             zeros[:].unsqueeze(1).to_broadcast([P, BLOCK_ROWS // P, D])).then_inc(zeros_written, 16)
                sp.wait_ge(x_loaded, 16)

            @block.vector
            def _(dve):
                nc.vector.memset(zeros[:], 0.0).then_inc(zeros_set, 1)
                nc.vector.memset(ones_mean[:], 1.0 / D)

            @block.gpsimd
            def _(pool):
                nc.gpsimd.memset(ident[:], 0.0).then_inc(zeroed, 1)
                pool.wait_ge(zeroed, 1)
                nc.gpsimd.affine_select(out=ident[:], in_=ident[:], compare_op=ALU.not_equal, fill=1.0, base=0,
                                        pattern=[[-1, P]], channel_multiplier=1)

        delta_stage(nc, X, ones_mean, ident, w)
        cross_attention_stage(nc, X, ones_mean, ident, w, gated=True)
        expert_stage(nc, X, ones_mean, ident, w, sorted_in, sorted_out, zeros_written)
        recurrence_stage(nc, X, ones_mean, ident, w)
        cross_attention_stage(nc, X, ones_mean, ident, w, gated=False)
        lora_ffn_stage(nc, X, ones_mean, w)

        with Phase(nc, "store") as ph:
            stored = ph.sem("stored")
            block = ph.block()

            @block.sync
            def _(sp):
                sp.dma_start(out.rearrange("(c p) t -> p c t", p=P), X[:]).then_inc(stored, 16)
                sp.wait_ge(stored, 16)


def _layout(name, a):
    import numpy as _np
    if name == "x":
        return a.reshape(TOK, D).T
    if name == "ctx_1024":
        return a.reshape(-1, D).T
    if name in TRANSPOSED:
        return a.T
    if name in ("L0_ffn_w1", "L0_ffn_w2"):
        return a.transpose(0, 2, 1)
    if name in ("L0_ffn_ln_g", "L0_ffn_ln_b", "L0_ffn_b1"):
        return a.reshape(a.shape[0], -1, P).transpose(2, 0, 1)
    if name == "L0_attn_gate_w":
        return a.reshape(-1, D).T
    if name.startswith("L0_attn_fir"):
        return a.reshape(D, -1)
    if name == "L0_attn_norm_w":
        return a.reshape(-1, 1)
    if name in ("L0_attn_gate_b", "L0_attn_log_temp", "L0_attn_eps_param"):
        return a.reshape(1, -1)
    if name in PARTITIONED:
        return a.reshape(-1, P).T
    return a


TRANSPOSED = ("L0_attn_Wq", "L0_attn_Wk", "L0_attn_Wv", "L0_attn_Wb", "L0_attn_Wo", "L0_xattn_Wq", "L0_xattn_Wk",
              "L0_xattn_Wv", "L0_xattn_Wg", "L0_xattn_Wo", "L0_ffn_centroids", "L1_attn_Wf1", "L1_attn_Wog1",
              "L1_xattn_Wq", "L1_xattn_Wk", "L1_xattn_Wv", "L1_xattn_Wo",
              "L1_ffn_W_fc", "L1_ffn_B_fc", "L1_ffn_W_proj", "L1_ffn_B_proj")
PARTITIONED = ("L1_ffn_b_fc", "L1_ffn_b_proj", "L1_xattn_bq", "L1_xattn_bk", "L1_xattn_bv", "L1_xattn_bo",
               "L0_xattn_qln_g", "L0_xattn_qln_b", "L0_xattn_kvln_g", "L0_xattn_kvln_b", "L0_xattn_bg",
               "L1_attn_norm_w")


def kernel(**inputs):
    import numpy as _np
    import concourse.bacc as _bacc
    from concourse import mybir as _mybir
    from concourse.bass_utils import run_bass_kernel_spmd as _run

    nc = _bacc.Bacc("TRN2", target_bir_lowering=False, num_devices=1)
    arrays, w = {}, {}
    for name, a in inputs.items():
        a = _np.ascontiguousarray(_layout(name, _np.asarray(a)))
        arrays[f"in_{name}"] = a
        w[name] = nc.dram_tensor(f"in_{name}", a.shape, _mybir.dt.from_np(a.dtype), kind="ExternalInput").ap()
    out = nc.dram_tensor("out_x", (D, TOK), F32, kind="ExternalOutput").ap()
    program(nc, w, out)
    r = _run(nc, [arrays], core_ids=[0])
    return _np.ascontiguousarray(_np.asarray(r.results[0]["out_x"]).reshape(D, BATCH, SEQ).transpose(1, 2, 0))
```
